# Optimizing a Trainium2 kernel written in Bass

```python
import numpy as np
import jax
import jax.numpy as jnp

def _softmax(x, axis=-1):
    return jax.nn.softmax(x, axis=axis)

def _gelu(x):
    return jax.nn.gelu(x, approximate=True)

def _silu(x):
    return jax.nn.silu(x)

def _sigmoid(x):
    return jax.nn.sigmoid(x)

def _layernorm(x, axis=-1, eps=1e-05):
    m = jnp.mean(x, axis=axis, keepdims=True)
    v = jnp.var(x, axis=axis, keepdims=True)
    return (x - m) / jnp.sqrt(v + eps)

def _scatter_add(tgt, idx, src, axis=0):
    return tgt.at[idx].add(src)

def _segment_sum(src, seg, n):
    return jax.ops.segment_sum(src, seg, n)
kernel_name = 'mk_xattn_ffn_d4_seqx_r8_3784f4'

def setup_inputs(seed: int=0):
    np.random.seed(seed)
    _w = jnp.asarray

    def _rec_inputs():
        import jax
        import jax.numpy as jnp
        _rk = jax.random.key(seed)
        x = -0.0003929 + 0.9999 * jax.random.normal(jax.random.fold_in(_rk, 1), (8, 256, 128), jnp.float32)
        _lenS = 256 - jax.random.randint(jax.random.fold_in(_rk, 7), (8,), 0, max(1, 256 // 4) + 1, jnp.int32)
        _lenS2 = 512 - jax.random.randint(jax.random.fold_in(_rk, 8), (8,), 0, max(1, 512 // 4) + 1, jnp.int32)
        _ctx_1024P = jax.random.normal(jax.random.fold_in(_rk, 11), (8, 16, 128), jnp.float32)
        _ctx_1024c = jax.random.dirichlet(jax.random.fold_in(_rk, 511), 0.3 * jnp.ones((16,), jnp.float32), (8, 512))
        _ctx_1024t = jnp.einsum('bsk,bkd->bsd', _ctx_1024c, _ctx_1024P)
        _ctx_1024t = _ctx_1024t * jax.lax.rsqrt(jnp.mean(jnp.square(_ctx_1024t)) + 1e-12) * 0.953939
        ctx_1024 = 4.13588e-05 + 0.999923 * (_ctx_1024t + 0.3 * jax.random.normal(jax.random.fold_in(_rk, 611), (8, 512, 128), jnp.float32))
        fside_BxS2_0 = -0.00600047 + 0.990131 * jax.random.normal(jax.random.fold_in(_rk, 14), (8, 512), jnp.float32)
        _validS = jnp.arange(256)[None, :] < _lenS[:, None]
        _validS2 = jnp.arange(512)[None, :] < _lenS2[:, None]
        _causal = jnp.tril(jnp.ones((256, 256), dtype=bool))
        mask_Bx1xSxS2_ik0 = jnp.where(jnp.broadcast_to(_validS2[:, None, None, :], (8, 1, 256, 512)), 0, 1).astype(jnp.int32)
        mask_BxS2_bf1 = jnp.ones((8, 512), dtype=bool)
        return (x, ctx_1024, fside_BxS2_0, mask_Bx1xSxS2_ik0, mask_BxS2_bf1)
    x, ctx_1024, fside_BxS2_0, mask_Bx1xSxS2_ik0, mask_BxS2_bf1 = _rec_inputs()

    def _L0_xattn_setup():
        import jax, jax.numpy as jnp
        import numpy as np
        key = jax.random.key(seed)
        k1, k2 = jax.random.split(key)
        B, L, V, D = (8, 256, 128, 128)
        hidden_states = jax.random.normal(k1, (B, L, D), dtype=jnp.float32)
        visual_hidden_state = jax.random.normal(k2, (B, V, D), dtype=jnp.float32)
        return {'hidden_states': hidden_states, 'visual_hidden_state': visual_hidden_state}
    _L0_xattn_all = _L0_xattn_setup()
    _L0_xattn_in = {k: v for k, v in _L0_xattn_all.items() if k in ()}
    del _L0_xattn_all

    def _L0_ffn_setup():
        import jax, jax.numpy as jnp
        import numpy as np
        IN_F, OUT_F, BLOCK, NBLK = (128, 512, 32, 16)
        TOPK = NBLK // 4
        key = jax.random.key(seed)
        ks = jax.random.split(key, 7)
        s = 1.0 / np.sqrt(IN_F)
        s2 = 1.0 / np.sqrt(OUT_F)
        return {'x': jax.random.normal(ks[0], (4, 512, IN_F), jnp.float32), 'router_w': jax.random.uniform(ks[1], (NBLK, IN_F), jnp.float32, -s, s), 'router_b': jax.random.uniform(ks[2], (NBLK,), jnp.float32, -s, s), 'w1': jax.random.uniform(ks[3], (OUT_F, IN_F), jnp.float32, -s, s), 'b1': jax.random.uniform(ks[4], (OUT_F,), jnp.float32, -s, s), 'w2': jax.random.uniform(ks[5], (IN_F, OUT_F), jnp.float32, -s2, s2), 'b2': jax.random.uniform(ks[6], (IN_F,), jnp.float32, -s2, s2)}
    _L0_ffn_all = _L0_ffn_setup()
    _L0_ffn_in = {k: v for k, v in _L0_ffn_all.items() if k in ('router_w', 'router_b', 'w1', 'b1', 'w2', 'b2')}
    del _L0_ffn_all

    def _L1_xattn_setup():
        import jax, jax.numpy as jnp
        import numpy as np
        N, L, E, H = (2, 256, 128, 16)
        D = E // H
        key = jax.random.key(seed)
        ks = jax.random.split(key, 8)
        s = 0.02
        values = jax.random.normal(ks[0], (N, L, E), jnp.float32)
        keys_t = jax.random.normal(ks[1], (N, L, E), jnp.float32)
        query = jax.random.normal(ks[2], (N, L, E), jnp.float32)
        mask = jnp.tril(jnp.ones((L, L), jnp.int32))[None, None].repeat(N, axis=0)
        Wv = jax.random.normal(ks[3], (E, E), jnp.float32) * s
        Wk = jax.random.normal(ks[4], (E, E), jnp.float32) * s
        Wq = jax.random.normal(ks[5], (E, E), jnp.float32) * s
        Wo = jax.random.normal(ks[6], (E, E), jnp.float32) * s
        bo = jnp.zeros((E,), jnp.float32)
        return {'values': values, 'keys': keys_t, 'query': query, 'mask': mask, 'Wv': Wv, 'Wk': Wk, 'Wq': Wq, 'Wo': Wo, 'bo': bo}
    _L1_xattn_all = _L1_xattn_setup()
    _L1_xattn_in = {k: v for k, v in _L1_xattn_all.items() if k in ('Wv', 'Wk', 'Wq', 'Wo', 'bo')}
    del _L1_xattn_all

    def _L1_ffn_setup():
        import jax, jax.numpy as jnp
        import numpy as np
        EPS_NORM = 1e-08
        EPS_Q = 1e-05

        def rmsnorm(x, w):
            v = jnp.mean(jnp.square(x.astype(jnp.float32)), axis=-1, keepdims=True)
            x_hat = x * jax.lax.rsqrt(v + EPS_NORM)
            return (x_hat * w).astype(x.dtype)

        def activation_quant(x):
            scale = 127.0 / jnp.clip(jnp.max(jnp.abs(x), axis=-1, keepdims=True), EPS_Q, None)
            return jnp.clip(jnp.round(x * scale), -128, 127) / scale

        def weight_quant(w):
            scale = 1.0 / jnp.clip(jnp.mean(jnp.abs(w)), EPS_Q, None)
            return jnp.clip(jnp.round(w * scale), -1, 1) / scale

        def bitlinear(x, norm_w, w):
            x_norm = rmsnorm(x, norm_w)
            x_q = x_norm + jax.lax.stop_gradient(activation_quant(x_norm) - x_norm)
            w_q = w + jax.lax.stop_gradient(weight_quant(w) - w)
            return jnp.einsum('bsd,hd->bsh', x_q, w_q)
        key = jax.random.key(seed)
        k1, k2, k3 = jax.random.split(key, 3)
        dim, hidden = (128, 512)
        return {'x': jax.random.normal(k1, (4, 256, dim), dtype=jnp.float32), 'norm1_w': jnp.ones((dim,), jnp.float32), 'w1': jax.random.normal(k2, (hidden, dim), jnp.float32) * 0.02, 'act_scale': jnp.ones((1,), jnp.float32), 'act_bias': jnp.zeros((1,), jnp.float32), 'norm2_w': jnp.ones((hidden,), jnp.float32), 'w2': jax.random.normal(k3, (dim, hidden), jnp.float32) * 0.02}
    _L1_ffn_all = _L1_ffn_setup()
    _L1_ffn_in = {k: v for k, v in _L1_ffn_all.items() if k in ('norm1_w', 'w1', 'act_scale', 'act_bias', 'norm2_w', 'w2')}
    del _L1_ffn_all

    def _L2_xattn_setup():
        import jax, jax.numpy as jnp
        import numpy as np
        HEADS = 16
        DIM_HEAD = 64
        SCALE = DIM_HEAD ** (-0.5)
        key = jax.random.key(seed)
        ks = jax.random.split(key, 6)
        B, Nq, Nkv, D = (4, 256, 128, 128)
        inner = HEADS * DIM_HEAD
        return {'x': jax.random.normal(ks[0], (B, Nq, D), dtype=jnp.float32), 'context': jax.random.normal(ks[1], (B, Nkv, D), dtype=jnp.float32), 'mask': jnp.ones((B, Nkv), dtype=bool), 'Wq': jax.random.normal(ks[2], (inner, D), dtype=jnp.float32) * D ** (-0.5), 'Wkv': jax.random.normal(ks[3], (2 * inner, D), dtype=jnp.float32) * D ** (-0.5), 'Wout': jax.random.normal(ks[4], (D, inner), dtype=jnp.float32) * inner ** (-0.5), 'b_out': jnp.zeros((D,), dtype=jnp.float32)}
    _L2_xattn_all = _L2_xattn_setup()
    _L2_xattn_in = {k: v for k, v in _L2_xattn_all.items() if k in ('Wq', 'Wkv', 'Wout', 'b_out')}
    del _L2_xattn_all

    def _L2_ffn_setup():
        import jax, jax.numpy as jnp
        import numpy as np
        DIM = 128
        DEPTH = 2
        HEADS = 8
        DIM_HEAD = 64
        WINDOW = 64
        INNER = HEADS * DIM_HEAD
        HID = int(DIM * 4 * 2 / 3)
        B, N = (2, 1024)
        QK_SCALE = 8.0

        def shift_token(t):
            t1, t2 = jnp.split(t, 2, axis=-1)
            t2 = jnp.pad(t2, ((0, 0), (1, 0), (0, 0)))[:, :-1]
            return jnp.concatenate([t1, t2], axis=-1)

        def l2norm(t):
            return t / jnp.clip(jnp.linalg.norm(t, axis=-1, keepdims=True), 1e-12)

        def rotate_half(x):
            x1, x2 = jnp.split(x, 2, axis=-1)
            return jnp.concatenate([-x2, x1], axis=-1)

        def rotary_xpos(q, k):
            n = q.shape[-2]
            half_idx = jnp.arange(0, DIM_HEAD, 2, dtype=jnp.float32)
            inv_freq = 1.0 / 10000.0 ** (half_idx / DIM_HEAD)
            t = jnp.arange(n, dtype=jnp.float32)
            freqs = t[:, None] * inv_freq[None, :]
            freqs = jnp.concatenate([freqs, freqs], axis=-1)
            base = (half_idx + 0.4 * DIM_HEAD) / (1.4 * DIM_HEAD)
            power = (t - n // 2) / float(WINDOW // 2)
            scale = base[None, :] ** power[:, None]
            scale = jnp.concatenate([scale, scale], axis=-1)
            cos, sin = (jnp.cos(freqs), jnp.sin(freqs))
            q = q * cos * scale + rotate_half(q) * sin * scale
            k = k * cos / scale + rotate_half(k) * sin / scale
            return (q, k)

        def local_attention(q, k, v):
            b, h, n, d = q.shape
            w = n // WINDOW
            bq = q.reshape(b, h, w, WINDOW, d) * QK_SCALE
            bk = k.reshape(b, h, w, WINDOW, d)
            bv = v.reshape(b, h, w, WINDOW, d)

            def look_around(t):
                p = jnp.pad(t, ((0, 0), (0, 0), (1, 0), (0, 0), (0, 0)))
                return jnp.concatenate([p[:, :, :w], p[:, :, 1:]], axis=3)
            bk, bv = (look_around(bk), look_around(bv))
            bt = jnp.arange(n).reshape(w, WINDOW)
            btp = jnp.pad(bt, ((1, 0), (0, 0)), constant_values=-1)
            btk = jnp.concatenate([btp[:w], btp[1:]], axis=1)
            sim = jnp.einsum('bhwid,bhwjd->bhwij', bq, bk)
            i = bt[:, :, None]
            j = btk[:, None, :]
            mask = (i < j) | (i > j + WINDOW) | (j == -1)
            sim = jnp.where(mask, -jnp.finfo(sim.dtype).max, sim)
            attn = jax.nn.softmax(sim, axis=-1)
            out = jnp.einsum('bhwij,bhwjd->bhwid', attn, bv)
            return out.reshape(b, h, n, d)

        def _layer(x, wqkv, qs, ksc, wo, lg, lb, w1, b1, w2, b2):
            b, n, _ = x.shape
            h = shift_token(x)
            qkv = h @ wqkv
            q, k, v = jnp.split(qkv, 3, axis=-1)
            to_heads = lambda t: t.reshape(b, n, HEADS, DIM_HEAD).transpose(0, 2, 1, 3)
            q, k, v = (to_heads(q), to_heads(k), to_heads(v))
            q = l2norm(q) * qs
            k = l2norm(k) * ksc
            q, k = rotary_xpos(q, k)
            o = local_attention(q, k, v)
            o = o.transpose(0, 2, 1, 3).reshape(b, n, INNER)
            x = x + o @ wo
            h = shift_token(x)
            mu = h.mean(-1, keepdims=True)
            var = h.var(-1, keepdims=True)
            h = (h - mu) / jnp.sqrt(var + 1e-05) * lg + lb
            h = h @ w1 + b1
            a, g = jnp.split(h, 2, axis=-1)
            h = a * jax.nn.gelu(g, approximate=False)
            x = x + h @ w2 + b2
            return x
        key = jax.random.key(seed)
        ks = jax.random.split(key, 6)
        return {'x': jax.random.normal(ks[0], (B, N, DIM), jnp.float32), 'wqkv': jax.random.normal(ks[1], (DEPTH, DIM, 3 * INNER), jnp.float32) * 0.02, 'q_scale': jnp.ones((DEPTH, DIM_HEAD), jnp.float32), 'k_scale': jnp.ones((DEPTH, DIM_HEAD), jnp.float32), 'wo': jax.random.normal(ks[2], (DEPTH, INNER, DIM), jnp.float32) * 0.02, 'ln_g': jnp.ones((DEPTH, DIM), jnp.float32), 'ln_b': jnp.zeros((DEPTH, DIM), jnp.float32), 'w1': jax.random.normal(ks[3], (DEPTH, DIM, 2 * HID), jnp.float32) * 0.02, 'b1': jnp.zeros((DEPTH, 2 * HID), jnp.float32), 'w2': jax.random.normal(ks[4], (DEPTH, HID, DIM), jnp.float32) * 0.02, 'b2': jnp.zeros((DEPTH, DIM), jnp.float32)}
    _L2_ffn_all = _L2_ffn_setup()
    _L2_ffn_in = {k: v for k, v in _L2_ffn_all.items() if k in ('wqkv', 'q_scale', 'k_scale', 'wo', 'ln_g', 'ln_b', 'w1', 'b1', 'w2', 'b2')}
    del _L2_ffn_all

    def _L3_xattn_setup():
        import jax, jax.numpy as jnp
        import numpy as np
        D_MODEL = 128
        NUM_HEADS = 16
        DEPTH = D_MODEL // NUM_HEADS
        TEMPERATURE = 1.0
        B, S = (2, 256)

        def _split_heads(x):
            b, s, _ = x.shape
            return x.reshape(b, s, NUM_HEADS, DEPTH).transpose(0, 2, 1, 3)
        key = jax.random.key(seed)
        ks = jax.random.split(key, 13)
        s = 1.0 / np.sqrt(D_MODEL)
        return {'query': jax.random.normal(ks[0], (B, S, D_MODEL), jnp.float32), 'key': jax.random.normal(ks[1], (B, S, D_MODEL), jnp.float32), 'value': jax.random.normal(ks[2], (B, S, D_MODEL), jnp.float32), 'temporal_bias': jax.random.normal(ks[3], (B, S), jnp.float32), 'wq': jax.random.normal(ks[4], (D_MODEL, D_MODEL), jnp.float32) * s, 'bq': jnp.zeros((D_MODEL,), jnp.float32), 'wk': jax.random.normal(ks[5], (D_MODEL, D_MODEL), jnp.float32) * s, 'bk': jnp.zeros((D_MODEL,), jnp.float32), 'wv': jax.random.normal(ks[6], (D_MODEL, D_MODEL), jnp.float32) * s, 'bv': jnp.zeros((D_MODEL,), jnp.float32), 'wo': jax.random.normal(ks[7], (D_MODEL, D_MODEL), jnp.float32) * s, 'bo': jnp.zeros((D_MODEL,), jnp.float32)}
    _L3_xattn_all = _L3_xattn_setup()
    _L3_xattn_in = {k: v for k, v in _L3_xattn_all.items() if k in ('wq', 'bq', 'wk', 'bk', 'wv', 'bv', 'wo', 'bo')}
    del _L3_xattn_all

    def _L3_ffn_setup():
        import jax, jax.numpy as jnp
        import numpy as np
        QMAX = 127.0

        def _ste_round(v):
            return v + jax.lax.stop_gradient(jnp.round(v) - v)

        def _act_fake_quant(x, clip_factor):
            scale = jax.nn.sigmoid(clip_factor) * jnp.max(jnp.abs(x)) / QMAX
            return jnp.clip(_ste_round(x / scale), -QMAX - 1.0, QMAX) * scale

        def _weight_fake_quant(w):
            scale = jnp.max(jnp.abs(w), axis=1, keepdims=True) / QMAX
            return jnp.clip(_ste_round(w / scale), -QMAX - 1.0, QMAX) * scale
        key = jax.random.key(seed)
        k1, k2, k3, k4 = jax.random.split(key, 4)
        B, S, H, I = (8, 1024, 128, 352)
        return {'x': jax.random.normal(k1, (B, S, H), dtype=jnp.float32), 'clip_x': jnp.full((1,), 4.0, dtype=jnp.float32), 'clip_down': jnp.full((1,), 4.0, dtype=jnp.float32), 'w_gate': jax.random.normal(k2, (I, H), dtype=jnp.float32) * 0.02, 'w_up': jax.random.normal(k3, (I, H), dtype=jnp.float32) * 0.02, 'w_down': jax.random.normal(k4, (H, I), dtype=jnp.float32) * 0.02}
    _L3_ffn_all = _L3_ffn_setup()
    _L3_ffn_in = {k: v for k, v in _L3_ffn_all.items() if k in ('clip_x', 'clip_down', 'w_gate', 'w_up', 'w_down')}
    del _L3_ffn_all
    return {'x': x, 'ctx_1024': ctx_1024, 'fside_BxS2_0': fside_BxS2_0, 'mask_Bx1xSxS2_ik0': mask_Bx1xSxS2_ik0, 'mask_BxS2_bf1': mask_BxS2_bf1, 'L0_ffn_router_w': _L0_ffn_in['router_w'], 'L0_ffn_router_b': _L0_ffn_in['router_b'], 'L0_ffn_w1': _L0_ffn_in['w1'], 'L0_ffn_b1': _L0_ffn_in['b1'], 'L0_ffn_w2': _L0_ffn_in['w2'], 'L0_ffn_b2': _L0_ffn_in['b2'], 'L1_xattn_Wv': _L1_xattn_in['Wv'], 'L1_xattn_Wk': _L1_xattn_in['Wk'], 'L1_xattn_Wq': _L1_xattn_in['Wq'], 'L1_xattn_Wo': _L1_xattn_in['Wo'], 'L1_xattn_bo': _L1_xattn_in['bo'], 'L1_ffn_norm1_w': _L1_ffn_in['norm1_w'], 'L1_ffn_w1': _L1_ffn_in['w1'], 'L1_ffn_act_scale': _L1_ffn_in['act_scale'], 'L1_ffn_act_bias': _L1_ffn_in['act_bias'], 'L1_ffn_norm2_w': _L1_ffn_in['norm2_w'], 'L1_ffn_w2': _L1_ffn_in['w2'], 'L2_xattn_Wq': _L2_xattn_in['Wq'], 'L2_xattn_Wkv': _L2_xattn_in['Wkv'], 'L2_xattn_Wout': _L2_xattn_in['Wout'], 'L2_xattn_b_out': _L2_xattn_in['b_out'], 'L2_ffn_wqkv': _L2_ffn_in['wqkv'], 'L2_ffn_q_scale': _L2_ffn_in['q_scale'], 'L2_ffn_k_scale': _L2_ffn_in['k_scale'], 'L2_ffn_wo': _L2_ffn_in['wo'], 'L2_ffn_ln_g': _L2_ffn_in['ln_g'], 'L2_ffn_ln_b': _L2_ffn_in['ln_b'], 'L2_ffn_w1': _L2_ffn_in['w1'], 'L2_ffn_b1': _L2_ffn_in['b1'], 'L2_ffn_w2': _L2_ffn_in['w2'], 'L2_ffn_b2': _L2_ffn_in['b2'], 'L3_xattn_wq': _L3_xattn_in['wq'], 'L3_xattn_bq': _L3_xattn_in['bq'], 'L3_xattn_wk': _L3_xattn_in['wk'], 'L3_xattn_bk': _L3_xattn_in['bk'], 'L3_xattn_wv': _L3_xattn_in['wv'], 'L3_xattn_bv': _L3_xattn_in['bv'], 'L3_xattn_wo': _L3_xattn_in['wo'], 'L3_xattn_bo': _L3_xattn_in['bo'], 'L3_ffn_clip_x': _L3_ffn_in['clip_x'], 'L3_ffn_clip_down': _L3_ffn_in['clip_down'], 'L3_ffn_w_gate': _L3_ffn_in['w_gate'], 'L3_ffn_w_up': _L3_ffn_in['w_up'], 'L3_ffn_w_down': _L3_ffn_in['w_down']}

def reference(x, ctx_1024, fside_BxS2_0, mask_Bx1xSxS2_ik0, mask_BxS2_bf1, L0_ffn_router_w, L0_ffn_router_b, L0_ffn_w1, L0_ffn_b1, L0_ffn_w2, L0_ffn_b2, L1_xattn_Wv, L1_xattn_Wk, L1_xattn_Wq, L1_xattn_Wo, L1_xattn_bo, L1_ffn_norm1_w, L1_ffn_w1, L1_ffn_act_scale, L1_ffn_act_bias, L1_ffn_norm2_w, L1_ffn_w2, L2_xattn_Wq, L2_xattn_Wkv, L2_xattn_Wout, L2_xattn_b_out, L2_ffn_wqkv, L2_ffn_q_scale, L2_ffn_k_scale, L2_ffn_wo, L2_ffn_ln_g, L2_ffn_ln_b, L2_ffn_w1, L2_ffn_b1, L2_ffn_w2, L2_ffn_b2, L3_xattn_wq, L3_xattn_bq, L3_xattn_wk, L3_xattn_bk, L3_xattn_wv, L3_xattn_bv, L3_xattn_wo, L3_xattn_bo, L3_ffn_clip_x, L3_ffn_clip_down, L3_ffn_w_gate, L3_ffn_w_up, L3_ffn_w_down):
    import jax
    import jax.numpy as jnp

    def _L0_xattn_ref(hidden_states, visual_hidden_state):
        import jax, jax.numpy as jnp
        import numpy as np
        scores = jnp.einsum('bld,bvd->blv', hidden_states, visual_hidden_state)
        probs = jax.nn.softmax(scores, axis=-1)
        return jnp.einsum('blv,bvd->bld', probs, visual_hidden_state)

    def _L0_ffn_ref(x, router_w, router_b, w1, b1, w2, b2):
        import jax, jax.numpy as jnp
        import numpy as np
        IN_F, OUT_F, BLOCK, NBLK = (128, 512, 32, 16)
        TOPK = NBLK // 4
        x_shape = x.shape
        xf = x.reshape(-1, IN_F)
        n = xf.shape[0]
        prob = jax.nn.softmax(xf @ router_w.T + router_b, axis=-1)
        _, idx = jax.lax.top_k(prob, TOPK)
        mask = jnp.zeros((n, NBLK), bool).at[jnp.arange(n)[:, None], idx].set(True)
        w1b = w1.reshape(NBLK, BLOCK, IN_F)
        b1b = b1.reshape(NBLK, BLOCK)
        h = jnp.einsum('nd,ibd->nib', xf, w1b) + b1b
        h = jnp.where(mask[:, :, None], h, jnp.zeros((), h.dtype))
        h = jax.nn.relu(h)
        w2b = w2.reshape(IN_F, NBLK, BLOCK)
        y = jnp.einsum('nib,dib->nd', jnp.where(mask[:, :, None], h, 0.0), w2b) + b2
        return y.reshape(x_shape)

    def _L1_xattn_ref(values, keys, query, mask, Wv, Wk, Wq, Wo, bo):
        import jax, jax.numpy as jnp
        import numpy as np
        N, L, E, H = (2, 256, 128, 16)
        D = E // H
        n, lq, e = query.shape
        v = (values @ Wv.T).reshape(n, -1, H, D)
        k = (keys @ Wk.T).reshape(n, -1, H, D)
        q = (query @ Wq.T).reshape(n, lq, H, D)
        score = jnp.einsum('nqhd,nkhd->nhqk', q, k)
        score = jnp.where(mask == 0, jnp.float32(-1e+20), score)
        attn = jax.nn.softmax(score / jnp.sqrt(jnp.float32(D)), axis=-1)
        out = jnp.einsum('nhqk,nkhd->nqhd', attn, v).reshape(n, lq, H * D)
        return out @ Wo.T + bo

    def _L1_ffn_ref(x, norm1_w, w1, act_scale, act_bias, norm2_w, w2):
        import jax, jax.numpy as jnp
        import numpy as np
        EPS_NORM = 1e-08
        EPS_Q = 1e-05

        def rmsnorm(x, w):
            v = jnp.mean(jnp.square(x.astype(jnp.float32)), axis=-1, keepdims=True)
            x_hat = x * jax.lax.rsqrt(v + EPS_NORM)
            return (x_hat * w).astype(x.dtype)

        def activation_quant(x):
            scale = 127.0 / jnp.clip(jnp.max(jnp.abs(x), axis=-1, keepdims=True), EPS_Q, None)
            return jnp.clip(jnp.round(x * scale), -128, 127) / scale

        def weight_quant(w):
            scale = 1.0 / jnp.clip(jnp.mean(jnp.abs(w)), EPS_Q, None)
            return jnp.clip(jnp.round(w * scale), -1, 1) / scale

        def bitlinear(x, norm_w, w):
            x_norm = rmsnorm(x, norm_w)
            x_q = x_norm + jax.lax.stop_gradient(activation_quant(x_norm) - x_norm)
            w_q = w + jax.lax.stop_gradient(weight_quant(w) - w)
            return jnp.einsum('bsd,hd->bsh', x_q, w_q)
        h = bitlinear(x, norm1_w, w1)
        h = act_scale * jnp.square(jax.nn.relu(h)) + act_bias
        y = bitlinear(h, norm2_w, w2)
        return y

    def _L2_xattn_ref(x, context, mask, Wq, Wkv, Wout, b_out):
        import jax, jax.numpy as jnp
        import numpy as np
        HEADS = 16
        DIM_HEAD = 64
        SCALE = DIM_HEAD ** (-0.5)
        B, Nq, _ = x.shape
        Nkv = context.shape[1]
        q = x @ Wq.T
        kv = context @ Wkv.T
        k, v = jnp.split(kv, 2, axis=-1)
        q = q.reshape(B, Nq, HEADS, DIM_HEAD).transpose(0, 2, 1, 3)
        k = k.reshape(B, Nkv, HEADS, DIM_HEAD).transpose(0, 2, 1, 3)
        v = v.reshape(B, Nkv, HEADS, DIM_HEAD).transpose(0, 2, 1, 3)
        sim = jnp.einsum('bhid,bhjd->bhij', q, k) * SCALE
        max_neg = -jnp.finfo(sim.dtype).max
        sim = jnp.where(mask[:, None, None, :], sim, max_neg)
        attn = jax.nn.softmax(sim, axis=-1)
        out = jnp.einsum('bhij,bhjd->bhid', attn, v)
        out = out.transpose(0, 2, 1, 3).reshape(B, Nq, HEADS * DIM_HEAD)
        return out @ Wout.T + b_out

    def _L2_ffn_ref(x, wqkv, q_scale, k_scale, wo, ln_g, ln_b, w1, b1, w2, b2):
        import jax, jax.numpy as jnp
        import numpy as np
        DIM = 128
        DEPTH = 2
        HEADS = 8
        DIM_HEAD = 64
        WINDOW = 64
        INNER = HEADS * DIM_HEAD
        HID = int(DIM * 4 * 2 / 3)
        B, N = (2, 1024)
        QK_SCALE = 8.0

        def shift_token(t):
            t1, t2 = jnp.split(t, 2, axis=-1)
            t2 = jnp.pad(t2, ((0, 0), (1, 0), (0, 0)))[:, :-1]
            return jnp.concatenate([t1, t2], axis=-1)

        def l2norm(t):
            return t / jnp.clip(jnp.linalg.norm(t, axis=-1, keepdims=True), 1e-12)

        def rotate_half(x):
            x1, x2 = jnp.split(x, 2, axis=-1)
            return jnp.concatenate([-x2, x1], axis=-1)

        def rotary_xpos(q, k):
            n = q.shape[-2]
            half_idx = jnp.arange(0, DIM_HEAD, 2, dtype=jnp.float32)
            inv_freq = 1.0 / 10000.0 ** (half_idx / DIM_HEAD)
            t = jnp.arange(n, dtype=jnp.float32)
            freqs = t[:, None] * inv_freq[None, :]
            freqs = jnp.concatenate([freqs, freqs], axis=-1)
            base = (half_idx + 0.4 * DIM_HEAD) / (1.4 * DIM_HEAD)
            power = (t - n // 2) / float(WINDOW // 2)
            scale = base[None, :] ** power[:, None]
            scale = jnp.concatenate([scale, scale], axis=-1)
            cos, sin = (jnp.cos(freqs), jnp.sin(freqs))
            q = q * cos * scale + rotate_half(q) * sin * scale
            k = k * cos / scale + rotate_half(k) * sin / scale
            return (q, k)

        def local_attention(q, k, v):
            b, h, n, d = q.shape
            w = n // WINDOW
            bq = q.reshape(b, h, w, WINDOW, d) * QK_SCALE
            bk = k.reshape(b, h, w, WINDOW, d)
            bv = v.reshape(b, h, w, WINDOW, d)

            def look_around(t):
                p = jnp.pad(t, ((0, 0), (0, 0), (1, 0), (0, 0), (0, 0)))
                return jnp.concatenate([p[:, :, :w], p[:, :, 1:]], axis=3)
            bk, bv = (look_around(bk), look_around(bv))
            bt = jnp.arange(n).reshape(w, WINDOW)
            btp = jnp.pad(bt, ((1, 0), (0, 0)), constant_values=-1)
            btk = jnp.concatenate([btp[:w], btp[1:]], axis=1)
            sim = jnp.einsum('bhwid,bhwjd->bhwij', bq, bk)
            i = bt[:, :, None]
            j = btk[:, None, :]
            mask = (i < j) | (i > j + WINDOW) | (j == -1)
            sim = jnp.where(mask, -jnp.finfo(sim.dtype).max, sim)
            attn = jax.nn.softmax(sim, axis=-1)
            out = jnp.einsum('bhwij,bhwjd->bhwid', attn, bv)
            return out.reshape(b, h, n, d)

        def _layer(x, wqkv, qs, ksc, wo, lg, lb, w1, b1, w2, b2):
            b, n, _ = x.shape
            h = shift_token(x)
            qkv = h @ wqkv
            q, k, v = jnp.split(qkv, 3, axis=-1)
            to_heads = lambda t: t.reshape(b, n, HEADS, DIM_HEAD).transpose(0, 2, 1, 3)
            q, k, v = (to_heads(q), to_heads(k), to_heads(v))
            q = l2norm(q) * qs
            k = l2norm(k) * ksc
            q, k = rotary_xpos(q, k)
            o = local_attention(q, k, v)
            o = o.transpose(0, 2, 1, 3).reshape(b, n, INNER)
            x = x + o @ wo
            h = shift_token(x)
            mu = h.mean(-1, keepdims=True)
            var = h.var(-1, keepdims=True)
            h = (h - mu) / jnp.sqrt(var + 1e-05) * lg + lb
            h = h @ w1 + b1
            a, g = jnp.split(h, 2, axis=-1)
            h = a * jax.nn.gelu(g, approximate=False)
            x = x + h @ w2 + b2
            return x
        for l in range(DEPTH):
            x = _layer(x, wqkv[l], q_scale[l], k_scale[l], wo[l], ln_g[l], ln_b[l], w1[l], b1[l], w2[l], b2[l])
        return x

    def _L3_xattn_ref(query, key, value, temporal_bias, wq, bq, wk, bk, wv, bv, wo, bo):
        import jax, jax.numpy as jnp
        import numpy as np
        D_MODEL = 128
        NUM_HEADS = 16
        DEPTH = D_MODEL // NUM_HEADS
        TEMPERATURE = 1.0
        B, S = (2, 256)

        def _split_heads(x):
            b, s, _ = x.shape
            return x.reshape(b, s, NUM_HEADS, DEPTH).transpose(0, 2, 1, 3)
        q = _split_heads(query @ wq + bq)
        k = _split_heads(key @ wk + bk)
        v = _split_heads(value @ wv + bv)
        scale = jnp.sqrt(jnp.asarray(DEPTH, q.dtype)) * TEMPERATURE
        logits = jnp.einsum('bhqd,bhkd->bhqk', q, k) / scale
        logits = logits + temporal_bias[:, None, None, :]
        attn = jax.nn.softmax(logits, axis=-1)
        out = jnp.einsum('bhqk,bhkd->bhqd', attn, v)
        out = out.transpose(0, 2, 1, 3).reshape(query.shape[0], -1, D_MODEL)
        return out @ wo + bo

    def _L3_ffn_ref(x, clip_x, clip_down, w_gate, w_up, w_down):
        import jax, jax.numpy as jnp
        import numpy as np
        QMAX = 127.0

        def _ste_round(v):
            return v + jax.lax.stop_gradient(jnp.round(v) - v)

        def _act_fake_quant(x, clip_factor):
            scale = jax.nn.sigmoid(clip_factor) * jnp.max(jnp.abs(x)) / QMAX
            return jnp.clip(_ste_round(x / scale), -QMAX - 1.0, QMAX) * scale

        def _weight_fake_quant(w):
            scale = jnp.max(jnp.abs(w), axis=1, keepdims=True) / QMAX
            return jnp.clip(_ste_round(w / scale), -QMAX - 1.0, QMAX) * scale
        xq = _act_fake_quant(x, clip_x[0])
        gate = jnp.einsum('bsh,ih->bsi', xq, _weight_fake_quant(w_gate))
        up = jnp.einsum('bsh,ih->bsi', xq, _weight_fake_quant(w_up))
        h = _act_fake_quant(jax.nn.silu(gate) * up, clip_down[0])
        return jnp.einsum('bsi,hi->bsh', h, _weight_fake_quant(w_down))
    x = x + _L0_xattn_ref(_layernorm(x, axis=-1), ctx_1024)
    x = x + _L0_ffn_ref(_layernorm(x, axis=-1), L0_ffn_router_w, L0_ffn_router_b, L0_ffn_w1, L0_ffn_b1, L0_ffn_w2, L0_ffn_b2)
    x = x + _L1_xattn_ref(ctx_1024, ctx_1024, _layernorm(x, axis=-1), mask_Bx1xSxS2_ik0, L1_xattn_Wv, L1_xattn_Wk, L1_xattn_Wq, L1_xattn_Wo, L1_xattn_bo)
    x = x + _L1_ffn_ref(_layernorm(x, axis=-1), L1_ffn_norm1_w, L1_ffn_w1, L1_ffn_act_scale, L1_ffn_act_bias, L1_ffn_norm2_w, L1_ffn_w2)
    x = x + _L2_xattn_ref(_layernorm(x, axis=-1), ctx_1024, mask_BxS2_bf1, L2_xattn_Wq, L2_xattn_Wkv, L2_xattn_Wout, L2_xattn_b_out)
    x = x + _L2_ffn_ref(_layernorm(x, axis=-1), L2_ffn_wqkv, L2_ffn_q_scale, L2_ffn_k_scale, L2_ffn_wo, L2_ffn_ln_g, L2_ffn_ln_b, L2_ffn_w1, L2_ffn_b1, L2_ffn_w2, L2_ffn_b2)
    x = x + _L3_xattn_ref(_layernorm(x, axis=-1), ctx_1024, ctx_1024, fside_BxS2_0, L3_xattn_wq, L3_xattn_bq, L3_xattn_wk, L3_xattn_bk, L3_xattn_wv, L3_xattn_bv, L3_xattn_wo, L3_xattn_bo)
    x = x + _L3_ffn_ref(_layernorm(x, axis=-1), L3_ffn_clip_x, L3_ffn_clip_down, L3_ffn_w_gate, L3_ffn_w_up, L3_ffn_w_down)
    return x

_drawn_inputs = setup_inputs


def setup_inputs(seed=0):
    import zlib

    import numpy as np

    out = dict(_drawn_inputs(seed))
    spreads = {'L1_xattn_bo': (0.0, 0.1),
     'L1_ffn_norm1_w': (1.0, 0.2),
     'L1_ffn_norm2_w': (1.0, 0.2),
     'L2_xattn_b_out': (0.0, 0.1),
     'L2_ffn_q_scale': (1.0, 0.6),
     'L2_ffn_k_scale': (1.0, 0.6),
     'L2_ffn_ln_g': (1.0, 0.6),
     'L2_ffn_ln_b': (0.0, 0.8),
     'L2_ffn_b1': (0.0, 0.8),
     'L2_ffn_b2': (0.0, 0.76),
     'L3_xattn_bq': (0.0, 2.0),
     'L3_xattn_bk': (0.0, 2.0),
     'L3_xattn_bv': (0.0, 2.0),
     'L3_xattn_bo': (0.0, 0.8)}
    factors = {'L0_ffn_router_b': 3.043,
     'L0_ffn_b1': 8.0,
     'L0_ffn_b2': 3.746,
     'L1_xattn_Wv': 3.781,
     'L1_xattn_Wk': 8.0,
     'L1_xattn_Wq': 8.0,
     'L1_xattn_Wo': 3.571,
     'L2_ffn_w1': 8.0,
     'L2_ffn_w2': 8.0,
     'L3_ffn_w_gate': 8.0,
     'L3_ffn_w_up': 8.0,
     'L3_ffn_w_down': 8.0,
     'fside_BxS2_0': 8.0,
     'L3_xattn_wq': 5.168,
     'L3_xattn_wk': 4.627}
    for name, (base, spread) in spreads.items():
        noise = np.random.default_rng([zlib.crc32(name.encode()), seed]).standard_normal(out[name].shape)
        drawn = base * np.exp(spread * noise) if base else spread * noise
        out[name] = jnp.asarray(drawn.astype(out[name].dtype))
    for name, factor in factors.items():
        out[name] = (out[name] * factor).astype(out[name].dtype)
    return out
```

```python
import numpy as np
import concourse.bass as bass
from concourse import mybir
from contextlib import ExitStack

F32 = mybir.dt.float32
BF16 = mybir.dt.bfloat16
I32 = mybir.dt.int32
U8 = mybir.dt.uint8
ACT = mybir.ActivationFunctionType
ALU = mybir.AluOpType
AX = mybir.AxisListType

P = 128
B = 8
D = 128
S = 256
KV = 512
TPB = S // P
CPB = KV // P
NT = B * TPB
PAIRS = B // 2
AHEAD = 2
HEADS = 16
LN_EPS = 1e-5
MAGIC = 12582912.0


class Signal:

    def __init__(self, nc, ctx, name):
        self.sem = ctx.enter_context(nc.semaphore(name))
        self.before = 0

    def after(self, n):
        return self.sem, n + self.before


class Ring:

    def __init__(self, banks, filled, drained, per):
        self.banks, self.filled, self.drained, self.per = banks, filled, drained, per

    def at(self, i, u, m):
        n = u * self.per + m
        return n % 2, i * self.per + n // 2

    def bank(self, u, m):
        return self.banks[(u * self.per + m) % 2]

    def free(self, i, u, m):
        s, n = self.at(i, u, m)
        return self.drained[s].after(n)

    def full(self, i, u, m):
        s, n = self.at(i, u, m)
        return self.filled[s].after(n + 1)

    def empty(self, i, u, m):
        s, n = self.at(i, u, m)
        return self.drained[s].after(n + 1)

    def fills(self, u, m):
        return self.filled[(u * self.per + m) % 2].sem

    def drains(self, u, m):
        return self.drained[(u * self.per + m) % 2].sem

    def close(self):
        for s in self.filled + self.drained:
            s.before += self.per * PAIRS


class Machine:

    def __init__(self, nc, ctx, dram):
        self.nc, self.dram = nc, dram
        self.signals = []

        def sig(name):
            self.signals.append(Signal(nc, ctx, name))
            return self.signals[-1]
        self.loaded = sig("loaded")
        self.streamed = [sig("streamed_even"), sig("streamed_odd")]
        self.ready_made = sig("ready_made")
        self.row_stats = sig("row_stats")
        self.row_moments = sig("row_moments")
        self.var_eps = sig("var_eps")
        self.row_rstd = sig("row_rstd")
        self.normed = sig("normed")
        self.filled = [sig("bank0_filled"), sig("bank1_filled")]
        self.drained = [sig("bank0_drained"), sig("bank1_drained")]
        self.q_masked = sig("q_masked")
        self.scores_ready = sig("scores_ready")
        self.max_ready = sig("max_ready")
        self.probs_ready = sig("probs_ready")
        self.turned = sig("turned")
        self.turned_copied = sig("turned_copied")
        self.pv_done = sig("pv_done")
        self.pv_copied = sig("pv_copied")
        self.sums_inverted = sig("sums_inverted")
        self.sums_turned = sig("sums_turned")
        self.mask_ready = sig("mask_ready")
        self.x_updated = sig("x_updated")
        self.passed = sig("passed")
        self.squares_summed = sig("squares_summed")
        self.squares_ready = sig("squares_ready")
        self.powers_ready = sig("powers_ready")
        self.x_quantised = sig("x_quantised")
        self.h_squared = sig("h_squared")
        self.squared_affine = sig("squared_affine")
        self.unshifted = sig("unshifted")
        self.rotated = sig("rotated")
        self.row_max = sig("row_max")
        self.max_turned = sig("max_turned")
        self.max_found = sig("max_found")
        self.max_spread = sig("max_spread")
        self.x_turned = sig("x_turned")
        self.scales_ready = sig("scales_ready")
        self.gate_ready = sig("gate_ready")
        self.hidden_ready = sig("hidden_ready")
        self.hidden_clipped = sig("hidden_clipped")
        self.hidden_rounded = sig("hidden_rounded")
        self.hidden_quantised = sig("hidden_quantised")
        self.step = sig("step")
        self.act_step = sig("act_step")
        self.pool_step = sig("pool_step")
        self.x = ctx.enter_context(nc.sbuf_tensor("x_tok", [P, NT, D], F32))
        self.consts = {}


def sbuf(m, ctx, name, shape, dt=F32):
    return ctx.enter_context(m.nc.sbuf_tensor(name, shape, dt))


def psum(m, ctx, name, shape, dt=F32):
    return ctx.enter_context(m.nc.psum_tensor(name, shape, dt))


CONSTS = [("ident", P), ("ones", P), ("band", 3 * P), ("shift", P), ("last", P), ("head_cols", HEADS), ("spread4", 4 * P),
          ("spread2", 8 * P), ("minus_half", 64),
          ("rot_qa", 2 * 64), ("rot_qb", 2 * 64), ("rot_ka", 2 * 64), ("rot_kb", 2 * 64)]
CONSTS_BF = ("ident", "ones", "band")


def load_constants(m, ctx):
    nc, d = m.nc, m.dram
    widths = dict(CONSTS)
    width, width_bf = sum(widths.values()), sum(widths[n] for n in CONSTS_BF)
    c = sbuf(m, ctx, "consts", [P, width])
    cb = sbuf(m, ctx, "consts_bf", [P, width_bf], BF16)
    at = 0
    for name, w in CONSTS:
        m.consts[name] = c[:, at:at + w]
        if name in CONSTS_BF:
            m.consts[name + "_bf"] = cb[:, at:at + w]
        at += w
    with nc.Block() as block:
        @block.sync
        def _(sp):
            sp.dma_start(m.x[:], d["x"].rearrange("(t p) d -> p t d", p=P)).then_inc(m.loaded.sem, 16)
            sp.dma_start(c[:], d["consts"]).then_inc(m.loaded.sem, 16)
            sp.wait_ge(*m.loaded.after(32))

        @block.vector
        def _(dve):
            dve.wait_ge(*m.loaded.after(32))
            dve.tensor_copy(cb[:], c[:, 0:width_bf])

        @block.gpsimd
        def _(pool):
            for s in m.signals:
                if s is not m.loaded:
                    pool.sem_inc(s.sem, 1)
    for s in m.signals:
        s.before += 32 if s is m.loaded else 1


class Norm:

    def __init__(self, m, ctx, tiles, tag, buffers=2):
        self.m, self.tiles = m, tiles
        self.st = sbuf(m, ctx, f"st_{tag}", [P, tiles, 6])
        self.mv = sbuf(m, ctx, f"mv_{tag}", [P, tiles, 2])
        self.ve = sbuf(m, ctx, f"ve_{tag}", [P, tiles])
        self.rs = sbuf(m, ctx, f"rs_{tag}", [P, tiles])
        self.xn = [sbuf(m, ctx, f"xn{u}_{tag}", [P, tiles, D]) for u in range(buffers)]

    def vector(self, dve, b, u, src):
        m, t = self.m, self.tiles
        for j in range(t):
            dve.bn_stats(self.st[:, j, :], src(j)).then_inc(m.row_stats.sem, 1)
        dve.wait_ge(*m.row_stats.after(t * b + t))
        dve.sem_inc(m.passed.sem, 1)
        for j in range(t):
            dve.bn_aggr(self.mv[:, j, :], self.st[:, j, :]).then_inc(m.row_moments.sem, 1)
        dve.wait_ge(*m.row_moments.after(t * b + t))
        dve.tensor_scalar(self.ve[:], self.mv[:, :, 1], LN_EPS, None, ALU.add).then_inc(m.var_eps.sem, 1)
        dve.wait_ge(*m.row_rstd.after(b + 1))
        for j in range(t):
            dve.tensor_scalar(self.xn[u][:, j, :], src(j), self.mv[:, j, 0:1], self.rs[:, j:j + 1],
                              ALU.subtract, ALU.mult).then_inc(m.normed.sem, 1)

    def pool(self, pool, b):
        m = self.m
        pool.wait_ge(*m.var_eps.after(b + 1))
        pool.tensor_tensor(self.rs[:], self.ve[:], m.consts["minus_half"][:, 0:self.tiles], ALU.pow)\
            .then_inc(m.row_rstd.sem, 1)

    def close(self, steps):
        m, t = self.m, self.tiles
        for s, n in ((m.row_stats, t), (m.row_moments, t), (m.var_eps, 1), (m.row_rstd, 1), (m.normed, t)):
            s.before += n * steps


def l0_cross_attention(m):
    nc, d, x, k = m.nc, m.dram, m.x, m.consts
    with ExitStack() as ctx:
        norm = Norm(m, ctx, TPB, "l0x")
        ctxT = [sbuf(m, ctx, f"ctxT{u}_l0x", [P, KV]) for u in range(2)]
        rows = [sbuf(m, ctx, f"rows{u}_l0x", [P, CPB, D]) for u in range(2)]
        xnT = [sbuf(m, ctx, f"xnT{u}_l0x", [P, S]) for u in range(2)]
        nmax = sbuf(m, ctx, "nmax_l0x", [P, 2, TPB])
        sums = sbuf(m, ctx, "sums_l0x", [P, 2, TPB])
        inv = sbuf(m, ctx, "inv_l0x", [P, 2, TPB])
        probs = [sbuf(m, ctx, f"probs{j}_l0x", [P, KV]) for j in range(TPB)]
        pT = [sbuf(m, ctx, f"pT{j}_l0x", [P, CPB, P]) for j in range(TPB)]
        ring = Ring([psum(m, ctx, f"ring{n}_l0x", [P, 512]) for n in range(2)], m.filled, m.drained, 2)
        s_ps = [psum(m, ctx, f"s_ps{j}_l0x", [P, KV]) for j in range(TPB)]
        t_ps = [psum(m, ctx, f"t_ps{j}_l0x", [P, KV]) for j in range(TPB)]

        with nc.Block() as block:
            @block.sync
            def _(sp):
                def stream(b, u):
                    sp.dma_start(ctxT[u][:], d["ctxT"][:, bass.ds(b * KV, KV)]).then_inc(m.streamed[u].sem, 16)
                    sp.dma_start(rows[u][:], d["ctx"][bass.ds(b * KV, KV), :].rearrange("(c p) d -> p c d", p=P))\
                        .then_inc(m.streamed[u].sem, 16)
                for u in range(2):
                    stream(u, u)
                with sp.Fori(0, PAIRS) as i:
                    for u in range(2):
                        sp.wait_ge(*ring.full(i, u, 1))
                        stream(2 * i + u + AHEAD, u)
                for s in m.streamed:
                    sp.wait_ge(*s.after(32 * (PAIRS + 1)))

            @block.gpsimd
            def _(pool):
                with pool.Fori(0, PAIRS) as i:
                    for u in range(2):
                        norm.pool(pool, 2 * i + u)

            @block.vector
            def _(dve):
                with dve.Fori(0, PAIRS) as i:
                    for u in range(2):
                        b = 2 * i + u
                        norm.vector(dve, b, u, lambda j: x[:, TPB * b + j, :])
                        for j in range(TPB):
                            dve.wait_ge(*m.scores_ready.after(TPB * b + j + 1))
                            dve.tensor_reduce(nmax[:, u, j:j + 1], s_ps[j][:], AX.X, ALU.max, negate=True)\
                                .then_inc(m.max_ready.sem, 1)
                        for j in range(TPB):
                            dve.wait_ge(*m.turned.after(TPB * b + j + 1))
                            dve.tensor_copy(pT[j][:].rearrange("p c t -> p (c t)"), t_ps[j][:])\
                                .then_inc(m.turned_copied.sem, 1)
                        dve.wait_ge(*m.probs_ready.after(TPB * b + TPB))
                        dve.reciprocal(inv[:, u, :], sums[:, u, :]).then_inc(m.sums_inverted.sem, 1)
                        dve.wait_ge(*m.sums_inverted.after(b + 1))
                        dve.wait_ge(*ring.full(i, u, 1))
                        bank = ring.bank(u, 1)
                        for j in range(TPB):
                            ins = dve.scalar_tensor_tensor(out=x[:, TPB * b + j, :], in0=bank[:, j * D:(j + 1) * D],
                                                           scalar=inv[:, u, j:j + 1], in1=x[:, TPB * b + j, :],
                                                           op0=ALU.mult, op1=ALU.add)
                        ins.then_inc(ring.drains(u, 1), 1)

            @block.scalar
            def _(act):
                with act.Fori(0, PAIRS) as i:
                    for u in range(2):
                        b = 2 * i + u
                        act.wait_ge(*ring.full(i, u, 0))
                        act.activation(xnT[u][:], ring.bank(u, 0)[:, 0:S], ACT.Copy).then_inc(ring.drains(u, 0), 1)
                        for j in range(TPB):
                            act.wait_ge(*m.max_ready.after(TPB * b + j + 1))
                            act.activation(probs[j][:], s_ps[j][:], ACT.Exp, bias=nmax[:, u, j:j + 1],
                                           accum_out=sums[:, u, j:j + 1]).then_inc(m.probs_ready.sem, 1)

            @block.tensor
            def _(pe):
                with pe.Fori(0, PAIRS) as i:
                    for u in range(2):
                        b = 2 * i + u
                        pe.wait_ge(*m.normed.after(TPB * b + TPB))
                        pe.wait_ge(*ring.free(i, u, 0))
                        for j in range(TPB):
                            ins = pe.transpose(ring.bank(u, 0)[:, j * P:(j + 1) * P], norm.xn[u][:, j, :], k["ident"])
                        ins.then_inc(ring.fills(u, 0), 1)
                        pe.wait_ge(*ring.empty(i, u, 0))
                        pe.wait_ge(*m.streamed[u].after(32 * i + 32))
                        for j in range(TPB):
                            pe.matmul(s_ps[j][:], xnT[u][:, j * P:(j + 1) * P], ctxT[u][:], start=True, stop=True)\
                                .then_inc(m.scores_ready.sem, 1)
                        for j in range(TPB):
                            pe.wait_ge(*m.probs_ready.after(TPB * b + j + 1))
                            for c in range(CPB):
                                ins = pe.transpose(t_ps[j][:, c * P:(c + 1) * P], probs[j][:, c * P:(c + 1) * P], k["ident"])
                            ins.then_inc(m.turned.sem, 1)
                        pe.wait_ge(*ring.free(i, u, 1))
                        for j in range(TPB):
                            pe.wait_ge(*m.turned_copied.after(TPB * b + j + 1))
                            for c in range(CPB):
                                ins = pe.matmul(ring.bank(u, 1)[:, j * D:(j + 1) * D], pT[j][:, c, :], rows[u][:, c, :],
                                                start=(c == 0), stop=(c == CPB - 1))
                        ins.then_inc(ring.fills(u, 1), 1)
        norm.close(B)
        ring.close()
        for s, n in ((m.streamed[0], 32 * (PAIRS + 1)), (m.streamed[1], 32 * (PAIRS + 1)), (m.scores_ready, NT), (m.max_ready, NT), (m.probs_ready, NT),
                     (m.turned, NT), (m.turned_copied, NT), (m.sums_inverted, B)):
            s.before += n


def turn_normed(m, pe, norm, ring, i, u, fill, tiles=TPB):
    b = 2 * i + u
    pe.wait_ge(*m.normed.after(tiles * b + tiles))
    pe.wait_ge(*ring.free(i, u, fill))
    for j in range(tiles):
        ins = pe.transpose(ring.bank(u, fill)[:, j * P:(j + 1) * P], norm.xn[u][:, j, :], m.consts["ident"])
    ins.then_inc(ring.fills(u, fill), 1)


def add_to_x(m, dve, ring, i, u, fill):
    dve.wait_ge(*ring.full(i, u, fill))
    rows = m.x[:, bass.ds(TPB * (2 * i + u), TPB), :]
    dve.tensor_tensor(rows, ring.bank(u, fill)[:, 0:TPB * D].rearrange("p (t d) -> p t d", d=D),
                      rows, ALU.add).then_inc(ring.drains(u, fill), 1)


def l0_block_ffn(m):
    nc, d, x, k = m.nc, m.dram, m.x, m.consts
    NB, TOP, HC = 16, 4, 4
    LOW, CHOSEN = -3.0e38, 3.0e38
    with ExitStack() as ctx:
        norm = Norm(m, ctx, TPB, "l0f")
        router = sbuf(m, ctx, "router_l0f", [P, NB])
        router_b = sbuf(m, ctx, "router_b_l0f", [1, NB])
        w1 = sbuf(m, ctx, "w1_l0f", [P, HC * P])
        b1 = sbuf(m, ctx, "b1_l0f", [P, HC])
        w2 = sbuf(m, ctx, "w2_l0f", [P, HC, D])
        b2 = sbuf(m, ctx, "b2_l0f", [1, D])
        xnT = [sbuf(m, ctx, f"xnT{u}_l0f", [P, S]) for u in range(2)]
        logits = sbuf(m, ctx, "logits_l0f", [P, TPB, NB + TOP])
        top = sbuf(m, ctx, "top_l0f", [P, TPB, 8])
        marked = sbuf(m, ctx, "marked_l0f", [P, TPB, NB + TOP])
        chosen = sbuf(m, ctx, "chosen_l0f", [P, TPB, NB])
        chosenT = sbuf(m, ctx, "chosenT_l0f", [NB, S])
        hT = [sbuf(m, ctx, f"hT{u}_l0f", [P, HC, S]) for u in range(2)]
        TURN, LOGIT, CHOICE, HID, SPREAD, OUT = 0, 1, 2, 3, 3 + HC, 3 + 2 * HC
        ring = Ring([psum(m, ctx, f"ring{n}_l0f", [P, 512]) for n in range(2)], m.filled, m.drained, OUT + 1)

        with nc.Block() as block:
            @block.sync
            def _(sp):
                for dst, src in ((router[:], d["L0_ffn_router_w"]), (router_b[:], d["L0_ffn_router_b"]),
                                 (w1[:], d["L0_ffn_w1"]), (b2[:], d["L0_ffn_b2"]),
                                 (w2[:], d["L0_ffn_w2"].rearrange("(c p) d -> p c d", p=P))):
                    sp.dma_start(dst, src).then_inc(m.loaded.sem, 16)
                for c in range(HC):
                    sp.dma_start(b1[:, c:c + 1], d["L0_ffn_b1"][0, c * P:(c + 1) * P].rearrange("(p o) -> p o", o=1))\
                        .then_inc(m.loaded.sem, 16)
                sp.wait_ge(*m.loaded.after(16 * (5 + HC)))

            @block.gpsimd
            def _(pool):
                with pool.Fori(0, PAIRS) as i:
                    for u in range(2):
                        norm.pool(pool, 2 * i + u)

            @block.vector
            def _(dve):
                dve.memset(logits[:, :, NB:], LOW).then_inc(m.step.sem, 1)
                dve.wait_ge(*m.step.after(1))
                per = 2 * TPB + 1
                with dve.Fori(0, PAIRS) as i:
                    for u in range(2):
                        b = 2 * i + u
                        norm.vector(dve, b, u, lambda j: x[:, TPB * b + j, :])
                        at = per * b + 1
                        dve.wait_ge(*ring.full(i, u, LOGIT))
                        dve.tensor_copy(logits[:, :, 0:NB], ring.bank(u, LOGIT)[:, 0:TPB * NB]
                                        .rearrange("p (t n) -> p t n", n=NB)).then_inc(ring.drains(u, LOGIT), 1)
                        dve.wait_ge(*ring.empty(i, u, LOGIT))
                        dve.sem_inc(m.passed.sem, 1)
                        for j in range(TPB):
                            dve.max(top[:, j, :], logits[:, j, 0:NB]).then_inc(m.step.sem, 1)
                        dve.wait_ge(*m.step.after(at + TPB))
                        dve.tensor_copy(top[:, :, TOP:], logits[:, :, NB:]).then_inc(m.step.sem, 1)
                        dve.wait_ge(*m.step.after(at + TPB + 1))
                        dve.sem_inc(m.passed.sem, 1)
                        for j in range(TPB):
                            dve.match_replace(marked[:, j, :], top[:, j, :], logits[:, j, :], CHOSEN).then_inc(m.step.sem, 1)
                        dve.wait_ge(*m.step.after(at + 2 * TPB + 1))
                        dve.tensor_scalar(chosen[:], marked[:, :, 0:NB], CHOSEN, None, ALU.is_equal).then_inc(m.mask_ready.sem, 1)
                        for c in range(HC):
                            dve.wait_ge(*ring.full(i, u, SPREAD + c))
                            dve.wait_ge(*ring.empty(i, u, HID + c))
                            dve.tensor_tensor(hT[u][:, c, :], ring.bank(u, SPREAD + c)[:, 0:S],
                                              hT[u][:, c, :], ALU.mult).then_inc(ring.drains(u, SPREAD + c), 1)
                        add_to_x(m, dve, ring, i, u, OUT)

            @block.scalar
            def _(act):
                with act.Fori(0, PAIRS) as i:
                    for u in range(2):
                        act.wait_ge(*ring.full(i, u, TURN))
                        act.activation(xnT[u][:], ring.bank(u, TURN)[:, 0:S], ACT.Copy).then_inc(ring.drains(u, TURN), 1)
                        act.wait_ge(*ring.full(i, u, CHOICE))
                        act.activation(chosenT[:], ring.bank(u, CHOICE)[0:NB, 0:S], ACT.Copy).then_inc(ring.drains(u, CHOICE), 1)
                        for c in range(HC):
                            act.wait_ge(*ring.full(i, u, HID + c))
                            act.activation(hT[u][:, c, :], ring.bank(u, HID + c)[:, 0:S], ACT.Relu,
                                           bias=b1[:, c:c + 1]).then_inc(ring.drains(u, HID + c), 1)

            @block.tensor
            def _(pe):
                pe.wait_ge(*m.loaded.after(16 * (5 + HC)))
                with pe.Fori(0, PAIRS) as i:
                    for u in range(2):
                        b = 2 * i + u
                        turn_normed(m, pe, norm, ring, i, u, TURN)
                        pe.wait_ge(*ring.free(i, u, LOGIT))
                        pe.wait_ge(*ring.empty(i, u, TURN))
                        for j in range(TPB):
                            out = ring.bank(u, LOGIT)[:, j * NB:(j + 1) * NB]
                            pe.matmul(out, k["ones"][0:1, :], router_b[:], start=True, stop=False)
                            ins = pe.matmul(out, xnT[u][:, j * P:(j + 1) * P], router[:], start=False, stop=True)
                        ins.then_inc(ring.fills(u, LOGIT), 1)
                        pe.wait_ge(*ring.free(i, u, CHOICE))
                        pe.wait_ge(*m.mask_ready.after(b + 1))
                        for j in range(TPB):
                            ins = pe.transpose(ring.bank(u, CHOICE)[0:NB, j * P:(j + 1) * P], chosen[:, j, :], k["ident"])
                        ins.then_inc(ring.fills(u, CHOICE), 1)
                        for c in range(HC):
                            pe.wait_ge(*ring.free(i, u, HID + c))
                            pe.matmul(ring.bank(u, HID + c)[:, 0:S], w1[:, c * P:(c + 1) * P], xnT[u][:],
                                      start=True, stop=True).then_inc(ring.fills(u, HID + c), 1)
                        for c in range(HC):
                            pe.wait_ge(*ring.free(i, u, SPREAD + c))
                            pe.matmul(ring.bank(u, SPREAD + c)[:, 0:S],
                                      k["spread4"][0:NB, c * P:(c + 1) * P], chosenT[:],
                                      start=True, stop=True).then_inc(ring.fills(u, SPREAD + c), 1)
                        pe.wait_ge(*ring.free(i, u, OUT))
                        pe.wait_ge(*ring.empty(i, u, OUT - 1))
                        for j in range(TPB):
                            out = ring.bank(u, OUT)[:, j * D:(j + 1) * D]
                            pe.matmul(out, k["ones"][0:1, :], b2[:], start=True, stop=False)
                            for c in range(HC):
                                ins = pe.matmul(out, hT[u][:, c, j * P:(j + 1) * P], w2[:, c, :], start=False, stop=(c == HC - 1))
                        ins.then_inc(ring.fills(u, OUT), 1)
        norm.close(B)
        ring.close()
        for s, n in ((m.loaded, 16 * (5 + HC)), (m.step, (2 * TPB + 1) * B + 1), (m.mask_ready, B)):
            s.before += n


def head_attention(m, tag, hd, wq, wk, wv, wo, bo, bq=None, bk=None, bv=None, mask=None, key_mask=None, key_bias=None):
    nc, d, x, k = m.nc, m.dram, m.x, m.consts
    small = hd == D // HEADS
    G = 4 if small else 2
    NG = HEADS // G
    W = P // G
    NK = 1 if small else NG
    VW = HEADS * W
    VH = VW // 512
    UNITS = HEADS * TPB
    per_load = 32 if mask is not None else 16
    spread = k["spread4"] if small else k["spread2"]
    with ExitStack() as ctx:
        norm = Norm(m, ctx, TPB, tag)
        sb = lambda name, shape, dt=F32: sbuf(m, ctx, f"{name}_{tag}", shape, dt)
        wq_s, wk_s = sb("wq", [P, NK * P]), sb("wk", [P, NK * P])
        wv_s = sb("wv", [P, VW])
        wo_s = sb("wo", [P, NG, D])
        bo_s = sb("bo", [1, D])
        ctxT = [sb(f"ctxT{u}", [P, KV]) for u in range(2)]
        xnT = [sb(f"xnT{u}", [P, S]) for u in range(2)]
        q_all = sb("q_all", [P, S])
        q = [sb(f"q{u}", [P, HEADS, S]) for u in range(2)]
        kT = [sb(f"kT{u}", [P, NK, KV]) for u in range(2)]
        v = [sb(f"v{u}", [P, CPB, VW]) for u in range(2)]
        nmax = sb("nmax", [P, 2, UNITS])
        sums = sb("sums", [P, 2, TPB, HEADS])
        inv = sb("inv", [P, TPB * HEADS])
        invT = sb("invT", [HEADS, S])
        probs = [sb(f"probs{n}", [P, KV]) for n in range(2)]
        pT = [sb(f"pT{n}", [P, G, CPB, S]) for n in range(2)]
        o = sb("o", [P, NG, S])
        if small:
            wv_raw = sb("wv_raw", [P, D])
        if bq is not None:
            bq_s, bk_s, bv_raw, bv_s = sb("bq", [P, 1]), sb("bk", [P, 1]), sb("bv_raw", [1, D]), sb("bv", [1, VW])
        if mask is not None:
            mask_i = [sb(f"mask_i{u}", [P, TPB, KV], I32) for u in range(2)]
            mask_b = [sb(f"mask_b{u}", [P, TPB, KV], BF16) for u in range(2)]
        else:
            key_rows = sb("key_rows", [P, B * KV], BF16)
        if key_mask is not None:
            key_u8 = sb("key_u8", [1, B * KV], U8)
        if key_bias is not None:
            kb, kb_hi = sb("kb", [96, B * KV]), sb("kb_hi", [96, B * KV], BF16)

        NLOAD = 4 + (G if small else 1) + 3 * (bq is not None) + (key_mask is not None) + 3 * (key_bias is not None)
        NSTEP = (3 if small else 2) + 2 * (bq is not None) + (mask is None) + (key_mask is not None) + 8 * (key_bias is not None)
        TURN, Q = 0, 1
        K = Q + (1 if small else NK // 2)
        V = K + NK
        SUMS = V + CPB * VH
        SPREAD = SUMS + 1
        OUT = SPREAD + NG // 2
        ring = Ring([psum(m, ctx, f"ring{n}_{tag}", [P, 512]) for n in range(2)], m.filled, m.drained, OUT + 1)
        s_ps = [psum(m, ctx, f"s_ps{n}_{tag}", [P, KV]) for n in range(2)]
        t_ps = [psum(m, ctx, f"t_ps{n}_{tag}", [P, KV]) for n in range(2)]
        o_ps = [psum(m, ctx, f"o_ps{n}_{tag}", [P, 512]) for n in range(2)]

        with nc.Block() as block:
            @block.sync
            def _(sp):
                def stream(b, u):
                    sp.dma_start(ctxT[u][:], d["ctxT"][:, bass.ds(b * KV, KV)]).then_inc(m.streamed[u].sem, 16)
                    if mask is not None:
                        sp.dma_start(mask_i[u][:], mask[bass.ds(b * S, S), :].rearrange("(t p) k -> p t k", p=P))\
                            .then_inc(m.streamed[u].sem, 16)

                loads = [(wq_s[:], wq), (wk_s[:], wk), ((wv_raw if small else wv_s)[:], wv), (bo_s[:], bo)]
                if not small:
                    loads.append((wo_s[:], wo.rearrange("(g p) n -> p g n", p=P)))
                if bq is not None:
                    loads += [(bq_s[:], bq.rearrange("o (p n) -> (o p) n", n=1)),
                              (bk_s[:], bk.rearrange("o (p n) -> (o p) n", n=1)), (bv_raw[:], bv)]
                if key_mask is not None:
                    loads.append((key_u8[:], key_mask))
                for dst, src in loads:
                    sp.dma_start(dst, src).then_inc(m.loaded.sem, 16)
                n = len(loads)
                if small:
                    sp.wait_ge(*m.ready_made.after(1))
                    for h in range(G):
                        sp.dma_start(wo_s[W * h:W * h + hd, :, :], wo.rearrange("(g h e) n -> h e g n", h=G, e=hd)[h])\
                            .then_inc(m.loaded.sem, 16)
                    n += G
                if key_bias is not None:
                    for r in range(3):
                        sp.dma_start(kb[32 * r:32 * r + 1, :], key_bias).then_inc(m.loaded.sem, 16)
                    n += 3
                assert n == NLOAD
                for u in range(2):
                    stream(u, u)
                with sp.Fori(0, PAIRS) as i:
                    for u in range(2):
                        sp.wait_ge(*m.pv_done.after(NG * (2 * i + u) + 1))
                        stream(2 * i + u + AHEAD, u)
                for s in m.streamed:
                    sp.wait_ge(*s.after(per_load * (PAIRS + 1)))

            @block.gpsimd
            def _(pool):
                with pool.Fori(0, PAIRS) as i:
                    for u in range(2):
                        norm.pool(pool, 2 * i + u)

            @block.vector
            def _(dve):
                step = 0
                zeros = [(wv_s, wo_s)] if small else [tuple(q)]
                zeros = list(zeros[0]) + ([bv_s] if bq is not None else [])
                if mask is None:
                    zeros.append(key_rows)
                if key_bias is not None:
                    zeros.append(kb)
                for t in zeros[:-1]:
                    dve.memset(t[:], 0.0).then_inc(m.step.sem, 1)
                dve.memset(zeros[-1][:], 0.0).then_inc(m.step.sem, 1)
                step += len(zeros)
                dve.wait_ge(*m.step.after(step))
                dve.engine_nop().then_inc(m.ready_made.sem, 1)
                dve.wait_ge(*m.loaded.after(16 * NLOAD))
                if small:
                    dve.tensor_copy(wv_s[:].rearrange("p (h w) -> p h w", w=W)[:, :, 0:hd],
                                    wv_raw[:].rearrange("p (h e) -> p h e", e=hd)).then_inc(m.step.sem, 1)
                    step += 1
                if bq is not None:
                    dve.tensor_copy(bv_s[:].rearrange("p (h w) -> p h w", w=W)[:, :, 0:hd],
                                    bv_raw[:].rearrange("p (h e) -> p h e", e=hd)).then_inc(m.step.sem, 1)
                    step += 1
                if key_mask is not None:
                    dve.tensor_scalar(key_rows[0:1, :], key_u8[:], 0.0, -1e30, ALU.is_equal, ALU.mult).then_inc(m.step.sem, 1)
                    step += 1
                if key_bias is not None:
                    dve.tensor_copy(kb_hi[:], kb[:]).then_inc(m.step.sem, 1)
                    dve.wait_ge(*m.step.after(step + 1))
                    dve.tensor_copy(key_rows[0:1, :], kb_hi[0:1, :]).then_inc(m.step.sem, 1)
                    dve.tensor_tensor(kb[:], kb[:], kb_hi[:], ALU.subtract).then_inc(m.step.sem, 1)
                    dve.wait_ge(*m.step.after(step + 3))
                    dve.tensor_copy(kb_hi[:], kb[:]).then_inc(m.step.sem, 1)
                    dve.wait_ge(*m.step.after(step + 4))
                    dve.tensor_copy(key_rows[32:33, :], kb_hi[32:33, :]).then_inc(m.step.sem, 1)
                    dve.tensor_tensor(kb[:], kb[:], kb_hi[:], ALU.subtract).then_inc(m.step.sem, 1)
                    dve.wait_ge(*m.step.after(step + 6))
                    dve.tensor_copy(key_rows[64:65, :], kb[64:65, :]).then_inc(m.step.sem, 1)
                    step += 7
                dve.wait_ge(*m.step.after(step))
                dve.engine_nop().then_inc(m.ready_made.sem, 1)
                assert step == NSTEP

                def copy_turned(b, u, n):
                    h, j = divmod(n, TPB)
                    g, hh = divmod(h, G)
                    if g >= 2 and n % (G * TPB) == 0:
                        dve.wait_ge(*m.pv_done.after(NG * b + g - 1))
                    dve.wait_ge(*m.turned.after(UNITS * b + n + 1))
                    dve.tensor_copy(pT[g % 2][:, hh, :, j * P:(j + 1) * P],
                                    t_ps[n % 2][:].rearrange("p (c t) -> p c t", t=P)).then_inc(m.turned_copied.sem, 1)

                with dve.Fori(0, PAIRS) as i:
                    for u in range(2):
                        b = 2 * i + u
                        norm.vector(dve, b, u, lambda j: x[:, TPB * b + j, :])
                        if mask is not None:
                            dve.wait_ge(*m.streamed[u].after(per_load * (i + 1)))
                            dve.tensor_scalar(mask_b[u][:], mask_i[u][:], 0.0, -1e20, ALU.is_equal, ALU.mult)\
                                .then_inc(m.mask_ready.sem, 1)
                        if small:
                            dve.wait_ge(*ring.empty(i, u, Q))
                            for h in range(HEADS):
                                dve.tensor_scalar(q[u][:, h, :], q_all[:], k["head_cols"][:, h:h + 1], None, ALU.mult)\
                                    .then_inc(m.q_masked.sem, 1)
                        for c in range(CPB):
                            for half in range(VH):
                                f = V + c * VH + half
                                dve.wait_ge(*ring.full(i, u, f))
                                dve.tensor_copy(v[u][:, c, half * 512:half * 512 + 512], ring.bank(u, f)[:]).then_inc(ring.drains(u, f), 1)
                        for n in range(UNITS + 2):
                            if n < UNITS:
                                dve.wait_ge(*m.scores_ready.after(UNITS * b + n + 1))
                                dve.tensor_reduce(nmax[:, u, n:n + 1], s_ps[n % 2][:], AX.X, ALU.max, negate=True)\
                                    .then_inc(m.max_ready.sem, 1)
                            if n >= 2:
                                copy_turned(b, u, n - 2)
                        dve.wait_ge(*m.probs_ready.after(UNITS * (b + 1)))
                        dve.reciprocal(inv[:], sums[:, u].rearrange("p t h -> p (t h)")).then_inc(m.sums_inverted.sem, 1)
                        dve.wait_ge(*m.pv_copied.after(NG * (b + 1)))
                        for g in range(0, NG, 2):
                            f = SPREAD + g // 2
                            dve.wait_ge(*ring.full(i, u, f))
                            og = o[:, g:g + 2, :].rearrange("p g t -> p (g t)")
                            dve.tensor_tensor(og, ring.bank(u, f)[:], og, ALU.mult).then_inc(ring.drains(u, f), 1)
                        add_to_x(m, dve, ring, i, u, OUT)

            @block.scalar
            def _(act):
                act.wait_ge(*m.ready_made.after(2))
                with act.Fori(0, PAIRS) as i:
                    for u in range(2):
                        b = 2 * i + u
                        act.wait_ge(*ring.full(i, u, TURN))
                        act.activation(xnT[u][:], ring.bank(u, TURN)[:, 0:S], ACT.Copy).then_inc(ring.drains(u, TURN), 1)
                        if small:
                            act.wait_ge(*ring.full(i, u, Q))
                            src = ring.bank(u, Q)[:, 0:S]
                            (act.activation(q_all[:], src, ACT.Copy) if bq is None else
                       act.activation(q_all[:], src, ACT.Identity, bias=bq_s[:, 0:1])).then_inc(ring.drains(u, Q), 1)
                        else:
                            for f in range(NK // 2):
                                act.wait_ge(*ring.full(i, u, Q + f))
                                bank = ring.bank(u, Q + f)[:].rearrange("p (t s) -> p t s", s=S)
                                act.activation(q[u][0:W, 4 * f:4 * f + 4:2, :], bank[0:W], ACT.Copy, scale=hd ** -0.5)
                                act.activation(q[u][W:P, 4 * f + 1:4 * f + 4:2, :], bank[W:P], ACT.Copy,
                                               scale=hd ** -0.5).then_inc(ring.drains(u, Q + f), 1)
                        for t in range(NK):
                            act.wait_ge(*ring.full(i, u, K + t))
                            src = ring.bank(u, K + t)[:]
                            (act.activation(kT[u][:, t, :], src, ACT.Copy) if bk is None else
                   act.activation(kT[u][:, t, :], src, ACT.Identity, bias=bk_s[:, 0:1])).then_inc(ring.drains(u, K + t), 1)

                        def copy_group(g):
                            act.wait_ge(*m.pv_done.after(NG * b + g + 1))
                            act.activation(o[:, g, :], o_ps[g % 2][:, 0:S], ACT.Copy).then_inc(m.pv_copied.sem, 1)

                        for n in range(UNITS):
                            h, j = divmod(n, TPB)
                            act.wait_ge(*m.max_ready.after(UNITS * b + n + 1))
                            act.activation(probs[n % 2][:], s_ps[n % 2][:], ACT.Exp, bias=nmax[:, u, n:n + 1],
                                           accum_out=sums[:, u, j, h:h + 1]).then_inc(m.probs_ready.sem, 1)
                            g = (n - 4) // (G * TPB)
                            if n >= 4 and (n - 4) % (G * TPB) == G * TPB - 1:
                                copy_group(g)
                        copy_group(NG - 1)
                        act.wait_ge(*ring.full(i, u, SUMS))
                        act.activation(invT[:], ring.bank(u, SUMS)[0:HEADS, 0:S], ACT.Copy).then_inc(ring.drains(u, SUMS), 1)

            @block.tensor
            def _(pe):
                pe.wait_ge(*m.ready_made.after(2))
                with pe.Fori(0, PAIRS) as i:
                    for u in range(2):
                        b = 2 * i + u
                        turn_normed(m, pe, norm, ring, i, u, TURN)
                        pe.wait_ge(*ring.empty(i, u, TURN))
                        for f in range(1 if small else NK // 2):
                            pe.wait_ge(*ring.free(i, u, Q + f))
                            for t in range(1 if small else 2):
                                c0 = (2 * f + t) * P
                                ins = pe.matmul(ring.bank(u, Q + f)[:, t * S:(t + 1) * S], wq_s[:, c0:c0 + P], xnT[u][:],
                                                start=True, stop=True)
                            ins.then_inc(ring.fills(u, Q + f), 1)
                        pe.wait_ge(*m.streamed[u].after(per_load * (i + 1)))
                        for t in range(NK):
                            pe.wait_ge(*ring.free(i, u, K + t))
                            pe.matmul(ring.bank(u, K + t)[:], wk_s[:, t * P:(t + 1) * P], ctxT[u][:],
                                      start=True, stop=True).then_inc(ring.fills(u, K + t), 1)
                        for c in range(CPB):
                            for half in range(VH):
                                f = V + c * VH + half
                                cols = slice(half * 512, half * 512 + 512)
                                pe.wait_ge(*ring.free(i, u, f))
                                if bv is not None:
                                    pe.matmul(ring.bank(u, f)[:], k["ones"][0:1, :], bv_s[:, cols], start=True, stop=False)
                                pe.matmul(ring.bank(u, f)[:], ctxT[u][:, c * P:(c + 1) * P], wv_s[:, cols],
                                          start=(bv is None), stop=True).then_inc(ring.fills(u, f), 1)

                        def scores(n):
                            h, j = divmod(n, TPB)
                            out = s_ps[n % 2][:]
                            if mask is not None:
                                if n == 0:
                                    pe.wait_ge(*m.mask_ready.after(b + 1))
                                pe.matmul(out, k["ident_bf"], mask_b[u][:, j, :], start=True, stop=False)
                            else:
                                pe.matmul(out, k["ones_bf"], key_rows[:, bass.ds(b * KV, KV)], start=True, stop=False)
                            if small and j == 0:
                                pe.wait_ge(*m.q_masked.after(HEADS * b + h + 1))
                            if n == 0:
                                pe.wait_ge(*ring.empty(i, u, V - 1))
                                pe.wait_ge(*ring.empty(i, u, V - 2))
                            pe.matmul(out, q[u][:, h, j * P:(j + 1) * P], kT[u][:, h // G if not small else 0, :],
                                      start=False, stop=True).then_inc(m.scores_ready.sem, 1)

                        def weigh(g):
                            pe.wait_ge(*m.turned_copied.after(UNITS * b + G * TPB * (g + 1)))
                            if g >= 2:
                                pe.wait_ge(*m.pv_copied.after(NG * b + g - 1))
                            if g == 0:
                                pe.wait_ge(*ring.empty(i, u, SUMS - 1))
                                pe.wait_ge(*ring.empty(i, u, SUMS - 2))
                            for c in range(CPB):
                                for hh in range(G):
                                    ins = pe.matmul(o_ps[g % 2][W * hh:W * (hh + 1), 0:S],
                                                    v[u][:, c, (G * g + hh) * W:(G * g + hh + 1) * W],
                                                    pT[g % 2][:, hh, c, :], start=(c == 0), stop=(c == CPB - 1))
                            ins.then_inc(m.pv_done.sem, 1)

                        scores(0)
                        scores(1)
                        for n in range(UNITS):
                            pe.wait_ge(*m.probs_ready.after(UNITS * b + n + 1))
                            if n >= 2:
                                pe.wait_ge(*m.turned_copied.after(UNITS * b + n - 1))
                            for c in range(CPB):
                                ins = pe.transpose(t_ps[n % 2][:, c * P:(c + 1) * P], probs[n % 2][:, c * P:(c + 1) * P],
                                                   k["ident"])
                            ins.then_inc(m.turned.sem, 1)
                            if n + 2 < UNITS:
                                scores(n + 2)
                            g = (n - 2) // (G * TPB)
                            if n >= 2 and (n - 2) % (G * TPB) == G * TPB - 1:
                                weigh(g)
                        weigh(NG - 1)
                        pe.wait_ge(*m.sums_inverted.after(b + 1))
                        pe.wait_ge(*ring.free(i, u, SUMS))
                        for j in range(TPB):
                            ins = pe.transpose(ring.bank(u, SUMS)[0:HEADS, j * P:(j + 1) * P],
                                               inv[:, j * HEADS:(j + 1) * HEADS], k["ident"])
                        ins.then_inc(ring.fills(u, SUMS), 1)
                        pe.wait_ge(*ring.empty(i, u, SUMS))
                        for g in range(0, NG, 2):
                            f = SPREAD + g // 2
                            pe.wait_ge(*ring.free(i, u, f))
                            for t in range(2):
                                ins = pe.matmul(ring.bank(u, f)[:, t * S:(t + 1) * S],
                                                spread[0:HEADS, (g + t) * P:(g + t + 1) * P], invT[:], start=True, stop=True)
                            ins.then_inc(ring.fills(u, f), 1)
                        pe.wait_ge(*ring.free(i, u, OUT))
                        pe.wait_ge(*ring.empty(i, u, OUT - 1))
                        for j in range(TPB):
                            out = ring.bank(u, OUT)[:, j * D:(j + 1) * D]
                            pe.matmul(out, k["ones"][0:1, :], bo_s[:], start=True, stop=False)
                            for g in range(NG):
                                ins = pe.matmul(out, o[:, g, j * P:(j + 1) * P], wo_s[:, g, :], start=False, stop=(g == NG - 1))
                        ins.then_inc(ring.fills(u, OUT), 1)
        norm.close(B)
        ring.close()
        for s, n in ((m.loaded, 16 * NLOAD), (m.step, NSTEP), (m.ready_made, 2), (m.streamed[0], per_load * (PAIRS + 1)),
                     (m.streamed[1], per_load * (PAIRS + 1)), (m.mask_ready, B if mask is not None else 0),
                     (m.q_masked, HEADS * B if small else 0), (m.scores_ready, UNITS * B), (m.max_ready, UNITS * B),
                     (m.probs_ready, UNITS * B), (m.turned, UNITS * B), (m.turned_copied, UNITS * B), (m.pv_done, NG * B),
                     (m.pv_copied, NG * B), (m.sums_inverted, B)):
            s.before += n


def l1_cross_attention(m):
    d = m.dram
    head_attention(m, "l1x", 8, d["L1_xattn_Wq"], d["L1_xattn_Wk"], d["L1_xattn_Wv"], d["L1_xattn_Wo"], d["L1_xattn_bo"],
                   mask=d["mask"])


def l2_cross_attention(m):
    d = m.dram
    inner = HEADS * 64
    head_attention(m, "l2x", 64, d["L2_xattn_Wq"], d["L2_xattn_Wkv"][:, 0:inner], d["L2_xattn_Wkv"][:, inner:],
                   d["L2_xattn_Wout"], d["L2_xattn_b_out"], key_mask=d["key_mask"])


def l3_cross_attention(m):
    d = m.dram
    head_attention(m, "l3x", 8, d["L3_xattn_wq"], d["L3_xattn_wk"], d["L3_xattn_wv"], d["L3_xattn_wo"], d["L3_xattn_bo"],
                   bq=d["L3_xattn_bq"], bk=d["L3_xattn_bk"], bv=d["L3_xattn_bv"], key_bias=d["time_bias"])


def turn_bf16(m, pe, ring, i, u, fill, src, n):
    pe.wait_ge(*ring.free(i, u, fill))
    out = ring.bank(u, fill)[:, 0:n * P // 2].bitcast(BF16)
    for c in range(n):
        ins = pe.transpose(out[:, c * P:(c + 1) * P], src(c), m.consts["ident_bf"])
    ins.then_inc(ring.fills(u, fill), 1)


def l1_bit_ffn(m):
    nc, d, x, k = m.nc, m.dram, m.x, m.consts
    H = 512
    HC = H // P
    EPS_NORM, EPS_Q, QMAX = 1e-8, 1e-5, 127.0
    CHAIN = 2 * TPB + 5
    with ExitStack() as ctx:
        sb = lambda name, shape, dt=F32: sbuf(m, ctx, f"{name}_l1f", shape, dt)
        norm = Norm(m, ctx, TPB, "l1f")
        w = sb("w", [P, 2, H])
        wq = sb("wq", [P, 2, H], BF16)
        n1w, n2w = sb("n1w", [P, D]), sb("n2w", [P, H])
        gain, offset = sb("gain", [P, 1]), sb("offset", [P, 1])
        wsum, wmean, wscale = sb("wsum", [P, 2]), sb("wmean", [P, 2]), sb("wscale", [P, 2])
        small = lambda name: [sb(f"{name}{s}", [P, TPB]) for s in range(2)]
        ss, ms, rr, am, qs, cc = small("ss"), small("ms"), small("rr"), small("am"), small("qs"), small("cc")
        junk = sb("junk", [P, TPB, H])
        xr = sb("xr", [P, TPB, D])
        xq = sb("xq", [P, TPB, D], BF16)
        xqT = [sb(f"xqT{u}", [P, S], BF16) for u in range(2)]
        h = sb("h", [P, TPB, H])
        hh = sb("hh", [P, TPB, H])
        hr = sb("hr", [P, TPB, H])
        hq = sb("hq", [P, TPB, H], BF16)
        hqT = [sb(f"hqT{u}", [P, TPB, HC, P], BF16) for u in range(2)]
        TURN, TURN_H, OUT = 0, 1, 1 + TPB
        ring = Ring([psum(m, ctx, f"ring{n}_l1f", [P, 512]) for n in range(2)], m.filled, m.drained, OUT + 1)
        h_ps = [psum(m, ctx, f"h_ps{j}_l1f", [P, H]) for j in range(TPB)]
        w_ps = psum(m, ctx, "w_ps_l1f", [P, 2])

        with nc.Block() as block:
            @block.sync
            def _(sp):
                for dst, src in ((w[:, 0, :], d["L1_ffn_w1"]),
                                 (w[:, 1, :].rearrange("p (c d) -> p c d", d=D), d["L1_ffn_w2"].rearrange("(c p) d -> p c d", p=P)),
                                 (n1w[:], d["L1_ffn_norm1_w"][0, :].partition_broadcast(P)),
                                 (n2w[:], d["L1_ffn_norm2_w"][0, :].partition_broadcast(P)),
                                 (gain[:], d["L1_ffn_act_scale"][0, :].partition_broadcast(P)),
                                 (offset[:], d["L1_ffn_act_bias"][0, :].partition_broadcast(P))):
                    sp.dma_start(dst, src).then_inc(m.loaded.sem, 16)
                sp.wait_ge(*m.loaded.after(96))

            @block.gpsimd
            def _(pool):
                with pool.Fori(0, PAIRS) as i:
                    for u in range(2):
                        b = 2 * i + u
                        norm.pool(pool, b)
                        for s in range(2):
                            pool.wait_ge(*m.squares_ready.after(2 * b + s + 1))
                            pool.tensor_tensor(rr[s][:], ms[s][:], k["minus_half"][:, 0:TPB], ALU.pow)\
                                .then_inc(m.powers_ready.sem, 1)

            @block.vector
            def _(dve):
                dve.wait_ge(*m.loaded.after(96))
                dve.tensor_reduce(wsum[:], w[:], AX.X, ALU.add, apply_absolute_value=True).then_inc(m.ready_made.sem, 1)
                dve.wait_ge(*m.turned.after(1))
                dve.tensor_scalar(wmean[:], w_ps[:], 1.0 / (H * D), EPS_Q, ALU.mult, ALU.max).then_inc(m.step.sem, 1)
                dve.wait_ge(*m.step.after(1))
                dve.reciprocal(wscale[:], wmean[:]).then_inc(m.step.sem, 1)
                dve.wait_ge(*m.step.after(2))
                for n in range(2):
                    dve.tensor_scalar(w[:, n, :], w[:, n, :], wscale[:, n:n + 1], MAGIC, ALU.mult, ALU.add).then_inc(m.step.sem, 1)
                dve.wait_ge(*m.step.after(4))
                dve.tensor_scalar(w[:], w[:], MAGIC, 1.0, ALU.subtract, ALU.min).then_inc(m.step.sem, 1)
                dve.wait_ge(*m.step.after(5))
                dve.tensor_scalar(wq[:], w[:], -1.0, None, ALU.max).then_inc(m.step.sem, 1)
                dve.wait_ge(*m.step.after(6))
                dve.engine_nop().then_inc(m.ready_made.sem, 1)
                def quantise(b, s, src, factor, r, dst, width):
                    at = 6 + CHAIN * (2 * b + s)
                    dve.wait_ge(*m.squares_summed.after(TPB * (2 * b + s + 1)))
                    dve.tensor_scalar(ms[s][:], ss[s][:], 1.0 / width, EPS_NORM, ALU.mult, ALU.add).then_inc(m.squares_ready.sem, 1)
                    dve.wait_ge(*m.powers_ready.after(2 * b + s + 1))
                    for j in range(TPB):
                        dve.scalar_tensor_tensor(out=r[:, j, :], in0=src[:, j, :], scalar=rr[s][:, j:j + 1], in1=factor[:],
                                                 op0=ALU.mult, op1=ALU.mult).then_inc(m.step.sem, 1)
                    dve.wait_ge(*m.step.after(at + TPB))
                    dve.tensor_reduce(am[s][:], r[:], AX.X, ALU.max, apply_absolute_value=True).then_inc(m.step.sem, 1)
                    dve.wait_ge(*m.step.after(at + TPB + 1))
                    dve.tensor_scalar(am[s][:], am[s][:], EPS_Q, None, ALU.max).then_inc(m.step.sem, 1)
                    dve.wait_ge(*m.step.after(at + TPB + 2))
                    dve.reciprocal(qs[s][:], am[s][:]).then_inc(m.step.sem, 1)
                    dve.tensor_scalar(cc[s][:], am[s][:], 1.0 / QMAX, wmean[:, s:s + 1], ALU.mult, ALU.mult).then_inc(m.step.sem, 1)
                    dve.wait_ge(*m.step.after(at + TPB + 4))
                    dve.tensor_scalar(qs[s][:], qs[s][:], QMAX, None, ALU.mult).then_inc(m.step.sem, 1)
                    dve.wait_ge(*m.step.after(at + TPB + 5))
                    for j in range(TPB):
                        dve.tensor_scalar(r[:, j, :], r[:, j, :], qs[s][:, j:j + 1], MAGIC, ALU.mult, ALU.add)\
                            .then_inc(m.step.sem, 1)
                    dve.wait_ge(*m.step.after(at + CHAIN))
                    dve.tensor_scalar(dst[:], r[:], MAGIC, QMAX, ALU.subtract, ALU.min).then_inc(m.x_quantised.sem, 1)

                with dve.Fori(0, PAIRS) as i:
                    for u in range(2):
                        b = 2 * i + u
                        norm.vector(dve, b, u, lambda j: x[:, TPB * b + j, :])
                        quantise(b, 0, norm.xn[u], n1w, xr, xq, D)
                        dve.wait_ge(*m.h_squared.after(b + 1))
                        dve.tensor_scalar(hh[:], h[:], gain[:], offset[:], ALU.mult, ALU.add).then_inc(m.squared_affine.sem, 1)
                        quantise(b, 1, hh, n2w, hr, hq, H)
                        dve.wait_ge(*ring.full(i, u, OUT))
                        for j in range(TPB):
                            rows = x[:, TPB * b + j, :]
                            ins = dve.scalar_tensor_tensor(out=rows, in0=ring.bank(u, OUT)[:, j * D:(j + 1) * D],
                                                           scalar=cc[1][:, j:j + 1], in1=rows, op0=ALU.mult, op1=ALU.add)
                        ins.then_inc(ring.drains(u, OUT), 1)

            @block.scalar
            def _(act):
                with act.Fori(0, PAIRS) as i:
                    for u in range(2):
                        b = 2 * i + u
                        act.wait_ge(*m.normed.after(TPB * (b + 1)))
                        for j in range(TPB):
                            act.activation(junk[:, j, 0:D], norm.xn[u][:, j, :], ACT.Square, accum_out=ss[0][:, j:j + 1])\
                                .then_inc(m.squares_summed.sem, 1)
                        act.wait_ge(*ring.full(i, u, TURN))
                        act.activation(xqT[u][:], ring.bank(u, TURN)[:, 0:P].bitcast(BF16), ACT.Copy).then_inc(ring.drains(u, TURN), 1)
                        for j in range(TPB):
                            act.wait_ge(*m.scores_ready.after(TPB * b + j + 1))
                            act.activation(h[:, j, :], h_ps[j][:], ACT.Relu, scale=cc[0][:, j:j + 1]).then_inc(m.act_step.sem, 1)
                        act.wait_ge(*m.act_step.after(TPB * (b + 1)))
                        act.activation(h[:], h[:], ACT.Square).then_inc(m.h_squared.sem, 1)
                        act.wait_ge(*m.squared_affine.after(b + 1))
                        for j in range(TPB):
                            act.activation(junk[:, j, :], hh[:, j, :], ACT.Square, accum_out=ss[1][:, j:j + 1])\
                                .then_inc(m.squares_summed.sem, 1)
                        for j in range(TPB):
                            act.wait_ge(*ring.full(i, u, TURN_H + j))
                            act.activation(hqT[u][:, j].rearrange("p c t -> p (c t)"),
                                           ring.bank(u, TURN_H + j)[:, 0:HC * P // 2].bitcast(BF16), ACT.Copy).then_inc(ring.drains(u, TURN_H + j), 1)

            @block.tensor
            def _(pe):
                pe.wait_ge(*m.ready_made.after(1))
                pe.matmul(w_ps[:], k["ones"], wsum[:], start=True, stop=True).then_inc(m.turned.sem, 1)
                pe.wait_ge(*m.ready_made.after(2))
                with pe.Fori(0, PAIRS) as i:
                    for u in range(2):
                        b = 2 * i + u
                        pe.wait_ge(*m.x_quantised.after(2 * b + 1))
                        turn_bf16(m, pe, ring, i, u, TURN, lambda c: xq[:, c, :], TPB)
                        pe.wait_ge(*ring.empty(i, u, TURN))
                        for j in range(TPB):
                            pe.matmul(h_ps[j][:], xqT[u][:, j * P:(j + 1) * P], wq[:, 0, :], start=True, stop=True)\
                                .then_inc(m.scores_ready.sem, 1)
                        pe.wait_ge(*m.x_quantised.after(2 * b + 2))
                        for j in range(TPB):
                            turn_bf16(m, pe, ring, i, u, TURN_H + j, lambda c: hq[:, j, c * P:(c + 1) * P], HC)
                        pe.wait_ge(*ring.free(i, u, OUT))
                        for j in range(TPB):
                            pe.wait_ge(*ring.empty(i, u, TURN_H + j))
                            for c in range(HC):
                                ins = pe.matmul(ring.bank(u, OUT)[:, j * D:(j + 1) * D], hqT[u][:, j, c, :],
                                                wq[:, 1, c * D:(c + 1) * D], start=(c == 0), stop=(c == HC - 1))
                        ins.then_inc(ring.fills(u, OUT), 1)
        norm.close(B)
        ring.close()
        for s, n in ((m.loaded, 96), (m.ready_made, 2), (m.turned, 1), (m.step, 6 + 2 * CHAIN * B), (m.squares_ready, 2 * B),
                     (m.powers_ready, 2 * B), (m.act_step, TPB * B), (m.squares_summed, 2 * TPB * B), (m.h_squared, B), (m.scores_ready, TPB * B), (m.x_quantised, 2 * B),
                     (m.squared_affine, B)):
            s.before += n


def shift_tokens(m, pe, dve, act, ring, i, u, fill, hb):
    b = 2 * i + u
    x, k = m.x, m.consts
    half = D // 2
    if pe is not None:
        pe.wait_ge(*ring.free(i, u, fill))
        bank = ring.bank(u, fill)
        pe.matmul(bank[:, 0:half], k["shift"], x[:, TPB * b, half:D], start=True, stop=True)
        pe.matmul(bank[:, half:D], k["shift"], x[:, TPB * b + 1, half:D], start=True, stop=False)
        pe.matmul(bank[:, half:D], k["last"], x[:, TPB * b, half:D], start=False, stop=True).then_inc(ring.fills(u, fill), 1)
    if dve is not None:
        dve.tensor_copy(hb[u][:, :, 0:half], x[:, bass.ds(TPB * b, TPB), 0:half]).then_inc(m.unshifted.sem, 1)
    if act is not None:
        act.wait_ge(*ring.full(i, u, fill))
        act.activation(hb[u][:, :, half:D], ring.bank(u, fill)[:, 0:D].rearrange("p (t d) -> p t d", d=half),
                       ACT.Copy).then_inc(ring.drains(u, fill), 1)


def local_attention(m, layer):
    nc, d, x, k = m.nc, m.dram, m.x, m.consts
    NH, HD = 8, 64
    INNER = NH * HD
    NG = NH // 2
    BAND = 3 * P
    with ExitStack() as ctx:
        sb = lambda name, shape, dt=F32: sbuf(m, ctx, f"{name}_l2a{layer}", shape, dt)
        wqkv = sb("wqkv", [P, 3 * INNER])
        wo = sb("wo", [P, NG, D])
        scales = sb("scales", [P, 2, HD])
        ta, tb = sb("ta", [P, 2, TPB, HD]), sb("tb", [P, 2, TPB, HD])
        hb = [sb(f"hb{u}", [P, TPB, D]) for u in range(2)]
        hT = [sb(f"hT{u}", [P, S]) for u in range(2)]
        qk = [sb(f"qk{u}", [P, TPB, 2, NH, HD]) for u in range(2)]
        sq = sb("sq", [P, TPB, 2 * INNER])
        ss = sb("ss", [P, TPB, 2 * NH])
        ssc = sb("ssc", [P, TPB * 2 * NH])
        rn = sb("rn", [P, TPB * 2 * NH])
        own, other = sb("own", [P, TPB, 2, NH, HD]), sb("other", [P, TPB, 2, NH, HD])
        q = [sb(f"q{u}", [P, NH, S]) for u in range(2)]
        kT = [sb(f"kT{u}", [P, NG, S]) for u in range(2)]
        v = [sb(f"v{u}", [P, TPB, INNER]) for u in range(2)]
        nmax = sb("nmax", [P, 2, NH * TPB])
        sums = sb("sums", [P, 2, TPB, NH])
        inv = sb("inv", [P, TPB * NH])
        invT = sb("invT", [NH, S])
        probs = [sb(f"probs{n}", [P, BAND]) for n in range(2)]
        pT = [sb(f"pT{n}", [P, 2, 3, P]) for n in range(2)]
        o = sb("o", [P, NG, S])
        SHIFT, TURN, QKV = 0, 1, 2
        TURN_QK = QKV + 3 * TPB
        SUMS = TURN_QK + 2 * TPB
        SPREAD = SUMS + 1
        OUT = SPREAD + NG // 2
        ring = Ring([psum(m, ctx, f"ring{n}_l2a{layer}", [P, 512]) for n in range(2)], m.filled, m.drained, OUT + 1)
        s_ps = [psum(m, ctx, f"s_ps{n}_l2a{layer}", [P, 512]) for n in range(2)]
        t_ps = [psum(m, ctx, f"t_ps{n}_l2a{layer}", [P, 512]) for n in range(2)]
        o_ps = [psum(m, ctx, f"o_ps{n}_l2a{layer}", [P, 512]) for n in range(2)]
        CHAIN = 2 + 2 + 1

        with nc.Block() as block:
            @block.sync
            def _(sp):
                for dst, src in ((wqkv[:], d["L2_ffn_wqkv"][layer]),
                                 (wo[:], d["L2_ffn_wo"][layer].rearrange("(g p) n -> p g n", p=P)),
                                 (scales[:, 0, :], d["L2_ffn_q_scale"][layer].partition_broadcast(P)),
                                 (scales[:, 1, :], d["L2_ffn_k_scale"][layer].partition_broadcast(P))):
                    sp.dma_start(dst, src).then_inc(m.loaded.sem, 16)
                sp.wait_ge(*m.loaded.after(64))

            @block.gpsimd
            def _(pool):
                pool.wait_ge(*m.ready_made.after(6))
                with pool.Fori(0, PAIRS) as i:
                    for u in range(2):
                        b = 2 * i + u
                        for j in range(TPB):
                            for w in range(2):
                                pool.wait_ge(*ring.empty(i, u, QKV + 3 * j + w))
                                for hf in range(2):
                                    to, of = slice(32 * hf, 32 * hf + 32), slice(32 - 32 * hf, 64 - 32 * hf)
                                    pool.tensor_tensor(other[:, j, w, :, to], qk[u][:, j, w, :, of],
                                                       tb[:, w, j, to].unsqueeze(1).to_broadcast([P, NH, 32]), ALU.mult)\
                                        .then_inc(m.rotated.sem, 1)
                        pool.wait_ge(*m.squares_ready.after(b + 1))
                        pool.tensor_tensor(rn[:], ssc[:], k["minus_half"][:, 0:TPB * 2 * NH], ALU.pow).then_inc(m.powers_ready.sem, 1)

            @block.vector
            def _(dve):
                for t in q:
                    dve.memset(t[:], 0.0).then_inc(m.step.sem, 1)
                dve.wait_ge(*m.loaded.after(64))
                for w, (a, bb) in enumerate((("rot_qa", "rot_qb"), ("rot_ka", "rot_kb"))):
                    sc = lambda lo, n: scales[:, w, lo:lo + n].unsqueeze(1).to_broadcast([P, TPB, n])
                    fa = k[a].rearrange("p (t e) -> p t e", e=HD)
                    fb = k[bb].rearrange("p (t e) -> p t e", e=HD)
                    dve.tensor_tensor(ta[:, w], fa, sc(0, HD), ALU.mult).then_inc(m.ready_made.sem, 1)
                    dve.tensor_tensor(tb[:, w, :, 0:32], fb[:, :, 0:32], sc(32, 32), ALU.mult).then_inc(m.ready_made.sem, 1)
                    dve.tensor_tensor(tb[:, w, :, 32:64], fb[:, :, 32:64], sc(0, 32), ALU.mult).then_inc(m.ready_made.sem, 1)
                dve.wait_ge(*m.ready_made.after(6))

                def copy_turned(b, n):
                    g, hh = divmod(n, 2)
                    if g >= 2 and hh == 0:
                        dve.wait_ge(*m.pv_done.after(NG * b + g - 1))
                    dve.wait_ge(*m.turned.after(NH * b + n + 1))
                    dve.tensor_copy(pT[g % 2][:, hh].rearrange("p c t -> p (c t)"), t_ps[n % 2][:, 0:BAND])\
                        .then_inc(m.turned_copied.sem, 1)

                with dve.Fori(0, PAIRS) as i:
                    for u in range(2):
                        b = 2 * i + u
                        at = 2 + CHAIN * b
                        shift_tokens(m, None, dve, None, ring, i, u, SHIFT, hb)
                        for j in range(TPB):
                            f = QKV + 3 * j + 2
                            dve.wait_ge(*ring.full(i, u, f))
                            dve.tensor_copy(v[u][:, j, :], ring.bank(u, f)[:]).then_inc(ring.drains(u, f), 1)
                        for j in range(TPB):
                            dve.wait_ge(*m.h_squared.after(TPB * b + j + 1))
                            dve.tensor_reduce(ss[:, j, :], sq[:, j].rearrange("p (h e) -> p h e", e=HD), AX.X, ALU.add)\
                                .then_inc(m.step.sem, 1)
                        dve.wait_ge(*m.step.after(at + 2))
                        dve.tensor_scalar(ssc[:], ss[:].rearrange("p t h -> p (t h)"), 1e-24, None, ALU.max)\
                            .then_inc(m.squares_ready.sem, 1)
                        for j in range(TPB):
                            dve.tensor_tensor(own[:, j], qk[u][:, j], ta[:, :, j, :].unsqueeze(2).to_broadcast([P, 2, NH, HD]),
                                              ALU.mult).then_inc(m.step.sem, 1)
                        dve.wait_ge(*m.step.after(at + 4))
                        dve.wait_ge(*m.rotated.after(4 * TPB * (b + 1)))
                        flat = lambda t: t[:].rearrange("p t w h e -> p (t w h e)")
                        dve.tensor_tensor(flat(own), flat(own), flat(other), ALU.add).then_inc(m.step.sem, 1)
                        dve.wait_ge(*m.step.after(at + 5))
                        dve.wait_ge(*m.powers_ready.after(b + 1))
                        heads = own[:].rearrange("p t w h e -> p (t w h) e")
                        dve.tensor_tensor(heads, heads, rn[:].unsqueeze(2).to_broadcast([P, TPB * 2 * NH, HD]), ALU.mult)\
                            .then_inc(m.normed.sem, 1)
                        for j in range(TPB):
                            f = TURN_QK + 2 * j + 1
                            dve.wait_ge(*ring.full(i, u, f))
                            dve.tensor_copy(kT[u][:, :, j * P:(j + 1) * P],
                                            ring.bank(u, f)[:].rearrange("p (g t) -> p g t", t=P)).then_inc(ring.drains(u, f), 1)
                        for n in range(NH + 2):
                            if n < NH:
                                dve.wait_ge(*m.scores_ready.after(NH * b + n + 1))
                                for j, cols in enumerate((slice(0, P), slice(P, BAND))):
                                    dve.tensor_reduce(nmax[:, u, TPB * n + j:TPB * n + j + 1], s_ps[n % 2][:, cols], AX.X, ALU.max,
                                                      negate=True).then_inc(m.max_ready.sem, 1)
                            if n >= 2:
                                copy_turned(b, n - 2)
                        dve.wait_ge(*m.probs_ready.after(TPB * NH * (b + 1)))
                        dve.reciprocal(inv[:], sums[:, u].rearrange("p t h -> p (t h)")).then_inc(m.sums_inverted.sem, 1)
                        dve.wait_ge(*m.pv_copied.after(NG * (b + 1)))
                        for g in range(0, NG, 2):
                            f = SPREAD + g // 2
                            dve.wait_ge(*ring.full(i, u, f))
                            og = o[:, g:g + 2, :].rearrange("p g t -> p (g t)")
                            dve.tensor_tensor(og, ring.bank(u, f)[:], og, ALU.mult).then_inc(ring.drains(u, f), 1)
                        add_to_x(m, dve, ring, i, u, OUT)

            @block.scalar
            def _(act):
                act.wait_ge(*m.ready_made.after(6))
                with act.Fori(0, PAIRS) as i:
                    for u in range(2):
                        b = 2 * i + u
                        shift_tokens(m, None, None, act, ring, i, u, SHIFT, hb)
                        act.wait_ge(*ring.full(i, u, TURN))
                        act.activation(hT[u][:], ring.bank(u, TURN)[:, 0:S], ACT.Copy).then_inc(ring.drains(u, TURN), 1)
                        for j in range(TPB):
                            for w in range(2):
                                f = QKV + 3 * j + w
                                act.wait_ge(*ring.full(i, u, f))
                                act.activation(qk[u][:, j, w].rearrange("p h e -> p (h e)"), ring.bank(u, f)[:],
                                               ACT.Copy).then_inc(ring.drains(u, f), 1)
                            for w in range(2):
                                act.wait_ge(*ring.empty(i, u, QKV + 3 * j + w))
                            act.activation(sq[:, j], qk[u][:, j].rearrange("p w h e -> p (w h e)"), ACT.Square)\
                                .then_inc(m.h_squared.sem, 1)
                        for j in range(TPB):
                            f = TURN_QK + 2 * j
                            act.wait_ge(*ring.full(i, u, f))
                            bank = ring.bank(u, f)[:].rearrange("p (g t) -> p g t", t=P)
                            cols = slice(j * P, (j + 1) * P)
                            act.activation(q[u][0:HD, 0:NH:2, cols], bank[0:HD], ACT.Copy)
                            act.activation(q[u][HD:P, 1:NH:2, cols], bank[HD:P], ACT.Copy).then_inc(ring.drains(u, f), 1)

                        def copy_group(g):
                            act.wait_ge(*m.pv_done.after(NG * b + g + 1))
                            act.activation(o[:, g, :], o_ps[g % 2][:, 0:S], ACT.Copy).then_inc(m.pv_copied.sem, 1)

                        for n in range(NH):
                            act.wait_ge(*m.max_ready.after(TPB * (NH * b + n + 1)))
                            for j, cols in enumerate((slice(0, P), slice(P, BAND))):
                                act.activation(probs[n % 2][:, cols], s_ps[n % 2][:, cols], ACT.Exp,
                                               bias=nmax[:, u, TPB * n + j:TPB * n + j + 1],
                                               accum_out=sums[:, u, j, n:n + 1]).then_inc(m.probs_ready.sem, 1)
                            if n >= 4 and n % 2:
                                copy_group((n - 4) // 2)
                        copy_group(NG - 2)
                        copy_group(NG - 1)
                        act.wait_ge(*ring.full(i, u, SUMS))
                        act.activation(invT[:], ring.bank(u, SUMS)[0:NH, 0:S], ACT.Copy).then_inc(ring.drains(u, SUMS), 1)

            @block.tensor
            def _(pe):
                pe.wait_ge(*m.ready_made.after(6))
                with pe.Fori(0, PAIRS) as i:
                    for u in range(2):
                        b = 2 * i + u
                        shift_tokens(m, pe, None, None, ring, i, u, SHIFT, hb)
                        pe.wait_ge(*ring.empty(i, u, SHIFT))
                        pe.wait_ge(*m.unshifted.after(b + 1))
                        pe.wait_ge(*ring.free(i, u, TURN))
                        for j in range(TPB):
                            ins = pe.transpose(ring.bank(u, TURN)[:, j * P:(j + 1) * P], hb[u][:, j, :], k["ident"])
                        ins.then_inc(ring.fills(u, TURN), 1)
                        pe.wait_ge(*ring.empty(i, u, TURN))
                        for j in range(TPB):
                            for w in range(3):
                                f = QKV + 3 * j + w
                                pe.wait_ge(*ring.free(i, u, f))
                                pe.matmul(ring.bank(u, f)[:], hT[u][:, j * P:(j + 1) * P],
                                          wqkv[:, w * INNER:(w + 1) * INNER], start=True, stop=True).then_inc(ring.fills(u, f), 1)
                        pe.wait_ge(*m.normed.after(b + 1))
                        for j in range(TPB):
                            for w in range(2):
                                f = TURN_QK + 2 * j + w
                                pe.wait_ge(*ring.free(i, u, f))
                                for g in range(NG):
                                    ins = pe.transpose(ring.bank(u, f)[:, g * P:(g + 1) * P],
                                                       own[:, j, w, 2 * g:2 * g + 2, :].rearrange("p h e -> p (h e)"), k["ident"])
                                ins.then_inc(ring.fills(u, f), 1)

                        def scores(n):
                            out = s_ps[n % 2]
                            pe.matmul(out[:, 0:BAND], k["ident_bf"], k["band_bf"], start=True, stop=False)
                            if n == 0:
                                for f in range(SUMS - 2, SUMS):
                                    pe.wait_ge(*ring.empty(i, u, f))
                            pe.matmul(out[:, 0:P], q[u][:, n, 0:P], kT[u][:, n // 2, 0:P], start=False, stop=False)
                            pe.matmul(out[:, P:BAND], q[u][:, n, P:S], kT[u][:, n // 2, :], start=False, stop=True)\
                                .then_inc(m.scores_ready.sem, 1)

                        def weigh(g):
                            pe.wait_ge(*m.turned_copied.after(NH * b + 2 * (g + 1)))
                            if g >= 2:
                                pe.wait_ge(*m.pv_copied.after(NG * b + g - 1))
                            for c in range(TPB):
                                for hh in range(2):
                                    rows = slice(HD * hh, HD * (hh + 1))
                                    vc = v[u][:, c, (2 * g + hh) * HD:(2 * g + hh + 1) * HD]
                                    if c == 0:
                                        ins = pe.matmul(o_ps[g % 2][rows, 0:S], vc, pT[g % 2][:, hh, 0:2, :].rearrange("p c t -> p (c t)"),
                                                        start=True, stop=False)
                                    else:
                                        ins = pe.matmul(o_ps[g % 2][rows, P:S], vc, pT[g % 2][:, hh, 2, :], start=False, stop=True)
                            ins.then_inc(m.pv_done.sem, 1)

                        scores(0)
                        scores(1)
                        for n in range(NH):
                            pe.wait_ge(*m.probs_ready.after(TPB * (NH * b + n + 1)))
                            if n >= 2:
                                pe.wait_ge(*m.turned_copied.after(NH * b + n - 1))
                            for c in range(3):
                                ins = pe.transpose(t_ps[n % 2][:, c * P:(c + 1) * P], probs[n % 2][:, c * P:(c + 1) * P], k["ident"])
                            ins.then_inc(m.turned.sem, 1)
                            if n + 2 < NH:
                                scores(n + 2)
                            if n >= 3 and n % 2:
                                weigh((n - 3) // 2)
                        weigh(NG - 1)
                        pe.wait_ge(*m.sums_inverted.after(b + 1))
                        pe.wait_ge(*ring.free(i, u, SUMS))
                        for j in range(TPB):
                            ins = pe.transpose(ring.bank(u, SUMS)[0:NH, j * P:(j + 1) * P], inv[:, j * NH:(j + 1) * NH], k["ident"])
                        ins.then_inc(ring.fills(u, SUMS), 1)
                        pe.wait_ge(*ring.empty(i, u, SUMS))
                        for g in range(0, NG, 2):
                            f = SPREAD + g // 2
                            pe.wait_ge(*ring.free(i, u, f))
                            for t in range(2):
                                ins = pe.matmul(ring.bank(u, f)[:, t * S:(t + 1) * S], k["spread2"][0:NH, (g + t) * P:(g + t + 1) * P],
                                                invT[:], start=True, stop=True)
                            ins.then_inc(ring.fills(u, f), 1)
                        pe.wait_ge(*ring.free(i, u, OUT))
                        pe.wait_ge(*ring.empty(i, u, OUT - 1))
                        for j in range(TPB):
                            out = ring.bank(u, OUT)[:, j * D:(j + 1) * D]
                            for g in range(NG):
                                ins = pe.matmul(out, o[:, g, j * P:(j + 1) * P], wo[:, g, :], start=(g == 0), stop=(g == NG - 1))
                        ins.then_inc(ring.fills(u, OUT), 1)
        ring.close()
        for s, n in ((m.loaded, 64), (m.ready_made, 6), (m.step, 2 + CHAIN * B), (m.unshifted, B),
                     (m.h_squared, TPB * B), (m.rotated, 4 * TPB * B), (m.squares_ready, B), (m.powers_ready, B), (m.normed, B),
                     (m.scores_ready, NH * B), (m.max_ready, TPB * NH * B), (m.probs_ready, TPB * NH * B), (m.turned, NH * B),
                     (m.turned_copied, NH * B), (m.pv_done, NG * B), (m.pv_copied, NG * B), (m.sums_inverted, B)):
            s.before += n


def gelu_ffn(m, layer):
    nc, d, x, k = m.nc, m.dram, m.x, m.consts
    HID = int(D * 4 * 2 / 3)
    ROWS = [min(P, HID - c * P) for c in range(-(-HID // P))]
    NC = len(ROWS)
    with ExitStack() as ctx:
        sb = lambda name, shape, dt=F32: sbuf(m, ctx, f"{name}_l2f{layer}", shape, dt)
        norm = Norm(m, ctx, TPB, f"l2f{layer}")
        w1 = sb("w1", [P, 2 * HID])
        b1 = sb("b1", [P, 2, NC])
        w2 = sb("w2", [P, NC, D])
        b2 = sb("b2", [1, D])
        lg, lb = sb("lg", [P, 1]), sb("lb", [P, 1])
        hb = [sb(f"hb{u}", [P, TPB, D]) for u in range(2)]
        hT = [sb(f"hT{u}", [P, S]) for u in range(2)]
        gate = [sb(f"gate{u}", [P, NC, S]) for u in range(2)]
        prod = [sb(f"prod{u}", [P, NC, S]) for u in range(2)]
        SHIFT, TURN, HID0 = 0, 1, 2
        OUT = HID0 + 2 * NC
        ring = Ring([psum(m, ctx, f"ring{n}_l2f{layer}", [P, 512]) for n in range(2)], m.filled, m.drained, OUT + 1)
        NLOAD = 4 + 3 * NC

        with nc.Block() as block:
            @block.sync
            def _(sp):
                loads = [(w1[:], d["L2_ffn_w1"][layer]), (b2[:], d["L2_ffn_b2"][layer:layer + 1, :]),
                         (lg[:], d["L2_ffn_ln_g"][layer].rearrange("(p o) -> p o", o=1)),
                         (lb[:], d["L2_ffn_ln_b"][layer].rearrange("(p o) -> p o", o=1))]
                for c, r in enumerate(ROWS):
                    loads.append((w2[0:r, c, :], d["L2_ffn_w2"][layer, c * P:c * P + r, :]))
                    for w in range(2):
                        lo = w * HID + c * P
                        loads.append((b1[0:r, w, c:c + 1], d["L2_ffn_b1"][layer, lo:lo + r].rearrange("(p o) -> p o", o=1)))
                assert len(loads) == NLOAD
                for dst, src in loads:
                    sp.dma_start(dst, src).then_inc(m.loaded.sem, 16)
                sp.wait_ge(*m.loaded.after(16 * NLOAD))

            @block.gpsimd
            def _(pool):
                with pool.Fori(0, PAIRS) as i:
                    for u in range(2):
                        norm.pool(pool, 2 * i + u)

            @block.vector
            def _(dve):
                dve.wait_ge(*m.loaded.after(16 * NLOAD))
                with dve.Fori(0, PAIRS) as i:
                    for u in range(2):
                        b = 2 * i + u
                        shift_tokens(m, None, dve, None, ring, i, u, SHIFT, hb)
                        dve.wait_ge(*m.unshifted.after(b + 1))
                        dve.wait_ge(*ring.empty(i, u, SHIFT))
                        norm.vector(dve, b, u, lambda j: hb[u][:, j, :])
                        for c, r in enumerate(ROWS):
                            fg, fa = HID0 + 2 * c, HID0 + 2 * c + 1
                            dve.wait_ge(*ring.empty(i, u, fg))
                            dve.wait_ge(*ring.full(i, u, fa))
                            dve.scalar_tensor_tensor(out=prod[u][0:r, c, :], in0=ring.bank(u, fa)[0:r, 0:S],
                                                     scalar=b1[0:r, 0, c:c + 1], in1=gate[u][0:r, c, :],
                                                     op0=ALU.add, op1=ALU.mult).then_inc(ring.drains(u, fa), 1)
                        add_to_x(m, dve, ring, i, u, OUT)

            @block.scalar
            def _(act):
                act.wait_ge(*m.loaded.after(16 * NLOAD))
                with act.Fori(0, PAIRS) as i:
                    for u in range(2):
                        shift_tokens(m, None, None, act, ring, i, u, SHIFT, hb)
                        act.wait_ge(*ring.full(i, u, TURN))
                        act.activation(hT[u][:], ring.bank(u, TURN)[:, 0:S], ACT.Identity,
                                       bias=lb[:, 0:1], scale=lg[:, 0:1]).then_inc(ring.drains(u, TURN), 1)
                        for c, r in enumerate(ROWS):
                            f = HID0 + 2 * c
                            act.wait_ge(*ring.full(i, u, f))
                            act.activation(gate[u][0:r, c, :], ring.bank(u, f)[0:r, 0:S], ACT.Gelu,
                                           bias=b1[0:r, 1, c:c + 1]).then_inc(ring.drains(u, f), 1)

            @block.tensor
            def _(pe):
                pe.wait_ge(*m.loaded.after(16 * NLOAD))
                with pe.Fori(0, PAIRS) as i:
                    for u in range(2):
                        shift_tokens(m, pe, None, None, ring, i, u, SHIFT, hb)
                        turn_normed(m, pe, norm, ring, i, u, TURN)
                        pe.wait_ge(*ring.empty(i, u, TURN))
                        for c, r in enumerate(ROWS):
                            for w, lo in ((0, HID), (1, 0)):
                                f = HID0 + 2 * c + w
                                pe.wait_ge(*ring.free(i, u, f))
                                pe.matmul(ring.bank(u, f)[0:r, 0:S], w1[:, lo + c * P:lo + c * P + r], hT[u][:],
                                          start=True, stop=True).then_inc(ring.fills(u, f), 1)
                        pe.wait_ge(*ring.free(i, u, OUT))
                        pe.wait_ge(*ring.empty(i, u, OUT - 1))
                        for j in range(TPB):
                            out = ring.bank(u, OUT)[:, j * D:(j + 1) * D]
                            pe.matmul(out, k["ones"][0:1, :], b2[:], start=True, stop=False)
                            for c, r in enumerate(ROWS):
                                ins = pe.matmul(out, prod[u][0:r, c, j * P:(j + 1) * P], w2[0:r, c, :], start=False, stop=(c == NC - 1))
                        ins.then_inc(ring.fills(u, OUT), 1)
        norm.close(B)
        ring.close()
        for s, n in ((m.loaded, 16 * NLOAD), (m.unshifted, B)):
            s.before += n


def l2_local_transformer(m):
    nc, x = m.nc, m.x
    with ExitStack() as ctx:
        norm = Norm(m, ctx, NT, "l2t", buffers=1)
        y = norm.xn[0]
        with nc.Block() as block:
            @block.gpsimd
            def _(pool):
                norm.pool(pool, 0)

            @block.vector
            def _(dve):
                norm.vector(dve, 0, 0, lambda j: x[:, j, :])
                dve.wait_ge(*m.normed.after(NT))
        norm.close(1)
        m.x = y
        for layer in range(2):
            local_attention(m, layer)
            gelu_ffn(m, layer)
        m.x = x
        with nc.Block() as block:
            @block.vector
            def _(dve):
                dve.tensor_tensor(x[:], x[:], y[:], ALU.add).then_inc(m.step.sem, 1)
                dve.wait_ge(*m.step.after(1))
        m.step.before += 1

def l3_quantised_ffn(m):
    nc, d, x, k = m.nc, m.dram, m.x, m.consts
    I = 352
    ROWS = [min(P, I - c * P) for c in range(-(-I // P))]
    NC, LAST = len(ROWS), ROWS[-1]
    QMAX = 127.0
    T = B * S
    BT = 512
    NB, TB = T // BT, BT // P
    with ExitStack() as ctx:
        sb = lambda name, shape, dt=F32: sbuf(m, ctx, f"{name}_l3f", shape, dt)
        norm = Norm(m, ctx, NT, "l3f", buffers=1)
        xn = norm.xn[0]
        w, wd = sb("w", [P, 2, NC, D]), sb("wd", [P, I])
        wq, wdq = sb("wq", [P, 2, NC, D], BF16), sb("wdq", [P, I], BF16)
        wT, wdT = sb("wT", [P, 2, I], BF16), sb("wdT", [P, NC, D], BF16)
        wscale, dscale = sb("wscale", [P, 2, NC]), sb("dscale", [P, 1])
        winv, dinv, inv = sb("winv", [P, 2, NC]), sb("dinv", [P, 1]), sb("inv", [P, 2])
        clips, sig = sb("clips", [P, 2]), sb("sig", [P, 2])
        diag, dB = sb("diag", [P, P]), sb("dB", [P, D])
        top, peak, scale = sb("top", [P, 2]), sb("peak", [1, 2]), sb("scale", [P, 2])
        hscale = sb("hscale", [P, 2, NC])
        xq, xqT = sb("xq", [P, NT, D], BF16), sb("xqT", [P, T], BF16)
        gate = [sb(f"gate{c}", [P, BT]) for c in range(NC)]
        hT, hq = sb("hT", [P, NC, T]), sb("hq", [P, NC, T], BF16)
        part = [sb(f"part{u}", [P, TB, D]) for u in range(2)]
        g_ps = [psum(m, ctx, f"g_ps{c}_l3f", [P, BT]) for c in range(NC)]
        u_ps = [psum(m, ctx, f"u_ps{c}_l3f", [P, BT]) for c in range(NC)]
        y_ps = [psum(m, ctx, f"y_ps{u}_l3f", [P, BT]) for u in range(2)]
        w_bank, wd_bank, d_bank, x_banks, max_banks = g_ps[0], g_ps[1], g_ps[2], u_ps[0:2], (u_ps[2], y_ps[0])

        with nc.Block() as block:
            @block.sync
            def _(sp):
                loads = [(wd[:], d["L3_ffn_w_down"]), (clips[:, 0:1], d["L3_ffn_clip_x"][0, :].partition_broadcast(P)),
                         (clips[:, 1:2], d["L3_ffn_clip_down"][0, :].partition_broadcast(P))]
                for n, name in enumerate(("L3_ffn_w_gate", "L3_ffn_w_up")):
                    for c, r in enumerate(ROWS):
                        loads.append((w[0:r, n, c, :], d[name][c * P:c * P + r, :]))
                assert len(loads) == 3 + 2 * NC
                for dst, src in loads:
                    sp.dma_start(dst, src).then_inc(m.loaded.sem, 16)
                sp.wait_ge(*m.loaded.after(16 * len(loads)))

            @block.gpsimd
            def _(pool):
                norm.pool(pool, 0)

            @block.vector
            def _(dve):
                rows = lambda n, c: w[0:ROWS[c], n, c, :]
                dve.memset(wscale[:], 1.0).then_inc(m.step.sem, 1)
                dve.memset(hT[LAST:P, NC - 1, :], 0.0).then_inc(m.step.sem, 1)
                dve.wait_ge(*m.loaded.after(16 * (3 + 2 * NC)))
                dve.wait_ge(*m.step.after(2))
                dve.tensor_reduce(wscale[:, :, 0:NC - 1], w[:, :, 0:NC - 1, :], AX.X, ALU.max, apply_absolute_value=True)\
                    .then_inc(m.step.sem, 1)
                dve.tensor_reduce(wscale[0:LAST, :, NC - 1], w[0:LAST, :, NC - 1, :], AX.X, ALU.max, apply_absolute_value=True)\
                    .then_inc(m.step.sem, 1)
                dve.tensor_reduce(dscale[:], wd[:], AX.X, ALU.max, apply_absolute_value=True).then_inc(m.step.sem, 1)
                dve.wait_ge(*m.step.after(5))
                dve.tensor_scalar(wscale[:], wscale[:], 1.0 / QMAX, None, ALU.mult).then_inc(m.step.sem, 1)
                dve.tensor_scalar(dscale[:], dscale[:], 1.0 / QMAX, None, ALU.mult).then_inc(m.step.sem, 1)
                dve.wait_ge(*m.step.after(7))
                dve.reciprocal(winv[:], wscale[:]).then_inc(m.step.sem, 1)
                dve.reciprocal(dinv[:], dscale[:]).then_inc(m.step.sem, 1)
                dve.wait_ge(*m.step.after(9))
                for n in range(2):
                    for c, r in enumerate(ROWS):
                        dve.tensor_scalar(rows(n, c), rows(n, c), winv[0:r, n, c:c + 1], MAGIC, ALU.mult, ALU.add)\
                            .then_inc(m.step.sem, 1)
                dve.tensor_scalar(wd[:], wd[:], dinv[:], MAGIC, ALU.mult, ALU.add).then_inc(m.step.sem, 1)
                dve.wait_ge(*m.step.after(10 + 2 * NC))
                for n in range(2):
                    for c, r in enumerate(ROWS):
                        dve.tensor_scalar(wq[0:r, n, c, :], rows(n, c), MAGIC, QMAX, ALU.subtract, ALU.min)\
                            .then_inc(m.ready_made.sem, 1)
                dve.tensor_scalar(wdq[:], wd[:], MAGIC, QMAX, ALU.subtract, ALU.min).then_inc(m.ready_made.sem, 1)
                dve.tensor_scalar(diag[:], k["ident"], dscale[:], None, ALU.mult).then_inc(m.ready_made.sem, 1)

                def find_scale(n, src, waited):
                    dve.tensor_reduce(top[:, n:n + 1], src, AX.X, ALU.max, apply_absolute_value=True).then_inc(m.row_max.sem, 1)
                    dve.wait_ge(*m.max_turned.after(n + 1))
                    dve.tensor_reduce(peak[0:1, n:n + 1], max_banks[n][0:1, 0:P], AX.X, ALU.max).then_inc(m.max_found.sem, 1)
                    dve.wait_ge(*m.max_spread.after(n + 1))
                    dve.wait_ge(*m.act_step.after(1))
                    dve.tensor_scalar(scale[:, n:n + 1], max_banks[n][:, P:P + 1], sig[:, n:n + 1], 1.0 / QMAX, ALU.mult, ALU.mult)\
                        .then_inc(m.step.sem, 1)
                    dve.wait_ge(*m.step.after(waited))
                    dve.reciprocal(inv[:, n:n + 1], scale[:, n:n + 1]).then_inc(m.step.sem, 1)
                    dve.wait_ge(*m.step.after(waited + 1))

                at = 10 + 2 * NC
                norm.vector(dve, 0, 0, lambda j: x[:, j, :])
                dve.wait_ge(*m.normed.after(NT))
                flat = xn[:].rearrange("p t d -> p (t d)")
                find_scale(0, flat, at + 1)
                dve.tensor_scalar(hscale[:], wscale[:], scale[:, 0:1], None, ALU.mult).then_inc(m.scales_ready.sem, 1)
                dve.tensor_scalar(flat, flat, inv[:, 0:1], -QMAX - 1, ALU.mult, ALU.max).then_inc(m.step.sem, 1)
                dve.wait_ge(*m.step.after(at + 3))
                dve.tensor_scalar(flat, flat, QMAX, MAGIC, ALU.min, ALU.add).then_inc(m.step.sem, 1)
                dve.wait_ge(*m.step.after(at + 4))
                dve.tensor_scalar(xq[:].rearrange("p t d -> p (t d)"), flat, MAGIC, None, ALU.subtract).then_inc(m.x_quantised.sem, 1)

                dve.wait_ge(*m.scales_ready.after(1))
                with dve.Fori(0, NB) as n:
                    for c, r in enumerate(ROWS):
                        dve.wait_ge(*m.gate_ready.after(NC * n + c + 1))
                        dve.scalar_tensor_tensor(out=hT[0:r, c, bass.ds(n * BT, BT)], in0=u_ps[c][0:r, :],
                                                 scalar=hscale[0:r, 1, c:c + 1], in1=gate[c][0:r, :], op0=ALU.mult, op1=ALU.mult)\
                            .then_inc(m.hidden_ready.sem, 1)
                dve.wait_ge(*m.hidden_ready.after(NC * NB))
                find_scale(1, hT[:].rearrange("p c t -> p (c t)"), at + 5)
                dve.tensor_scalar(dB[:], d_bank[:, 0:D], scale[:, 1:2], None, ALU.mult).then_inc(m.step.sem, 1)
                with dve.Fori(0, NB) as n:
                    h = hT[:, :, bass.ds(n * BT, BT)]
                    dve.tensor_scalar(h, h, inv[:, 1:2], -QMAX - 1, ALU.mult, ALU.max).then_inc(m.hidden_clipped.sem, 1)
                    dve.wait_ge(*m.hidden_clipped.after(n + 1))
                    dve.tensor_scalar(h, h, QMAX, MAGIC, ALU.min, ALU.add).then_inc(m.hidden_rounded.sem, 1)
                dve.wait_ge(*m.step.after(at + 7))
                with dve.Fori(0, NB // 2) as i:
                    for u in range(2):
                        n = 2 * i + u
                        dve.wait_ge(*m.pv_done.after(n + 1))
                        dve.tensor_tensor(part[u][:], y_ps[u][:].rearrange("p (t d) -> p t d", d=D),
                                          dB[:].unsqueeze(1).to_broadcast([P, TB, D]), ALU.mult).then_inc(m.pv_copied.sem, 1)
                        dve.wait_ge(*m.pv_copied.after(n + 1))
                        tiles = x[:, bass.ds(TB * n, TB), :]
                        dve.tensor_tensor(tiles, tiles, part[u][:], ALU.add).then_inc(m.x_updated.sem, 1)
                dve.wait_ge(*m.x_updated.after(NB))

            @block.scalar
            def _(act):
                act.wait_ge(*m.loaded.after(16 * (3 + 2 * NC)))
                act.activation(sig[:], clips[:], ACT.Sigmoid).then_inc(m.act_step.sem, 1)
                act.wait_ge(*m.turned.after(1))
                act.activation(wT[:].rearrange("p n i -> p (n i)"), w_bank[:, 0:I].bitcast(BF16), ACT.Copy)\
                    .then_inc(m.turned_copied.sem, 1)
                act.wait_ge(*m.turned.after(2))
                low = (NC - 1) * D
                act.activation(wdT[:, 0:NC - 1, :].rearrange("p c d -> p (c d)"), wd_bank[:, 0:low // 2].bitcast(BF16), ACT.Copy)\
                    .then_inc(m.turned_copied.sem, 1)
                act.activation(wdT[0:LAST, NC - 1, :], wd_bank[0:LAST, low // 2:(low + D) // 2].bitcast(BF16), ACT.Copy)\
                    .then_inc(m.turned_copied.sem, 1)
                for n in range(2):
                    act.wait_ge(*m.x_turned.after(n + 1))
                    act.activation(xqT[:, n * T // 2:(n + 1) * T // 2], x_banks[n][:].bitcast(BF16), ACT.Copy)\
                        .then_inc(m.turned_copied.sem, 1)
                act.wait_ge(*m.scales_ready.after(1))
                with act.Fori(0, NB) as n:
                    for c, r in enumerate(ROWS):
                        act.wait_ge(*m.scores_ready.after(NC * n + c + 1))
                        act.activation(gate[c][0:r, :], g_ps[c][0:r, :], ACT.Silu, scale=hscale[0:r, 0, c:c + 1])\
                            .then_inc(m.gate_ready.sem, 1)
                with act.Fori(0, NB) as n:
                    act.wait_ge(*m.hidden_rounded.after(n + 1))
                    act.activation(hq[:, :, bass.ds(n * BT, BT)], hT[:, :, bass.ds(n * BT, BT)], ACT.Copy, bias=-MAGIC)\
                        .then_inc(m.hidden_quantised.sem, 1)

            @block.tensor
            def _(pe):
                pe.wait_ge(*m.ready_made.after(2 * NC))
                bank = w_bank[:, 0:I].bitcast(BF16)
                for n in range(2):
                    for c, r in enumerate(ROWS):
                        ins = pe.transpose(bank[:, n * I + c * P:n * I + c * P + r], wq[0:r, n, c, :], k["ident_bf"][0:r, 0:r])
                ins.then_inc(m.turned.sem, 1)
                pe.wait_ge(*m.ready_made.after(2 * NC + 1))
                bank = wd_bank[:, 0:NC * D // 2].bitcast(BF16)
                for c, r in enumerate(ROWS):
                    ins = pe.transpose(bank[0:r, c * D:(c + 1) * D], wdq[:, c * P:c * P + r], k["ident_bf"])
                ins.then_inc(m.turned.sem, 1)

                def spread_max(n):
                    pe.wait_ge(*m.row_max.after(n + 1))
                    pe.transpose(max_banks[n][0:1, 0:P], top[:, n:n + 1], k["ident"]).then_inc(m.max_turned.sem, 1)
                    pe.wait_ge(*m.max_found.after(n + 1))
                    pe.matmul(max_banks[n][:, P:P + 1], k["ones"][0:1, :], peak[0:1, n:n + 1], start=True, stop=True)\
                        .then_inc(m.max_spread.sem, 1)

                spread_max(0)
                pe.wait_ge(*m.x_quantised.after(1))
                for n in range(2):
                    bank = x_banks[n][:].bitcast(BF16)
                    for j in range(NT // 2):
                        ins = pe.transpose(bank[:, j * P:(j + 1) * P], xq[:, n * NT // 2 + j, :], k["ident_bf"])
                    ins.then_inc(m.x_turned.sem, 1)
                pe.wait_ge(*m.turned_copied.after(5))
                with pe.Fori(0, NB) as n:
                    for c, r in enumerate(ROWS):
                        if c == 0:
                            pe.wait_ge(*m.hidden_ready.after(NC * n))
                        cols = bass.ds(n * BT, BT)
                        pe.matmul(g_ps[c][0:r, :], wT[:, 0, c * P:c * P + r], xqT[:, cols], start=True, stop=True)
                        pe.matmul(u_ps[c][0:r, :], wT[:, 1, c * P:c * P + r], xqT[:, cols], start=True, stop=True)\
                            .then_inc(m.scores_ready.sem, 1)
                pe.wait_ge(*m.hidden_ready.after(NC * NB))
                pe.wait_ge(*m.ready_made.after(2 * NC + 2))
                pe.matmul(d_bank[:, 0:D], k["ones"], diag[:], start=True, stop=True)
                spread_max(1)
                with pe.Fori(0, NB // 2) as i:
                    for u in range(2):
                        n = 2 * i + u
                        pe.wait_ge(*m.hidden_quantised.after(n + 1))
                        pe.wait_ge(*m.pv_copied.after(2 * i))
                        for t in range(TB):
                            for c, r in enumerate(ROWS):
                                ins = pe.matmul(y_ps[u][:, t * D:(t + 1) * D], hq[0:r, c, bass.ds((TB * n + t) * P, P)],
                                                wdT[0:r, c, :], start=(c == 0), stop=(c == NC - 1))
                        ins.then_inc(m.pv_done.sem, 1)
        norm.close(1)
        for s, n in ((m.loaded, 16 * (3 + 2 * NC)), (m.step, 17 + 2 * NC), (m.ready_made, 2 + 2 * NC), (m.act_step, 1), (m.turned, 2),
                     (m.turned_copied, 5), (m.row_max, 2), (m.max_turned, 2), (m.max_found, 2), (m.max_spread, 2), (m.x_quantised, 1),
                     (m.x_turned, 2), (m.scales_ready, 1), (m.scores_ready, NC * NB), (m.gate_ready, NC * NB), (m.hidden_ready, NC * NB),
                     (m.hidden_clipped, NB), (m.hidden_rounded, NB), (m.hidden_quantised, NB), (m.pv_done, NB), (m.pv_copied, NB),
                     (m.x_updated, NB)):
            s.before += n


def store(m, out):
    with m.nc.Block() as block:
        @block.sync
        def _(sp):
            sp.dma_start(out.rearrange("(t p) d -> p t d", p=P), m.x[:]).then_inc(m.loaded.sem, 16)
            sp.wait_ge(*m.loaded.after(16))
    m.loaded.before += 16


PHASES = [l0_cross_attention, l0_block_ffn, l1_cross_attention, l1_bit_ffn, l2_cross_attention,
          l2_local_transformer, l3_cross_attention, l3_quantised_ffn]
STAGE = [0, 1, 2, 3, 4, 5, 6, 7]


def program(nc, dram, out, upto=99):
    with ExitStack() as ctx:
        m = Machine(nc, ctx, dram)
        load_constants(m, ctx)
        for phase in PHASES[:upto]:
            phase(m)
        store(m, out)


def shape_constants():
    f = np.float32
    c = {}
    c["ident"] = np.eye(P, dtype=f)
    c["ones"] = np.ones((P, P), f)
    c["shift"] = np.eye(P, k=1, dtype=f)
    last = np.zeros((P, P), f)
    last[P - 1, 0] = 1
    c["last"] = last
    hd = D // HEADS
    c["head_cols"] = (np.arange(P)[:, None] // hd == np.arange(HEADS)[None, :]).astype(f) / np.sqrt(f(hd))
    for name, per in (("spread4", 4), ("spread2", 2)):
        groups = HEADS // per
        s = np.zeros((P, groups, P), f)
        for g in range(groups):
            for r in range(P):
                s[per * g + r // (P // per), g, r] = 1
        c[name] = s.reshape(P, groups * P)
    c["minus_half"] = np.full((P, 64), -0.5, f)
    half = np.arange(0, 64, 2, dtype=f)
    inv_freq = (f(1.0) / f(10000.0) ** (half / f(64))).astype(f)
    t = np.arange(S, dtype=f)
    freqs = (t[:, None] * inv_freq[None, :]).astype(f)
    freqs = np.concatenate([freqs, freqs], -1)
    base = ((half + f(0.4 * 64)) / f(1.4 * 64)).astype(f)
    power = ((t - S // 2) / f(32)).astype(f)
    scale = (base[None, :] ** power[:, None]).astype(f)
    scale = np.concatenate([scale, scale], -1)
    sign = np.concatenate([-np.ones(32, f), np.ones(32, f)])
    tables = {"rot_qa": 8 * np.cos(freqs) * scale, "rot_qb": 8 * np.sin(freqs) * scale * sign,
              "rot_ka": np.cos(freqs) / scale, "rot_kb": np.sin(freqs) / scale * sign}
    for name, v in tables.items():
        c[name] = v.astype(f).reshape(TPB, P, 64).transpose(1, 0, 2).reshape(P, TPB * 64)
    i = np.arange(P)[:, None]
    band = []
    for q0, k0, n in ((0, 0, P), (P, 0, 2 * P)):
        q, j = q0 + i, k0 + np.arange(n)[None, :]
        band.append(np.where((q < j) | (q > j + 64), -1e30, 0.0))
    c["band"] = np.concatenate(band, 1)
    return np.concatenate([c[n] for n, _ in CONSTS], 1).astype(f)


def lay_out(inputs):
    i = {n: np.asarray(v) for n, v in inputs.items()}
    a = {}
    a["x"] = i["x"].reshape(B * S, D)
    ctx = np.concatenate([i["ctx_1024"], np.zeros((AHEAD, KV, D), np.float32)]).reshape(-1, D)
    a["ctx"] = ctx
    a["ctxT"] = ctx.T
    mask = np.concatenate([i["mask_Bx1xSxS2_ik0"][:, 0], np.zeros((AHEAD, S, KV), np.int32)])
    a["mask"] = mask.reshape(-1, KV)
    a["key_mask"] = i["mask_BxS2_bf1"].view(np.uint8).reshape(1, B * KV)
    a["time_bias"] = i["fside_BxS2_0"].reshape(1, B * KV)
    for n, v in i.items():
        if n[0] != "L":
            continue
        if n in ("L0_ffn_router_w", "L0_ffn_w1", "L0_ffn_w2", "L1_xattn_Wv", "L1_xattn_Wk", "L1_xattn_Wq", "L1_xattn_Wo",
                 "L1_ffn_w1", "L1_ffn_w2", "L2_xattn_Wq", "L2_xattn_Wkv", "L2_xattn_Wout"):
            v = v.T
        elif v.ndim == 1:
            v = v.reshape(1, -1)
        a[n] = v
    a["consts"] = shape_constants()
    return {n: np.ascontiguousarray(v) for n, v in a.items()}


def kernel(**inputs):
    import concourse.bacc as bacc
    from concourse.bass_utils import run_bass_kernel_spmd

    arrays = lay_out(inputs)
    nc = bacc.Bacc("TRN2", target_bir_lowering=False, num_devices=1)
    dram = {n: nc.dram_tensor(f"in_{n}", v.shape, mybir.dt.from_np(v.dtype), kind="ExternalInput").ap()
            for n, v in arrays.items()}
    out = nc.dram_tensor("out_x", (B * S, D), F32, kind="ExternalOutput").ap()
    program(nc, dram, out)
    r = run_bass_kernel_spmd(nc, [{f"in_{n}": v for n, v in arrays.items()}], core_ids=[0])
    return np.asarray(r.results[0]["out_x"]).reshape(B, S, D)
```

```python
import numpy as np
import concourse.bass as bass
from concourse import mybir
from contextlib import ExitStack

F32 = mybir.dt.float32
BF16 = mybir.dt.bfloat16
I32 = mybir.dt.int32
U8 = mybir.dt.uint8
ACT = mybir.ActivationFunctionType
ALU = mybir.AluOpType
AX = mybir.AxisListType

P = 128
B = 8
D = 128
S = 256
KV = 512
TPB = S // P
CPB = KV // P
NT = B * TPB
PAIRS = B // 2
AHEAD = 2
HEADS = 16
LN_EPS = 1e-5
MAGIC = 12582912.0


class Signal:

    def __init__(self, nc, ctx, name):
        self.sem = ctx.enter_context(nc.semaphore(name))
        self.before = 0

    def after(self, n):
        return self.sem, n + self.before


class Ring:

    def __init__(self, banks, filled, drained, per, lead=0):
        self.banks, self.filled, self.drained, self.per, self.lead = banks, filled, drained, per, lead
        assert 2 * per % len(banks) == 0

    def at(self, i, u, m):
        n, size = self.lead + u * self.per + m, len(self.banks)
        return n % size, i * (2 * self.per // size) + n // size

    def index(self, u, m):
        return (self.lead + u * self.per + m) % len(self.banks)

    def bank(self, u, m):
        return self.banks[self.index(u, m)]

    def free(self, i, u, m):
        s, n = self.at(i, u, m)
        return self.drained[s].after(n)

    def full(self, i, u, m):
        s, n = self.at(i, u, m)
        return self.filled[s].after(n + 1)

    def empty(self, i, u, m):
        s, n = self.at(i, u, m)
        return self.drained[s].after(n + 1)

    def fills(self, u, m):
        return self.filled[self.index(u, m)].sem

    def drains(self, u, m):
        return self.drained[self.index(u, m)].sem

    def close(self, tail=0):
        total, size = self.lead + self.per * B + tail, len(self.banks)
        for n in range(size):
            for s in (self.filled[n], self.drained[n]):
                s.before += (total + size - 1 - n) // size


class Machine:

    def __init__(self, nc, ctx, dram):
        self.nc, self.dram = nc, dram
        self.signals = []

        def sig(name):
            self.signals.append(Signal(nc, ctx, name))
            return self.signals[-1]
        self.loaded = sig("loaded")
        self.streamed = [sig("streamed_even"), sig("streamed_odd")]
        self.ready_made = sig("ready_made")
        self.row_stats = sig("row_stats")
        self.row_moments = sig("row_moments")
        self.var_eps = sig("var_eps")
        self.row_rstd = sig("row_rstd")
        self.normed = sig("normed")
        self.filled = [sig(f"bank{n}_filled") for n in range(6)]
        self.drained = [sig(f"bank{n}_drained") for n in range(6)]
        self.parts_split = sig("parts_split")
        self.stacked = [sig("stacked_even"), sig("stacked_odd")]
        self.unit_copied = [sig("even_unit_copied"), sig("odd_unit_copied")]
        self.scores_ready = sig("scores_ready")
        self.max_ready = sig("max_ready")
        self.probs_ready = sig("probs_ready")
        self.turned = sig("turned")
        self.turned_copied = sig("turned_copied")
        self.pv_done = sig("pv_done")
        self.pv_copied = sig("pv_copied")
        self.sums_inverted = sig("sums_inverted")
        self.sums_turned = sig("sums_turned")
        self.mask_ready = sig("mask_ready")
        self.x_updated = sig("x_updated")
        self.passed = sig("passed")
        self.squares_summed = sig("squares_summed")
        self.squares_ready = sig("squares_ready")
        self.powers_ready = sig("powers_ready")
        self.x_quantised = sig("x_quantised")
        self.h_squared = sig("h_squared")
        self.squared_affine = sig("squared_affine")
        self.unshifted = sig("unshifted")
        self.rotated = sig("rotated")
        self.row_max = sig("row_max")
        self.max_turned = sig("max_turned")
        self.max_found = sig("max_found")
        self.max_spread = sig("max_spread")
        self.x_turned = sig("x_turned")
        self.scales_ready = sig("scales_ready")
        self.gate_ready = sig("gate_ready")
        self.hidden_ready = sig("hidden_ready")
        self.hidden_clipped = sig("hidden_clipped")
        self.hidden_rounded = sig("hidden_rounded")
        self.hidden_quantised = sig("hidden_quantised")
        self.parts_ready = sig("parts_ready")
        self.rows_moved = sig("rows_moved")
        self.qk_loaded = sig("qk_loaded")
        self.zeroed = sig("zeroed")
        self.h_moved = sig("h_moved")
        self.step = sig("step")
        self.act_step = sig("act_step")
        self.pool_step = sig("pool_step")
        self.x_padded = ctx.enter_context(nc.sbuf_tensor("x_tok", [P, TPB + NT, D], F32))
        self.x = self.x_padded[:, TPB:TPB + NT, :]
        self.consts = {}


def sbuf(m, ctx, name, shape, dt=F32):
    return ctx.enter_context(m.nc.sbuf_tensor(name, shape, dt))


def psum(m, ctx, name, shape, dt=F32):
    return ctx.enter_context(m.nc.psum_tensor(name, shape, dt))


CONSTS = [("ident", P), ("ones", P), ("band", 3 * P), ("shift", P), ("last", P), ("head_cols", HEADS), ("spread4", 4 * P),
          ("spread2", 8 * P), ("minus_half", 64),
          ("rot_qa", 2 * 64), ("rot_qb", 2 * 64), ("rot_ka", 2 * 64), ("rot_kb", 2 * 64)]
CONSTS_BF = ("ident", "ones", "band")


def load_constants(m, ctx):
    nc, d = m.nc, m.dram
    widths = dict(CONSTS)
    width, width_bf = sum(widths.values()), sum(widths[n] for n in CONSTS_BF)
    c = sbuf(m, ctx, "consts", [P, width])
    cb = sbuf(m, ctx, "consts_bf", [P, width_bf], BF16)
    at = 0
    for name, w in CONSTS:
        m.consts[name] = c[:, at:at + w]
        if name in CONSTS_BF:
            m.consts[name + "_bf"] = cb[:, at:at + w]
        at += w
    with nc.Block() as block:
        @block.sync
        def _(sp):
            sp.dma_start(m.x, d["x"].rearrange("(t p) d -> p t d", p=P)).then_inc(m.loaded.sem, 16)
            sp.dma_start(c[:], d["consts"]).then_inc(m.loaded.sem, 16)
            sp.wait_ge(*m.loaded.after(32))

        @block.vector
        def _(dve):
            dve.wait_ge(*m.loaded.after(32))
            dve.tensor_copy(cb[:], c[:, 0:width_bf])
            dve.memset(m.x_padded[:, 0:TPB, :], 0.0)

        @block.gpsimd
        def _(pool):
            for s in m.signals:
                if s is not m.loaded:
                    pool.sem_inc(s.sem, 2)
    for s in m.signals:
        s.before += 32 if s is m.loaded else 2


class Norm:

    def __init__(self, m, ctx, tiles, tag, buffers=2, dummies=0):
        self.m, self.tiles = m, tiles
        self.st = sbuf(m, ctx, f"st_{tag}", [P, tiles, 6])
        self.mv = sbuf(m, ctx, f"mv_{tag}", [P, tiles, 2])
        self.ve = sbuf(m, ctx, f"ve_{tag}", [P, tiles])
        self.rs = sbuf(m, ctx, f"rs_{tag}", [P, tiles])
        self.padded = [sbuf(m, ctx, f"xn{u}_{tag}", [P, dummies + tiles, D]) for u in range(buffers)]
        self.xn = [t[:, dummies:, :] for t in self.padded]

    def vector(self, dve, b, u, src):
        m, t = self.m, self.tiles
        for j in range(t):
            dve.bn_stats(self.st[:, j, :], src(j)).then_inc(m.row_stats.sem, 1)
        dve.wait_ge(*m.row_stats.after(t * b + t))
        dve.sem_inc(m.passed.sem, 1)
        for j in range(t):
            dve.bn_aggr(self.mv[:, j, :], self.st[:, j, :]).then_inc(m.row_moments.sem, 1)
        dve.wait_ge(*m.row_moments.after(t * b + t))
        dve.tensor_scalar(self.ve[:], self.mv[:, :, 1], LN_EPS, None, ALU.add).then_inc(m.var_eps.sem, 1)
        dve.wait_ge(*m.row_rstd.after(b + 1))
        for j in range(t):
            dve.tensor_scalar(self.xn[u][:, j, :], src(j), self.mv[:, j, 0:1], self.rs[:, j:j + 1],
                              ALU.subtract, ALU.mult).then_inc(m.normed.sem, 1)

    def pool(self, pool, b):
        m = self.m
        pool.wait_ge(*m.var_eps.after(b + 1))
        pool.tensor_tensor(self.rs[:], self.ve[:], m.consts["minus_half"][:, 0:self.tiles], ALU.pow)\
            .then_inc(m.row_rstd.sem, 1)

    def close(self, steps):
        m, t = self.m, self.tiles
        for s, n in ((m.row_stats, t), (m.row_moments, t), (m.var_eps, 1), (m.row_rstd, 1), (m.normed, t)):
            s.before += n * steps


def l0_cross_attention(m):
    nc, d, x, k = m.nc, m.dram, m.x, m.consts
    with ExitStack() as ctx:
        norm = Norm(m, ctx, TPB, "l0x")
        ctxT = [sbuf(m, ctx, f"ctxT{u}_l0x", [P, KV]) for u in range(2)]
        rows = [sbuf(m, ctx, f"rows{u}_l0x", [P, CPB, D]) for u in range(2)]
        xnT = [sbuf(m, ctx, f"xnT{u}_l0x", [P, S]) for u in range(2)]
        nmax = sbuf(m, ctx, "nmax_l0x", [P, 2, TPB])
        sums = sbuf(m, ctx, "sums_l0x", [P, 2, TPB])
        inv = sbuf(m, ctx, "inv_l0x", [P, 2, TPB])
        probs = [sbuf(m, ctx, f"probs{j}_l0x", [P, KV]) for j in range(TPB)]
        pT = [sbuf(m, ctx, f"pT{j}_l0x", [P, CPB, P]) for j in range(TPB)]
        ring = Ring([psum(m, ctx, f"ring{n}_l0x", [P, 512]) for n in range(2)], m.filled, m.drained, 2)
        s_ps = [psum(m, ctx, f"s_ps{j}_l0x", [P, KV]) for j in range(TPB)]
        t_ps = [psum(m, ctx, f"t_ps{j}_l0x", [P, KV]) for j in range(TPB)]

        with nc.Block() as block:
            @block.sync
            def _(sp):
                def stream(b, u):
                    sp.dma_start(ctxT[u][:], d["ctxT"][:, bass.ds(b * KV, KV)]).then_inc(m.streamed[u].sem, 16)
                    sp.dma_start(rows[u][:], d["ctx"][bass.ds(b * KV, KV), :].rearrange("(c p) d -> p c d", p=P))\
                        .then_inc(m.streamed[u].sem, 16)
                for u in range(2):
                    stream(u, u)
                with sp.Fori(0, PAIRS) as i:
                    for u in range(2):
                        sp.wait_ge(*ring.full(i, u, 1))
                        stream(2 * i + u + AHEAD, u)
                for s in m.streamed:
                    sp.wait_ge(*s.after(32 * (PAIRS + 1)))

            @block.gpsimd
            def _(pool):
                with pool.Fori(0, PAIRS) as i:
                    for u in range(2):
                        norm.pool(pool, 2 * i + u)

            @block.vector
            def _(dve):
                with dve.Fori(0, PAIRS) as i:
                    for u in range(2):
                        b = 2 * i + u
                        norm.vector(dve, b, u, lambda j: x[:, TPB * b + j, :])
                        for j in range(TPB):
                            dve.wait_ge(*m.scores_ready.after(TPB * b + j + 1))
                            dve.tensor_reduce(nmax[:, u, j:j + 1], s_ps[j][:], AX.X, ALU.max, negate=True)\
                                .then_inc(m.max_ready.sem, 1)
                        for j in range(TPB):
                            dve.wait_ge(*m.turned.after(TPB * b + j + 1))
                            dve.tensor_copy(pT[j][:].rearrange("p c t -> p (c t)"), t_ps[j][:])\
                                .then_inc(m.turned_copied.sem, 1)
                        dve.wait_ge(*m.probs_ready.after(TPB * b + TPB))
                        dve.reciprocal(inv[:, u, :], sums[:, u, :]).then_inc(m.sums_inverted.sem, 1)
                        dve.wait_ge(*m.sums_inverted.after(b + 1))
                        dve.wait_ge(*ring.full(i, u, 1))
                        bank = ring.bank(u, 1)
                        for j in range(TPB):
                            ins = dve.scalar_tensor_tensor(out=x[:, TPB * b + j, :], in0=bank[:, j * D:(j + 1) * D],
                                                           scalar=inv[:, u, j:j + 1], in1=x[:, TPB * b + j, :],
                                                           op0=ALU.mult, op1=ALU.add)
                        ins.then_inc(ring.drains(u, 1), 1)

            @block.scalar
            def _(act):
                with act.Fori(0, PAIRS) as i:
                    for u in range(2):
                        b = 2 * i + u
                        act.wait_ge(*ring.full(i, u, 0))
                        act.activation(xnT[u][:], ring.bank(u, 0)[:, 0:S], ACT.Copy).then_inc(ring.drains(u, 0), 1)
                        for j in range(TPB):
                            act.wait_ge(*m.max_ready.after(TPB * b + j + 1))
                            act.activation(probs[j][:], s_ps[j][:], ACT.Exp, bias=nmax[:, u, j:j + 1],
                                           accum_out=sums[:, u, j:j + 1]).then_inc(m.probs_ready.sem, 1)

            @block.tensor
            def _(pe):
                with pe.Fori(0, PAIRS) as i:
                    for u in range(2):
                        b = 2 * i + u
                        pe.wait_ge(*m.normed.after(TPB * b + TPB))
                        pe.wait_ge(*ring.free(i, u, 0))
                        for j in range(TPB):
                            ins = pe.transpose(ring.bank(u, 0)[:, j * P:(j + 1) * P], norm.xn[u][:, j, :], k["ident"])
                        ins.then_inc(ring.fills(u, 0), 1)
                        pe.wait_ge(*ring.empty(i, u, 0))
                        pe.wait_ge(*m.streamed[u].after(32 * i + 32))
                        for j in range(TPB):
                            pe.matmul(s_ps[j][:], xnT[u][:, j * P:(j + 1) * P], ctxT[u][:], start=True, stop=True)\
                                .then_inc(m.scores_ready.sem, 1)
                        for j in range(TPB):
                            pe.wait_ge(*m.probs_ready.after(TPB * b + j + 1))
                            for c in range(CPB):
                                ins = pe.transpose(t_ps[j][:, c * P:(c + 1) * P], probs[j][:, c * P:(c + 1) * P], k["ident"])
                            ins.then_inc(m.turned.sem, 1)
                        pe.wait_ge(*ring.free(i, u, 1))
                        for j in range(TPB):
                            pe.wait_ge(*m.turned_copied.after(TPB * b + j + 1))
                            for c in range(CPB):
                                ins = pe.matmul(ring.bank(u, 1)[:, j * D:(j + 1) * D], pT[j][:, c, :], rows[u][:, c, :],
                                                start=(c == 0), stop=(c == CPB - 1))
                        ins.then_inc(ring.fills(u, 1), 1)
        norm.close(B)
        ring.close()
        for s, n in ((m.streamed[0], 32 * (PAIRS + 1)), (m.streamed[1], 32 * (PAIRS + 1)), (m.scores_ready, NT), (m.max_ready, NT), (m.probs_ready, NT),
                     (m.turned, NT), (m.turned_copied, NT), (m.sums_inverted, B)):
            s.before += n


def turn_normed(m, pe, norm, ring, i, u, fill, tiles=TPB):
    b = 2 * i + u
    pe.wait_ge(*m.normed.after(tiles * b + tiles))
    pe.wait_ge(*ring.free(i, u, fill))
    for j in range(tiles):
        ins = pe.transpose(ring.bank(u, fill)[:, j * P:(j + 1) * P], norm.xn[u][:, j, :], m.consts["ident"])
    ins.then_inc(ring.fills(u, fill), 1)


def add_to_x(m, dve, ring, i, u, fill):
    dve.wait_ge(*ring.full(i, u, fill))
    rows = m.x[:, bass.ds(TPB * (2 * i + u), TPB), :]
    dve.tensor_tensor(rows, ring.bank(u, fill)[:, 0:TPB * D].rearrange("p (t d) -> p t d", d=D),
                      rows, ALU.add).then_inc(ring.drains(u, fill), 1)


def l0_block_ffn(m):
    nc, d, x, k = m.nc, m.dram, m.x, m.consts
    NB, TOP, HC = 16, 4, 4
    LOW, CHOSEN = -3.0e38, 3.0e38
    with ExitStack() as ctx:
        norm = Norm(m, ctx, TPB, "l0f")
        router = sbuf(m, ctx, "router_l0f", [P, NB])
        router_b = sbuf(m, ctx, "router_b_l0f", [1, NB])
        w1 = sbuf(m, ctx, "w1_l0f", [P, HC * P])
        b1 = sbuf(m, ctx, "b1_l0f", [P, HC])
        w2 = sbuf(m, ctx, "w2_l0f", [P, HC, D])
        b2 = sbuf(m, ctx, "b2_l0f", [1, D])
        xnT = [sbuf(m, ctx, f"xnT{u}_l0f", [P, S]) for u in range(2)]
        logits = sbuf(m, ctx, "logits_l0f", [P, TPB, NB + TOP])
        top = sbuf(m, ctx, "top_l0f", [P, TPB, 8])
        marked = sbuf(m, ctx, "marked_l0f", [P, TPB, NB + TOP])
        chosen = sbuf(m, ctx, "chosen_l0f", [P, TPB, NB])
        chosenT = sbuf(m, ctx, "chosenT_l0f", [NB, S])
        hT = [sbuf(m, ctx, f"hT{u}_l0f", [P, HC, S]) for u in range(2)]
        TURN, LOGIT, CHOICE, HID, SPREAD, OUT = 0, 1, 2, 3, 3 + HC, 3 + 2 * HC
        ring = Ring([psum(m, ctx, f"ring{n}_l0f", [P, 512]) for n in range(2)], m.filled, m.drained, OUT + 1)

        with nc.Block() as block:
            @block.sync
            def _(sp):
                for dst, src in ((router[:], d["L0_ffn_router_w"]), (router_b[:], d["L0_ffn_router_b"]),
                                 (w1[:], d["L0_ffn_w1"]), (b2[:], d["L0_ffn_b2"]),
                                 (w2[:], d["L0_ffn_w2"].rearrange("(c p) d -> p c d", p=P))):
                    sp.dma_start(dst, src).then_inc(m.loaded.sem, 16)
                for c in range(HC):
                    sp.dma_start(b1[:, c:c + 1], d["L0_ffn_b1"][0, c * P:(c + 1) * P].rearrange("(p o) -> p o", o=1))\
                        .then_inc(m.loaded.sem, 16)
                sp.wait_ge(*m.loaded.after(16 * (5 + HC)))

            @block.gpsimd
            def _(pool):
                with pool.Fori(0, PAIRS) as i:
                    for u in range(2):
                        norm.pool(pool, 2 * i + u)

            @block.vector
            def _(dve):
                dve.memset(logits[:, :, NB:], LOW).then_inc(m.step.sem, 1)
                dve.wait_ge(*m.step.after(1))
                per = 2 * TPB + 1
                with dve.Fori(0, PAIRS) as i:
                    for u in range(2):
                        b = 2 * i + u
                        norm.vector(dve, b, u, lambda j: x[:, TPB * b + j, :])
                        at = per * b + 1
                        dve.wait_ge(*ring.full(i, u, LOGIT))
                        dve.tensor_copy(logits[:, :, 0:NB], ring.bank(u, LOGIT)[:, 0:TPB * NB]
                                        .rearrange("p (t n) -> p t n", n=NB)).then_inc(ring.drains(u, LOGIT), 1)
                        dve.wait_ge(*ring.empty(i, u, LOGIT))
                        dve.sem_inc(m.passed.sem, 1)
                        for j in range(TPB):
                            dve.max(top[:, j, :], logits[:, j, 0:NB]).then_inc(m.step.sem, 1)
                        dve.wait_ge(*m.step.after(at + TPB))
                        dve.tensor_copy(top[:, :, TOP:], logits[:, :, NB:]).then_inc(m.step.sem, 1)
                        dve.wait_ge(*m.step.after(at + TPB + 1))
                        dve.sem_inc(m.passed.sem, 1)
                        for j in range(TPB):
                            dve.match_replace(marked[:, j, :], top[:, j, :], logits[:, j, :], CHOSEN).then_inc(m.step.sem, 1)
                        dve.wait_ge(*m.step.after(at + 2 * TPB + 1))
                        dve.tensor_scalar(chosen[:], marked[:, :, 0:NB], CHOSEN, None, ALU.is_equal).then_inc(m.mask_ready.sem, 1)
                        for c in range(HC):
                            dve.wait_ge(*ring.full(i, u, SPREAD + c))
                            dve.wait_ge(*ring.empty(i, u, HID + c))
                            dve.tensor_tensor(hT[u][:, c, :], ring.bank(u, SPREAD + c)[:, 0:S],
                                              hT[u][:, c, :], ALU.mult).then_inc(ring.drains(u, SPREAD + c), 1)
                        add_to_x(m, dve, ring, i, u, OUT)

            @block.scalar
            def _(act):
                with act.Fori(0, PAIRS) as i:
                    for u in range(2):
                        act.wait_ge(*ring.full(i, u, TURN))
                        act.activation(xnT[u][:], ring.bank(u, TURN)[:, 0:S], ACT.Copy).then_inc(ring.drains(u, TURN), 1)
                        act.wait_ge(*ring.full(i, u, CHOICE))
                        act.activation(chosenT[:], ring.bank(u, CHOICE)[0:NB, 0:S], ACT.Copy).then_inc(ring.drains(u, CHOICE), 1)
                        for c in range(HC):
                            act.wait_ge(*ring.full(i, u, HID + c))
                            act.activation(hT[u][:, c, :], ring.bank(u, HID + c)[:, 0:S], ACT.Relu,
                                           bias=b1[:, c:c + 1]).then_inc(ring.drains(u, HID + c), 1)

            @block.tensor
            def _(pe):
                pe.wait_ge(*m.loaded.after(16 * (5 + HC)))
                with pe.Fori(0, PAIRS) as i:
                    for u in range(2):
                        b = 2 * i + u
                        turn_normed(m, pe, norm, ring, i, u, TURN)
                        pe.wait_ge(*ring.free(i, u, LOGIT))
                        pe.wait_ge(*ring.empty(i, u, TURN))
                        for j in range(TPB):
                            out = ring.bank(u, LOGIT)[:, j * NB:(j + 1) * NB]
                            pe.matmul(out, k["ones"][0:1, :], router_b[:], start=True, stop=False)
                            ins = pe.matmul(out, xnT[u][:, j * P:(j + 1) * P], router[:], start=False, stop=True)
                        ins.then_inc(ring.fills(u, LOGIT), 1)
                        pe.wait_ge(*ring.free(i, u, CHOICE))
                        pe.wait_ge(*m.mask_ready.after(b + 1))
                        for j in range(TPB):
                            ins = pe.transpose(ring.bank(u, CHOICE)[0:NB, j * P:(j + 1) * P], chosen[:, j, :], k["ident"])
                        ins.then_inc(ring.fills(u, CHOICE), 1)
                        for c in range(HC):
                            pe.wait_ge(*ring.free(i, u, HID + c))
                            pe.matmul(ring.bank(u, HID + c)[:, 0:S], w1[:, c * P:(c + 1) * P], xnT[u][:],
                                      start=True, stop=True).then_inc(ring.fills(u, HID + c), 1)
                        for c in range(HC):
                            pe.wait_ge(*ring.free(i, u, SPREAD + c))
                            pe.matmul(ring.bank(u, SPREAD + c)[:, 0:S],
                                      k["spread4"][0:NB, c * P:(c + 1) * P], chosenT[:],
                                      start=True, stop=True).then_inc(ring.fills(u, SPREAD + c), 1)
                        pe.wait_ge(*ring.free(i, u, OUT))
                        pe.wait_ge(*ring.empty(i, u, OUT - 1))
                        for j in range(TPB):
                            out = ring.bank(u, OUT)[:, j * D:(j + 1) * D]
                            pe.matmul(out, k["ones"][0:1, :], b2[:], start=True, stop=False)
                            for c in range(HC):
                                ins = pe.matmul(out, hT[u][:, c, j * P:(j + 1) * P], w2[:, c, :], start=False, stop=(c == HC - 1))
                        ins.then_inc(ring.fills(u, OUT), 1)
        norm.close(B)
        ring.close()
        for s, n in ((m.loaded, 16 * (5 + HC)), (m.step, (2 * TPB + 1) * B + 1), (m.mask_ready, B)):
            s.before += n


def head_attention(m, tag, hd, wq, wk, wv, wo, bo, bq=None, bk=None, bv=None, mask=None, key_mask=None, key_bias=None):
    nc, d, x, k = m.nc, m.dram, m.x, m.consts
    small = hd == D // HEADS
    G = 4 if small else 2
    NG = HEADS // G
    W = P // G
    NK = 1 if small else NG
    VW = HEADS * W
    VF = 1 if small else CPB * VW // 512
    UNITS = HEADS * TPB
    per_load = 32 if mask is not None else 16
    spread = k["spread4"] if small else k["spread2"]
    TURNS = B * S // 512
    DEEP, RING = (4, 2) if small else (2, 4)
    SUMS, SPREAD = 0, 1
    OUT = SPREAD + NG // 2
    Q = OUT + 1
    K = Q + (0 if small else NK // 2)
    V = K + NK
    GROUP = V + VF
    PER = GROUP + NG
    after = {SUMS: 1, OUT: 14 if small else 9}
    after.update({SPREAD + n: 2 + DEEP + n for n in range(OUT - SPREAD)})
    after.update({K: 0} if small else {Q + n: 10 + n for n in range(V - Q)})
    after.update({V + n: (16 if small else 10 + V - Q + n) for n in range(GROUP - V)})
    after.update({GROUP + g: min(G * TPB * (g + 1) + 1, UNITS) for g in range(NG)})
    order = sorted(range(PER), key=lambda f: (after[f], f < GROUP, f))
    due = [[f for f in order if after[f] == n] for n in range(UNITS + 1)]
    assert max(after[f] for f in range(Q, V)) < UNITS - DEEP and max(after[f] for f in range(GROUP)) < UNITS - 1
    with ExitStack() as ctx:
        norm = Norm(m, ctx, NT, tag, buffers=1)
        sb = lambda name, shape, dt=F32: sbuf(m, ctx, f"{name}_{tag}", shape, dt)
        wq_s, wk_s = sb("wq", [P, NK * P]), sb("wk", [P, NK * P])
        wv_s = sb("wv", [P, D if small else VW])
        wo_s = sb("wo", [P, NG, D])
        bo_s = sb("bo", [1, D])
        ctxT = [sb(f"ctxT{u}", [P, KV]) for u in range(2)]
        xnT = sb("xnT", [P, (B + 1) * S])
        QK_DT, PAIR = (BF16, HEADS // 2) if small else (F32, NK)
        q = [sb(f"q{u}", [P, HEADS, S], QK_DT) for u in range(2)]
        kT = [sb(f"kT{u}", [P, PAIR, KV], QK_DT) for u in range(2)]
        v = [sb(f"v{u}", [P, CPB, VW]) for u in range(2)]
        nmax = sb("nmax", [P, 2, UNITS])
        sums = sb("sums", [P, 2, TPB, HEADS])
        inv = sb("inv", [P, TPB * HEADS])
        invT = sb("invT", [HEADS, S])
        probs = [sb(f"probs{n}", [P, KV]) for n in range(DEEP)]
        pT = [sb(f"pT{n}", [P, G, CPB, S]) for n in range(2)]
        o = [sb(f"o{u}", [P, NG, S]) for u in range(2)]
        first_zeros, later_zeros, zeros = [], [], [o[1][:], xnT[:, B * S:]]
        if small:
            q_all = sb("q_all", [P, (B + 1) * S])
            k_all = sb("k_all", [P, KV])
            rest = sb("rest", [P, KV + S])
            parts = sb("parts", [P, 3, KV + S], BF16)
            zero = sb("zero", [P, KV])
            first_zeros += [wo_s[:], zero[:], kT[0][:]]
            later_zeros += [kT[1][:]]
            zeros += [q_all[:, B * S:]] + [t[:] for t in v]
            STACK = [(0, 0, 0), (8, 0, 1), (16, 1, 0), (24, 1, 1), (48, 0, 2), (56, 2, 0)]
            BIAS = 32
            NSTACK = 4 * len(STACK) + 2 * (key_bias is not None)
        first_zeros += [q[0][:]]
        later_zeros += [q[1][:]]
        if bq is not None:
            bq_s, bk_s, bv_s = sb("bq", [P, 1]), sb("bk", [P, 1]), sb("bv", [P, NG])
            first_zeros = [bv_s[:]] + first_zeros
        if mask is not None:
            mask_i = [sb(f"mask_i{u}", [P, TPB, KV], I32) for u in range(2)]
            mask_b = [sb(f"mask_b{u}", [P, TPB, KV], BF16) for u in range(2)]
        if key_mask is not None:
            key_rows = sb("key_rows", [P, (B + 1) * KV], BF16)
            zeros += [key_rows[:]]
        KBW = B * KV // P
        if key_mask is not None:
            key_u8, key_part = sb("key_u8", [P, KBW], U8), sb("key_part", [P, KBW], BF16)
        if key_bias is not None:
            kb, kb_part = sb("kb", [P, KBW]), sb("kb_part", [P, 3, KBW], BF16)
            bias_rows = sb("bias_rows", [3, (B + 1) * KV], BF16)
            zeros += [bias_rows[:]]

        NLOAD = 2 + (G if small else 1) + (2 + G) * (bq is not None) + (key_mask is not None) + (key_bias is not None)
        NZERO = len(zeros) + 1
        if key_bias is not None:
            ones_of = [[t[64 * w + BIAS:64 * w + BIAS + 3, w:HEADS:2, :] for w in range(2)] for t in q]
        else:
            ones_of = [[], []]
        NFIRST, NLATER = len(first_zeros) + len(ones_of[0]), len(later_zeros) + len(ones_of[1])
        NSTEP = NZERO + 2 * (bq is not None) + (key_mask is not None) + 5 * (key_bias is not None)
        ring = Ring([psum(m, ctx, f"ring{n}_{tag}", [P, 512]) for n in range(RING)], m.filled, m.drained, PER,
                    lead=TURNS + (TURNS if small else 0) + GROUP - Q)
        T0 = 1 if small else 0
        s_ps = [psum(m, ctx, f"s_ps{n}_{tag}", [P, KV]) for n in range(DEEP)]
        t_ps = [psum(m, ctx, f"t_ps{n}_{tag}", [P, KV]) for n in range(2)]
        turn = lambda i, u, f: (i, u, order.index(f))
        prepared = lambda f: first(0) if small and f == K else (0, 0, f - GROUP)
        last_turn = lambda i, u: (i - 1 + u, 1 - u)

        def bank_before(b_i, u, c):
            g = c // (G * TPB) - 2
            return turn(b_i, u, GROUP + g) if g >= 0 else turn(*last_turn(b_i, u), GROUP + NG + g)

        first = lambda f: (0, 0, f - ring.lead)
        scalar_copies = lambda n: small and n % 2
        unit_turned = lambda n: t_ps[n % 2][:].rearrange("p (c t) -> p c t", t=P)

        def unit_pT(n):
            h, j = divmod(n, TPB)
            return pT[h // G % 2][:, h % G, :, j * P:(j + 1) * P]
        cols512 = lambda f: slice(512 * f, 512 * f + 512)

        with nc.Block() as block:
            @block.sync
            def _(sp):
                def stream(b, u):
                    sp.dma_start(ctxT[u][:], d["ctxT"][:, bass.ds(b * KV, KV)]).then_inc(m.streamed[u].sem, 16)
                    if mask is not None:
                        sp.dma_start(mask_i[u][:], mask[bass.ds(b * S, S), :].rearrange("(t p) k -> p t k", p=P))\
                            .then_inc(m.streamed[u].sem, 16)

                for dst, src in ((wk_s[:], wk), (wq_s[:], wq)):
                    sp.dma_start(dst, src).then_inc(m.qk_loaded.sem, 16)
                for u in range(2):
                    stream(u, u)
                loads = [(wv_s[:], wv), (bo_s[:], bo)]
                if key_bias is not None:
                    loads.append((kb[:], key_bias.rearrange("o (p n) -> (o p) n", p=P)))
                if not small:
                    loads.append((wo_s[:], wo.rearrange("(g p) n -> p g n", p=P)))
                if bq is not None:
                    loads += [(bq_s[:], bq.rearrange("o (p n) -> (o p) n", n=1)),
                              (bk_s[:], bk.rearrange("o (p n) -> (o p) n", n=1))]
                if key_mask is not None:
                    loads.append((key_u8[:], key_mask.rearrange("o (p n) -> (o p) n", p=P)))
                for dst, src in loads:
                    sp.dma_start(dst, src).then_inc(m.loaded.sem, 16)
                n = len(loads)
                if small:
                    sp.wait_ge(*m.zeroed.after(NFIRST))
                    for h in range(G):
                        sp.dma_start(wo_s[W * h:W * h + hd, :, :], wo.rearrange("(g h e) n -> h e g n", h=G, e=hd)[h])\
                            .then_inc(m.loaded.sem, 16)
                    n += G
                if bv is not None:
                    for h in range(G):
                        sp.dma_start(bv_s[W * h:W * h + hd, :], bv[hd * h:hd * (h + 1), :])\
                            .then_inc(m.loaded.sem, 16)
                    n += G
                assert n == NLOAD
                if key_mask is not None:
                    sp.wait_ge(*m.parts_ready.after(1))
                    sp.dma_start(key_rows[0:1, 0:B * KV], key_part[:]).then_inc(m.rows_moved.sem, 16)
                if key_bias is not None:
                    sp.wait_ge(*m.parts_ready.after(1))
                    for r in range(3):
                        sp.dma_start(bias_rows[r:r + 1, 0:B * KV], kb_part[:, r, :]).then_inc(m.rows_moved.sem, 16)
                    sp.wait_ge(*m.rows_moved.after(48))

                def stack(i, u):
                    b = 2 * i + u + 1
                    sp.wait_ge(*m.parts_split.after(2 * b + 1))
                    for w in range(2):
                        for row, _, of_k in STACK:
                            sp.dma_start(kT[1 - u][64 * w + row:64 * w + row + hd, :, :], parts[64 * w:64 * w + 64, of_k, 0:KV])\
                                .then_inc(m.stacked[1 - u].sem, 16)
                    sp.wait_ge(*m.parts_split.after(2 * b + 2))
                    for w in range(2):
                        for row, of_q, _ in STACK:
                            sp.dma_start(q[1 - u][64 * w + row:64 * w + row + hd, w:HEADS:2, :],
                                         parts[64 * w:64 * w + 64, of_q, KV:KV + S]).then_inc(m.stacked[1 - u].sem, 16)
                        if key_bias is not None:
                            sp.dma_start(kT[1 - u][64 * w + BIAS:64 * w + BIAS + 3, :, :],
                                         bias_rows[:, bass.ds(b * KV, KV)].unsqueeze(1).to_broadcast([3, PAIR, KV]))\
                                .then_inc(m.stacked[1 - u].sem, 16)

                if small:
                    stack(-1, 1)
                    sp.wait_ge(*m.zeroed.after(NFIRST + NLATER))
                with sp.Fori(0, PAIRS) as i:
                    for u in range(2):
                        sp.wait_ge(*ring.full(*turn(i, u, GROUP)))
                        stream(2 * i + u + AHEAD, u)
                        if small:
                            stack(i, u)
                for u in range(2):
                    sp.wait_ge(*m.streamed[u].after(per_load * (PAIRS + 1)))
                    if small:
                        sp.wait_ge(*m.stacked[u].after(16 * NSTACK * (PAIRS + 1 - u)))

            @block.gpsimd
            def _(pool):
                for t in first_zeros:
                    pool.memset(t, 0.0).then_inc(m.zeroed.sem, 1)
                for n, t in enumerate(ones_of[0]):
                    pool.wait_ge(*m.zeroed.after(len(first_zeros) + n))
                    pool.sem_inc(m.passed.sem, 1)
                    pool.memset(t, 1.0).then_inc(m.zeroed.sem, 1)
                pool.wait_ge(*m.zeroed.after(NFIRST))
                pool.sem_inc(m.passed.sem, 1)
                norm.pool(pool, 0)

                def split(i, u, at_k):
                    b = 2 * i + u + 1
                    pool.wait_ge(*ring.empty(*at_k))
                    sides = ((k_all[:], slice(0, KV)), (q_all[:, bass.ds(b * S, S)], slice(KV, KV + S)))
                    for side, (src, cols) in enumerate(sides):
                        at = 6 * b + 3 * side
                        nothing = zero[:, 0:cols.stop - cols.start]
                        pool.tensor_tensor(parts[:, 0, cols], src, nothing, ALU.add).then_inc(m.pool_step.sem, 1)
                        pool.wait_ge(*m.pool_step.after(at + 1))
                        pool.sem_inc(m.passed.sem, 1)
                        pool.tensor_tensor(rest[:, cols], src, parts[:, 0, cols], ALU.subtract).then_inc(m.pool_step.sem, 1)
                        pool.wait_ge(*m.pool_step.after(at + 2))
                        pool.tensor_tensor(parts[:, 1, cols], rest[:, cols], nothing, ALU.add).then_inc(m.pool_step.sem, 1)
                        pool.wait_ge(*m.pool_step.after(at + 3))
                        pool.tensor_tensor(parts[:, 2, cols], rest[:, cols], parts[:, 1, cols], ALU.subtract)\
                            .then_inc(m.parts_split.sem, 1)
                        if isinstance(i, int) and side == 0:
                            pool.wait_ge(*ring.empty(*first(T0 + 2 * TURNS - 2)))
                            pool.wait_ge(*ring.empty(*first(T0 + 2 * TURNS - 1)))

                if small:
                    split(-1, 1, prepared(K))
                for t in later_zeros:
                    pool.memset(t, 0.0).then_inc(m.zeroed.sem, 1)
                for n, t in enumerate(ones_of[1]):
                    pool.wait_ge(*m.zeroed.after(NFIRST + len(later_zeros) + n))
                    pool.sem_inc(m.passed.sem, 1)
                    pool.memset(t, 1.0).then_inc(m.zeroed.sem, 1)
                pool.wait_ge(*m.zeroed.after(NFIRST + NLATER))
                pool.sem_inc(m.passed.sem, 1)
                if small:
                    with pool.Fori(0, PAIRS) as i:
                        for u in range(2):
                            split(i, u, turn(i, u, K))

            @block.vector
            def _(dve):
                norm.vector(dve, 0, 0, lambda j: x[:, j, :])
                for t in zeros:
                    dve.memset(t, 0.0).then_inc(m.step.sem, 1)
                dve.memset(sums[:, 1], 1.0).then_inc(m.step.sem, 1)
                done = NZERO
                dve.wait_ge(*m.loaded.after(16 * NLOAD))
                if bv is not None:
                    dve.wait_ge(*m.turned.after(1))
                    dve.tensor_copy(bo_s[:], t_ps[0][0:1, 0:D]).then_inc(m.step.sem, 1)
                    done += 1
                if bq is not None:
                    dve.tensor_scalar(bq_s[:], bq_s[:], hd ** -0.5, None, ALU.mult).then_inc(m.step.sem, 1)
                    done += 1
                if key_mask is not None:
                    dve.tensor_scalar(key_part[:], key_u8[:], 0.0, -1e30, ALU.is_equal, ALU.mult).then_inc(m.step.sem, 1)
                    done += 1
                if key_bias is not None:
                    for r in range(2):
                        dve.tensor_copy(kb_part[:, r, :], kb[:]).then_inc(m.step.sem, 1)
                        dve.wait_ge(*m.step.after(done + 1))
                        dve.tensor_tensor(kb[:], kb[:], kb_part[:, r, :], ALU.subtract).then_inc(m.step.sem, 1)
                        dve.wait_ge(*m.step.after(done + 2))
                        done += 2
                    dve.tensor_copy(kb_part[:, 2, :], kb[:]).then_inc(m.step.sem, 1)
                    done += 1
                dve.wait_ge(*m.step.after(done))
                if key_bias is not None or key_mask is not None:
                    dve.engine_nop().then_inc(m.parts_ready.sem, 1)
                dve.engine_nop().then_inc(m.ready_made.sem, 1)
                assert done == NSTEP

                def drain(i, u, f, at):
                    if SPREAD <= f < OUT:
                        if f == SPREAD:
                            dve.wait_ge(*ring.empty(*turn(*last_turn(i, u), PER - 1)))
                        dve.wait_ge(*ring.full(*at))
                        g = 2 * (f - SPREAD)
                        og = o[1 - u][:, g:g + 2, :].rearrange("p g t -> p (g t)")
                        dve.tensor_tensor(og, ring.bank(*at[1:])[:], og, ALU.mult).then_inc(ring.drains(*at[1:]), 1)
                    if f == OUT:
                        dve.wait_ge(*ring.full(*at))
                        rows = m.x_padded[:, bass.ds(TPB * (2 * i + u), TPB), :]
                        dve.tensor_tensor(rows, ring.bank(*at[1:])[:, 0:TPB * D].rearrange("p (t d) -> p t d", d=D), rows, ALU.add)\
                            .then_inc(ring.drains(*at[1:]), 1)
                    if V <= f < GROUP:
                        dve.wait_ge(*ring.full(*at))
                        if small:
                            to = v[1 - u][:].rearrange("p c (h w) -> p (c h) w", w=W)[:, :, 0:hd]
                            dve.tensor_copy(to, ring.bank(*at[1:])[:].rearrange("p (n e) -> p n e", e=hd)).then_inc(ring.drains(*at[1:]), 1)
                        else:
                            c, half = divmod(f - V, VW // 512)
                            dve.tensor_copy(v[1 - u][:, c, cols512(half)], ring.bank(*at[1:])[:]).then_inc(ring.drains(*at[1:]), 1)

                def convert_mask(i, u):
                    b = 2 * i + u + 1
                    dve.wait_ge(*m.streamed[1 - u].after(per_load * (i + u + 1)))
                    dve.tensor_scalar(mask_b[1 - u][:], mask_i[1 - u][:], 0.0, -1e20, ALU.is_equal, ALU.mult)\
                        .then_inc(m.mask_ready.sem, 1)

                def invert_sums(b, u):
                    dve.wait_ge(*m.probs_ready.after(UNITS * b))
                    dve.reciprocal(inv[:], sums[:, 1 - u].rearrange("p t h -> p (t h)")).then_inc(m.sums_inverted.sem, 1)

                if mask is not None:
                    convert_mask(-1, 1)
                for f in range(V, GROUP):
                    drain(-1, 1, f, prepared(f))
                with dve.Fori(0, PAIRS) as i:
                    for u in range(2):
                        b = 2 * i + u
                        invert_sums(b, u)
                        for n in range(UNITS + DEEP):
                            c = n - DEEP
                            if c >= 0 and not scalar_copies(c):
                                if c % (G * TPB) <= 1:
                                    dve.wait_ge(*ring.full(*bank_before(i, u, c)))
                                dve.wait_ge(*m.turned.after(UNITS * b + c + 1 + (bv is not None)))
                                dve.tensor_copy(unit_pT(c), unit_turned(c)).then_inc(m.unit_copied[c % 2].sem, 1)
                            if n < UNITS:
                                dve.wait_ge(*m.scores_ready.after(UNITS * b + n + 1))
                                dve.tensor_reduce(nmax[:, u, n:n + 1], s_ps[n % DEEP][:], AX.X, ALU.max, negate=True)\
                                    .then_inc(m.max_ready.sem, 1)
                            if DEEP <= n:
                                for f in due[n - DEEP]:
                                    drain(i, u, f, turn(i, u, f))
                            if n == UNITS // 2 and mask is not None:
                                convert_mask(i, u)
                invert_sums(B, 0)
                for f in range(Q):
                    drain(PAIRS, 0, f, (PAIRS, 0, f))

            @block.scalar
            def _(act):
                def drain(i, u, f, at):
                    if f >= GROUP:
                        act.wait_ge(*ring.full(*at))
                        act.activation(o[u][:, f - GROUP, :], ring.bank(*at[1:])[:, 0:S], ACT.Copy).then_inc(ring.drains(*at[1:]), 1)
                    if f == SUMS:
                        act.wait_ge(*ring.full(*at))
                        act.activation(invT[:], ring.bank(*at[1:])[0:HEADS, 0:S], ACT.Copy).then_inc(ring.drains(*at[1:]), 1)
                    if Q <= f < K:
                        act.wait_ge(*ring.full(*at))
                        bank = ring.bank(*at[1:])[:].rearrange("p (t s) -> p t s", s=S)
                        h = 4 * (f - Q)
                        act.activation(q[1 - u][0:W, h:h + 4:2, :], bank[0:W], ACT.Copy, scale=hd ** -0.5)
                        act.activation(q[1 - u][W:P, h + 1:h + 4:2, :], bank[W:P], ACT.Copy, scale=hd ** -0.5)\
                            .then_inc(ring.drains(*at[1:]), 1)
                    if K <= f < V:
                        act.wait_ge(*ring.full(*at))
                        to = k_all[:] if small else kT[1 - u][:, f - K, :]
                        if bk is None:
                            act.activation(to, ring.bank(*at[1:])[:], ACT.Copy).then_inc(ring.drains(*at[1:]), 1)
                        else:
                            act.activation(to, ring.bank(*at[1:])[:], ACT.Identity, bias=bk_s[:, 0:1]).then_inc(ring.drains(*at[1:]), 1)

                act.wait_ge(*m.zeroed.after(NFIRST + NLATER) if not small else m.loaded.after(16 * NLOAD))
                if small:
                    drain(-1, 1, K, prepared(K))
                for f in range(TURNS):
                    at = first(T0 + f)
                    act.wait_ge(*ring.full(*at))
                    act.activation(xnT[:, cols512(f)], ring.bank(*at[1:])[:], ACT.Copy).then_inc(ring.drains(*at[1:]), 1)
                if small:
                    act.wait_ge(*m.ready_made.after(1))
                    for f in range(TURNS):
                        at = first(T0 + TURNS + f)
                        act.wait_ge(*ring.full(*at))
                        if bq is None:
                            act.activation(q_all[:, cols512(f)], ring.bank(*at[1:])[:], ACT.Copy, scale=hd ** -0.5)\
                                .then_inc(ring.drains(*at[1:]), 1)
                        else:
                            act.activation(q_all[:, cols512(f)], ring.bank(*at[1:])[:], ACT.Identity, bias=bq_s[:, 0:1],
                                           scale=hd ** -0.5).then_inc(ring.drains(*at[1:]), 1)
                for f in range(V if small else Q, GROUP):
                    drain(-1, 1, f, prepared(f))
                with act.Fori(0, PAIRS) as i:
                    for u in range(2):
                        b = 2 * i + u
                        for n in range(UNITS + DEEP):
                            h, j = divmod(n, TPB)
                            c = n - DEEP + 1
                            if 0 <= c < UNITS and scalar_copies(c):
                                if c % (G * TPB) <= 1:
                                    act.wait_ge(*ring.full(*bank_before(i, u, c)))
                                act.wait_ge(*m.turned.after(UNITS * b + c + 1 + (bv is not None)))
                                act.activation(unit_pT(c), unit_turned(c), ACT.Copy).then_inc(m.unit_copied[c % 2].sem, 1)
                            if n < UNITS:
                                act.wait_ge(*m.max_ready.after(UNITS * b + n + 1))
                                act.activation(probs[n % DEEP][:], s_ps[n % DEEP][:], ACT.Exp, bias=nmax[:, u, n:n + 1],
                                               accum_out=sums[:, u, j, h:h + 1]).then_inc(m.probs_ready.sem, 1)
                            if DEEP <= n:
                                for f in due[n - DEEP]:
                                    drain(i, u, f, turn(i, u, f))
                        for f in due[UNITS]:
                            drain(i, u, f, turn(i, u, f))
                for f in range(Q):
                    drain(PAIRS, 0, f, (PAIRS, 0, f))

            @block.tensor
            def _(pe):
                def fold_bias():
                    pe.wait_ge(*m.loaded.after(16 * NLOAD))
                    pe.matmul(t_ps[0][0:1, 0:D], k["ones"][0:1, 0:1], bo_s[:], start=True, stop=False)
                    for g in range(NG):
                        ins = pe.matmul(t_ps[0][0:1, 0:D], bv_s[:, g:g + 1], wo_s[:, g, :], start=False, stop=(g == NG - 1))
                    ins.then_inc(m.turned.sem, 1)
                def fill(i, u, f, at):
                    b = 2 * i + u
                    bank = ring.bank(*at[1:])
                    if f == SUMS:
                        pe.wait_ge(*m.sums_inverted.after(b + 1))
                        pe.wait_ge(*ring.free(*at))
                        for j in range(TPB):
                            ins = pe.transpose(bank[0:HEADS, j * P:(j + 1) * P], inv[:, j * HEADS:(j + 1) * HEADS], k["ident"])
                    elif f < OUT:
                        if f == SPREAD:
                            pe.wait_ge(*ring.empty(at[0], at[1], at[2] + (order.index(SUMS) - order.index(SPREAD) if i is not PAIRS else -1)))
                        pe.wait_ge(*ring.free(*at))
                        for t in range(2):
                            g = 2 * (f - SPREAD) + t
                            ins = pe.matmul(bank[:, t * S:(t + 1) * S], spread[0:HEADS, g * P:(g + 1) * P], invT[:],
                                            start=True, stop=True)
                    elif f == OUT:
                        pe.wait_ge(*ring.free(*at))
                        pe.wait_ge(*ring.empty(at[0], at[1], at[2] + (order.index(OUT - 1) - order.index(OUT) if i is not PAIRS else -1)))
                        for j in range(TPB):
                            out = bank[:, j * D:(j + 1) * D]
                            pe.matmul(out, k["ones"][0:1, :], bo_s[:], start=True, stop=False)
                            for g in range(NG):
                                ins = pe.matmul(out, o[1 - u][:, g, j * P:(j + 1) * P], wo_s[:, g, :], start=False, stop=(g == NG - 1))
                    elif f < K:
                        pe.wait_ge(*ring.free(*at))
                        for t in range(2):
                            c0 = (2 * (f - Q) + t) * P
                            ins = pe.matmul(bank[:, t * S:(t + 1) * S], wq_s[:, c0:c0 + P], xnT[:, bass.ds((b + 1) * S, S)],
                                            start=True, stop=True)
                    elif f < V:
                        if f == K:
                            pe.wait_ge(*m.streamed[1 - u].after(per_load * (i + u + 1)))
                        pe.wait_ge(*ring.free(*at))
                        ins = pe.matmul(bank[:], wk_s[:, (f - K) * P:(f - K + 1) * P], ctxT[1 - u][:], start=True, stop=True)
                    elif f >= GROUP:
                        g = f - GROUP
                        for copied in m.unit_copied:
                            pe.wait_ge(*copied.after(UNITS // 2 * b + G * TPB // 2 * (g + 1)))
                        pe.wait_ge(*ring.free(*at))
                        for c in range(CPB):
                            for hh in range(G):
                                ins = pe.matmul(bank[W * hh:W * (hh + 1), 0:S], v[u][:, c, (G * g + hh) * W:(G * g + hh + 1) * W],
                                                pT[g % 2][:, hh, c, :], start=(c == 0), stop=(c == CPB - 1))
                    else:
                        pe.wait_ge(*ring.free(*at))
                        if small:
                            for c in range(CPB):
                                ins = pe.matmul(bank[:, c * D:(c + 1) * D], ctxT[1 - u][:, c * P:(c + 1) * P], wv_s[:], start=True, stop=True)
                        else:
                            c, half = divmod(f - V, VW // 512)
                            ins = pe.matmul(bank[:], ctxT[1 - u][:, c * P:(c + 1) * P], wv_s[:, cols512(half)], start=True, stop=True)
                    ins.then_inc(ring.fills(*at[1:]), 1)

                def scores(i, u, n):
                    h, j = divmod(n, TPB)
                    b = 2 * i + u
                    out = s_ps[n % DEEP][:]
                    if mask is not None:
                        if n == 0:
                            pe.wait_ge(*m.mask_ready.after(b + 1))
                        pe.matmul(out, k["ident_bf"], mask_b[u][:, j, :], start=True, stop=False)
                    if key_mask is not None:
                        pe.matmul(out, k["ones_bf"], key_rows[:, bass.ds(b * KV, KV)], start=True, stop=False)
                    if small and n == 0:
                        pe.wait_ge(*m.stacked[u].after(16 * NSTACK * (i + 1)))
                    pe.matmul(out, q[u][:, h, j * P:(j + 1) * P], kT[u][:, h // 2, :], start=(mask is None and key_mask is None),
                              stop=True).then_inc(m.scores_ready.sem, 1)

                pe.wait_ge(*m.qk_loaded.after(32))
                if small:
                    fill(-1, 1, K, prepared(K))
                for f in range(TURNS):
                    at = first(T0 + f)
                    pe.wait_ge(*m.normed.after(4 * f + 4))
                    pe.wait_ge(*ring.free(*at))
                    for j in range(4):
                        ins = pe.transpose(ring.bank(*at[1:])[:, j * P:(j + 1) * P], norm.xn[0][:, 4 * f + j, :], k["ident"])
                    ins.then_inc(ring.fills(*at[1:]), 1)
                if bv is not None:
                    fold_bias()
                for f in range(TURNS if small else 0):
                    at = first(T0 + TURNS + f)
                    pe.wait_ge(*ring.empty(*first(T0 + f)))
                    pe.wait_ge(*ring.free(*at))
                    pe.matmul(ring.bank(*at[1:])[:], wq_s[:], xnT[:, cols512(f)], start=True, stop=True)\
                        .then_inc(ring.fills(*at[1:]), 1)
                pe.wait_ge(*m.ready_made.after(1))
                for f in range(max(0, TURNS - RING), TURNS):
                    pe.wait_ge(*ring.empty(*first(T0 + f)))
                for f in range(V if small else Q, GROUP):
                    fill(-1, 1, f, prepared(f))
                for f in range(max(V, GROUP - RING), GROUP):
                    pe.wait_ge(*ring.empty(*prepared(f)))
                if key_mask is not None:
                    pe.wait_ge(*m.rows_moved.after(16))
                for n in range(DEEP):
                    scores(0, 0, n)
                with pe.Fori(0, PAIRS) as i:
                    for u in range(2):
                        b = 2 * i + u
                        for n in range(UNITS):
                            pe.wait_ge(*m.probs_ready.after(UNITS * b + n + 1))
                            pe.wait_ge(*m.unit_copied[n % 2].after(UNITS // 2 * b + n // 2))
                            for c in range(CPB):
                                ins = pe.transpose(t_ps[n % 2][:, c * P:(c + 1) * P], probs[n % DEEP][:, c * P:(c + 1) * P],
                                                   k["ident"])
                            ins.then_inc(m.turned.sem, 1)
                            if n + DEEP < UNITS:
                                scores(i, u, n + DEEP)
                            else:
                                if n + DEEP == UNITS:
                                    for f in range(max(Q, V - RING), V):
                                        pe.wait_ge(*ring.empty(*turn(i, u, f)))
                                scores(i + u, 1 - u, n + DEEP - UNITS)
                            for f in due[n]:
                                fill(i, u, f, turn(i, u, f))
                        for f in range(max(V, GROUP - 4), GROUP):
                            pe.wait_ge(*ring.empty(*turn(i, u, f)))
                        for f in due[UNITS]:
                            fill(i, u, f, turn(i, u, f))
                for f in range(Q):
                    fill(PAIRS, 0, f, (PAIRS, 0, f))
        norm.close(1)
        ring.close(Q)
        for s, n in ((m.loaded, 16 * NLOAD), (m.step, NSTEP), (m.ready_made, 1), (m.qk_loaded, 32), (m.zeroed, NFIRST + NLATER), (m.streamed[0], per_load * (PAIRS + 1)),
                     (m.streamed[1], per_load * (PAIRS + 1)), (m.mask_ready, B + 1 if mask is not None else 0),
                     (m.parts_ready, mask is None), (m.rows_moved, 48 * (key_bias is not None) + 16 * (key_mask is not None)),
                     (m.pool_step, 6 * (B + 1) if small else 0), (m.parts_split, 2 * (B + 1) if small else 0),
                     (m.stacked[0], 16 * NSTACK * (PAIRS + 1) if small else 0), (m.stacked[1], 16 * NSTACK * PAIRS if small else 0),
                     (m.scores_ready, UNITS * B + DEEP), (m.max_ready, UNITS * B), (m.probs_ready, UNITS * B), (m.turned, UNITS * B + (bv is not None)),
                     (m.unit_copied[0], UNITS * B // 2), (m.unit_copied[1], UNITS * B // 2),
                     (m.sums_inverted, B + 1)):
            s.before += n


def l1_cross_attention(m):
    d = m.dram
    head_attention(m, "l1x", 8, d["L1_xattn_Wq"], d["L1_xattn_Wk"], d["L1_xattn_Wv"], d["L1_xattn_Wo"], d["L1_xattn_bo"],
                   mask=d["mask"])


def l2_cross_attention(m):
    d = m.dram
    inner = HEADS * 64
    head_attention(m, "l2x", 64, d["L2_xattn_Wq"], d["L2_xattn_Wkv"][:, 0:inner], d["L2_xattn_Wkv"][:, inner:],
                   d["L2_xattn_Wout"], d["L2_xattn_b_out"], key_mask=d["key_mask"])


def l3_cross_attention(m):
    d = m.dram
    head_attention(m, "l3x", 8, d["L3_xattn_wq"], d["L3_xattn_wk"], d["L3_xattn_wv"], d["L3_xattn_wo"], d["L3_xattn_bo"],
                   bq=d["L3_xattn_bq"], bk=d["L3_xattn_bk"], bv=d["L3_xattn_bv"], key_bias=d["time_bias"])


def turn_bf16(m, pe, ring, i, u, fill, src, n):
    pe.wait_ge(*ring.free(i, u, fill))
    out = ring.bank(u, fill)[:, 0:n * P // 2].bitcast(BF16)
    for c in range(n):
        ins = pe.transpose(out[:, c * P:(c + 1) * P], src(c), m.consts["ident_bf"])
    ins.then_inc(ring.fills(u, fill), 1)


def l1_bit_ffn(m):
    nc, d, x, k = m.nc, m.dram, m.x, m.consts
    H = 512
    HC = H // P
    EPS_NORM, EPS_Q, QMAX = 1e-8, 1e-5, 127.0
    CHAIN = 2 * TPB + 5
    with ExitStack() as ctx:
        sb = lambda name, shape, dt=F32: sbuf(m, ctx, f"{name}_l1f", shape, dt)
        norm = Norm(m, ctx, TPB, "l1f")
        w = sb("w", [P, 2, H])
        wq = sb("wq", [P, 2, H], BF16)
        n1w, n2w = sb("n1w", [P, D]), sb("n2w", [P, H])
        gain, offset = sb("gain", [P, 1]), sb("offset", [P, 1])
        wsum, wmean, wscale = sb("wsum", [P, 2]), sb("wmean", [P, 2]), sb("wscale", [P, 2])
        small = lambda name: [sb(f"{name}{s}", [P, TPB]) for s in range(2)]
        ss, ms, rr, am, qs, cc = small("ss"), small("ms"), small("rr"), small("am"), small("qs"), small("cc")
        junk = sb("junk", [P, TPB, H])
        xr = sb("xr", [P, TPB, D])
        xq = sb("xq", [P, TPB, D], BF16)
        xqT = [sb(f"xqT{u}", [P, S], BF16) for u in range(2)]
        h = sb("h", [P, TPB, H])
        hh = sb("hh", [P, TPB, H])
        hr = sb("hr", [P, TPB, H])
        hq = sb("hq", [P, TPB, H], BF16)
        hqT = [sb(f"hqT{u}", [P, TPB, HC, P], BF16) for u in range(2)]
        TURN, TURN_H, OUT = 0, 1, 1 + TPB
        ring = Ring([psum(m, ctx, f"ring{n}_l1f", [P, 512]) for n in range(2)], m.filled, m.drained, OUT + 1)
        h_ps = [psum(m, ctx, f"h_ps{j}_l1f", [P, H]) for j in range(TPB)]
        w_ps = psum(m, ctx, "w_ps_l1f", [P, 2])

        with nc.Block() as block:
            @block.sync
            def _(sp):
                for dst, src in ((w[:, 0, :], d["L1_ffn_w1"]),
                                 (w[:, 1, :].rearrange("p (c d) -> p c d", d=D), d["L1_ffn_w2"].rearrange("(c p) d -> p c d", p=P)),
                                 (n1w[:], d["L1_ffn_norm1_w"][0, :].partition_broadcast(P)),
                                 (n2w[:], d["L1_ffn_norm2_w"][0, :].partition_broadcast(P)),
                                 (gain[:], d["L1_ffn_act_scale"][0, :].partition_broadcast(P)),
                                 (offset[:], d["L1_ffn_act_bias"][0, :].partition_broadcast(P))):
                    sp.dma_start(dst, src).then_inc(m.loaded.sem, 16)
                sp.wait_ge(*m.loaded.after(96))

            @block.gpsimd
            def _(pool):
                with pool.Fori(0, PAIRS) as i:
                    for u in range(2):
                        b = 2 * i + u
                        norm.pool(pool, b)
                        for s in range(2):
                            pool.wait_ge(*m.squares_ready.after(2 * b + s + 1))
                            pool.tensor_tensor(rr[s][:], ms[s][:], k["minus_half"][:, 0:TPB], ALU.pow)\
                                .then_inc(m.powers_ready.sem, 1)

            @block.vector
            def _(dve):
                dve.wait_ge(*m.loaded.after(96))
                dve.tensor_reduce(wsum[:], w[:], AX.X, ALU.add, apply_absolute_value=True).then_inc(m.ready_made.sem, 1)
                dve.wait_ge(*m.turned.after(1))
                dve.tensor_scalar(wmean[:], w_ps[:], 1.0 / (H * D), EPS_Q, ALU.mult, ALU.max).then_inc(m.step.sem, 1)
                dve.wait_ge(*m.step.after(1))
                dve.reciprocal(wscale[:], wmean[:]).then_inc(m.step.sem, 1)
                dve.wait_ge(*m.step.after(2))
                for n in range(2):
                    dve.tensor_scalar(w[:, n, :], w[:, n, :], wscale[:, n:n + 1], MAGIC, ALU.mult, ALU.add).then_inc(m.step.sem, 1)
                dve.wait_ge(*m.step.after(4))
                dve.tensor_scalar(w[:], w[:], MAGIC, 1.0, ALU.subtract, ALU.min).then_inc(m.step.sem, 1)
                dve.wait_ge(*m.step.after(5))
                dve.tensor_scalar(wq[:], w[:], -1.0, None, ALU.max).then_inc(m.step.sem, 1)
                dve.wait_ge(*m.step.after(6))
                dve.engine_nop().then_inc(m.ready_made.sem, 1)
                def quantise(b, s, src, factor, r, dst, width):
                    at = 6 + CHAIN * (2 * b + s)
                    dve.wait_ge(*m.squares_summed.after(TPB * (2 * b + s + 1)))
                    dve.tensor_scalar(ms[s][:], ss[s][:], 1.0 / width, EPS_NORM, ALU.mult, ALU.add).then_inc(m.squares_ready.sem, 1)
                    dve.wait_ge(*m.powers_ready.after(2 * b + s + 1))
                    for j in range(TPB):
                        dve.scalar_tensor_tensor(out=r[:, j, :], in0=src[:, j, :], scalar=rr[s][:, j:j + 1], in1=factor[:],
                                                 op0=ALU.mult, op1=ALU.mult).then_inc(m.step.sem, 1)
                    dve.wait_ge(*m.step.after(at + TPB))
                    dve.tensor_reduce(am[s][:], r[:], AX.X, ALU.max, apply_absolute_value=True).then_inc(m.step.sem, 1)
                    dve.wait_ge(*m.step.after(at + TPB + 1))
                    dve.tensor_scalar(am[s][:], am[s][:], EPS_Q, None, ALU.max).then_inc(m.step.sem, 1)
                    dve.wait_ge(*m.step.after(at + TPB + 2))
                    dve.reciprocal(qs[s][:], am[s][:]).then_inc(m.step.sem, 1)
                    dve.tensor_scalar(cc[s][:], am[s][:], 1.0 / QMAX, wmean[:, s:s + 1], ALU.mult, ALU.mult).then_inc(m.step.sem, 1)
                    dve.wait_ge(*m.step.after(at + TPB + 4))
                    dve.tensor_scalar(qs[s][:], qs[s][:], QMAX, None, ALU.mult).then_inc(m.step.sem, 1)
                    dve.wait_ge(*m.step.after(at + TPB + 5))
                    for j in range(TPB):
                        dve.tensor_scalar(r[:, j, :], r[:, j, :], qs[s][:, j:j + 1], MAGIC, ALU.mult, ALU.add)\
                            .then_inc(m.step.sem, 1)
                    dve.wait_ge(*m.step.after(at + CHAIN))
                    dve.tensor_scalar(dst[:], r[:], MAGIC, QMAX, ALU.subtract, ALU.min).then_inc(m.x_quantised.sem, 1)

                with dve.Fori(0, PAIRS) as i:
                    for u in range(2):
                        b = 2 * i + u
                        norm.vector(dve, b, u, lambda j: x[:, TPB * b + j, :])
                        quantise(b, 0, norm.xn[u], n1w, xr, xq, D)
                        dve.wait_ge(*m.h_squared.after(b + 1))
                        dve.tensor_scalar(hh[:], h[:], gain[:], offset[:], ALU.mult, ALU.add).then_inc(m.squared_affine.sem, 1)
                        quantise(b, 1, hh, n2w, hr, hq, H)
                        dve.wait_ge(*ring.full(i, u, OUT))
                        for j in range(TPB):
                            rows = x[:, TPB * b + j, :]
                            ins = dve.scalar_tensor_tensor(out=rows, in0=ring.bank(u, OUT)[:, j * D:(j + 1) * D],
                                                           scalar=cc[1][:, j:j + 1], in1=rows, op0=ALU.mult, op1=ALU.add)
                        ins.then_inc(ring.drains(u, OUT), 1)

            @block.scalar
            def _(act):
                with act.Fori(0, PAIRS) as i:
                    for u in range(2):
                        b = 2 * i + u
                        act.wait_ge(*m.normed.after(TPB * (b + 1)))
                        for j in range(TPB):
                            act.activation(junk[:, j, 0:D], norm.xn[u][:, j, :], ACT.Square, accum_out=ss[0][:, j:j + 1])\
                                .then_inc(m.squares_summed.sem, 1)
                        act.wait_ge(*ring.full(i, u, TURN))
                        act.activation(xqT[u][:], ring.bank(u, TURN)[:, 0:P].bitcast(BF16), ACT.Copy).then_inc(ring.drains(u, TURN), 1)
                        for j in range(TPB):
                            act.wait_ge(*m.scores_ready.after(TPB * b + j + 1))
                            act.activation(h[:, j, :], h_ps[j][:], ACT.Relu, scale=cc[0][:, j:j + 1]).then_inc(m.act_step.sem, 1)
                        act.wait_ge(*m.act_step.after(TPB * (b + 1)))
                        act.activation(h[:], h[:], ACT.Square).then_inc(m.h_squared.sem, 1)
                        act.wait_ge(*m.squared_affine.after(b + 1))
                        for j in range(TPB):
                            act.activation(junk[:, j, :], hh[:, j, :], ACT.Square, accum_out=ss[1][:, j:j + 1])\
                                .then_inc(m.squares_summed.sem, 1)
                        for j in range(TPB):
                            act.wait_ge(*ring.full(i, u, TURN_H + j))
                            act.activation(hqT[u][:, j].rearrange("p c t -> p (c t)"),
                                           ring.bank(u, TURN_H + j)[:, 0:HC * P // 2].bitcast(BF16), ACT.Copy).then_inc(ring.drains(u, TURN_H + j), 1)

            @block.tensor
            def _(pe):
                pe.wait_ge(*m.ready_made.after(1))
                pe.matmul(w_ps[:], k["ones"], wsum[:], start=True, stop=True).then_inc(m.turned.sem, 1)
                pe.wait_ge(*m.ready_made.after(2))
                with pe.Fori(0, PAIRS) as i:
                    for u in range(2):
                        b = 2 * i + u
                        pe.wait_ge(*m.x_quantised.after(2 * b + 1))
                        turn_bf16(m, pe, ring, i, u, TURN, lambda c: xq[:, c, :], TPB)
                        pe.wait_ge(*ring.empty(i, u, TURN))
                        for j in range(TPB):
                            pe.matmul(h_ps[j][:], xqT[u][:, j * P:(j + 1) * P], wq[:, 0, :], start=True, stop=True)\
                                .then_inc(m.scores_ready.sem, 1)
                        pe.wait_ge(*m.x_quantised.after(2 * b + 2))
                        for j in range(TPB):
                            turn_bf16(m, pe, ring, i, u, TURN_H + j, lambda c: hq[:, j, c * P:(c + 1) * P], HC)
                        pe.wait_ge(*ring.free(i, u, OUT))
                        for j in range(TPB):
                            pe.wait_ge(*ring.empty(i, u, TURN_H + j))
                            for c in range(HC):
                                ins = pe.matmul(ring.bank(u, OUT)[:, j * D:(j + 1) * D], hqT[u][:, j, c, :],
                                                wq[:, 1, c * D:(c + 1) * D], start=(c == 0), stop=(c == HC - 1))
                        ins.then_inc(ring.fills(u, OUT), 1)
        norm.close(B)
        ring.close()
        for s, n in ((m.loaded, 96), (m.ready_made, 2), (m.turned, 1), (m.step, 6 + 2 * CHAIN * B), (m.squares_ready, 2 * B),
                     (m.powers_ready, 2 * B), (m.act_step, TPB * B), (m.squares_summed, 2 * TPB * B), (m.h_squared, B), (m.scores_ready, TPB * B), (m.x_quantised, 2 * B),
                     (m.squared_affine, B)):
            s.before += n


def shift_tokens(m, pe, dve, act, ring, first, hb):
    x, k = m.x, m.consts
    half, tiles = D // 2, NT // 2
    if dve is not None:
        dve.tensor_copy(hb[:, :, 0:half], x[:, :, 0:half]).then_inc(m.unshifted.sem, 1)
    for w in range(2):
        at = first(w)
        bank = ring.bank(*at[1:])[:].rearrange("p (t e) -> p t e", e=half)
        if pe is not None:
            pe.wait_ge(*ring.free(*at))
            pe.matmul(bank, k["shift"], x[:, tiles * w:tiles * (w + 1), half:D], start=True, stop=False)
            pe.matmul(bank[:, 1:tiles:2, :], k["last"], x[:, tiles * w:tiles * (w + 1):2, half:D], start=False, stop=True)\
                .then_inc(ring.fills(*at[1:]), 1)
        if act is not None:
            act.wait_ge(*ring.full(*at))
            act.activation(hb[:, tiles * w:tiles * (w + 1), half:D], bank, ACT.Copy).then_inc(ring.drains(*at[1:]), 1)


def local_attention(m, layer):
    nc, d, x, k = m.nc, m.dram, m.x, m.consts
    NH, HD = 8, 64
    INNER = NH * HD
    NG = NH // 2
    BAND = 3 * P
    TILES = (slice(0, P), slice(P, BAND))
    DEEP, RING = 2, 4
    QK = 0
    TURN = QK + 2 * TPB
    V = TURN + 2 * TPB
    SUMS = V + TPB
    SPREAD = SUMS + 1
    OUT = SPREAD + NG // 2
    GROUP = OUT + 1
    PER = GROUP + NG
    after = {QK: 0, QK + 1: 0, QK + 2: 1, QK + 3: 2, SUMS: 1, TURN: 2, TURN + 1: 3, TURN + 2: 3, TURN + 3: 4, SPREAD: 5,
             SPREAD + 1: 5, V: 6, V + 1: 6, OUT: 7}
    after.update({GROUP + g: min(2 * g + 3, NH) for g in range(NG)})
    order = sorted(range(PER), key=lambda f: (after[f], f < GROUP, f))
    due = [[f for f in order if after[f] == n] for n in range(NH + 1)]
    SHIFTS, TURNS = 2, NT // 4
    AHEAD_OF_LOOP = [(0, f) for f in range(SUMS)] + [(1, f) for f in range(QK, TURN)]
    CHAIN = 3 * TPB
    with ExitStack() as ctx:
        sb = lambda name, shape, dt=F32: sbuf(m, ctx, f"{name}_l2a{layer}", shape, dt)
        wqkv = sb("wqkv", [P, 3 * INNER])
        wo = sb("wo", [P, NG, D])
        scales = sb("scales", [P, 2, HD])
        ta, tb = sb("ta", [P, 2, TPB, HD]), sb("tb", [P, 2, TPB, HD])
        hb = sb("hb", [P, NT, D])
        hT = sb("hT", [P, (B + 3) * S])
        hs = [sb(f"hs{u}", [P, S]) for u in range(2)]
        qk = sb("qk", [P, TPB, 2, NH, HD])
        sq = sb("sq", [P, TPB, 2 * INNER])
        ss = sb("ss", [P, TPB, 2 * NH])
        ssc, rn = sb("ssc", [P, TPB * 2 * NH]), sb("rn", [P, TPB * 2 * NH])
        own, other = sb("own", [P, TPB, 2, NH, HD]), sb("other", [P, TPB, 2, NH, HD])
        q = [sb(f"q{u}", [P, NH, S]) for u in range(2)]
        kT = [sb(f"kT{u}", [P, NG, S]) for u in range(2)]
        v = [sb(f"v{u}", [P, TPB, INNER]) for u in range(2)]
        nmax = sb("nmax", [P, 2, NH * TPB])
        sums = sb("sums", [P, 2, TPB, NH])
        inv = sb("inv", [P, TPB * NH])
        invT = sb("invT", [NH, S])
        probs = [sb(f"probs{n}", [P, BAND]) for n in range(DEEP)]
        pT = [sb(f"pT{n}", [P, 2, 3, P]) for n in range(2)]
        o = [sb(f"o{u}", [P, NG, S]) for u in range(2)]
        ring = Ring([psum(m, ctx, f"ring{n}_l2a{layer}", [P, 512]) for n in range(RING)], m.filled, m.drained, PER,
                    lead=SHIFTS + TURNS + len(AHEAD_OF_LOOP))
        s_ps = [psum(m, ctx, f"s_ps{n}_l2a{layer}", [P, 512]) for n in range(DEEP)]
        t_ps = [psum(m, ctx, f"t_ps{n}_l2a{layer}", [P, 512]) for n in range(2)]
        first = lambda f: (0, 0, f - ring.lead)
        prepared = lambda b, f: first(SHIFTS + TURNS + AHEAD_OF_LOOP.index((b, f)))
        turn = lambda i, u, f: (i, u, order.index(f))
        last_turn = lambda i, u: (i - 1 + u, 1 - u)

        def group_before(i, u, g):
            return turn(i, u, GROUP + g - 2) if g >= 2 else turn(*last_turn(i, u), GROUP + NG + g - 2)

        with nc.Block() as block:
            @block.sync
            def _(sp):
                for dst, src in ((wqkv[:], d["L2_ffn_wqkv"][layer]),
                                 (wo[:], d["L2_ffn_wo"][layer].rearrange("(g p) n -> p g n", p=P)),
                                 (scales[:, 0, :], d["L2_ffn_q_scale"][layer].partition_broadcast(P)),
                                 (scales[:, 1, :], d["L2_ffn_k_scale"][layer].partition_broadcast(P))):
                    sp.dma_start(dst, src).then_inc(m.loaded.sem, 16)
                sp.wait_ge(*m.loaded.after(64))

            @block.gpsimd
            def _(pool):
                zeros = [hT[:, B * S:], o[1][:]] + [t[:] for t in q]
                for t in zeros:
                    pool.memset(t, 0.0).then_inc(m.zeroed.sem, 1)
                pool.memset(sums[:, 1], 1.0).then_inc(m.zeroed.sem, 1)
                pool.wait_ge(*m.ready_made.after(6))
                pool.sem_inc(m.passed.sem, 1)

                def rotate(b, at):
                    for j in range(TPB):
                        for w in range(2):
                            pool.wait_ge(*ring.empty(*at(QK + 2 * j + w)))
                            for hf in range(2):
                                to, of = slice(32 * hf, 32 * hf + 32), slice(32 - 32 * hf, 64 - 32 * hf)
                                pool.tensor_tensor(other[:, j, w, :, to], qk[:, j, w, :, of],
                                                   tb[:, w, j, to].unsqueeze(1).to_broadcast([P, NH, 32]), ALU.mult)\
                                    .then_inc(m.rotated.sem, 1)
                    pool.wait_ge(*m.squares_ready.after(b + 1))
                    pool.tensor_tensor(rn[:], ssc[:], k["minus_half"][:, 0:TPB * 2 * NH], ALU.pow).then_inc(m.powers_ready.sem, 1)

                for b in range(2):
                    rotate(b, lambda f: prepared(b, f))
                with pool.Fori(0, PAIRS) as i:
                    for u in range(2):
                        rotate(2 * i + u + 2, lambda f: turn(i, u, f))

            @block.vector
            def _(dve):
                shift_tokens(m, None, dve, None, ring, first, hb)
                dve.wait_ge(*m.loaded.after(64))
                for w, (a, bb) in enumerate((("rot_qa", "rot_qb"), ("rot_ka", "rot_kb"))):
                    sc = lambda lo, n: scales[:, w, lo:lo + n].unsqueeze(1).to_broadcast([P, TPB, n])
                    fa = k[a].rearrange("p (t e) -> p t e", e=HD)
                    fb = k[bb].rearrange("p (t e) -> p t e", e=HD)
                    dve.tensor_tensor(ta[:, w], fa, sc(0, HD), ALU.mult).then_inc(m.ready_made.sem, 1)
                    dve.tensor_tensor(tb[:, w, :, 0:32], fb[:, :, 0:32], sc(32, 32), ALU.mult).then_inc(m.ready_made.sem, 1)
                    dve.tensor_tensor(tb[:, w, :, 32:64], fb[:, :, 32:64], sc(0, 32), ALU.mult).then_inc(m.ready_made.sem, 1)
                dve.wait_ge(*m.ready_made.after(6))
                dve.wait_ge(*m.zeroed.after(5))
                dve.sem_inc(m.passed.sem, 1)

                def sum_squares(b, j):
                    dve.wait_ge(*m.h_squared.after(TPB * b + j + 1))
                    dve.tensor_reduce(ss[:, j, :], sq[:, j].rearrange("p (h e) -> p h e", e=HD), AX.X, ALU.add)\
                        .then_inc(m.step.sem, 1)
                    if j == TPB - 1:
                        dve.wait_ge(*m.step.after(CHAIN * b + 2 * TPB - 1))
                        dve.tensor_scalar(ssc[:], ss[:].rearrange("p t h -> p (t h)"), 1e-24, None, ALU.max)\
                            .then_inc(m.squares_ready.sem, 1)

                def own_part(b, j, at):
                    for w in range(2):
                        dve.wait_ge(*ring.empty(*at(QK + 2 * j + w)))
                    dve.tensor_tensor(own[:, j], qk[:, j], ta[:, :, j, :].unsqueeze(2).to_broadcast([P, 2, NH, HD]), ALU.mult)\
                        .then_inc(m.step.sem, 1)

                def add_parts(b):
                    dve.wait_ge(*m.step.after(CHAIN * b + 2 * TPB))
                    for j in range(TPB):
                        dve.wait_ge(*m.rotated.after(4 * TPB * b + 4 * (j + 1)))
                        flat = lambda t: t[:, j].rearrange("p w h e -> p (w h e)")
                        dve.tensor_tensor(flat(own), flat(own), flat(other), ALU.add).then_inc(m.step.sem, 1)

                def normalise(b):
                    dve.wait_ge(*m.step.after(CHAIN * b + 3 * TPB))
                    dve.wait_ge(*m.powers_ready.after(b + 1))
                    for j in range(TPB):
                        heads = own[:, j].rearrange("p w h e -> p (w h) e")
                        dve.tensor_tensor(heads, heads, rn[:, j * 2 * NH:(j + 1) * 2 * NH].unsqueeze(2).to_broadcast([P, 2 * NH, HD]),
                                          ALU.mult).then_inc(m.normed.sem, 1)

                def drain(i, u, f, at):
                    if TURN <= f < V and (f - TURN) % 2:
                        j = (f - TURN) // 2
                        dve.wait_ge(*ring.full(*at))
                        dve.tensor_copy(kT[1 - u][:, :, j * P:(j + 1) * P], ring.bank(*at[1:])[:].rearrange("p (g t) -> p g t", t=P))\
                            .then_inc(ring.drains(*at[1:]), 1)
                    if V <= f < SUMS:
                        dve.wait_ge(*ring.full(*at))
                        dve.tensor_copy(v[1 - u][:, f - V, :], ring.bank(*at[1:])[:]).then_inc(ring.drains(*at[1:]), 1)
                    if SPREAD <= f < OUT:
                        if f == SPREAD:
                            dve.wait_ge(*ring.empty(*turn(*last_turn(i, u), PER - 1)))
                        dve.wait_ge(*ring.full(*at))
                        g = 2 * (f - SPREAD)
                        og = o[1 - u][:, g:g + 2, :].rearrange("p g t -> p (g t)")
                        dve.tensor_tensor(og, ring.bank(*at[1:])[:], og, ALU.mult).then_inc(ring.drains(*at[1:]), 1)
                    if f == OUT:
                        dve.wait_ge(*ring.full(*at))
                        rows = m.y_padded[:, bass.ds(TPB * (2 * i + u), TPB), :]
                        dve.tensor_tensor(rows, ring.bank(*at[1:])[:, 0:TPB * D].rearrange("p (t d) -> p t d", d=D), rows, ALU.add)\
                            .then_inc(ring.drains(*at[1:]), 1)

                def invert_sums(b, u):
                    dve.wait_ge(*m.probs_ready.after(TPB * NH * b))
                    dve.reciprocal(inv[:], sums[:, 1 - u].rearrange("p t h -> p (t h)")).then_inc(m.sums_inverted.sem, 1)

                for b in range(2):
                    at = lambda f: prepared(b, f)
                    for j in range(TPB):
                        sum_squares(b, j)
                        own_part(b, j, at)
                    add_parts(b)
                    normalise(b)
                    if b == 0:
                        for f in range(TURN, SUMS):
                            drain(-1, 1, f, prepared(0, f))
                with dve.Fori(0, PAIRS) as i:
                    for u in range(2):
                        b = 2 * i + u
                        at = lambda f: turn(i, u, f)
                        invert_sums(b, u)
                        for n in range(NH + DEEP):
                            c = n - DEEP
                            if c >= 0:
                                if c % 2 == 0:
                                    dve.wait_ge(*ring.full(*group_before(i, u, c // 2)))
                                dve.wait_ge(*m.turned.after(NH * b + c + 1))
                                dve.tensor_copy(pT[c // 2 % 2][:, c % 2].rearrange("p c t -> p (c t)"), t_ps[c % 2][:, 0:BAND])\
                                    .then_inc(m.turned_copied.sem, 1)
                            if n < NH:
                                dve.wait_ge(*m.scores_ready.after(NH * b + n + 1))
                                for j, cols in enumerate(TILES):
                                    dve.tensor_reduce(nmax[:, u, TPB * n + j:TPB * n + j + 1], s_ps[n % DEEP][:, cols], AX.X, ALU.max,
                                                      negate=True).then_inc(m.max_ready.sem, 1)
                            if c >= 0:
                                for f in due[c]:
                                    drain(i, u, f, turn(i, u, f))
                            if n == 4:
                                sum_squares(b + 2, 0)
                            if n == 5:
                                own_part(b + 2, 0, at)
                            if n == 6:
                                sum_squares(b + 2, 1)
                            if n == 7:
                                own_part(b + 2, 1, at)
                            if n == NH:
                                add_parts(b + 2)
                        normalise(b + 2)
                invert_sums(B, 0)
                for n, f in enumerate(range(SUMS, GROUP)):
                    drain(PAIRS, 0, f, (PAIRS, 0, n))

            @block.scalar
            def _(act):
                shift_tokens(m, None, None, act, ring, first, hb)

                def square(b, j, at):
                    for w in range(2):
                        act.wait_ge(*ring.empty(*at(QK + 2 * j + w)))
                    act.activation(sq[:, j], qk[:, j].rearrange("p w h e -> p (w h e)"), ACT.Square).then_inc(m.h_squared.sem, 1)

                def drain(i, u, f, at):
                    if QK <= f < TURN:
                        j, w = divmod(f - QK, 2)
                        act.wait_ge(*ring.full(*at))
                        act.activation(qk[:, j, w].rearrange("p h e -> p (h e)"), ring.bank(*at[1:])[:], ACT.Copy)\
                            .then_inc(ring.drains(*at[1:]), 1)
                    if TURN <= f < V and (f - TURN) % 2 == 0:
                        cols = slice((f - TURN) // 2 * P, ((f - TURN) // 2 + 1) * P)
                        act.wait_ge(*ring.full(*at))
                        bank = ring.bank(*at[1:])[:].rearrange("p (g t) -> p g t", t=P)
                        act.activation(q[1 - u][0:HD, 0:NH:2, cols], bank[0:HD], ACT.Copy)
                        act.activation(q[1 - u][HD:P, 1:NH:2, cols], bank[HD:P], ACT.Copy).then_inc(ring.drains(*at[1:]), 1)
                    if f == SUMS:
                        act.wait_ge(*ring.full(*at))
                        act.activation(invT[:], ring.bank(*at[1:])[0:NH, 0:S], ACT.Copy).then_inc(ring.drains(*at[1:]), 1)
                    if f >= GROUP:
                        act.wait_ge(*ring.full(*at))
                        act.activation(o[u][:, f - GROUP, :], ring.bank(*at[1:])[:, 0:S], ACT.Copy).then_inc(ring.drains(*at[1:]), 1)

                for f in range(TURNS):
                    at = first(SHIFTS + f)
                    act.wait_ge(*ring.full(*at))
                    act.activation(hT[:, f * 512:(f + 1) * 512], ring.bank(*at[1:])[:], ACT.Copy).then_inc(ring.drains(*at[1:]), 1)
                act.wait_ge(*m.zeroed.after(5))
                for f in range(TURNS):
                    act.wait_ge(*ring.empty(*first(SHIFTS + f)))
                for b in (1, 2):
                    act.activation(hs[b % 2][:], hT[:, b * S:(b + 1) * S], ACT.Copy).then_inc(m.h_moved.sem, 1)
                for b, f in AHEAD_OF_LOOP:
                    drain(-1, 1, f, prepared(b, f))
                    if f in (QK + 1, QK + 3):
                        square(b, (f - QK) // 2, lambda f: prepared(b, f))
                with act.Fori(0, PAIRS) as i:
                    for u in range(2):
                        b = 2 * i + u
                        for n in range(NH + DEEP):
                            if n < NH:
                                act.wait_ge(*m.max_ready.after(TPB * (NH * b + n + 1)))
                                for j, cols in enumerate(TILES):
                                    act.activation(probs[n % DEEP][:, cols], s_ps[n % DEEP][:, cols], ACT.Exp,
                                                   bias=nmax[:, u, TPB * n + j:TPB * n + j + 1],
                                                   accum_out=sums[:, u, j, n:n + 1]).then_inc(m.probs_ready.sem, 1)
                            if n >= DEEP:
                                for f in due[n - DEEP]:
                                    drain(i, u, f, turn(i, u, f))
                            if n in (3, 5):
                                square(b + 2, (n - 3) // 2, lambda f: turn(i, u, f))
                        for f in due[NH]:
                            drain(i, u, f, turn(i, u, f))
                        act.wait_ge(*ring.full(*turn(i, u, V + TPB - 1)))
                        act.sem_inc(m.passed.sem, 1)
                        act.activation(hs[1 - u][:], hT[:, bass.ds((b + 3) * S, S)], ACT.Copy).then_inc(m.h_moved.sem, 1)
                for n, f in enumerate(range(SUMS, GROUP)):
                    drain(PAIRS, 0, f, (PAIRS, 0, n))

            @block.tensor
            def _(pe):
                shift_tokens(m, pe, None, None, ring, first, hb)
                pe.wait_ge(*m.unshifted.after(1))
                for f in range(SHIFTS):
                    pe.wait_ge(*ring.empty(*first(f)))
                for f in range(TURNS):
                    at = first(SHIFTS + f)
                    pe.wait_ge(*ring.free(*at))
                    for j in range(4):
                        ins = pe.transpose(ring.bank(*at[1:])[:, j * P:(j + 1) * P], hb[:, 4 * f + j, :], k["ident"])
                    ins.then_inc(ring.fills(*at[1:]), 1)
                pe.wait_ge(*m.loaded.after(64))
                for f in range(TURNS):
                    pe.wait_ge(*ring.empty(*first(SHIFTS + f)))
                pe.wait_ge(*m.zeroed.after(5))

                def fill(i, u, f, at, ahead=None):
                    b = 2 * i + u
                    bank = ring.bank(*at[1:])
                    if f < TURN:
                        j, w = divmod(f - QK, 2)
                        if ahead is None and f == QK:
                            pe.wait_ge(*m.h_moved.after(b + 2))
                        pe.wait_ge(*ring.free(*at))
                        tokens = hs[u][:, j * P:(j + 1) * P] if ahead is None else hT[:, (TPB * ahead + j) * P:(TPB * ahead + j + 1) * P]
                        ins = pe.matmul(bank[:], tokens, wqkv[:, w * INNER:(w + 1) * INNER], start=True, stop=True)
                    elif f < V:
                        j, w = divmod(f - TURN, 2)
                        if f == TURN:
                            pe.wait_ge(*m.normed.after(TPB * (b + 2)))
                        pe.wait_ge(*ring.free(*at))
                        for g in range(NG):
                            ins = pe.transpose(bank[:, g * P:(g + 1) * P], own[:, j, w, 2 * g:2 * g + 2, :].rearrange("p h e -> p (h e)"),
                                               k["ident"])
                    elif f < SUMS:
                        j = f - V
                        pe.wait_ge(*ring.free(*at))
                        tokens = hs[1 - u][:, j * P:(j + 1) * P] if ahead is None else hT[:, (TPB * ahead + j) * P:(TPB * ahead + j + 1) * P]
                        ins = pe.matmul(bank[:], tokens, wqkv[:, 2 * INNER:], start=True, stop=True)
                    elif f == SUMS:
                        pe.wait_ge(*m.sums_inverted.after(b + 1))
                        pe.wait_ge(*ring.free(*at))
                        for j in range(TPB):
                            ins = pe.transpose(bank[0:NH, j * P:(j + 1) * P], inv[:, j * NH:(j + 1) * NH], k["ident"])
                    elif f < OUT:
                        if f == SPREAD:
                            pe.wait_ge(*(ring.empty(*turn(i, u, SUMS)) if i is not PAIRS else ring.empty(PAIRS, 0, 0)))
                        pe.wait_ge(*ring.free(*at))
                        for t in range(2):
                            g = 2 * (f - SPREAD) + t
                            ins = pe.matmul(bank[:, t * S:(t + 1) * S], k["spread2"][0:NH, g * P:(g + 1) * P], invT[:], start=True, stop=True)
                    elif f == OUT:
                        pe.wait_ge(*ring.free(*at))
                        pe.wait_ge(*(ring.empty(*turn(i, u, OUT - 1)) if i is not PAIRS else ring.empty(PAIRS, 0, OUT - 1 - SUMS)))
                        for j in range(TPB):
                            for g in range(NG):
                                ins = pe.matmul(bank[:, j * D:(j + 1) * D], o[1 - u][:, g, j * P:(j + 1) * P], wo[:, g, :], start=(g == 0),
                                                stop=(g == NG - 1))
                    else:
                        g = f - GROUP
                        pe.wait_ge(*m.turned_copied.after(NH * b + 2 * (g + 1)))
                        pe.wait_ge(*ring.free(*at))
                        for c in range(TPB):
                            for hh in range(2):
                                rows = slice(HD * hh, HD * (hh + 1))
                                vc = v[u][:, c, (2 * g + hh) * HD:(2 * g + hh + 1) * HD]
                                if c == 0:
                                    ins = pe.matmul(bank[rows, 0:S], vc, pT[g % 2][:, hh, 0:2, :].rearrange("p c t -> p (c t)"),
                                                    start=True, stop=False)
                                else:
                                    ins = pe.matmul(bank[rows, P:S], vc, pT[g % 2][:, hh, 2, :], start=False, stop=True)
                    ins.then_inc(ring.fills(*at[1:]), 1)

                def scores(b, u, n):
                    out = s_ps[n % DEEP]
                    pe.matmul(out[:, 0:BAND], k["ident_bf"], k["band_bf"], start=True, stop=False)
                    pe.matmul(out[:, 0:P], q[u][:, n, 0:P], kT[u][:, n // 2, 0:P], start=False, stop=False)
                    pe.matmul(out[:, P:BAND], q[u][:, n, P:S], kT[u][:, n // 2, :], start=False, stop=True)\
                        .then_inc(m.scores_ready.sem, 1)

                for b, f in AHEAD_OF_LOOP:
                    fill(-1, 1, f, prepared(b, f), ahead=b)
                for f in range(TURN, SUMS):
                    pe.wait_ge(*ring.empty(*prepared(0, f)))
                for n in range(DEEP):
                    scores(0, 0, n)
                with pe.Fori(0, PAIRS) as i:
                    for u in range(2):
                        b = 2 * i + u
                        for n in range(NH):
                            pe.wait_ge(*m.probs_ready.after(TPB * (NH * b + n + 1)))
                            pe.wait_ge(*m.turned_copied.after(NH * b + n - 1))
                            for c in range(3):
                                ins = pe.transpose(t_ps[n % 2][:, c * P:(c + 1) * P], probs[n % DEEP][:, c * P:(c + 1) * P], k["ident"])
                            ins.then_inc(m.turned.sem, 1)
                            if n + DEEP < NH:
                                scores(b, u, n + DEEP)
                            else:
                                if n + DEEP == NH:
                                    for f in range(TURN, V):
                                        pe.wait_ge(*ring.empty(*turn(i, u, f)))
                                scores(b + 1, 1 - u, n + DEEP - NH)
                            for f in due[n]:
                                fill(i, u, f, turn(i, u, f))
                        for f in range(V, SUMS):
                            pe.wait_ge(*ring.empty(*turn(i, u, f)))
                        for f in due[NH]:
                            fill(i, u, f, turn(i, u, f))
                for n, f in enumerate(range(SUMS, GROUP)):
                    fill(PAIRS, 0, f, (PAIRS, 0, n))
        ring.close(GROUP - SUMS)
        for s, n in ((m.loaded, 64), (m.ready_made, 6), (m.step, CHAIN * (B + 2)), (m.unshifted, 1), (m.zeroed, 5), (m.h_moved, B + 2),
                     (m.h_squared, TPB * (B + 2)), (m.rotated, 4 * TPB * (B + 2)), (m.squares_ready, B + 2), (m.powers_ready, B + 2),
                     (m.normed, TPB * (B + 2)), (m.scores_ready, NH * B + DEEP), (m.max_ready, TPB * NH * B),
                     (m.probs_ready, TPB * NH * B), (m.turned, NH * B), (m.turned_copied, NH * B), (m.sums_inverted, B + 1)):
            s.before += n


def gelu_ffn(m, layer):
    nc, d, x, k = m.nc, m.dram, m.x, m.consts
    HID = int(D * 4 * 2 / 3)
    ROWS = [min(P, HID - c * P) for c in range(-(-HID // P))]
    NC = len(ROWS)
    T, BT = B * S, 512
    NB, TB = T // BT, BT // P
    with ExitStack() as ctx:
        sb = lambda name, shape, dt=F32: sbuf(m, ctx, f"{name}_l2f{layer}", shape, dt)
        norm = Norm(m, ctx, NT, f"l2f{layer}", buffers=1)
        w1 = sb("w1", [P, 2 * HID])
        b1 = sb("b1", [P, 2, NC])
        w2 = sb("w2", [P, NC, D])
        b2 = sb("b2", [P, 1])
        yT = [sb(f"yT{u}", [P, BT]) for u in range(2)]
        lg, lb = sb("lg", [P, 1]), sb("lb", [P, 1])
        hb = sb("hb", [P, NT, D])
        hT = sb("hT", [P, T])
        gate = sb("gate", [P, NC, BT])
        prod = sb("prod", [P, NC, T])
        NLOAD = 4 + 3 * NC
        SHIFTS, TURNS = 2, NT // 4
        ring = Ring([psum(m, ctx, f"ring{n}_l2f{layer}", [P, BT]) for n in range(2 * NC)], m.filled, m.drained, NC,
                    lead=SHIFTS + TURNS)
        y_ps = [psum(m, ctx, f"y_ps{u}_l2f{layer}", [P, BT]) for u in range(2)]
        yT_ps = ring.banks[0:2]
        first = lambda f: (0, 0, f - ring.lead)
        assert PAIRS == NB

        with nc.Block() as block:
            @block.sync
            def _(sp):
                loads = [(w1[:], d["L2_ffn_w1"][layer]), (b2[:], d["L2_ffn_b2"][layer].rearrange("(p o) -> p o", o=1)),
                         (lg[:], d["L2_ffn_ln_g"][layer].rearrange("(p o) -> p o", o=1)),
                         (lb[:], d["L2_ffn_ln_b"][layer].rearrange("(p o) -> p o", o=1))]
                for c, r in enumerate(ROWS):
                    loads.append((w2[0:r, c, :], d["L2_ffn_w2"][layer, c * P:c * P + r, :]))
                    for w in range(2):
                        lo = w * HID + c * P
                        loads.append((b1[0:r, w, c:c + 1], d["L2_ffn_b1"][layer, lo:lo + r].rearrange("(p o) -> p o", o=1)))
                assert len(loads) == NLOAD
                for dst, src in loads:
                    sp.dma_start(dst, src).then_inc(m.loaded.sem, 16)
                sp.wait_ge(*m.loaded.after(16 * NLOAD))

            @block.gpsimd
            def _(pool):
                norm.pool(pool, 0)

            @block.vector
            def _(dve):
                shift_tokens(m, None, dve, None, ring, first, hb)
                for w in range(SHIFTS):
                    dve.wait_ge(*ring.empty(*first(w)))
                dve.wait_ge(*m.unshifted.after(1))
                norm.vector(dve, 0, 0, lambda j: hb[:, j, :])
                dve.wait_ge(*m.loaded.after(16 * NLOAD))
                with dve.Fori(0, NB) as i:
                    for c, r in enumerate(ROWS):
                        dve.wait_ge(*ring.empty(i, 0, 2 * c))
                        dve.wait_ge(*ring.full(i, 0, 2 * c + 1))
                        dve.scalar_tensor_tensor(out=prod[0:r, c, bass.ds(i * BT, BT)], in0=ring.bank(0, 2 * c + 1)[0:r, :],
                                                 scalar=b1[0:r, 0, c:c + 1], in1=gate[0:r, c, :], op0=ALU.add, op1=ALU.mult)\
                            .then_inc(ring.drains(0, 2 * c + 1), 1)
                with dve.Fori(0, NB // 2) as i:
                    for u in range(2):
                        n = 2 * i + u
                        dve.wait_ge(*m.turned.after(n + 1))
                        tiles = x[:, bass.ds(TB * n, TB), :]
                        dve.tensor_tensor(tiles, y_ps[u][:].rearrange("p (t d) -> p t d", d=D), tiles, ALU.add)\
                            .then_inc(m.x_updated.sem, 1)
                dve.wait_ge(*m.x_updated.after(NB))

            @block.scalar
            def _(act):
                shift_tokens(m, None, None, act, ring, first, hb)
                act.wait_ge(*m.loaded.after(16 * NLOAD))
                for f in range(TURNS):
                    at = first(SHIFTS + f)
                    act.wait_ge(*ring.full(*at))
                    act.activation(hT[:, f * BT:(f + 1) * BT], ring.bank(*at[1:])[:], ACT.Identity, bias=lb[:, 0:1],
                                   scale=lg[:, 0:1]).then_inc(ring.drains(*at[1:]), 1)
                with act.Fori(0, NB) as i:
                    for c, r in enumerate(ROWS):
                        act.wait_ge(*ring.free(i, 0, 2 * c + 1))
                        act.wait_ge(*ring.full(i, 0, 2 * c))
                        act.activation(gate[0:r, c, :], ring.bank(0, 2 * c)[0:r, :], ACT.Gelu, bias=b1[0:r, 1, c:c + 1])\
                            .then_inc(ring.drains(0, 2 * c), 1)
                with act.Fori(0, NB // 2) as i:
                    for u in range(2):
                        act.wait_ge(*m.pv_done.after(2 * i + u + 1))
                        act.activation(yT[u][:], yT_ps[u][:], ACT.Identity, bias=b2[:, 0:1]).then_inc(m.pv_copied.sem, 1)

            @block.tensor
            def _(pe):
                shift_tokens(m, pe, None, None, ring, first, hb)
                for f in range(TURNS):
                    at = first(SHIFTS + f)
                    pe.wait_ge(*m.normed.after(4 * f + 4))
                    pe.wait_ge(*ring.free(*at))
                    for j in range(4):
                        ins = pe.transpose(ring.bank(*at[1:])[:, j * P:(j + 1) * P], norm.xn[0][:, 4 * f + j, :], k["ident"])
                    ins.then_inc(ring.fills(*at[1:]), 1)
                pe.wait_ge(*m.loaded.after(16 * NLOAD))
                for f in range(TURNS):
                    pe.wait_ge(*ring.empty(*first(SHIFTS + f)))
                with pe.Fori(0, NB) as i:
                    for c, r in enumerate(ROWS):
                        for w, lo in ((0, HID), (1, 0)):
                            pe.wait_ge(*ring.free(i, 0, 2 * c + w))
                            pe.matmul(ring.bank(0, 2 * c + w)[0:r, :], w1[:, lo + c * P:lo + c * P + r], hT[:, bass.ds(i * BT, BT)],
                                      start=True, stop=True).then_inc(ring.fills(0, 2 * c + w), 1)
                for f in range(2 * NC):
                    pe.wait_ge(*ring.empty(NB - 1, 0, f))
                with pe.Fori(0, NB // 2) as i:
                    for u in range(2):
                        for c, r in enumerate(ROWS):
                            ins = pe.matmul(yT_ps[u][:], w2[0:r, c, :], prod[0:r, c, bass.ds((2 * i + u) * BT, BT)], start=(c == 0),
                                            stop=(c == NC - 1))
                        ins.then_inc(m.pv_done.sem, 1)
                    for u in range(2):
                        pe.wait_ge(*m.pv_copied.after(2 * i + u + 1))
                        pe.wait_ge(*m.x_updated.after(2 * i))
                        for t in range(TB):
                            ins = pe.transpose(y_ps[u][:, t * D:(t + 1) * D], yT[u][:, t * P:(t + 1) * P], k["ident"])
                        ins.then_inc(m.turned.sem, 1)
        norm.close(1)
        ring.close()
        for s, n in ((m.loaded, 16 * NLOAD), (m.unshifted, 1), (m.pv_done, NB), (m.pv_copied, NB), (m.turned, NB), (m.x_updated, NB)):
            s.before += n


def l2_local_transformer(m):
    nc, x = m.nc, m.x
    with ExitStack() as ctx:
        norm = Norm(m, ctx, NT, "l2t", buffers=1, dummies=TPB)
        y, m.y_padded = norm.xn[0], norm.padded[0]
        with nc.Block() as block:
            @block.gpsimd
            def _(pool):
                norm.pool(pool, 0)

            @block.vector
            def _(dve):
                norm.vector(dve, 0, 0, lambda j: x[:, j, :])
                dve.memset(m.y_padded[:, 0:TPB, :], 0.0).then_inc(m.zeroed.sem, 1)
                dve.wait_ge(*m.normed.after(NT))
                dve.wait_ge(*m.zeroed.after(1))
        m.zeroed.before += 1
        norm.close(1)
        m.x = y
        for layer in range(2):
            local_attention(m, layer)
            gelu_ffn(m, layer)
        m.x = x
        with nc.Block() as block:
            @block.vector
            def _(dve):
                dve.tensor_tensor(x, x, y, ALU.add).then_inc(m.step.sem, 1)
                dve.wait_ge(*m.step.after(1))
        m.step.before += 1

def l3_quantised_ffn(m):
    nc, d, x, k = m.nc, m.dram, m.x, m.consts
    I = 352
    ROWS = [min(P, I - c * P) for c in range(-(-I // P))]
    NC, LAST = len(ROWS), ROWS[-1]
    QMAX = 127.0
    T = B * S
    BT = 512
    NB, TB = T // BT, BT // P
    with ExitStack() as ctx:
        sb = lambda name, shape, dt=F32: sbuf(m, ctx, f"{name}_l3f", shape, dt)
        norm = Norm(m, ctx, NT, "l3f", buffers=1)
        xn = norm.xn[0]
        w, wd = sb("w", [P, 2, NC, D]), sb("wd", [P, I])
        wq, wdq = sb("wq", [P, 2, NC, D], BF16), sb("wdq", [P, I], BF16)
        wT, wdT = sb("wT", [P, 2, I], BF16), sb("wdT", [P, NC, D], BF16)
        wscale, dscale = sb("wscale", [P, 2, NC]), sb("dscale", [P, 1])
        winv, dinv, inv = sb("winv", [P, 2, NC]), sb("dinv", [P, 1]), sb("inv", [P, 2])
        clips, sig = sb("clips", [P, 2]), sb("sig", [P, 2])
        diag, dB = sb("diag", [P, P]), sb("dB", [P, D])
        top, peak, scale = sb("top", [P, 2]), sb("peak", [1, 2]), sb("scale", [P, 2])
        hscale = sb("hscale", [P, 2, NC])
        xq, xqT = sb("xq", [P, NT, D], BF16), sb("xqT", [P, T], BF16)
        gate = [sb(f"gate{c}", [P, BT]) for c in range(NC)]
        hT, hq = sb("hT", [P, NC, T]), sb("hq", [P, NC, T], BF16)
        part = [sb(f"part{u}", [P, TB, D]) for u in range(2)]
        g_ps = [psum(m, ctx, f"g_ps{c}_l3f", [P, BT]) for c in range(NC)]
        u_ps = [psum(m, ctx, f"u_ps{c}_l3f", [P, BT]) for c in range(NC)]
        y_ps = [psum(m, ctx, f"y_ps{u}_l3f", [P, BT]) for u in range(2)]
        w_bank, wd_bank, d_bank, x_banks, max_banks = g_ps[0], g_ps[1], g_ps[2], u_ps[0:2], (u_ps[2], y_ps[0])

        with nc.Block() as block:
            @block.sync
            def _(sp):
                loads = [(wd[:], d["L3_ffn_w_down"]), (clips[:, 0:1], d["L3_ffn_clip_x"][0, :].partition_broadcast(P)),
                         (clips[:, 1:2], d["L3_ffn_clip_down"][0, :].partition_broadcast(P))]
                for n, name in enumerate(("L3_ffn_w_gate", "L3_ffn_w_up")):
                    for c, r in enumerate(ROWS):
                        loads.append((w[0:r, n, c, :], d[name][c * P:c * P + r, :]))
                assert len(loads) == 3 + 2 * NC
                for dst, src in loads:
                    sp.dma_start(dst, src).then_inc(m.loaded.sem, 16)
                sp.wait_ge(*m.loaded.after(16 * len(loads)))

            @block.gpsimd
            def _(pool):
                norm.pool(pool, 0)

            @block.vector
            def _(dve):
                rows = lambda n, c: w[0:ROWS[c], n, c, :]
                dve.memset(wscale[:], 1.0).then_inc(m.step.sem, 1)
                dve.memset(hT[LAST:P, NC - 1, :], 0.0).then_inc(m.step.sem, 1)
                dve.wait_ge(*m.loaded.after(16 * (3 + 2 * NC)))
                dve.wait_ge(*m.step.after(2))
                dve.tensor_reduce(wscale[:, :, 0:NC - 1], w[:, :, 0:NC - 1, :], AX.X, ALU.max, apply_absolute_value=True)\
                    .then_inc(m.step.sem, 1)
                dve.tensor_reduce(wscale[0:LAST, :, NC - 1], w[0:LAST, :, NC - 1, :], AX.X, ALU.max, apply_absolute_value=True)\
                    .then_inc(m.step.sem, 1)
                dve.tensor_reduce(dscale[:], wd[:], AX.X, ALU.max, apply_absolute_value=True).then_inc(m.step.sem, 1)
                dve.wait_ge(*m.step.after(5))
                dve.tensor_scalar(wscale[:], wscale[:], 1.0 / QMAX, None, ALU.mult).then_inc(m.step.sem, 1)
                dve.tensor_scalar(dscale[:], dscale[:], 1.0 / QMAX, None, ALU.mult).then_inc(m.step.sem, 1)
                dve.wait_ge(*m.step.after(7))
                dve.reciprocal(winv[:], wscale[:]).then_inc(m.step.sem, 1)
                dve.reciprocal(dinv[:], dscale[:]).then_inc(m.step.sem, 1)
                dve.wait_ge(*m.step.after(9))
                for n in range(2):
                    for c, r in enumerate(ROWS):
                        dve.tensor_scalar(rows(n, c), rows(n, c), winv[0:r, n, c:c + 1], MAGIC, ALU.mult, ALU.add)\
                            .then_inc(m.step.sem, 1)
                dve.tensor_scalar(wd[:], wd[:], dinv[:], MAGIC, ALU.mult, ALU.add).then_inc(m.step.sem, 1)
                dve.wait_ge(*m.step.after(10 + 2 * NC))
                for n in range(2):
                    for c, r in enumerate(ROWS):
                        dve.tensor_scalar(wq[0:r, n, c, :], rows(n, c), MAGIC, QMAX, ALU.subtract, ALU.min)\
                            .then_inc(m.ready_made.sem, 1)
                dve.tensor_scalar(wdq[:], wd[:], MAGIC, QMAX, ALU.subtract, ALU.min).then_inc(m.ready_made.sem, 1)
                dve.tensor_scalar(diag[:], k["ident"], dscale[:], None, ALU.mult).then_inc(m.ready_made.sem, 1)

                def find_scale(n, src, waited):
                    dve.tensor_reduce(top[:, n:n + 1], src, AX.X, ALU.max, apply_absolute_value=True).then_inc(m.row_max.sem, 1)
                    dve.wait_ge(*m.max_turned.after(n + 1))
                    dve.tensor_reduce(peak[0:1, n:n + 1], max_banks[n][0:1, 0:P], AX.X, ALU.max).then_inc(m.max_found.sem, 1)
                    dve.wait_ge(*m.max_spread.after(n + 1))
                    dve.wait_ge(*m.act_step.after(1))
                    dve.tensor_scalar(scale[:, n:n + 1], max_banks[n][:, P:P + 1], sig[:, n:n + 1], 1.0 / QMAX, ALU.mult, ALU.mult)\
                        .then_inc(m.step.sem, 1)
                    dve.wait_ge(*m.step.after(waited))
                    dve.reciprocal(inv[:, n:n + 1], scale[:, n:n + 1]).then_inc(m.step.sem, 1)
                    dve.wait_ge(*m.step.after(waited + 1))

                at = 10 + 2 * NC
                norm.vector(dve, 0, 0, lambda j: x[:, j, :])
                dve.wait_ge(*m.normed.after(NT))
                flat = xn[:].rearrange("p t d -> p (t d)")
                find_scale(0, flat, at + 1)
                dve.tensor_scalar(hscale[:], wscale[:], scale[:, 0:1], None, ALU.mult).then_inc(m.scales_ready.sem, 1)
                dve.tensor_scalar(flat, flat, inv[:, 0:1], -QMAX - 1, ALU.mult, ALU.max).then_inc(m.step.sem, 1)
                dve.wait_ge(*m.step.after(at + 3))
                dve.tensor_scalar(flat, flat, QMAX, MAGIC, ALU.min, ALU.add).then_inc(m.step.sem, 1)
                dve.wait_ge(*m.step.after(at + 4))
                dve.tensor_scalar(xq[:].rearrange("p t d -> p (t d)"), flat, MAGIC, None, ALU.subtract).then_inc(m.x_quantised.sem, 1)

                dve.wait_ge(*m.scales_ready.after(1))
                with dve.Fori(0, NB) as n:
                    for c, r in enumerate(ROWS):
                        dve.wait_ge(*m.gate_ready.after(NC * n + c + 1))
                        dve.scalar_tensor_tensor(out=hT[0:r, c, bass.ds(n * BT, BT)], in0=u_ps[c][0:r, :],
                                                 scalar=hscale[0:r, 1, c:c + 1], in1=gate[c][0:r, :], op0=ALU.mult, op1=ALU.mult)\
                            .then_inc(m.hidden_ready.sem, 1)
                dve.wait_ge(*m.hidden_ready.after(NC * NB))
                find_scale(1, hT[:].rearrange("p c t -> p (c t)"), at + 5)
                dve.tensor_scalar(dB[:], d_bank[:, 0:D], scale[:, 1:2], None, ALU.mult).then_inc(m.step.sem, 1)
                with dve.Fori(0, NB) as n:
                    h = hT[:, :, bass.ds(n * BT, BT)]
                    dve.tensor_scalar(h, h, inv[:, 1:2], -QMAX - 1, ALU.mult, ALU.max).then_inc(m.hidden_clipped.sem, 1)
                    dve.wait_ge(*m.hidden_clipped.after(n + 1))
                    dve.tensor_scalar(h, h, QMAX, MAGIC, ALU.min, ALU.add).then_inc(m.hidden_rounded.sem, 1)
                dve.wait_ge(*m.step.after(at + 7))
                with dve.Fori(0, NB // 2) as i:
                    for u in range(2):
                        n = 2 * i + u
                        dve.wait_ge(*m.pv_done.after(n + 1))
                        dve.tensor_tensor(part[u][:], y_ps[u][:].rearrange("p (t d) -> p t d", d=D),
                                          dB[:].unsqueeze(1).to_broadcast([P, TB, D]), ALU.mult).then_inc(m.pv_copied.sem, 1)
                        dve.wait_ge(*m.pv_copied.after(n + 1))
                        tiles = x[:, bass.ds(TB * n, TB), :]
                        dve.tensor_tensor(tiles, tiles, part[u][:], ALU.add).then_inc(m.x_updated.sem, 1)
                dve.wait_ge(*m.x_updated.after(NB))

            @block.scalar
            def _(act):
                act.wait_ge(*m.loaded.after(16 * (3 + 2 * NC)))
                act.activation(sig[:], clips[:], ACT.Sigmoid).then_inc(m.act_step.sem, 1)
                act.wait_ge(*m.turned.after(1))
                act.activation(wT[:].rearrange("p n i -> p (n i)"), w_bank[:, 0:I].bitcast(BF16), ACT.Copy)\
                    .then_inc(m.turned_copied.sem, 1)
                act.wait_ge(*m.turned.after(2))
                low = (NC - 1) * D
                act.activation(wdT[:, 0:NC - 1, :].rearrange("p c d -> p (c d)"), wd_bank[:, 0:low // 2].bitcast(BF16), ACT.Copy)\
                    .then_inc(m.turned_copied.sem, 1)
                act.activation(wdT[0:LAST, NC - 1, :], wd_bank[0:LAST, low // 2:(low + D) // 2].bitcast(BF16), ACT.Copy)\
                    .then_inc(m.turned_copied.sem, 1)
                for n in range(2):
                    act.wait_ge(*m.x_turned.after(n + 1))
                    act.activation(xqT[:, n * T // 2:(n + 1) * T // 2], x_banks[n][:].bitcast(BF16), ACT.Copy)\
                        .then_inc(m.turned_copied.sem, 1)
                act.wait_ge(*m.scales_ready.after(1))
                with act.Fori(0, NB) as n:
                    for c, r in enumerate(ROWS):
                        act.wait_ge(*m.scores_ready.after(NC * n + c + 1))
                        act.activation(gate[c][0:r, :], g_ps[c][0:r, :], ACT.Silu, scale=hscale[0:r, 0, c:c + 1])\
                            .then_inc(m.gate_ready.sem, 1)
                with act.Fori(0, NB) as n:
                    act.wait_ge(*m.hidden_rounded.after(n + 1))
                    act.activation(hq[:, :, bass.ds(n * BT, BT)], hT[:, :, bass.ds(n * BT, BT)], ACT.Copy, bias=-MAGIC)\
                        .then_inc(m.hidden_quantised.sem, 1)

            @block.tensor
            def _(pe):
                pe.wait_ge(*m.ready_made.after(2 * NC))
                bank = w_bank[:, 0:I].bitcast(BF16)
                for n in range(2):
                    for c, r in enumerate(ROWS):
                        ins = pe.transpose(bank[:, n * I + c * P:n * I + c * P + r], wq[0:r, n, c, :], k["ident_bf"][0:r, 0:r])
                ins.then_inc(m.turned.sem, 1)
                pe.wait_ge(*m.ready_made.after(2 * NC + 1))
                bank = wd_bank[:, 0:NC * D // 2].bitcast(BF16)
                for c, r in enumerate(ROWS):
                    ins = pe.transpose(bank[0:r, c * D:(c + 1) * D], wdq[:, c * P:c * P + r], k["ident_bf"])
                ins.then_inc(m.turned.sem, 1)

                def spread_max(n):
                    pe.wait_ge(*m.row_max.after(n + 1))
                    pe.transpose(max_banks[n][0:1, 0:P], top[:, n:n + 1], k["ident"]).then_inc(m.max_turned.sem, 1)
                    pe.wait_ge(*m.max_found.after(n + 1))
                    pe.matmul(max_banks[n][:, P:P + 1], k["ones"][0:1, :], peak[0:1, n:n + 1], start=True, stop=True)\
                        .then_inc(m.max_spread.sem, 1)

                spread_max(0)
                pe.wait_ge(*m.x_quantised.after(1))
                for n in range(2):
                    bank = x_banks[n][:].bitcast(BF16)
                    for j in range(NT // 2):
                        ins = pe.transpose(bank[:, j * P:(j + 1) * P], xq[:, n * NT // 2 + j, :], k["ident_bf"])
                    ins.then_inc(m.x_turned.sem, 1)
                pe.wait_ge(*m.turned_copied.after(5))
                with pe.Fori(0, NB) as n:
                    for c, r in enumerate(ROWS):
                        if c == 0:
                            pe.wait_ge(*m.hidden_ready.after(NC * n))
                        cols = bass.ds(n * BT, BT)
                        pe.matmul(g_ps[c][0:r, :], wT[:, 0, c * P:c * P + r], xqT[:, cols], start=True, stop=True)
                        pe.matmul(u_ps[c][0:r, :], wT[:, 1, c * P:c * P + r], xqT[:, cols], start=True, stop=True)\
                            .then_inc(m.scores_ready.sem, 1)
                pe.wait_ge(*m.hidden_ready.after(NC * NB))
                pe.wait_ge(*m.ready_made.after(2 * NC + 2))
                pe.matmul(d_bank[:, 0:D], k["ones"], diag[:], start=True, stop=True)
                spread_max(1)
                with pe.Fori(0, NB // 2) as i:
                    for u in range(2):
                        n = 2 * i + u
                        pe.wait_ge(*m.hidden_quantised.after(n + 1))
                        pe.wait_ge(*m.pv_copied.after(2 * i))
                        for t in range(TB):
                            for c, r in enumerate(ROWS):
                                ins = pe.matmul(y_ps[u][:, t * D:(t + 1) * D], hq[0:r, c, bass.ds((TB * n + t) * P, P)],
                                                wdT[0:r, c, :], start=(c == 0), stop=(c == NC - 1))
                        ins.then_inc(m.pv_done.sem, 1)
        norm.close(1)
        for s, n in ((m.loaded, 16 * (3 + 2 * NC)), (m.step, 17 + 2 * NC), (m.ready_made, 2 + 2 * NC), (m.act_step, 1), (m.turned, 2),
                     (m.turned_copied, 5), (m.row_max, 2), (m.max_turned, 2), (m.max_found, 2), (m.max_spread, 2), (m.x_quantised, 1),
                     (m.x_turned, 2), (m.scales_ready, 1), (m.scores_ready, NC * NB), (m.gate_ready, NC * NB), (m.hidden_ready, NC * NB),
                     (m.hidden_clipped, NB), (m.hidden_rounded, NB), (m.hidden_quantised, NB), (m.pv_done, NB), (m.pv_copied, NB),
                     (m.x_updated, NB)):
            s.before += n


def store(m, out):
    with m.nc.Block() as block:
        @block.sync
        def _(sp):
            sp.dma_start(out.rearrange("(t p) d -> p t d", p=P), m.x).then_inc(m.loaded.sem, 16)
            sp.wait_ge(*m.loaded.after(16))
    m.loaded.before += 16


PHASES = [l0_cross_attention, l0_block_ffn, l1_cross_attention, l1_bit_ffn, l2_cross_attention,
          l2_local_transformer, l3_cross_attention, l3_quantised_ffn]
STAGE = [0, 1, 2, 3, 4, 5, 6, 7]


def program(nc, dram, out, upto=99):
    with ExitStack() as ctx:
        m = Machine(nc, ctx, dram)
        load_constants(m, ctx)
        for phase in PHASES[:upto]:
            phase(m)
        store(m, out)


def shape_constants():
    f = np.float32
    c = {}
    c["ident"] = np.eye(P, dtype=f)
    c["ones"] = np.ones((P, P), f)
    c["shift"] = np.eye(P, k=1, dtype=f)
    last = np.zeros((P, P), f)
    last[P - 1, 0] = 1
    c["last"] = last
    hd = D // HEADS
    c["head_cols"] = (np.arange(P)[:, None] // hd == np.arange(HEADS)[None, :]).astype(f) / np.sqrt(f(hd))
    for name, per in (("spread4", 4), ("spread2", 2)):
        groups = HEADS // per
        s = np.zeros((P, groups, P), f)
        for g in range(groups):
            for r in range(P):
                s[per * g + r // (P // per), g, r] = 1
        c[name] = s.reshape(P, groups * P)
    c["minus_half"] = np.full((P, 64), -0.5, f)
    half = np.arange(0, 64, 2, dtype=f)
    inv_freq = (f(1.0) / f(10000.0) ** (half / f(64))).astype(f)
    t = np.arange(S, dtype=f)
    freqs = (t[:, None] * inv_freq[None, :]).astype(f)
    freqs = np.concatenate([freqs, freqs], -1)
    base = ((half + f(0.4 * 64)) / f(1.4 * 64)).astype(f)
    power = ((t - S // 2) / f(32)).astype(f)
    scale = (base[None, :] ** power[:, None]).astype(f)
    scale = np.concatenate([scale, scale], -1)
    sign = np.concatenate([-np.ones(32, f), np.ones(32, f)])
    tables = {"rot_qa": 8 * np.cos(freqs) * scale, "rot_qb": 8 * np.sin(freqs) * scale * sign,
              "rot_ka": np.cos(freqs) / scale, "rot_kb": np.sin(freqs) / scale * sign}
    for name, v in tables.items():
        c[name] = v.astype(f).reshape(TPB, P, 64).transpose(1, 0, 2).reshape(P, TPB * 64)
    i = np.arange(P)[:, None]
    band = []
    for q0, k0, n in ((0, 0, P), (P, 0, 2 * P)):
        q, j = q0 + i, k0 + np.arange(n)[None, :]
        band.append(np.where((q < j) | (q > j + 64), -1e30, 0.0))
    c["band"] = np.concatenate(band, 1)
    return np.concatenate([c[n] for n, _ in CONSTS], 1).astype(f)


def lay_out(inputs):
    i = {n: np.asarray(v) for n, v in inputs.items()}
    a = {}
    a["x"] = i["x"].reshape(B * S, D)
    ctx = np.concatenate([i["ctx_1024"], np.zeros((AHEAD, KV, D), np.float32)]).reshape(-1, D)
    a["ctx"] = ctx
    a["ctxT"] = ctx.T
    mask = np.concatenate([i["mask_Bx1xSxS2_ik0"][:, 0], np.zeros((AHEAD, S, KV), np.int32)])
    a["mask"] = mask.reshape(-1, KV)
    a["key_mask"] = i["mask_BxS2_bf1"].view(np.uint8).reshape(1, B * KV)
    a["time_bias"] = i["fside_BxS2_0"].reshape(1, B * KV)
    by_parity = np.arange(D).reshape(HEADS // 2, 2, D // HEADS).transpose(1, 2, 0).reshape(-1)
    for n, v in i.items():
        if n[0] != "L":
            continue
        if n in ("L0_ffn_router_w", "L0_ffn_w1", "L0_ffn_w2", "L1_xattn_Wv", "L1_xattn_Wk", "L1_xattn_Wq", "L1_xattn_Wo",
                 "L1_ffn_w1", "L1_ffn_w2", "L2_xattn_Wq", "L2_xattn_Wkv", "L2_xattn_Wout"):
            v = v.T
        elif v.ndim == 1:
            v = v.reshape(1, -1)
        if n in ("L1_xattn_Wq", "L1_xattn_Wk", "L3_xattn_wq", "L3_xattn_wk", "L3_xattn_bq", "L3_xattn_bk"):
            v = v[:, by_parity]
        if n == "L3_xattn_bv":
            v = v.reshape(4, 4 * D // HEADS).T
        a[n] = v
    a["consts"] = shape_constants()
    return {n: np.ascontiguousarray(v) for n, v in a.items()}


def kernel(**inputs):
    import concourse.bacc as bacc
    from concourse.bass_utils import run_bass_kernel_spmd

    arrays = lay_out(inputs)
    nc = bacc.Bacc("TRN2", target_bir_lowering=False, num_devices=1)
    dram = {n: nc.dram_tensor(f"in_{n}", v.shape, mybir.dt.from_np(v.dtype), kind="ExternalInput").ap()
            for n, v in arrays.items()}
    out = nc.dram_tensor("out_x", (B * S, D), F32, kind="ExternalOutput").ap()
    program(nc, dram, out)
    r = run_bass_kernel_spmd(nc, [{f"in_{n}": v for n, v in arrays.items()}], core_ids=[0])
    return np.asarray(r.results[0]["out_x"]).reshape(B, S, D)
```

```python
import numpy as np
import concourse.bass as bass
from concourse import mybir
from contextlib import ExitStack

F32 = mybir.dt.float32
BF16 = mybir.dt.bfloat16
I32 = mybir.dt.int32
U8 = mybir.dt.uint8
ACT = mybir.ActivationFunctionType
ALU = mybir.AluOpType
AX = mybir.AxisListType

P = 128
B = 8
D = 128
S = 256
KV = 512
TPB = S // P
CPB = KV // P
NT = B * TPB
PAIRS = B // 2
AHEAD = 2
HEADS = 16
LN_EPS = 1e-5
MAGIC = 12582912.0


class Signal:

    def __init__(self, nc, ctx, name):
        self.sem = ctx.enter_context(nc.semaphore(name))
        self.before = 0

    def after(self, n):
        return self.sem, n + self.before


class Ring:

    def __init__(self, banks, filled, drained, per, lead=0):
        self.banks, self.filled, self.drained, self.per, self.lead = banks, filled, drained, per, lead
        assert 2 * per % len(banks) == 0

    def at(self, i, u, m):
        n, size = self.lead + u * self.per + m, len(self.banks)
        return n % size, i * (2 * self.per // size) + n // size

    def index(self, u, m):
        return (self.lead + u * self.per + m) % len(self.banks)

    def bank(self, u, m):
        return self.banks[self.index(u, m)]

    def free(self, i, u, m):
        s, n = self.at(i, u, m)
        return self.drained[s].after(n)

    def full(self, i, u, m):
        s, n = self.at(i, u, m)
        return self.filled[s].after(n + 1)

    def empty(self, i, u, m):
        s, n = self.at(i, u, m)
        return self.drained[s].after(n + 1)

    def fills(self, u, m):
        return self.filled[self.index(u, m)].sem

    def drains(self, u, m):
        return self.drained[self.index(u, m)].sem

    def close(self, tail=0):
        total, size = self.lead + self.per * B + tail, len(self.banks)
        for n in range(size):
            for s in (self.filled[n], self.drained[n]):
                s.before += (total + size - 1 - n) // size


class Machine:

    def __init__(self, nc, ctx, dram):
        self.nc, self.dram = nc, dram
        self.signals = []

        def sig(name):
            self.signals.append(Signal(nc, ctx, name))
            return self.signals[-1]
        self.loaded = sig("loaded")
        self.tables_loaded = sig("tables_loaded")
        self.streamed = [sig("streamed_even"), sig("streamed_odd")]
        self.ready_made = sig("ready_made")
        self.row_stats = sig("row_stats")
        self.row_moments = sig("row_moments")
        self.var_eps = sig("var_eps")
        self.row_rstd = sig("row_rstd")
        self.normed = sig("normed")
        self.filled = [sig(f"bank{n}_filled") for n in range(6)]
        self.drained = [sig(f"bank{n}_drained") for n in range(6)]
        self.parts_split = sig("parts_split")
        self.stacked = [sig("stacked_even"), sig("stacked_odd")]
        self.unit_copied = [sig("even_unit_copied"), sig("odd_unit_copied")]
        self.scores_ready = sig("scores_ready")
        self.max_ready = sig("max_ready")
        self.probs_ready = sig("probs_ready")
        self.turned = sig("turned")
        self.turned_copied = sig("turned_copied")
        self.pv_done = sig("pv_done")
        self.pv_copied = sig("pv_copied")
        self.sums_inverted = sig("sums_inverted")
        self.inv_step = sig("inv_step")
        self.inv_split = sig("inv_split")
        self.weights_folded = sig("weights_folded")
        self.folds_copied = sig("folds_copied")
        self.mask_ready = sig("mask_ready")
        self.x_updated = sig("x_updated")
        self.passed = sig("passed")
        self.squares_summed = sig("squares_summed")
        self.squares_ready = sig("squares_ready")
        self.powers_ready = sig("powers_ready")
        self.x_quantised = sig("x_quantised")
        self.h_squared = sig("h_squared")
        self.squared_affine = sig("squared_affine")
        self.unshifted = sig("unshifted")
        self.rotated = sig("rotated")
        self.row_max = sig("row_max")
        self.max_turned = sig("max_turned")
        self.max_found = sig("max_found")
        self.max_spread = sig("max_spread")
        self.x_turned = sig("x_turned")
        self.scales_ready = sig("scales_ready")
        self.gate_ready = sig("gate_ready")
        self.hidden_ready = sig("hidden_ready")
        self.hidden_clipped = sig("hidden_clipped")
        self.hidden_rounded = sig("hidden_rounded")
        self.hidden_quantised = sig("hidden_quantised")
        self.bias_moved = [sig("bias_moved_even"), sig("bias_moved_odd")]
        self.qk_loaded = sig("qk_loaded")
        self.zeroed = sig("zeroed")
        self.h_moved = sig("h_moved")
        self.step = sig("step")
        self.act_step = sig("act_step")
        self.pool_step = sig("pool_step")
        self.x_padded = ctx.enter_context(nc.sbuf_tensor("x_tok", [P, TPB + NT, D], F32))
        self.x = self.x_padded[:, TPB:TPB + NT, :]
        self.consts = {}


def sbuf(m, ctx, name, shape, dt=F32):
    return ctx.enter_context(m.nc.sbuf_tensor(name, shape, dt))


def psum(m, ctx, name, shape, dt=F32):
    return ctx.enter_context(m.nc.psum_tensor(name, shape, dt))


CONSTS = [("minus_half", 64), ("ident", P), ("spread4", 4 * P), ("spread2", 8 * P),
          ("ones", P), ("band", 3 * P), ("shift", P), ("last", P),
          ("rot_qa", 2 * 64), ("rot_qb", 2 * 64), ("rot_ka", 2 * 64), ("rot_kb", 2 * 64)]
CONSTS_BF = ("ident", "spread4", "spread2")
FIRST_CONSTS = 64 + P


def load_constants(m, ctx):
    nc, d = m.nc, m.dram
    widths = dict(CONSTS)
    c = sbuf(m, ctx, "consts", [P, sum(widths.values())])
    m.consts_bf = sbuf(m, ctx, "consts_bf", [P, sum(widths[n] for n in CONSTS_BF)], BF16)
    at = at_bf = 0
    for name, w in CONSTS:
        m.consts[name] = c[:, at:at + w]
        if name == CONSTS_BF[0]:
            m.consts_source = c[:, at:at + m.consts_bf.shape[1]]
        if name in CONSTS_BF:
            m.consts[name + "_bf"] = m.consts_bf[:, at_bf:at_bf + w]
            at_bf += w
        at += w
    with nc.Block() as block:
        @block.sync
        def _(sp):
            sp.dma_start(m.x, d["x"].rearrange("(t p) d -> p t d", p=P)).then_inc(m.loaded.sem, 16)
            sp.dma_start(c[:, 0:FIRST_CONSTS], d["consts"][:, 0:FIRST_CONSTS]).then_inc(m.loaded.sem, 16)
            sp.dma_start(c[:, FIRST_CONSTS:], d["consts"][:, FIRST_CONSTS:]).then_inc(m.tables_loaded.sem, 16)
            sp.wait_ge(*m.loaded.after(32))

        @block.vector
        def _(dve):
            dve.memset(m.x_padded[:, 0:TPB, :], 0.0)

        @block.gpsimd
        def _(pool):
            for s in m.signals:
                if s not in (m.loaded, m.tables_loaded):
                    pool.sem_inc(s.sem, 2)
    for s in m.signals:
        s.before += {m.loaded: 32, m.tables_loaded: 0}.get(s, 2)


def convert_constants(m):
    with m.nc.Block() as block:
        @block.vector
        def _(dve):
            dve.wait_ge(*m.tables_loaded.after(16))
            dve.tensor_copy(m.consts_bf[:], m.consts_source)


class Norm:

    def __init__(self, m, ctx, tiles, tag, buffers=2, dummies=0):
        self.m, self.tiles = m, tiles
        self.st = sbuf(m, ctx, f"st_{tag}", [P, tiles, 6])
        self.mv = sbuf(m, ctx, f"mv_{tag}", [P, tiles, 2])
        self.ve = sbuf(m, ctx, f"ve_{tag}", [P, tiles])
        self.rs = sbuf(m, ctx, f"rs_{tag}", [P, tiles])
        self.padded = [sbuf(m, ctx, f"xn{u}_{tag}", [P, dummies + tiles, D]) for u in range(buffers)]
        self.xn = [t[:, dummies:, :] for t in self.padded]

        self.halves = [range(w * tiles // 2, (w + 1) * tiles // 2) for w in range(2)]

    def vector(self, dve, b, u, src):
        self.moments(dve, b, src)
        self.scale(dve, b, u, src)

    def moments(self, dve, b, src):
        m, half = self.m, self.tiles // 2
        for w, js in enumerate(self.halves):
            for j in js:
                dve.bn_stats(self.st[:, j, :], src(j)).then_inc(m.row_stats.sem, 1)
            dve.wait_ge(*m.row_stats.after(half * (2 * b + w + 1)))
            dve.sem_inc(m.passed.sem, 1)
            for j in js:
                dve.bn_aggr(self.mv[:, j, :], self.st[:, j, :]).then_inc(m.row_moments.sem, 1)
            dve.wait_ge(*m.row_moments.after(half * (2 * b + w + 1)))
            dve.tensor_scalar(self.ve[:, js.start:js.stop], self.mv[:, js.start:js.stop, 1], LN_EPS, None, ALU.add).then_inc(m.var_eps.sem, 1)

    def scale(self, dve, b, u, src):
        m = self.m
        for w, js in enumerate(self.halves):
            dve.wait_ge(*m.row_rstd.after(2 * b + w + 1))
            for j in js:
                dve.tensor_scalar(self.xn[u][:, j, :], src(j), self.mv[:, j, 0:1], self.rs[:, j:j + 1],
                                  ALU.subtract, ALU.mult).then_inc(m.normed.sem, 1)

    def pool(self, pool, b):
        m, half = self.m, self.tiles // 2
        for w in range(2):
            pool.wait_ge(*m.var_eps.after(2 * b + w + 1))
            pool.tensor_tensor(self.rs[:, w * half:w * half + half], self.ve[:, w * half:w * half + half],
                               m.consts["minus_half"][:, 0:half], ALU.pow).then_inc(m.row_rstd.sem, 1)

    def close(self, steps):
        m, t = self.m, self.tiles
        for s, n in ((m.row_stats, t), (m.row_moments, t), (m.var_eps, 2), (m.row_rstd, 2), (m.normed, t)):
            s.before += n * steps


def l0_cross_attention(m):
    nc, d, x, k = m.nc, m.dram, m.x, m.consts
    with ExitStack() as ctx:
        sb = lambda name, shape, dt=F32: sbuf(m, ctx, f"{name}_l0x", shape, dt)
        norm = Norm(m, ctx, NT, "l0x", buffers=1)
        ctxT = sb("ctxT", [P, (B + 1) * KV])
        rows = sb("rows", [P, (B + 1) * CPB, D])
        xnT = sb("xnT", [P, (B + 2) * S])
        xs = [sb(f"xs{u}", [P, S]) for u in range(2)]
        nmax, sums, inv = sb("nmax", [P, 2, TPB]), sb("sums", [P, 2, TPB]), sb("inv", [P, 2, TPB])
        probs = [sb(f"probs{j}", [P, KV]) for j in range(TPB)]
        pT = [sb(f"pT{j}", [P, CPB, P]) for j in range(TPB)]
        TURNS = NT // 4
        ring = Ring([psum(m, ctx, f"ring{n}_l0x", [P, 512]) for n in range(2)], m.filled, m.drained, 0, lead=TURNS)
        first = lambda f: (0, 0, f - ring.lead)
        s_ps = [psum(m, ctx, f"s_ps{j}_l0x", [P, KV]) for j in range(TPB)]
        t_ps = [psum(m, ctx, f"t_ps{j}_l0x", [P, KV]) for j in range(TPB)]
        y_ps = [psum(m, ctx, f"y_ps{u}_l0x", [P, TPB * D]) for u in range(2)]

        with nc.Block() as block:
            @block.sync
            def _(sp):
                for b in range(B + 1):
                    if b >= 2:
                        sp.wait_ge(*m.streamed[b % 2].after(32 * (b // 2)))
                    sp.dma_start(ctxT[:, b * KV:(b + 1) * KV], d["ctxT"][:, b * KV:(b + 1) * KV]).then_inc(m.streamed[b % 2].sem, 16)
                    sp.dma_start(rows[:, b * CPB:(b + 1) * CPB, :], d["ctx"][b * KV:(b + 1) * KV, :].rearrange("(c p) d -> p c d", p=P))\
                        .then_inc(m.streamed[b % 2].sem, 16)
                sp.wait_ge(*m.streamed[0].after(32 * (PAIRS + 1)))
                sp.wait_ge(*m.streamed[1].after(32 * PAIRS))

            @block.gpsimd
            def _(pool):
                pool.memset(xnT[:, B * S:], 0.0).then_inc(m.zeroed.sem, 1)
                norm.pool(pool, 0)

            @block.vector
            def _(dve):
                norm.vector(dve, 0, 0, lambda j: x[:, j, :])

                def find_max(b, u, j):
                    dve.wait_ge(*m.scores_ready.after(TPB * b + j + 1))
                    dve.tensor_reduce(nmax[:, u, j:j + 1], s_ps[j][:], AX.X, ALU.max, negate=True).then_inc(m.max_ready.sem, 1)

                for j in range(TPB):
                    find_max(0, 0, j)
                with dve.Fori(0, PAIRS) as i:
                    for u in range(2):
                        b = 2 * i + u
                        for j in range(TPB):
                            dve.wait_ge(*m.turned.after(TPB * b + j + 1))
                            dve.tensor_copy(pT[j][:].rearrange("p c t -> p (c t)"), t_ps[j][:]).then_inc(m.turned_copied.sem, 1)
                            find_max(b + 1, 1 - u, j)
                        dve.wait_ge(*m.probs_ready.after(TPB * b + TPB))
                        dve.reciprocal(inv[:, u, :], sums[:, u, :]).then_inc(m.sums_inverted.sem, 1)
                        dve.wait_ge(*m.sums_inverted.after(b + 1))
                        dve.wait_ge(*m.pv_done.after(b + 1))
                        for j in range(TPB):
                            ins = dve.scalar_tensor_tensor(out=x[:, TPB * b + j, :], in0=y_ps[u][:, j * D:(j + 1) * D],
                                                           scalar=inv[:, u, j:j + 1], in1=x[:, TPB * b + j, :],
                                                           op0=ALU.mult, op1=ALU.add)
                        ins.then_inc(m.pv_copied.sem, 1)
                dve.wait_ge(*m.pv_copied.after(B))

            @block.scalar
            def _(act):
                turn_all(m, None, act, ring, first, None, xnT)

                def exponential(b, u, j):
                    act.wait_ge(*m.max_ready.after(TPB * b + j + 1))
                    act.activation(probs[j][:], s_ps[j][:], ACT.Exp, bias=nmax[:, u, j:j + 1],
                                   accum_out=sums[:, u, j:j + 1]).then_inc(m.probs_ready.sem, 1)

                act.wait_ge(*m.zeroed.after(1))
                for f in range(TURNS):
                    act.wait_ge(*ring.empty(*first(f)))
                for b in range(2):
                    act.activation(xs[b][:], xnT[:, b * S:(b + 1) * S], ACT.Copy).then_inc(m.h_moved.sem, 1)
                for j in range(TPB):
                    exponential(0, 0, j)
                with act.Fori(0, PAIRS) as i:
                    for u in range(2):
                        b = 2 * i + u
                        act.activation(xs[u][:], xnT[:, bass.ds((b + 2) * S, S)], ACT.Copy).then_inc(m.h_moved.sem, 1)
                        for j in range(TPB):
                            exponential(b + 1, 1 - u, j)

            @block.tensor
            def _(pe):
                turn_all(m, pe, None, ring, first, norm.xn[0], None)

                def scores(i, u, j):
                    b = 2 * i + u
                    if j == 0:
                        pe.wait_ge(*m.h_moved.after(b + 1))
                    pe.matmul(s_ps[j][:], xs[u][:, j * P:(j + 1) * P], ctxT[:, bass.ds(b * KV, KV)], start=True, stop=True)\
                        .then_inc(m.scores_ready.sem, 1)

                pe.wait_ge(*m.streamed[0].after(32))
                for j in range(TPB):
                    scores(0, 0, j)
                with pe.Fori(0, PAIRS) as i:
                    for u in range(2):
                        b = 2 * i + u
                        pe.wait_ge(*m.streamed[1 - u].after(32 * (i + u + 1)))
                        for j in range(TPB):
                            pe.wait_ge(*m.probs_ready.after(TPB * b + j + 1))
                            pe.wait_ge(*m.turned_copied.after(TPB * b + j - 1))
                            for c in range(CPB):
                                ins = pe.transpose(t_ps[j][:, c * P:(c + 1) * P], probs[j][:, c * P:(c + 1) * P], k["ident"])
                            ins.then_inc(m.turned.sem, 1)
                            scores(i + u, 1 - u, j)
                        pe.wait_ge(*m.pv_copied.after(b - 1))
                        for j in range(TPB):
                            pe.wait_ge(*m.turned_copied.after(TPB * b + j + 1))
                            for c in range(CPB):
                                ins = pe.matmul(y_ps[u][:, j * D:(j + 1) * D], pT[j][:, c, :], rows[:, bass.ds(CPB * b + c, 1), :],
                                                start=(c == 0), stop=(c == CPB - 1))
                        ins.then_inc(m.pv_done.sem, 1)
        norm.close(1)
        ring.close()
        for s, n in ((m.streamed[0], 32 * (PAIRS + 1)), (m.streamed[1], 32 * PAIRS), (m.zeroed, 1), (m.h_moved, B + 2),
                     (m.scores_ready, NT + TPB), (m.max_ready, NT + TPB), (m.probs_ready, NT + TPB), (m.turned, NT),
                     (m.turned_copied, NT), (m.sums_inverted, B), (m.pv_done, B), (m.pv_copied, B)):
            s.before += n


def turn_all(m, pe, act, ring, first, src, dst, at0=0):
    for f in range(NT // 4):
        at = first(at0 + f)
        if pe is not None:
            pe.wait_ge(*m.normed.after(4 * f + 4))
            pe.wait_ge(*ring.free(*at))
            for j in range(4):
                ins = pe.transpose(ring.bank(*at[1:])[:, j * P:(j + 1) * P], src[:, 4 * f + j, :], m.consts["ident"])
            ins.then_inc(ring.fills(*at[1:]), 1)
        if act is not None:
            act.wait_ge(*ring.full(*at))
            act.activation(dst[:, f * 512:(f + 1) * 512], ring.bank(*at[1:])[:], ACT.Copy).then_inc(ring.drains(*at[1:]), 1)


def l0_block_ffn(m):
    nc, d, x, k = m.nc, m.dram, m.x, m.consts
    NB, TOP, HC = 16, 4, 4
    LOW, CHOSEN = -3.0e38, 3.0e38
    T, BT = B * S, 512
    STEPS, TS = T // BT, BT // P
    with ExitStack() as ctx:
        sb = lambda name, shape, dt=F32: sbuf(m, ctx, f"{name}_l0f", shape, dt)
        norm = Norm(m, ctx, NT, "l0f", buffers=1)
        router, router_b = sb("router", [P, NB]), sb("router_b", [1, NB])
        w1, b1 = sb("w1", [P, HC * P]), sb("b1", [P, HC])
        w2, b2 = sb("w2", [P, HC, D]), sb("b2", [P, 1])
        xnT = sb("xnT", [P, T])
        logits = sb("logits", [P, NT, NB + TOP])
        top = sb("top", [P, NT, 8])
        marked = sb("marked", [P, NT, NB + TOP])
        chosen, chosenT = sb("chosen", [P, NT, NB], BF16), sb("chosenT", [P, T], BF16)
        hT = sb("hT", [P, HC, T])
        yT = [sb(f"yT{u}", [P, BT]) for u in range(2)]
        TURNS = NT // 4
        LOGIT, HID = TURNS, 0
        CHOICE = STEPS * HC
        SPREAD = CHOICE + 2
        ring = Ring([psum(m, ctx, f"ring{n}_l0f", [P, BT]) for n in range(4)], m.filled, m.drained, HC // 2, lead=TURNS + 1)
        first = lambda f: (0, 0, f - ring.lead)
        yT_ps = [psum(m, ctx, f"yT_ps{u}_l0f", [P, BT]) for u in range(2)]
        y_ps = [psum(m, ctx, f"y_ps{u}_l0f", [P, BT]) for u in range(2)]
        assert STEPS == PAIRS

        with nc.Block() as block:
            @block.sync
            def _(sp):
                for dst, src in ((router[:], d["L0_ffn_router_w"]), (router_b[:], d["L0_ffn_router_b"]), (w1[:], d["L0_ffn_w1"]),
                                 (b2[:], d["L0_ffn_b2"].rearrange("o (p n) -> (o p) n", n=1)),
                                 (w2[:], d["L0_ffn_w2"].rearrange("(c p) d -> p c d", p=P))):
                    sp.dma_start(dst, src).then_inc(m.loaded.sem, 16)
                for c in range(HC):
                    sp.dma_start(b1[:, c:c + 1], d["L0_ffn_b1"][0, c * P:(c + 1) * P].rearrange("(p o) -> p o", o=1))\
                        .then_inc(m.loaded.sem, 16)
                sp.wait_ge(*m.loaded.after(16 * (5 + HC)))

            @block.gpsimd
            def _(pool):
                pool.memset(chosenT[:], 0.0).then_inc(m.zeroed.sem, 1)
                norm.pool(pool, 0)

            @block.vector
            def _(dve):
                norm.vector(dve, 0, 0, lambda j: x[:, j, :])
                dve.memset(logits[:, :, NB:], LOW).then_inc(m.step.sem, 1)
                at = first(LOGIT)
                dve.wait_ge(*ring.full(*at))
                dve.tensor_copy(logits[:, :, 0:NB], ring.bank(*at[1:])[:, 0:NT * NB].rearrange("p (t n) -> p t n", n=NB))\
                    .then_inc(ring.drains(*at[1:]), 1)
                dve.wait_ge(*m.step.after(1))
                dve.wait_ge(*ring.empty(*at))
                dve.sem_inc(m.passed.sem, 1)
                for j in range(NT):
                    dve.max(top[:, j, :], logits[:, j, 0:NB]).then_inc(m.step.sem, 1)
                dve.wait_ge(*m.step.after(NT + 1))
                dve.tensor_copy(top[:, :, TOP:], logits[:, :, NB:]).then_inc(m.step.sem, 1)
                dve.wait_ge(*m.step.after(NT + 2))
                dve.sem_inc(m.passed.sem, 1)
                for j in range(NT):
                    dve.match_replace(marked[:, j, :], top[:, j, :], logits[:, j, :], CHOSEN).then_inc(m.step.sem, 1)
                dve.wait_ge(*m.step.after(2 * NT + 2))
                dve.tensor_scalar(chosen[:], marked[:, :, 0:NB], CHOSEN, None, ALU.is_equal).then_inc(m.mask_ready.sem, 1)
                for c in range(HC):
                    dve.wait_ge(*ring.empty(STEPS - 1, 0, HID + c))
                with dve.Fori(0, STEPS) as i:
                    for c in range(HC):
                        cols = hT[:, c, bass.ds(i * BT, BT)]
                        dve.wait_ge(*ring.full(i, 0, SPREAD + c))
                        dve.tensor_tensor(cols, ring.bank(0, SPREAD + c)[:], cols, ALU.mult).then_inc(ring.drains(0, SPREAD + c), 1)
                with dve.Fori(0, STEPS // 2) as i:
                    for u in range(2):
                        dve.wait_ge(*m.turned.after(2 * i + u + 1))
                        tiles = x[:, bass.ds(TS * (2 * i + u), TS), :]
                        dve.tensor_tensor(tiles, y_ps[u][:].rearrange("p (t d) -> p t d", d=D), tiles, ALU.add)\
                            .then_inc(m.x_updated.sem, 1)
                dve.wait_ge(*m.x_updated.after(STEPS))

            @block.scalar
            def _(act):
                turn_all(m, None, act, ring, first, None, xnT)
                act.wait_ge(*m.loaded.after(16 * (5 + HC)))
                with act.Fori(0, STEPS) as i:
                    for c in range(HC):
                        act.wait_ge(*ring.full(i, 0, HID + c))
                        act.activation(hT[:, c, bass.ds(i * BT, BT)], ring.bank(0, HID + c)[:], ACT.Relu, bias=b1[:, c:c + 1])\
                            .then_inc(ring.drains(0, HID + c), 1)
                act.wait_ge(*m.zeroed.after(1))
                for w in range(2):
                    act.wait_ge(*ring.full(0, 0, CHOICE + w))
                    act.activation(chosenT[0:NB, w * T // 2:(w + 1) * T // 2], ring.bank(0, CHOICE + w)[0:NB, :].bitcast(BF16), ACT.Copy)\
                        .then_inc(ring.drains(0, CHOICE + w), 1)
                with act.Fori(0, STEPS // 2) as i:
                    for u in range(2):
                        act.wait_ge(*m.pv_done.after(2 * i + u + 1))
                        act.activation(yT[u][:], yT_ps[u][:], ACT.Identity, bias=b2[:, 0:1]).then_inc(m.pv_copied.sem, 1)

            @block.tensor
            def _(pe):
                turn_all(m, pe, None, ring, first, norm.xn[0], None)
                pe.wait_ge(*m.loaded.after(16 * (5 + HC)))
                at = first(LOGIT)
                pe.wait_ge(*ring.free(*at))
                for f in range(TURNS):
                    pe.wait_ge(*ring.empty(*first(f)))
                for j in range(NT):
                    out = ring.bank(*at[1:])[:, j * NB:(j + 1) * NB]
                    pe.matmul(out, k["ones"][0:1, :], router_b[:], start=True, stop=False)
                    ins = pe.matmul(out, xnT[:, j * P:(j + 1) * P], router[:], start=False, stop=True)
                ins.then_inc(ring.fills(*at[1:]), 1)
                with pe.Fori(0, STEPS) as i:
                    for c in range(HC):
                        pe.wait_ge(*ring.free(i, 0, HID + c))
                        pe.matmul(ring.bank(0, HID + c)[:], w1[:, c * P:(c + 1) * P], xnT[:, bass.ds(i * BT, BT)], start=True, stop=True)\
                            .then_inc(ring.fills(0, HID + c), 1)
                pe.wait_ge(*m.mask_ready.after(1))
                for w in range(2):
                    at = (0, 0, CHOICE + w)
                    pe.wait_ge(*ring.free(*at))
                    bank = ring.bank(*at[1:])[:].bitcast(BF16)
                    for j in range(NT // 2):
                        ins = pe.transpose(bank[0:NB, j * P:(j + 1) * P], chosen[:, w * NT // 2 + j, :], k["ident_bf"])
                    ins.then_inc(ring.fills(*at[1:]), 1)
                for w in range(2):
                    pe.wait_ge(*ring.empty(0, 0, CHOICE + w))
                with pe.Fori(0, STEPS) as i:
                    for c in range(HC):
                        pe.wait_ge(*ring.free(i, 0, SPREAD + c))
                        pe.matmul(ring.bank(0, SPREAD + c)[:], k["spread4_bf"][:, c * P:(c + 1) * P], chosenT[:, bass.ds(i * BT, BT)],
                                  start=True, stop=True).then_inc(ring.fills(0, SPREAD + c), 1)
                with pe.Fori(0, STEPS // 2) as i:
                    for u in range(2):
                        for c in range(HC):
                            pe.wait_ge(*ring.empty(2 * i + u, 0, SPREAD + c))
                        for c in range(HC):
                            ins = pe.matmul(yT_ps[u][:], w2[:, c, :], hT[:, c, bass.ds((2 * i + u) * BT, BT)], start=(c == 0),
                                            stop=(c == HC - 1))
                        ins.then_inc(m.pv_done.sem, 1)
                    for u in range(2):
                        pe.wait_ge(*m.pv_copied.after(2 * i + u + 1))
                        pe.wait_ge(*m.x_updated.after(2 * i))
                        for t in range(TS):
                            ins = pe.transpose(y_ps[u][:, t * D:(t + 1) * D], yT[u][:, t * P:(t + 1) * P], k["ident"])
                        ins.then_inc(m.turned.sem, 1)
        norm.close(1)
        ring.close(2 + STEPS * HC)
        for s, n in ((m.loaded, 16 * (5 + HC)), (m.step, 2 * NT + 2), (m.zeroed, 1), (m.mask_ready, 1), (m.pv_done, STEPS), (m.pv_copied, STEPS),
                     (m.turned, STEPS), (m.x_updated, STEPS)):
            s.before += n


def head_attention(m, tag, hd, wq, wk, wv, wo, bo, bq=None, bk=None, bv=None, mask=None, key_mask=None, key_bias=None):
    nc, d, x, k = m.nc, m.dram, m.x, m.consts
    small = hd == D // HEADS
    G = 4 if small else 2
    NG = HEADS // G
    W = P // G
    NK = 1 if small else NG
    VW = HEADS * W
    VF = 1 if small else CPB * VW // 512
    UNITS = HEADS * TPB
    per_load = 32 if mask is not None else 16
    MASKED = -1e20 if mask is not None else -1e30
    spread = k["spread4_bf"] if small else k["spread2_bf"]
    masked = key_bias is None
    TURNS = B * S // 512
    DEEP, RING = (4, 2) if small else (2, 4)
    LAST, SUMS, SPREAD = 0, 1, 2
    OUT = SPREAD + NG // 2
    Q = OUT + 1
    K = Q + (0 if small else HEADS * S // 512)
    V = K + (1 if small else 0)
    GROUP = V + VF
    PER = GROUP + NG - 1
    after = {LAST: 2, SUMS: 3, OUT: 13} if small else {LAST: 1, SUMS: 2, OUT: 9}
    after.update({SPREAD + n: 3 + DEEP + n for n in range(OUT - SPREAD)})
    after.update({K: 0} if small else {Q + n: 10 + n for n in range(V - Q)})
    after.update({V + n: (15 if small else 10 + V - Q + n) for n in range(GROUP - V)})
    after.update({GROUP + g: G * TPB * (g + 1) + 1 for g in range(NG - 1)})
    order = sorted(range(PER), key=lambda f: (after[f], f < GROUP, f))
    in_halves = lambda f: f == LAST or f >= GROUP
    steps = [[(f, 1) for f in order if in_halves(f) and after[f] == n - 1] + [(f, 0) for f in order if after[f] == n] for n in range(UNITS)]
    due = [[f for f in order if after[f] + in_halves(f) == n] for n in range(UNITS)]
    assert max(after[f] for f in range(Q, V)) < UNITS - DEEP and max(after[f] for f in range(GROUP)) < UNITS - 1
    with ExitStack() as ctx:
        norm = Norm(m, ctx, NT, tag, buffers=1)
        sb = lambda name, shape, dt=F32: sbuf(m, ctx, f"{name}_{tag}", shape, dt)
        wq_s, wk_s = sb("wq", [P, NK, P]), sb("wk", [P, NK, P])
        wv_s = sb("wv", [P, D if small else VW])
        wo_s = sb("wo", [P, NG, D])
        bo_s = sb("bo", [1, D])
        ctxT = [sb(f"ctxT{u}", [P, KV]) for u in range(2)]
        xnT = sb("xnT", [P, (B + 1) * S])
        q = [sb(f"q{u}", [P, HEADS, S], BF16 if small else F32) for u in range(2)]
        v = [sb(f"v{u}", [P, CPB, VW]) for u in range(2)]
        nmax = sb("nmax", [P, 2, UNITS])
        sums = sb("sums", [P, 2, TPB, HEADS])
        inv = sb("inv", [P, TPB * HEADS])
        inv_rest, nothing = sb("inv_rest", [P, TPB * HEADS]), sb("nothing", [P, TPB * HEADS])
        inv_parts = sb("inv_parts", [P, TPB, 3, HEADS], BF16)
        invT = sb("invT", [P, S], BF16)
        probs = [sb(f"probs{n}", [P, KV]) for n in range(2 * DEEP)]
        minus_s = [sb(f"minus_s{n}", [P, KV]) for n in range(2 * DEEP)]
        pT = [sb(f"pT{n}", [P, G, CPB, S]) for n in range(2)]
        o = [sb(f"o{u}", [P, NG, S]) for u in range(2)]
        padded, first_zeros, later_zeros, zeros = [], [], [], [o[1][:], xnT[:, B * S:], nothing[:], invT[:]]
        if small:
            PAIR = HEADS // 2
            kT = [sb(f"kT{u}", [P, PAIR, KV], BF16) for u in range(2)]
            q_all = sb("q_all", [P, (B + 1) * S])
            k_all = sb("k_all", [P, KV])
            rest = sb("rest", [P, KV + S])
            parts = sb("parts", [P, 3, KV + S], BF16)
            zero = sb("zero", [P, KV])
            padded += [wo_s[:]]
            first_zeros += [kT[0][:], zero[:], q[0][:]]
            later_zeros += [kT[1][:], q[1][:]]
            zeros += [q_all[:, B * S:]]
            STACK = [(0, 0, 0), (8, 0, 1), (16, 1, 0), (24, 1, 1), (48, 0, 2), (56, 2, 0)]
            NSTACK = 4 * len(STACK)
        else:
            wqk = sb("wqk", [P, HEADS, D])
            later_zeros += [pT[1][:], v[1][:]]
        if bq is not None:
            bq_s, bk_s, bv_s = sb("bq", [P, 1]), sb("bk", [P, 1]), sb("bv", [P, NG])
            padded += [bv_s[:]]
        if mask is not None:
            mask_i = [sb(f"mask_i{u}", [P, TPB, KV], I32) for u in range(2)]
        if key_mask is not None:
            key_u8 = sb("key_u8", [P, (B + 1) * KV], U8)
            zeros += [key_u8[:, B * KV:]]
        if masked:
            mask_b = [sb(f"mask_b{u}", [P, TPB if mask is not None else 1, KV], BF16) for u in range(2)]
            added = lambda u, n: mask_b[u][:, n % TPB if mask is not None else 0, :]
        else:
            bias_b = [sb(f"bias_b{u}", [P, KV]) for u in range(2)]
            added = lambda u, n: bias_b[u][:]

        NQK = 2 + 2 * (bq is not None)
        NLOAD = 2 + (G if small else 1) + G * (bq is not None) + (key_mask is not None)
        NZERO = len(zeros) + 1
        NPADDED, NK0 = len(padded), len(padded) + 2
        NFIRST, NLATER = len(padded) + len(first_zeros), len(later_zeros)
        NSTEP = NZERO + 2 * (bq is not None) + 3 * small
        ring = Ring([psum(m, ctx, f"ring{n}_{tag}", [P, 512]) for n in range(RING)], m.filled, m.drained, PER,
                    lead=TURNS + (TURNS if small else 0) + GROUP - Q)
        T0 = 1 if small else 0
        s_ps = [psum(m, ctx, f"s_ps{n}_{tag}", [P, KV]) for n in range(DEEP)]
        t_ps = [psum(m, ctx, f"t_ps{n}_{tag}", [P, KV]) for n in range(2)]
        if not small:
            folds = s_ps + t_ps
            QUART = HEADS // 4
            folded_heads = lambda n: wqk[:, n // 2 * 2 * QUART + n % 2:n // 2 * 2 * QUART + 2 * QUART:2, :]
        turn = lambda i, u, f: (i, u, order.index(f))
        prepared = lambda f: first(0) if small and f == K else (0, 0, f - GROUP)
        last_turn = lambda i, u: (i - 1 + u, 1 - u)
        ahead = lambda i, u, n: (i, u, n) if n < UNITS else (i + u, 1 - u, n - UNITS)

        def bank_before(b_i, u, c):
            g = c // (G * TPB) - 2
            return turn(b_i, u, GROUP + g) if g >= 0 else turn(b_i, u, LAST) if g == -1 else turn(*last_turn(b_i, u), GROUP + NG + g)

        first = lambda f: (0, 0, f - ring.lead)
        scalar_copies = lambda n: small and n % 2
        unit_turned = lambda n: t_ps[n % 2][:].rearrange("p (c t) -> p c t", t=P)

        def unit_pT(n):
            h, j = divmod(n, TPB)
            return pT[h // G % 2][:, h % G, :, j * P:(j + 1) * P]
        cols512 = lambda f: slice(512 * f, 512 * f + 512)

        with nc.Block() as block:
            @block.sync
            def _(sp):
                def stream(b, u):
                    sp.dma_start(ctxT[u][:], d["ctxT"][:, bass.ds(b * KV, KV)]).then_inc(m.streamed[u].sem, 16)
                    if mask is not None:
                        sp.dma_start(mask_i[u][:], mask[bass.ds(b * S, S), :].rearrange("(t p) k -> p t k", p=P))\
                            .then_inc(m.streamed[u].sem, 16)

                for dst, src in ((wk_s[:], wk), (wq_s[:], wq)):
                    sp.dma_start(dst, src.rearrange("(g p) n -> p g n", p=P)).then_inc(m.qk_loaded.sem, 16)
                if bq is not None:
                    for dst, src in ((bk_s, bk), (bq_s, bq)):
                        sp.dma_start(dst[:], src.rearrange("o (p n) -> (o p) n", n=1)).then_inc(m.qk_loaded.sem, 16)
                def stream_bias(b, u):
                    sp.dma_start(bias_b[u][:], key_bias[0, bass.ds(b * KV, KV)].partition_broadcast(P)).then_inc(m.bias_moved[u].sem, 16)

                for u in range(2):
                    stream(u, u)
                    if key_bias is not None:
                        stream_bias(u, u)
                loads = [(wv_s[:], wv), (bo_s[:], bo)]
                if not small:
                    loads.append((wo_s[:], wo.rearrange("(g p) n -> p g n", p=P)))
                if key_mask is not None:
                    loads.append((key_u8[:, 0:B * KV], key_mask[0].partition_broadcast(P)))
                for dst, src in loads:
                    sp.dma_start(dst, src).then_inc(m.loaded.sem, 16)
                n = len(loads)
                if small:
                    sp.wait_ge(*m.zeroed.after(NPADDED))
                    for h in range(G):
                        sp.dma_start(wo_s[W * h:W * h + hd, :, :], wo.rearrange("(g h e) n -> h e g n", h=G, e=hd)[h])\
                            .then_inc(m.loaded.sem, 16)
                    n += G
                if bv is not None:
                    for h in range(G):
                        sp.dma_start(bv_s[W * h:W * h + hd, :], bv[hd * h:hd * (h + 1), :])\
                            .then_inc(m.loaded.sem, 16)
                    n += G
                assert n == NLOAD
                def stack(i, u):
                    b = 2 * i + u + 1
                    sp.wait_ge(*m.parts_split.after(2 * b + 1))
                    for w in range(2):
                        for row, _, of_k in STACK:
                            sp.dma_start(kT[1 - u][64 * w + row:64 * w + row + hd, :, :], parts[64 * w:64 * w + 64, of_k, 0:KV])\
                                .then_inc(m.stacked[1 - u].sem, 16)
                    if isinstance(i, int):
                        sp.wait_ge(*m.zeroed.after(NFIRST))
                    sp.wait_ge(*m.parts_split.after(2 * b + 2))
                    for w in range(2):
                        for row, of_q, _ in STACK:
                            sp.dma_start(q[1 - u][64 * w + row:64 * w + row + hd, w:HEADS:2, :],
                                         parts[64 * w:64 * w + 64, of_q, KV:KV + S]).then_inc(m.stacked[1 - u].sem, 16)

                if small:
                    sp.wait_ge(*m.zeroed.after(NK0))
                    stack(-1, 1)
                    sp.wait_ge(*m.zeroed.after(NFIRST + NLATER))
                with sp.Fori(0, PAIRS) as i:
                    for u in range(2):
                        if small:
                            sp.wait_ge(*ring.full(*turn(i, u, GROUP)))
                        else:
                            sp.wait_ge(*m.scores_ready.after(UNITS * (2 * i + u + 1)))
                        stream(2 * i + u + AHEAD, u)
                        if small:
                            stack(i, u)
                        if key_bias is not None:
                            sp.wait_ge(*m.max_ready.after(UNITS * (2 * i + u + 1)))
                            stream_bias(2 * i + u + AHEAD, u)
                for u in range(2):
                    sp.wait_ge(*m.streamed[u].after(per_load * (PAIRS + 1)))
                    if key_bias is not None:
                        sp.wait_ge(*m.bias_moved[u].after(16 * (PAIRS + 1)))
                    if small:
                        sp.wait_ge(*m.stacked[u].after(16 * NSTACK * (PAIRS + 1 - u)))

            @block.gpsimd
            def _(pool):
                for t in padded + first_zeros[:1]:
                    pool.memset(t, 0.0).then_inc(m.zeroed.sem, 1)
                norm.pool(pool, 0)

                def split(i, u, side):
                    b = 2 * i + u + 1
                    src, cols = ((k_all[:], slice(0, KV)), (q_all[:, bass.ds(b * S, S)], slice(KV, KV + S)))[side]
                    at = 6 * b + 3 * side
                    nothing = zero[:, 0:cols.stop - cols.start]
                    pool.tensor_tensor(parts[:, 0, cols], src, nothing, ALU.add).then_inc(m.pool_step.sem, 1)
                    pool.wait_ge(*m.pool_step.after(at + 1))
                    pool.sem_inc(m.passed.sem, 1)
                    pool.tensor_tensor(rest[:, cols], src, parts[:, 0, cols], ALU.subtract).then_inc(m.pool_step.sem, 1)
                    pool.wait_ge(*m.pool_step.after(at + 2))
                    pool.tensor_tensor(parts[:, 1, cols], rest[:, cols], nothing, ALU.add).then_inc(m.pool_step.sem, 1)
                    pool.wait_ge(*m.pool_step.after(at + 3))
                    pool.tensor_tensor(parts[:, 2, cols], rest[:, cols], parts[:, 1, cols], ALU.subtract)\
                        .then_inc(m.parts_split.sem, 1)

                def split_inv(b):
                    part = lambda r: inv_parts[:, :, r, :]
                    heads = lambda t: t[:].rearrange("p (t h) -> p t h", h=HEADS)
                    pool.wait_ge(*m.sums_inverted.after(b + 1))
                    pool.tensor_tensor(part(0), heads(inv), heads(nothing), ALU.add).then_inc(m.inv_step.sem, 1)
                    pool.wait_ge(*m.inv_step.after(3 * b + 1))
                    pool.tensor_tensor(heads(inv_rest), heads(inv), part(0), ALU.subtract).then_inc(m.inv_step.sem, 1)
                    pool.wait_ge(*m.inv_step.after(3 * b + 2))
                    pool.tensor_tensor(part(1), heads(inv_rest), heads(nothing), ALU.add).then_inc(m.inv_step.sem, 1)
                    pool.wait_ge(*m.inv_step.after(3 * b + 3))
                    pool.tensor_tensor(part(2), heads(inv_rest), part(1), ALU.subtract).then_inc(m.inv_split.sem, 1)

                if small:
                    pool.memset(first_zeros[1], 0.0).then_inc(m.zeroed.sem, 1)
                    pool.wait_ge(*m.zeroed.after(NK0))
                    pool.wait_ge(*ring.empty(*prepared(K)))
                    split(-1, 1, 0)
                    pool.memset(first_zeros[2], 0.0).then_inc(m.zeroed.sem, 1)
                    pool.wait_ge(*m.zeroed.after(NFIRST))
                    for f in range(TURNS - 2, TURNS):
                        pool.wait_ge(*ring.empty(*first(T0 + TURNS + f)))
                    split(-1, 1, 1)
                for t in later_zeros:
                    pool.memset(t, 0.0).then_inc(m.zeroed.sem, 1)
                pool.wait_ge(*m.zeroed.after(NFIRST + NLATER))
                pool.sem_inc(m.passed.sem, 1)
                pool.wait_ge(*m.ready_made.after(1))
                pool.sem_inc(m.passed.sem, 1)
                with pool.Fori(0, PAIRS) as i:
                    for u in range(2):
                        split_inv(2 * i + u)
                        if small:
                            pool.wait_ge(*ring.empty(*turn(i, u, K)))
                            for side in range(2):
                                split(i, u, side)
                split_inv(B)

            @block.vector
            def _(dve):
                norm.moments(dve, 0, lambda j: x[:, j, :])
                for t in zeros:
                    dve.memset(t, 0.0).then_inc(m.step.sem, 1)
                dve.memset(sums[:, 1], 1.0).then_inc(m.step.sem, 1)
                norm.scale(dve, 0, 0, lambda j: x[:, j, :])
                done = NZERO
                dve.wait_ge(*m.qk_loaded.after(16 * NQK))
                dve.wait_ge(*m.loaded.after(16 * NLOAD))
                if bv is not None:
                    dve.wait_ge(*m.turned.after(1))
                    dve.tensor_copy(bo_s[:], t_ps[0][0:1, 0:D]).then_inc(m.step.sem, 1)
                    done += 1
                if bq is not None:
                    dve.tensor_scalar(bq_s[:], bq_s[:], hd ** -0.5, None, ALU.mult).then_inc(m.step.sem, 1)
                    done += 1
                dve.wait_ge(*m.step.after(done))
                dve.engine_nop().then_inc(m.ready_made.sem, 1)
                if small:
                    for t in (v[0], v[1], pT[1]):
                        dve.memset(t[:], 0.0).then_inc(m.step.sem, 1)
                    done += 3
                    dve.wait_ge(*m.step.after(done))
                    dve.sem_inc(m.passed.sem, 1)
                assert done == NSTEP

                def drain(i, u, f, at, unused=False):
                    if unused and V <= f:
                        dve.wait_ge(*ring.full(*at))
                        dve.sem_inc(ring.drains(*at[1:]), 1)
                        return
                    if SPREAD <= f < OUT:
                        if f == SPREAD:
                            dve.wait_ge(*(ring.empty(*turn(i, u, LAST)) if i is not PAIRS else ring.empty(PAIRS, 0, LAST)))
                        dve.wait_ge(*ring.full(*at))
                        g = 2 * (f - SPREAD)
                        og = o[1 - u][:, g:g + 2, :].rearrange("p g t -> p (g t)")
                        dve.tensor_tensor(og, ring.bank(*at[1:])[:], og, ALU.mult).then_inc(ring.drains(*at[1:]), 1)
                    if f == OUT:
                        dve.wait_ge(*ring.full(*at))
                        rows = m.x_padded[:, bass.ds(TPB * (2 * i + u), TPB), :]
                        dve.tensor_tensor(rows, ring.bank(*at[1:])[:, 0:TPB * D].rearrange("p (t d) -> p t d", d=D), rows, ALU.add)\
                            .then_inc(ring.drains(*at[1:]), 1)
                    if V <= f < GROUP:
                        dve.wait_ge(*ring.full(*at))
                        if small:
                            to = v[1 - u][:].rearrange("p c (h w) -> p (c h) w", w=W)[:, :, 0:hd]
                            dve.tensor_copy(to, ring.bank(*at[1:])[:].rearrange("p (n e) -> p n e", e=hd)).then_inc(ring.drains(*at[1:]), 1)
                        else:
                            c, half = divmod(f - V, VW // 512)
                            dve.tensor_copy(v[1 - u][:, c, cols512(half)], ring.bank(*at[1:])[:]).then_inc(ring.drains(*at[1:]), 1)

                def convert_mask(i, u):
                    b = 2 * i + u + 1
                    if mask is not None:
                        dve.wait_ge(*m.streamed[1 - u].after(per_load * (i + u + 1)))
                        of = mask_i[1 - u][:]
                    else:
                        of = key_u8[:, bass.ds(b * KV, KV)].unsqueeze(1)
                    dve.tensor_scalar(mask_b[1 - u][:], of, 0.0, MASKED, ALU.is_equal, ALU.mult).then_inc(m.mask_ready.sem, 1)

                def invert_sums(b, u):
                    dve.wait_ge(*m.probs_ready.after(UNITS * b))
                    dve.wait_ge(*m.inv_split.after(b))
                    dve.reciprocal(inv[:], sums[:, 1 - u].rearrange("p t h -> p (t h)")).then_inc(m.sums_inverted.sem, 1)

                def maximum(i, u, n):
                    dve.wait_ge(*m.scores_ready.after(UNITS * (2 * i + u) + n + 1))
                    if n == 0:
                        dve.wait_ge(*(m.mask_ready.after(2 * i + u + 1) if masked else m.bias_moved[u].after(16 * (i + 1))))
                    dve.sem_inc(m.passed.sem, 1)
                    dve.tensor_tensor_reduce(out=minus_s[n % (2 * DEEP)][:], in0=s_ps[n % DEEP][:], in1=added(u, n), scale=-1.0, scalar=3e38,
                                             op0=ALU.add, op1=ALU.min, accum_out=nmax[:, u, n:n + 1]).then_inc(m.max_ready.sem, 1)

                if masked:
                    convert_mask(-1, 1)
                for f in range(V, GROUP):
                    drain(-1, 1, f, prepared(f))
                for n in range(DEEP):
                    maximum(0, 0, n)
                def attend(i, u, last=False):
                    b = 2 * i + u
                    for n in range(DEEP, UNITS + DEEP):
                        c = n - DEEP
                        if not (last and n >= UNITS):
                            maximum(*ahead(i, u, n))
                        if not scalar_copies(c):
                            if c % (G * TPB) <= 1:
                                dve.wait_ge(*ring.full(*bank_before(i, u, c)))
                            dve.wait_ge(*m.turned.after(UNITS * b + c + 1 + (bv is not None)))
                            dve.tensor_copy(unit_pT(c), unit_turned(c)).then_inc(m.unit_copied[c % 2].sem, 1)
                        if c == 0:
                            invert_sums(b, u)
                        for f in due[c]:
                            drain(i, u, f, turn(i, u, f), unused=last and Q <= f < GROUP)
                        if c == UNITS // 2 and masked:
                            convert_mask(i, u)

                with dve.Fori(0, PAIRS - 1) as i:
                    for u in range(2):
                        attend(i, u)
                attend(PAIRS - 1, 0)
                attend(PAIRS - 1, 1, last=True)
                invert_sums(B, 0)
                for f in range(Q):
                    drain(PAIRS, 0, f, (PAIRS, 0, f))

            @block.scalar
            def _(act):
                def drain(i, u, f, at, unused=False):
                    if unused and f < V:
                        act.wait_ge(*ring.full(*at))
                        act.sem_inc(ring.drains(*at[1:]), 1)
                        return
                    if in_halves(f):
                        act.wait_ge(*ring.full(*at))
                        to = o[1 - u][:, NG - 1, :] if f == LAST else o[u][:, f - GROUP, :]
                        act.activation(to, ring.bank(*at[1:])[:, 0:S], ACT.Copy).then_inc(ring.drains(*at[1:]), 1)
                    if f == SUMS:
                        act.wait_ge(*ring.full(*at))
                        act.activation(invT[0:3 * HEADS, :], ring.bank(*at[1:])[0:3 * HEADS, 0:S], ACT.Copy).then_inc(ring.drains(*at[1:]), 1)
                    if Q <= f < K:
                        act.wait_ge(*ring.full(*at))
                        h = 2 * (f - Q)
                        act.activation(q[1 - u][:, h:h + 2, :].rearrange("p h s -> p (h s)"), ring.bank(*at[1:])[:], ACT.Copy)\
                            .then_inc(ring.drains(*at[1:]), 1)
                    if K <= f < V:
                        act.wait_ge(*ring.full(*at))
                        to = k_all[:]
                        if bk is None:
                            act.activation(to, ring.bank(*at[1:])[:], ACT.Copy).then_inc(ring.drains(*at[1:]), 1)
                        else:
                            act.activation(to, ring.bank(*at[1:])[:], ACT.Identity, bias=bk_s[:, 0:1]).then_inc(ring.drains(*at[1:]), 1)

                if small:
                    act.wait_ge(*m.qk_loaded.after(16 * NQK))
                    drain(-1, 1, K, prepared(K))
                else:
                    for n in range(4):
                        act.wait_ge(*m.weights_folded.after(n + 1))
                        act.activation(folded_heads(n), folds[n][:].rearrange("p (h d) -> p h d", d=D), ACT.Copy, scale=hd ** -0.5)\
                            .then_inc(m.folds_copied.sem, 1)
                for f in range(TURNS):
                    at = first(T0 + f)
                    act.wait_ge(*ring.full(*at))
                    act.activation(xnT[:, cols512(f)], ring.bank(*at[1:])[:], ACT.Copy).then_inc(ring.drains(*at[1:]), 1)
                if small:
                    act.wait_ge(*m.ready_made.after(1))
                    for f in range(TURNS):
                        at = first(T0 + TURNS + f)
                        act.wait_ge(*ring.full(*at))
                        if bq is None:
                            act.activation(q_all[:, cols512(f)], ring.bank(*at[1:])[:], ACT.Copy, scale=hd ** -0.5)\
                                .then_inc(ring.drains(*at[1:]), 1)
                        else:
                            act.activation(q_all[:, cols512(f)], ring.bank(*at[1:])[:], ACT.Identity, bias=bq_s[:, 0:1],
                                           scale=hd ** -0.5).then_inc(ring.drains(*at[1:]), 1)
                for f in range(V if small else Q, GROUP):
                    drain(-1, 1, f, prepared(f))
                def exponential(i, u, n):
                    h, j = divmod(n, TPB)
                    act.wait_ge(*m.max_ready.after(UNITS * (2 * i + u) + n + 1))
                    act.activation(probs[n % (2 * DEEP)][:], minus_s[n % (2 * DEEP)][:], ACT.Exp, bias=nmax[:, u, n:n + 1], scale=-1.0,
                                   accum_out=sums[:, u, j, h:h + 1]).then_inc(m.probs_ready.sem, 1)

                for n in range(DEEP):
                    exponential(0, 0, n)
                def attend(i, u, last=False):
                    b = 2 * i + u
                    for n in range(DEEP, UNITS + DEEP):
                        c = n - DEEP + 1
                        if c < UNITS and scalar_copies(c):
                            if c % (G * TPB) <= 1:
                                act.wait_ge(*ring.full(*bank_before(i, u, c)))
                            act.wait_ge(*m.turned.after(UNITS * b + c + 1 + (bv is not None)))
                            act.activation(unit_pT(c), unit_turned(c), ACT.Copy).then_inc(m.unit_copied[c % 2].sem, 1)
                        if not (last and n >= UNITS):
                            exponential(*ahead(i, u, n))
                        for f in due[n - DEEP]:
                            drain(i, u, f, turn(i, u, f), unused=last and Q <= f < GROUP)

                with act.Fori(0, PAIRS - 1) as i:
                    for u in range(2):
                        attend(i, u)
                attend(PAIRS - 1, 0)
                attend(PAIRS - 1, 1, last=True)
                for f in range(Q):
                    drain(PAIRS, 0, f, (PAIRS, 0, f))

            @block.tensor
            def _(pe):
                def fold_bias():
                    pe.wait_ge(*m.loaded.after(16 * NLOAD))
                    pe.matmul(t_ps[0][0:1, 0:D], k["ones"][0:1, 0:1], bo_s[:], start=True, stop=False)
                    for g in range(NG):
                        ins = pe.matmul(t_ps[0][0:1, 0:D], bv_s[:, g:g + 1], wo_s[:, g, :], start=False, stop=(g == NG - 1))
                    ins.then_inc(m.turned.sem, 1)
                def group_outputs(i, u, f, at, halves=range(2)):
                    b = 2 * i + u
                    bank = ring.bank(*at[1:])
                    of, g = (1 - u, NG - 1) if f == LAST else (u, f - GROUP)
                    if 0 in halves:
                        for copied in m.unit_copied:
                            pe.wait_ge(*copied.after(UNITS // 2 * b + (0 if f == LAST else G * TPB // 2 * (g + 1))))
                        pe.wait_ge(*ring.free(*at))
                    for half in halves:
                        for c in range(half * CPB // 2, (half + 1) * CPB // 2):
                            for hh in range(G):
                                ins = pe.matmul(bank[W * hh:W * (hh + 1), 0:S], v[of][:, c, (G * g + hh) * W:(G * g + hh + 1) * W],
                                                pT[g % 2][:, hh, c, :], start=(c == 0), stop=(c == CPB - 1))
                    if 1 in halves:
                        ins.then_inc(ring.fills(*at[1:]), 1)

                def fill(i, u, f, at, unused=False):
                    if unused:
                        pe.wait_ge(*ring.free(*at))
                        pe.sem_inc(ring.fills(*at[1:]), 1)
                        return
                    b = 2 * i + u
                    bank = ring.bank(*at[1:])
                    if f == SUMS:
                        pe.wait_ge(*m.inv_split.after(b + 1))
                        pe.wait_ge(*ring.free(*at))
                        for j in range(TPB):
                            ins = pe.matmul(bank[0:3 * HEADS, j * P:(j + 1) * P], inv_parts[:, j].rearrange("p r h -> p (r h)"), k["ident_bf"],
                                            start=True, stop=True)
                    elif f < OUT:
                        if f == SPREAD:
                            pe.wait_ge(*ring.empty(at[0], at[1], at[2] + (order.index(SUMS) - order.index(SPREAD) if i is not PAIRS else -1)))
                        pe.wait_ge(*ring.free(*at))
                        for t in range(2):
                            g = 2 * (f - SPREAD) + t
                            ins = pe.matmul(bank[:, t * S:(t + 1) * S], spread[:, g * P:(g + 1) * P], invT[:],
                                            start=True, stop=True)
                    elif f == OUT:
                        pe.wait_ge(*ring.free(*at))
                        pe.wait_ge(*ring.empty(at[0], at[1], at[2] + (order.index(OUT - 1) - order.index(OUT) if i is not PAIRS else -1)))
                        for j in range(TPB):
                            out = bank[:, j * D:(j + 1) * D]
                            pe.matmul(out, k["ones"][0:1, :], bo_s[:], start=True, stop=False)
                            for g in range(NG):
                                ins = pe.matmul(out, o[1 - u][:, g, j * P:(j + 1) * P], wo_s[:, g, :], start=False, stop=(g == NG - 1))
                    elif f < K:
                        pe.wait_ge(*ring.free(*at))
                        for t in range(2):
                            ins = pe.matmul(bank[:, t * S:(t + 1) * S], wqk[:, 2 * (f - Q) + t, :], xnT[:, bass.ds((b + 1) * S, S)],
                                            start=True, stop=True)
                    elif f < V:
                        pe.wait_ge(*m.streamed[1 - u].after(per_load * (i + u + 1)))
                        pe.wait_ge(*ring.free(*at))
                        ins = pe.matmul(bank[:], wk_s[:, 0, :], ctxT[1 - u][:], start=True, stop=True)
                    else:
                        if not small and f == V:
                            pe.wait_ge(*m.streamed[1 - u].after(per_load * (i + u + 1)))
                        pe.wait_ge(*ring.free(*at))
                        if small:
                            for c in range(CPB):
                                ins = pe.matmul(bank[:, c * D:(c + 1) * D], ctxT[1 - u][:, c * P:(c + 1) * P], wv_s[:], start=True, stop=True)
                        else:
                            c, half = divmod(f - V, VW // 512)
                            ins = pe.matmul(bank[:], ctxT[1 - u][:, c * P:(c + 1) * P], wv_s[:, cols512(half)], start=True, stop=True)
                    ins.then_inc(ring.fills(*at[1:]), 1)

                def scores(i, u, n):
                    h, j = divmod(n, TPB)
                    out = s_ps[n % DEEP][:]
                    if small and n == 0:
                        pe.wait_ge(*m.stacked[u].after(16 * NSTACK * (i + 1)))
                    pe.matmul(out, q[u][:, h, j * P:(j + 1) * P], kT[u][:, h // 2, :] if small else ctxT[u][:], start=True, stop=True)\
                        .then_inc(m.scores_ready.sem, 1)

                pe.wait_ge(*m.qk_loaded.after(16 * NQK))
                if small:
                    fill(-1, 1, K, prepared(K))
                else:
                    for n in range(4):
                        for h in range(QUART):
                            own, pair = slice(hd * (n % 2), hd * (n % 2 + 1)), n // 2 * QUART + h
                            ins = pe.matmul(folds[n][:, h * D:(h + 1) * D], wq_s[own, pair, :], wk_s[own, pair, :], start=True, stop=True)
                        ins.then_inc(m.weights_folded.sem, 1)
                for f in range(TURNS):
                    at = first(T0 + f)
                    pe.wait_ge(*m.normed.after(4 * f + 4))
                    pe.wait_ge(*ring.free(*at))
                    for j in range(4):
                        ins = pe.transpose(ring.bank(*at[1:])[:, j * P:(j + 1) * P], norm.xn[0][:, 4 * f + j, :], k["ident"])
                    ins.then_inc(ring.fills(*at[1:]), 1)
                if bv is not None:
                    fold_bias()
                for f in range(TURNS if small else 0):
                    at = first(T0 + TURNS + f)
                    pe.wait_ge(*ring.empty(*first(T0 + f)))
                    pe.wait_ge(*ring.free(*at))
                    pe.matmul(ring.bank(*at[1:])[:], wq_s[:, 0, :], xnT[:, cols512(f)], start=True, stop=True)\
                        .then_inc(ring.fills(*at[1:]), 1)
                pe.wait_ge(*m.ready_made.after(1))
                if not small:
                    pe.wait_ge(*m.folds_copied.after(4))
                for f in range(max(0, TURNS - RING), TURNS):
                    pe.wait_ge(*ring.empty(*first(T0 + f)))
                for f in range(V if small else Q, GROUP):
                    fill(-1, 1, f, prepared(f))
                for f in range(max(V, GROUP - RING), GROUP):
                    pe.wait_ge(*ring.empty(*prepared(f)))
                for n in range(DEEP):
                    scores(0, 0, n)
                pe.wait_ge(*m.zeroed.after(NFIRST + NLATER))
                pe.wait_ge(*m.step.after(NSTEP))
                def attend(i, u, last=False):
                    b = 2 * i + u
                    for n in range(UNITS):
                        if n + DEEP == UNITS and not last:
                            for f in range(max(Q, V - RING), V):
                                pe.wait_ge(*ring.empty(*turn(i, u, f)))
                        if not (last and n + DEEP >= UNITS):
                            pe.wait_ge(*m.max_ready.after(UNITS * b + n + 1))
                            scores(*ahead(i, u, n + DEEP))
                        pe.wait_ge(*m.probs_ready.after(UNITS * b + n + 1))
                        pe.wait_ge(*m.unit_copied[n % 2].after(UNITS // 2 * b + n // 2))
                        for c in range(CPB):
                            ins = pe.transpose(t_ps[n % 2][:, c * P:(c + 1) * P], probs[n % (2 * DEEP)][:, c * P:(c + 1) * P],
                                               k["ident"])
                        ins.then_inc(m.turned.sem, 1)
                        for f, half in steps[n]:
                            if in_halves(f):
                                group_outputs(i, u, f, turn(i, u, f), [half])
                            else:
                                fill(i, u, f, turn(i, u, f), unused=last and Q <= f < GROUP)
                    for f in range(max(V, GROUP - 4), GROUP):
                        pe.wait_ge(*ring.empty(*turn(i, u, f)))

                with pe.Fori(0, PAIRS - 1) as i:
                    for u in range(2):
                        attend(i, u)
                attend(PAIRS - 1, 0)
                attend(PAIRS - 1, 1, last=True)
                group_outputs(PAIRS, 0, LAST, (PAIRS, 0, LAST))
                for f in range(SUMS, Q):
                    fill(PAIRS, 0, f, (PAIRS, 0, f))
        norm.close(1)
        ring.close(Q)
        for s, n in ((m.loaded, 16 * NLOAD), (m.step, NSTEP), (m.ready_made, 1), (m.qk_loaded, 16 * NQK),
                     (m.zeroed, NFIRST + NLATER), (m.streamed[0], per_load * (PAIRS + 1)),
                     (m.streamed[1], per_load * (PAIRS + 1)), (m.mask_ready, B + 1 if masked else 0),
                     (m.bias_moved[0], 0 if masked else 16 * (PAIRS + 1)), (m.bias_moved[1], 0 if masked else 16 * (PAIRS + 1)),
                     (m.pool_step, 6 * (B + 1) if small else 0), (m.parts_split, 2 * (B + 1) if small else 0),
                     (m.stacked[0], 16 * NSTACK * (PAIRS + 1) if small else 0), (m.stacked[1], 16 * NSTACK * PAIRS if small else 0),
                     (m.scores_ready, UNITS * B), (m.max_ready, UNITS * B), (m.probs_ready, UNITS * B), (m.turned, UNITS * B + (bv is not None)),
                     (m.unit_copied[0], UNITS * B // 2), (m.unit_copied[1], UNITS * B // 2),
                     (m.sums_inverted, B + 1), (m.inv_step, 3 * (B + 1)), (m.inv_split, B + 1), (m.weights_folded, 0 if small else 4),
                     (m.folds_copied, 0 if small else 4)):
            s.before += n


def l1_cross_attention(m):
    d = m.dram
    head_attention(m, "l1x", 8, d["L1_xattn_Wq"], d["L1_xattn_Wk"], d["L1_xattn_Wv"], d["L1_xattn_Wo"], d["L1_xattn_bo"],
                   mask=d["mask"])


def l2_cross_attention(m):
    d = m.dram
    head_attention(m, "l2x", 64, d["L2_xattn_Wq"], d["L2_xattn_Wk"], d["L2_xattn_Wv"],
                   d["L2_xattn_Wout"], d["L2_xattn_b_out"], key_mask=d["key_mask"])


def l3_cross_attention(m):
    d = m.dram
    head_attention(m, "l3x", 8, d["L3_xattn_wq"], d["L3_xattn_wk"], d["L3_xattn_wv"], d["L3_xattn_wo"], d["L3_xattn_bo"],
                   bq=d["L3_xattn_bq"], bk=d["L3_xattn_bk"], bv=d["L3_xattn_bv"], key_bias=d["time_bias"])


def l1_bit_ffn(m):
    nc, d, x, k = m.nc, m.dram, m.x, m.consts
    H = 512
    HC = H // P
    STEPS = 4
    TS = NT // STEPS
    EPS_NORM, EPS_Q, QMAX = 1e-8, 1e-5, 127.0
    with ExitStack() as ctx:
        sb = lambda name, shape, dt=F32: sbuf(m, ctx, f"{name}_l1f", shape, dt)
        norm = Norm(m, ctx, NT, "l1f", buffers=1)
        xn = norm.xn[0]
        w = sb("w", [P, 2, H])
        wq = sb("wq", [P, 2, H], BF16)
        n1w, n2w = sb("n1w", [P, D]), sb("n2w", [P, H])
        gain, offset = sb("gain", [P, 1]), sb("offset", [P, 1])
        wsum, wmean, wscale = sb("wsum", [P, 2]), sb("wmean", [P, 2]), sb("wscale", [P, 2])
        small = lambda name: [sb(f"{name}{s}", [P, NT]) for s in range(2)]
        ss, ms, rr, am, iv, qs, cc = small("ss"), small("ms"), small("rr"), small("am"), small("iv"), small("qs"), small("cc")
        junk = sb("junk", [P, TS, H])
        xr, xq = sb("xr", [P, NT, D]), sb("xq", [P, NT, D], BF16)
        xqT = sb("xqT", [P, NT * P], BF16)
        h, hr, hq = sb("h", [P, NT, H]), sb("hr", [P, NT, H]), sb("hq", [P, NT, H], BF16)
        hqT = sb("hqT", [P, NT, H], BF16)
        h_ps = [psum(m, ctx, f"h_ps{j}_l1f", [P, H]) for j in range(TS)]
        t_ps = [psum(m, ctx, f"t_ps{j}_l1f", [P, 512]) for j in range(2)]
        y_ps = psum(m, ctx, "y_ps_l1f", [P, TS * D])
        w_ps = psum(m, ctx, "w_ps_l1f", [P, 2])
        SETUP, ROW_STEPS = 6, 6 + TS

        def looped(eng, ahead, behind):
            for n in range(2):
                ahead(n)
            with eng.Fori(0, STEPS - 2) as i:
                ahead(i + 2)
                behind(i)
            for n in range(STEPS - 2, STEPS):
                behind(n)

        with nc.Block() as block:
            @block.sync
            def _(sp):
                for dst, src in ((w[:, 0, :], d["L1_ffn_w1"]),
                                 (w[:, 1, :].rearrange("p (c d) -> p c d", d=D), d["L1_ffn_w2"].rearrange("(c p) d -> p c d", p=P)),
                                 (n1w[:], d["L1_ffn_norm1_w"][0, :].partition_broadcast(P)),
                                 (n2w[:], d["L1_ffn_norm2_w"][0, :].partition_broadcast(P)),
                                 (gain[:], d["L1_ffn_act_scale"][0, :].partition_broadcast(P)),
                                 (offset[:], d["L1_ffn_act_bias"][0, :].partition_broadcast(P))):
                    sp.dma_start(dst, src).then_inc(m.loaded.sem, 16)
                sp.wait_ge(*m.loaded.after(96))

            @block.gpsimd
            def _(pool):
                norm.pool(pool, 0)
                pool.wait_ge(*m.squares_ready.after(1))
                pool.tensor_tensor(rr[0][:], ms[0][:], k["minus_half"][:, 0:NT], ALU.pow).then_inc(m.powers_ready.sem, 1)
                with pool.Fori(0, STEPS) as i:
                    rows = bass.ds(TS * i, TS)
                    pool.wait_ge(*m.squares_ready.after(i + 2))
                    pool.sem_inc(m.passed.sem, 1)
                    pool.tensor_tensor(rr[1][:, rows], ms[1][:, rows], k["minus_half"][:, 0:TS], ALU.pow).then_inc(m.powers_ready.sem, 1)

            @block.vector
            def _(dve):
                norm.vector(dve, 0, 0, lambda j: x[:, j, :])
                dve.wait_ge(*m.loaded.after(96))
                dve.tensor_reduce(wsum[:], w[:], AX.X, ALU.add, apply_absolute_value=True).then_inc(m.ready_made.sem, 1)
                dve.wait_ge(*m.max_spread.after(1))
                dve.tensor_scalar(wmean[:], w_ps[:], 1.0 / (H * D), EPS_Q, ALU.mult, ALU.max).then_inc(m.step.sem, 1)
                dve.wait_ge(*m.step.after(1))
                dve.reciprocal(wscale[:], wmean[:]).then_inc(m.step.sem, 1)
                dve.wait_ge(*m.step.after(2))
                for n in range(2):
                    dve.tensor_scalar(w[:, n, :], w[:, n, :], wscale[:, n:n + 1], MAGIC, ALU.mult, ALU.add).then_inc(m.step.sem, 1)
                dve.wait_ge(*m.step.after(4))
                dve.tensor_scalar(w[:], w[:], MAGIC, 1.0, ALU.subtract, ALU.min).then_inc(m.step.sem, 1)
                dve.wait_ge(*m.step.after(5))
                dve.tensor_scalar(wq[:], w[:], -1.0, None, ALU.max).then_inc(m.step.sem, 1)
                dve.wait_ge(*m.step.after(6))
                dve.engine_nop().then_inc(m.ready_made.sem, 1)

                def quantise(s, n, at, tiles, rows, src, weight, r, dst, summed, width):
                    dve.tensor_tensor(r[:, rows, :], src[:, rows, :], weight[:].unsqueeze(1).to_broadcast([P, tiles, width]), ALU.mult)\
                        .then_inc(m.step.sem, 1)
                    dve.wait_ge(*m.squares_summed.after(summed))
                    dve.tensor_scalar(ms[s][:, rows], ss[s][:, rows], 1.0 / width, EPS_NORM, ALU.mult, ALU.add)\
                        .then_inc(m.squares_ready.sem, 1)
                    dve.wait_ge(*m.step.after(at + 1))
                    dve.tensor_reduce(am[s][:, rows], r[:, rows, :], AX.X, ALU.max, apply_absolute_value=True).then_inc(m.step.sem, 1)
                    dve.wait_ge(*m.step.after(at + 2))
                    dve.wait_ge(*m.powers_ready.after(n))
                    dve.tensor_tensor(am[s][:, rows], am[s][:, rows], rr[s][:, rows], ALU.mult).then_inc(m.step.sem, 1)
                    dve.wait_ge(*m.step.after(at + 3))
                    dve.tensor_scalar(am[s][:, rows], am[s][:, rows], EPS_Q, None, ALU.max).then_inc(m.step.sem, 1)
                    dve.wait_ge(*m.step.after(at + 4))
                    dve.reciprocal(iv[s][:, rows], am[s][:, rows]).then_inc(m.step.sem, 1)
                    dve.tensor_scalar(cc[s][:, rows], am[s][:, rows], 1.0 / QMAX, wmean[:, s:s + 1], ALU.mult, ALU.mult)\
                        .then_inc(m.scales_ready.sem, 1)
                    dve.wait_ge(*m.step.after(at + 5))
                    dve.scalar_tensor_tensor(out=qs[s][:, rows], in0=iv[s][:, rows], scalar=QMAX, in1=rr[s][:, rows],
                                             op0=ALU.mult, op1=ALU.mult).then_inc(m.step.sem, 1)
                    dve.wait_ge(*m.step.after(at + 6))

                def round_rows(s, at, tiles, tile, r, dst, rows):
                    for j in range(tiles):
                        row = r[:, tile(j), :]
                        dve.tensor_scalar(row, row, qs[s][:, tile(j)], MAGIC, ALU.mult, ALU.add).then_inc(m.step.sem, 1)
                    dve.wait_ge(*m.step.after(at + tiles))
                    dve.tensor_scalar(dst[:, rows, :], r[:, rows, :], MAGIC, QMAX, ALU.subtract, ALU.min).then_inc(m.x_quantised.sem, 1)

                dve.wait_ge(*m.normed.after(NT))
                quantise(0, 1, SETUP, NT, slice(0, NT), xn, n1w, xr, xq, NT, D)
                round_rows(0, SETUP + 6, NT, lambda j: slice(j, j + 1), xr, xq, slice(0, NT))

                def quantise_hidden(i):
                    at = SETUP + 6 + NT + ROW_STEPS * i
                    rows = slice(0, TS) if isinstance(i, int) and i == 0 else bass.ds(TS * i, TS)
                    dve.wait_ge(*m.squared_affine.after(i + 1))
                    quantise(1, i + 2, at, TS, rows, h, n2w, hr, hq, NT + TS * (i + 1), H)
                    round_rows(1, at + 6, TS, lambda j: bass.ds(TS * i + j, 1), hr, hq, rows)

                def add_output(i):
                    dve.wait_ge(*m.pv_done.after(i + 1))
                    for j in range(TS):
                        rows = x[:, bass.ds(TS * i + j, 1), :].rearrange("p t d -> p (t d)")
                        ins = dve.scalar_tensor_tensor(out=rows, in0=y_ps[:, j * D:(j + 1) * D], scalar=cc[1][:, bass.ds(TS * i + j, 1)],
                                                       in1=rows, op0=ALU.mult, op1=ALU.add)
                    ins.then_inc(m.x_updated.sem, 1)

                looped(dve, quantise_hidden, add_output)
                dve.wait_ge(*m.x_updated.after(STEPS))

            @block.scalar
            def _(act):
                for j in range(NT):
                    act.wait_ge(*m.normed.after(j + 1))
                    act.activation(junk[:, 0, 0:D], xn[:, j, :], ACT.Square, accum_out=ss[0][:, j:j + 1]).then_inc(m.squares_summed.sem, 1)
                    act.wait_ge(*m.squares_summed.after(j + 1))
                for u in range(2):
                    act.wait_ge(*m.x_turned.after(u + 1))
                    act.activation(xqT[:, u * NT // 2 * P:(u + 1) * NT // 2 * P], t_ps[u][:].bitcast(BF16), ACT.Copy)\
                        .then_inc(m.turned_copied.sem, 1)

                def square_hidden(i):
                    act.wait_ge(*m.scales_ready.after(1))
                    for j in range(TS):
                        act.wait_ge(*m.scores_ready.after(TS * i + j + 1))
                        act.sem_inc(m.passed.sem, 1)
                        act.activation(h[:, bass.ds(TS * i + j, 1), :].rearrange("p t n -> p (t n)"), h_ps[j][:], ACT.Relu,
                                       scale=cc[0][:, bass.ds(TS * i + j, 1)]).then_inc(m.act_step.sem, 1)
                    rows = h[:, bass.ds(TS * i, TS), :]
                    act.wait_ge(*m.act_step.after(TS * (i + 1)))
                    act.sem_inc(m.passed.sem, 1)
                    act.activation(rows, rows, ACT.Square).then_inc(m.h_squared.sem, 1)
                    act.wait_ge(*m.h_squared.after(i + 1))
                    act.sem_inc(m.passed.sem, 1)
                    act.activation(rows, rows, ACT.Identity, scale=gain[:, 0:1], bias=offset[:, 0:1]).then_inc(m.squared_affine.sem, 1)
                    act.wait_ge(*m.squared_affine.after(i + 1))
                    act.sem_inc(m.passed.sem, 1)
                    for j in range(TS):
                        act.activation(junk[:, j, :], h[:, bass.ds(TS * i + j, 1), :].rearrange("p t n -> p (t n)"), ACT.Square,
                                       accum_out=ss[1][:, bass.ds(TS * i + j, 1)]).then_inc(m.squares_summed.sem, 1)

                def copy_turned(i):
                    for u in range(2):
                        act.wait_ge(*m.turned.after(2 * i + u + 1))
                        act.activation(hqT[:, bass.ds(TS * i + 2 * u, 2), :].rearrange("p t n -> p (t n)"), t_ps[u][:].bitcast(BF16), ACT.Copy)\
                            .then_inc(m.turned_copied.sem, 1)

                looped(act, square_hidden, copy_turned)

            @block.tensor
            def _(pe):
                pe.wait_ge(*m.ready_made.after(1))
                pe.matmul(w_ps[:], k["ones"], wsum[:], start=True, stop=True).then_inc(m.max_spread.sem, 1)
                pe.wait_ge(*m.x_quantised.after(1))
                for u in range(2):
                    for j in range(NT // 2):
                        ins = pe.transpose(t_ps[u][:].bitcast(BF16)[:, j * P:(j + 1) * P], xq[:, u * NT // 2 + j, :], k["ident_bf"])
                    ins.then_inc(m.x_turned.sem, 1)
                pe.wait_ge(*m.ready_made.after(2))
                pe.wait_ge(*m.turned_copied.after(2))

                def hidden(i):
                    for j in range(TS):
                        if not (isinstance(i, int) and i == 0):
                            pe.wait_ge(*m.act_step.after(TS * (i - 1) + j + 1))
                        pe.matmul(h_ps[j][:], xqT[:, bass.ds((TS * i + j) * P, P)], wq[:, 0, :], start=True, stop=True)\
                            .then_inc(m.scores_ready.sem, 1)

                def output(i):
                    pe.wait_ge(*m.x_quantised.after(i + 2))
                    for u in range(2):
                        pe.wait_ge(*m.turned_copied.after(2 * i + u + 1))
                        for j in range(2):
                            for c in range(HC):
                                ins = pe.transpose(t_ps[u][:].bitcast(BF16)[:, (j * HC + c) * P:(j * HC + c + 1) * P],
                                                   hq[:, bass.ds(TS * i + 2 * u + j, 1), c * P:(c + 1) * P].rearrange("p t n -> p (t n)"),
                                                   k["ident_bf"])
                        ins.then_inc(m.turned.sem, 1)
                    pe.wait_ge(*m.x_updated.after(i))
                    for u in range(2):
                        pe.wait_ge(*m.turned_copied.after(2 * i + u + 3))
                        for j in range(2):
                            t = 2 * u + j
                            for c in range(HC):
                                ins = pe.matmul(y_ps[:, t * D:(t + 1) * D],
                                                hqT[:, bass.ds(TS * i + t, 1), c * P:(c + 1) * P].rearrange("p t n -> p (t n)"),
                                                wq[:, 1, c * D:(c + 1) * D], start=(c == 0), stop=(c == HC - 1))
                    ins.then_inc(m.pv_done.sem, 1)

                looped(pe, hidden, output)
        norm.close(1)
        for s, n in ((m.loaded, 96), (m.ready_made, 2), (m.max_spread, 1), (m.step, SETUP + 6 + NT + ROW_STEPS * STEPS),
                     (m.squares_ready, 1 + STEPS), (m.powers_ready, 1 + STEPS), (m.scales_ready, 1 + STEPS), (m.act_step, NT),
                     (m.squares_summed, 2 * NT), (m.h_squared, STEPS), (m.squared_affine, STEPS), (m.scores_ready, NT),
                     (m.x_quantised, 1 + STEPS), (m.x_turned, 2), (m.turned, 2 * STEPS), (m.turned_copied, 2 + 2 * STEPS),
                     (m.pv_done, STEPS), (m.x_updated, STEPS)):
            s.before += n


def shift_tokens(m, pe, dve, act, ring, first, hb):
    x, k = m.x, m.consts
    half, tiles = D // 2, NT // 2
    if dve is not None:
        dve.tensor_copy(hb[:, :, 0:half], x[:, :, 0:half]).then_inc(m.unshifted.sem, 1)
    for w in range(2):
        at = first(w)
        bank = ring.bank(*at[1:])[:].rearrange("p (t e) -> p t e", e=half)
        if pe is not None:
            pe.wait_ge(*ring.free(*at))
            pe.matmul(bank, k["shift"], x[:, tiles * w:tiles * (w + 1), half:D], start=True, stop=False)
            pe.matmul(bank[:, 1:tiles:2, :], k["last"], x[:, tiles * w:tiles * (w + 1):2, half:D], start=False, stop=True)\
                .then_inc(ring.fills(*at[1:]), 1)
        if act is not None:
            act.wait_ge(*ring.full(*at))
            act.activation(hb[:, tiles * w:tiles * (w + 1), half:D], bank, ACT.Copy).then_inc(ring.drains(*at[1:]), 1)


def local_attention(m, layer):
    nc, d, x, k = m.nc, m.dram, m.x, m.consts
    NH, HD = 8, 64
    INNER = NH * HD
    NG = NH // 2
    BAND = 3 * P
    TILES = (slice(0, P), slice(P, BAND))
    DEEP, RING = 2, 4
    QK = 0
    TURN = QK + 2 * TPB
    V = TURN + 2 * TPB
    LAST = V + TPB
    SUMS = LAST + 1
    SPREAD = SUMS + 1
    OUT = SPREAD + NG // 2
    GROUP = OUT + 1
    PER = GROUP + NG - 1
    after = {QK: 1, QK + 1: 1, QK + 2: 2, QK + 3: 2, LAST: 1, SUMS: 2, TURN: 1, TURN + 1: 3, TURN + 2: 3, TURN + 3: 4, SPREAD: 5,
             SPREAD + 1: 5, V: 4, V + 1: 6, OUT: 6}
    after.update({GROUP + g: 2 * g + 3 for g in range(NG - 1)})
    SQUARED, SUMMED, OWN = (1, 4), (2, 6), (4, 6)
    order = sorted(range(PER), key=lambda f: (after[f], f < GROUP, f))
    due = [[f for f in order if after[f] == n] for n in range(NH)]
    SHIFTS, TURNS = 2, NT // 4
    AHEAD_OF_LOOP = [(0, f) for f in range(LAST)] + [(1, f) for f in range(QK, TURN)]
    CHAIN = 3 * TPB
    with ExitStack() as ctx:
        sb = lambda name, shape, dt=F32: sbuf(m, ctx, f"{name}_l2a{layer}", shape, dt)
        wqkv = sb("wqkv", [P, 3 * INNER])
        wo = sb("wo", [P, NG, D])
        scales = sb("scales", [P, 2, HD])
        ta, tb = sb("ta", [P, 2, TPB, HD]), sb("tb", [P, 2, TPB, HD])
        hb = sb("hb", [P, NT, D])
        hT = sb("hT", [P, (B + 3) * S])
        hs = [sb(f"hs{u}", [P, S]) for u in range(2)]
        qk = sb("qk", [P, TPB, 2, NH, HD])
        sq = sb("sq", [P, TPB, 2 * INNER])
        ss = sb("ss", [P, TPB, 2 * NH])
        ssc, rn = sb("ssc", [P, TPB * 2 * NH]), sb("rn", [P, TPB * 2 * NH])
        own, other = sb("own", [P, TPB, 2, NH, HD]), sb("other", [P, TPB, 2, NH, HD])
        q = [sb(f"q{u}", [P, NH, S]) for u in range(2)]
        kT = [sb(f"kT{u}", [P, NG, S]) for u in range(2)]
        v = [sb(f"v{u}", [P, TPB, INNER]) for u in range(2)]
        nmax = sb("nmax", [P, 2, NH * TPB])
        sums = sb("sums", [P, 2, TPB, NH])
        inv, inv_rest, nothing = [sb(n, [P, TPB * NH]) for n in ("inv", "inv_rest", "nothing")]
        inv_parts = sb("inv_parts", [P, TPB, 3, HEADS], BF16)
        invT = sb("invT", [P, S], BF16)
        minus_s = [sb(f"minus_s{n}", [P, BAND]) for n in range(2 * DEEP)]
        probs = [sb(f"probs{n}", [P, BAND]) for n in range(2 * DEEP)]
        pT = [sb(f"pT{n}", [P, 2, 3, P]) for n in range(2)]
        o = [sb(f"o{u}", [P, NG, S]) for u in range(2)]
        ring = Ring([psum(m, ctx, f"ring{n}_l2a{layer}", [P, 512]) for n in range(RING)], m.filled, m.drained, PER,
                    lead=SHIFTS + TURNS + len(AHEAD_OF_LOOP))
        s_ps = [psum(m, ctx, f"s_ps{n}_l2a{layer}", [P, 512]) for n in range(DEEP)]
        t_ps = [psum(m, ctx, f"t_ps{n}_l2a{layer}", [P, 512]) for n in range(2)]
        first = lambda f: (0, 0, f - ring.lead)
        prepared = lambda b, f: first(SHIFTS + TURNS + AHEAD_OF_LOOP.index((b, f)))
        turn = lambda i, u, f: (i, u, order.index(f))
        last_turn = lambda i, u: (i - 1 + u, 1 - u)
        ahead = lambda i, u, n: (i, u, n) if n < NH else (i + u, 1 - u, n - NH)

        def group_before(i, u, g):
            return turn(i, u, GROUP + g - 2) if g >= 2 else turn(i, u, LAST) if g == 1 else turn(*last_turn(i, u), GROUP + NG + g - 2)

        def other_half(eng, j, w):
            for hf in range(2):
                to, of = slice(32 * hf, 32 * hf + 32), slice(32 - 32 * hf, 64 - 32 * hf)
                eng.tensor_tensor(other[:, j, w, :, to], qk[:, j, w, :, of], tb[:, w, j, to].unsqueeze(1).to_broadcast([P, NH, 32]),
                                  ALU.mult).then_inc(m.rotated.sem, 1)

        with nc.Block() as block:
            @block.sync
            def _(sp):
                for dst, src in ((wqkv[:], d["L2_ffn_wqkv"][layer]),
                                 (wo[:], d["L2_ffn_wo"][layer].rearrange("(g p) n -> p g n", p=P)),
                                 (scales[:, 0, :], d["L2_ffn_q_scale"][layer].partition_broadcast(P)),
                                 (scales[:, 1, :], d["L2_ffn_k_scale"][layer].partition_broadcast(P))):
                    sp.dma_start(dst, src).then_inc(m.loaded.sem, 16)
                sp.wait_ge(*m.loaded.after(64))

            @block.gpsimd
            def _(pool):
                zeros = [hT[:, B * S:], o[1][:], nothing[:], inv_parts[:], invT[:]] + [t[:] for t in q]
                for t in zeros:
                    pool.memset(t, 0.0).then_inc(m.zeroed.sem, 1)
                pool.memset(sums[:, 1], 1.0).then_inc(m.zeroed.sem, 1)
                pool.wait_ge(*m.ready_made.after(6))
                pool.sem_inc(m.passed.sem, 1)
                pool.wait_ge(*m.zeroed.after(8))
                pool.sem_inc(m.passed.sem, 1)

                def split_inv(b):
                    part = lambda r: inv_parts[:, :, r, 0:NH]
                    heads = lambda t: t[:].rearrange("p (t h) -> p t h", h=NH)
                    pool.wait_ge(*m.sums_inverted.after(b + 1))
                    pool.tensor_tensor(part(0), heads(inv), heads(nothing), ALU.add).then_inc(m.inv_step.sem, 1)
                    pool.wait_ge(*m.inv_step.after(3 * b + 1))
                    pool.tensor_tensor(heads(inv_rest), heads(inv), part(0), ALU.subtract).then_inc(m.inv_step.sem, 1)
                    pool.wait_ge(*m.inv_step.after(3 * b + 2))
                    pool.tensor_tensor(part(1), heads(inv_rest), heads(nothing), ALU.add).then_inc(m.inv_step.sem, 1)
                    pool.wait_ge(*m.inv_step.after(3 * b + 3))
                    pool.tensor_tensor(part(2), heads(inv_rest), part(1), ALU.subtract).then_inc(m.inv_split.sem, 1)

                def rotate(b, at):
                    for j in range(TPB):
                        if not (isinstance(b, int) and b == 0):
                            pool.wait_ge(*m.step.after(CHAIN * (b - 1) + 2 * TPB + j + 1))
                            pool.sem_inc(m.passed.sem, 1)
                        for w in range(1 if isinstance(b, int) and b == 0 else 2):
                            pool.wait_ge(*ring.empty(*at(QK + 2 * j + w)))
                            other_half(pool, j, w)
                    for j in range(TPB):
                        cols = slice(j * 2 * NH, (j + 1) * 2 * NH)
                        pool.wait_ge(*m.squares_ready.after(TPB * b + j + 1))
                        pool.tensor_tensor(rn[:, cols], ssc[:, cols], k["minus_half"][:, 0:2 * NH], ALU.pow).then_inc(m.powers_ready.sem, 1)

                for b in range(2):
                    rotate(b, lambda f: prepared(b, f))
                def attend(i, u, left=2):
                    split_inv(2 * i + u)
                    if left >= 2:
                        rotate(2 * i + u + 2, lambda f: turn(i, u, f))

                with pool.Fori(0, PAIRS - 1) as i:
                    for u in range(2):
                        attend(i, u)
                attend(PAIRS - 1, 0, left=1)
                attend(PAIRS - 1, 1, left=0)
                split_inv(B)

            @block.vector
            def _(dve):
                shift_tokens(m, None, dve, None, ring, first, hb)
                dve.wait_ge(*m.loaded.after(64))
                for w, (a, bb) in enumerate((("rot_qa", "rot_qb"), ("rot_ka", "rot_kb"))):
                    sc = lambda lo, n: scales[:, w, lo:lo + n].unsqueeze(1).to_broadcast([P, TPB, n])
                    fa = k[a].rearrange("p (t e) -> p t e", e=HD)
                    fb = k[bb].rearrange("p (t e) -> p t e", e=HD)
                    dve.tensor_tensor(ta[:, w], fa, sc(0, HD), ALU.mult).then_inc(m.ready_made.sem, 1)
                    dve.tensor_tensor(tb[:, w, :, 0:32], fb[:, :, 0:32], sc(32, 32), ALU.mult).then_inc(m.ready_made.sem, 1)
                    dve.tensor_tensor(tb[:, w, :, 32:64], fb[:, :, 32:64], sc(0, 32), ALU.mult).then_inc(m.ready_made.sem, 1)
                dve.wait_ge(*m.ready_made.after(6))
                dve.memset(v[1][:], 0.0).then_inc(m.ready_made.sem, 1)
                dve.memset(pT[(NG - 1) % 2][:], 0.0).then_inc(m.ready_made.sem, 1)
                dve.wait_ge(*m.zeroed.after(8))
                dve.sem_inc(m.passed.sem, 1)

                def sum_squares(b, j):
                    dve.wait_ge(*m.h_squared.after(TPB * b + j + 1))
                    dve.tensor_reduce(ss[:, j, :], sq[:, j].rearrange("p (h e) -> p h e", e=HD), AX.X, ALU.add)\
                        .then_inc(m.step.sem, 1)
                    dve.wait_ge(*m.step.after(CHAIN * b + 2 * j + 1))
                    dve.tensor_scalar(ssc[:, j * 2 * NH:(j + 1) * 2 * NH], ss[:, j, :], 1e-24, None, ALU.max).then_inc(m.squares_ready.sem, 1)

                def own_part(b, j, at):
                    if not (isinstance(b, int) and b < 2):
                        dve.wait_ge(*ring.full(*at(TURN + 2 * j + 1)))
                    elif b > 0:
                        dve.wait_ge(*ring.full(*prepared(b - 1, TURN + 2 * j + 1)))
                    dve.wait_ge(*ring.empty(*at(QK + 2 * j + 1)))
                    dve.tensor_tensor(own[:, j], qk[:, j], ta[:, :, j, :].unsqueeze(2).to_broadcast([P, 2, NH, HD]), ALU.mult)\
                        .then_inc(m.step.sem, 1)

                def normalise(b, j):
                    if j == 0:
                        dve.wait_ge(*m.step.after(CHAIN * b + 2 * TPB))
                    if isinstance(b, int) and b == 0:
                        dve.wait_ge(*m.rotated.after(2 * TPB + 2 * (j + 1)))
                    else:
                        dve.wait_ge(*m.rotated.after(4 * TPB * b + 4 * (j + 1)))
                    flat = lambda t: t[:, j].rearrange("p w h e -> p (w h e)")
                    dve.tensor_tensor(flat(own), flat(own), flat(other), ALU.add).then_inc(m.step.sem, 1)
                    dve.wait_ge(*m.step.after(CHAIN * b + 2 * TPB + j + 1))
                    dve.wait_ge(*m.powers_ready.after(TPB * b + j + 1))
                    heads = own[:, j].rearrange("p w h e -> p (w h) e")
                    dve.tensor_tensor(heads, heads, rn[:, j * 2 * NH:(j + 1) * 2 * NH].unsqueeze(2).to_broadcast([P, 2 * NH, HD]),
                                      ALU.mult).then_inc(m.normed.sem, 1)

                def drain(i, u, f, at):
                    if SPREAD <= f < OUT:
                        if f == SPREAD:
                            dve.wait_ge(*(ring.empty(*turn(i, u, LAST)) if i is not PAIRS else ring.empty(PAIRS, 0, 0)))
                        dve.wait_ge(*ring.full(*at))
                        g = 2 * (f - SPREAD)
                        og = o[1 - u][:, g:g + 2, :].rearrange("p g t -> p (g t)")
                        dve.tensor_tensor(og, ring.bank(*at[1:])[:], og, ALU.mult).then_inc(ring.drains(*at[1:]), 1)
                    if f == OUT:
                        dve.wait_ge(*ring.full(*at))
                        rows = m.y_padded[:, bass.ds(TPB * (2 * i + u), TPB), :]
                        dve.tensor_tensor(rows, ring.bank(*at[1:])[:, 0:TPB * D].rearrange("p (t d) -> p t d", d=D), rows, ALU.add)\
                            .then_inc(ring.drains(*at[1:]), 1)

                def invert_sums(b, u):
                    dve.wait_ge(*m.probs_ready.after(TPB * NH * b))
                    dve.wait_ge(*m.inv_split.after(b))
                    dve.reciprocal(inv[:], sums[:, 1 - u].rearrange("p t h -> p (t h)")).then_inc(m.sums_inverted.sem, 1)

                for b in range(2):
                    at = lambda f: prepared(b, f)
                    for j in range(TPB):
                        sum_squares(b, j)
                        own_part(b, j, at)
                    if b == 0:
                        for j in range(TPB):
                            other_half(dve, j, 1)
                            normalise(b, j)
                def maxima(i, u, n):
                    dve.wait_ge(*m.scores_ready.after(NH * (2 * i + u) + n + 1))
                    dve.sem_inc(m.passed.sem, 1)
                    for j, cols in enumerate(TILES):
                        dve.tensor_tensor_reduce(out=minus_s[n % (2 * DEEP)][:, cols], in0=s_ps[n % DEEP][:, cols], in1=k["band"][:, cols],
                                                 scale=-1.0, scalar=3e38, op0=ALU.add, op1=ALU.min,
                                                 accum_out=nmax[:, u, TPB * n + j:TPB * n + j + 1]).then_inc(m.max_ready.sem, 1)

                for n in range(DEEP):
                    maxima(0, 0, n)
                def attend(i, u, left=2):
                    b = 2 * i + u
                    at = lambda f: turn(i, u, f)
                    for n in range(DEEP, NH + DEEP):
                        c = n - DEEP
                        if n < NH or left >= 1:
                            maxima(*ahead(i, u, n))
                        if c % 2 == 0:
                            dve.wait_ge(*ring.full(*group_before(i, u, c // 2)))
                        dve.wait_ge(*m.turned.after(NH * b + c + 1))
                        dve.tensor_copy(pT[c // 2 % 2][:, c % 2].rearrange("p c t -> p (c t)"), t_ps[c % 2][:, 0:BAND])\
                            .then_inc(m.turned_copied.sem, 1)
                        if c in SUMMED and left >= 2:
                            sum_squares(b + 2, SUMMED.index(c))
                        for f in due[c]:
                            drain(i, u, f, turn(i, u, f))
                        if c == 0:
                            invert_sums(b, u)
                        if c < TPB and left >= 1:
                            normalise(b + 1, c)
                        if c in OWN and left >= 2:
                            own_part(b + 2, OWN.index(c), at)

                with dve.Fori(0, PAIRS - 1) as i:
                    for u in range(2):
                        attend(i, u)
                attend(PAIRS - 1, 0, left=1)
                attend(PAIRS - 1, 1, left=0)
                invert_sums(B, 0)
                for n, f in enumerate(range(LAST, GROUP)):
                    drain(PAIRS, 0, f, (PAIRS, 0, n))

            @block.scalar
            def _(act):
                shift_tokens(m, None, None, act, ring, first, hb)

                def square(b, j, at):
                    for w in range(2):
                        act.wait_ge(*ring.empty(*at(QK + 2 * j + w)))
                    act.activation(sq[:, j], qk[:, j].rearrange("p w h e -> p (w h e)"), ACT.Square).then_inc(m.h_squared.sem, 1)

                def drain(i, u, f, at, unused=False):
                    if unused:
                        act.wait_ge(*ring.full(*at))
                        act.sem_inc(ring.drains(*at[1:]), 1)
                        return
                    if QK <= f < TURN:
                        j, w = divmod(f - QK, 2)
                        act.wait_ge(*ring.full(*at))
                        act.activation(qk[:, j, w].rearrange("p h e -> p (h e)"), ring.bank(*at[1:])[:], ACT.Copy)\
                            .then_inc(ring.drains(*at[1:]), 1)
                    if TURN <= f < V and (f - TURN) % 2 == 0:
                        cols = slice((f - TURN) // 2 * P, ((f - TURN) // 2 + 1) * P)
                        act.wait_ge(*ring.full(*at))
                        bank = ring.bank(*at[1:])[:].rearrange("p (g t) -> p g t", t=P)
                        act.activation(q[1 - u][0:HD, 0:NH:2, cols], bank[0:HD], ACT.Copy)
                        act.activation(q[1 - u][HD:P, 1:NH:2, cols], bank[HD:P], ACT.Copy).then_inc(ring.drains(*at[1:]), 1)
                    if TURN <= f < V and (f - TURN) % 2:
                        j = (f - TURN) // 2
                        act.wait_ge(*ring.full(*at))
                        act.activation(kT[1 - u][:, :, j * P:(j + 1) * P], ring.bank(*at[1:])[:].rearrange("p (g t) -> p g t", t=P), ACT.Copy)\
                            .then_inc(ring.drains(*at[1:]), 1)
                    if V <= f < LAST:
                        act.wait_ge(*ring.full(*at))
                        act.activation(v[1 - u][:, f - V, :], ring.bank(*at[1:])[:], ACT.Copy).then_inc(ring.drains(*at[1:]), 1)
                    if f == SUMS:
                        act.wait_ge(*ring.full(*at))
                        act.activation(invT[0:3 * HEADS, :], ring.bank(*at[1:])[0:3 * HEADS, 0:S], ACT.Copy).then_inc(ring.drains(*at[1:]), 1)
                    if f == LAST or f >= GROUP:
                        act.wait_ge(*ring.full(*at))
                        to = o[1 - u][:, NG - 1, :] if f == LAST else o[u][:, f - GROUP, :]
                        act.activation(to, ring.bank(*at[1:])[:, 0:S], ACT.Copy).then_inc(ring.drains(*at[1:]), 1)

                for f in range(TURNS):
                    at = first(SHIFTS + f)
                    act.wait_ge(*ring.full(*at))
                    act.activation(hT[:, f * 512:(f + 1) * 512], ring.bank(*at[1:])[:], ACT.Copy).then_inc(ring.drains(*at[1:]), 1)
                act.wait_ge(*m.zeroed.after(8))
                for f in range(TURNS):
                    act.wait_ge(*ring.empty(*first(SHIFTS + f)))
                for b in (1, 2):
                    act.activation(hs[b % 2][:], hT[:, b * S:(b + 1) * S], ACT.Copy).then_inc(m.h_moved.sem, 1)
                for b, f in AHEAD_OF_LOOP:
                    drain(-1, 1, f, prepared(b, f))
                    if f in (QK + 1, QK + 3):
                        square(b, (f - QK) // 2, lambda f: prepared(b, f))
                def exponentials(i, u, n):
                    for j, cols in enumerate(TILES):
                        act.wait_ge(*m.max_ready.after(TPB * (NH * (2 * i + u) + n) + j + 1))
                        act.activation(probs[n % (2 * DEEP)][:, cols], minus_s[n % (2 * DEEP)][:, cols], ACT.Exp,
                                       bias=nmax[:, u, TPB * n + j:TPB * n + j + 1], scale=-1.0,
                                       accum_out=sums[:, u, j, n:n + 1]).then_inc(m.probs_ready.sem, 1)

                for n in range(DEEP):
                    exponentials(0, 0, n)
                def attend(i, u, left=2):
                    b = 2 * i + u
                    for n in range(DEEP, NH + DEEP):
                        if n < NH or left >= 1:
                            exponentials(*ahead(i, u, n))
                        for f in due[n - DEEP]:
                            drain(i, u, f, turn(i, u, f), unused=f < (LAST, TURN, 0)[left])
                        if n - DEEP in SQUARED and left >= 2:
                            square(b + 2, SQUARED.index(n - DEEP), lambda f: turn(i, u, f))
                    if left == 0:
                        return
                    act.wait_ge(*ring.full(*turn(i, u, V + TPB - 1)))
                    act.sem_inc(m.passed.sem, 1)
                    act.activation(hs[1 - u][:], hT[:, bass.ds((b + 3) * S, S)], ACT.Copy).then_inc(m.h_moved.sem, 1)

                with act.Fori(0, PAIRS - 1) as i:
                    for u in range(2):
                        attend(i, u)
                attend(PAIRS - 1, 0, left=1)
                attend(PAIRS - 1, 1, left=0)
                for n, f in enumerate(range(LAST, GROUP)):
                    drain(PAIRS, 0, f, (PAIRS, 0, n))

            @block.tensor
            def _(pe):
                shift_tokens(m, pe, None, None, ring, first, hb)
                pe.wait_ge(*m.unshifted.after(1))
                for f in range(SHIFTS):
                    pe.wait_ge(*ring.empty(*first(f)))
                for f in range(TURNS):
                    at = first(SHIFTS + f)
                    pe.wait_ge(*ring.free(*at))
                    for j in range(4):
                        ins = pe.transpose(ring.bank(*at[1:])[:, j * P:(j + 1) * P], hb[:, 4 * f + j, :], k["ident"])
                    ins.then_inc(ring.fills(*at[1:]), 1)
                pe.wait_ge(*m.loaded.after(64))
                for f in range(TURNS):
                    pe.wait_ge(*ring.empty(*first(SHIFTS + f)))
                pe.wait_ge(*m.zeroed.after(8))

                def fill(i, u, f, at, prepares=None, unused=False):
                    b = 2 * i + u
                    bank = ring.bank(*at[1:])
                    if unused:
                        pe.wait_ge(*ring.free(*at))
                        pe.sem_inc(ring.fills(*at[1:]), 1)
                        return
                    if f < TURN:
                        j, w = divmod(f - QK, 2)
                        if prepares is None and f == QK:
                            pe.wait_ge(*m.h_moved.after(b + 2))
                        pe.wait_ge(*ring.free(*at))
                        tokens = hs[u][:, j * P:(j + 1) * P] if prepares is None else hT[:, (TPB * prepares + j) * P:(TPB * prepares + j + 1) * P]
                        ins = pe.matmul(bank[:], tokens, wqkv[:, w * INNER:(w + 1) * INNER], start=True, stop=True)
                    elif f < V:
                        j, w = divmod(f - TURN, 2)
                        pe.wait_ge(*m.normed.after(TPB * (b + 1) + j + 1))
                        pe.wait_ge(*ring.free(*at))
                        for g in range(NG):
                            ins = pe.transpose(bank[:, g * P:(g + 1) * P], own[:, j, w, 2 * g:2 * g + 2, :].rearrange("p h e -> p (h e)"),
                                               k["ident"])
                    elif f < LAST:
                        j = f - V
                        pe.wait_ge(*ring.free(*at))
                        tokens = hs[1 - u][:, j * P:(j + 1) * P] if prepares is None else hT[:, (TPB * prepares + j) * P:(TPB * prepares + j + 1) * P]
                        ins = pe.matmul(bank[:], tokens, wqkv[:, 2 * INNER:], start=True, stop=True)
                    elif f == SUMS:
                        pe.wait_ge(*m.inv_split.after(b + 1))
                        pe.wait_ge(*ring.free(*at))
                        for j in range(TPB):
                            ins = pe.matmul(bank[0:3 * HEADS, j * P:(j + 1) * P], inv_parts[:, j].rearrange("p r h -> p (r h)"), k["ident_bf"],
                                            start=True, stop=True)
                    elif SPREAD <= f < OUT:
                        if f == SPREAD:
                            pe.wait_ge(*(ring.empty(*turn(i, u, SUMS)) if i is not PAIRS else ring.empty(PAIRS, 0, SUMS - LAST)))
                        pe.wait_ge(*ring.free(*at))
                        for t in range(2):
                            g = 2 * (f - SPREAD) + t
                            ins = pe.matmul(bank[:, t * S:(t + 1) * S], k["spread2_bf"][:, g * P:(g + 1) * P], invT[:], start=True, stop=True)
                    elif f == OUT:
                        pe.wait_ge(*ring.free(*at))
                        pe.wait_ge(*(ring.empty(*turn(i, u, OUT - 1)) if i is not PAIRS else ring.empty(PAIRS, 0, OUT - 1 - LAST)))
                        for j in range(TPB):
                            for g in range(NG):
                                ins = pe.matmul(bank[:, j * D:(j + 1) * D], o[1 - u][:, g, j * P:(j + 1) * P], wo[:, g, :], start=(g == 0),
                                                stop=(g == NG - 1))
                    else:
                        of, g = (1 - u, NG - 1) if f == LAST else (u, f - GROUP)
                        pe.wait_ge(*m.turned_copied.after(NH * b + (0 if f == LAST else 2 * (g + 1))))
                        pe.wait_ge(*ring.free(*at))
                        for c in range(TPB):
                            for hh in range(2):
                                rows = slice(HD * hh, HD * (hh + 1))
                                vc = v[of][:, c, (2 * g + hh) * HD:(2 * g + hh + 1) * HD]
                                if c == 0:
                                    ins = pe.matmul(bank[rows, 0:S], vc, pT[g % 2][:, hh, 0:2, :].rearrange("p c t -> p (c t)"),
                                                    start=True, stop=False)
                                else:
                                    ins = pe.matmul(bank[rows, P:S], vc, pT[g % 2][:, hh, 2, :], start=False, stop=True)
                    ins.then_inc(ring.fills(*at[1:]), 1)

                def scores(i, u, n):
                    out = s_ps[n % DEEP]
                    pe.matmul(out[:, 0:P], q[u][:, n, 0:P], kT[u][:, n // 2, 0:P], start=True, stop=True)
                    pe.matmul(out[:, P:BAND], q[u][:, n, P:S], kT[u][:, n // 2, :], start=True, stop=True)\
                        .then_inc(m.scores_ready.sem, 1)

                for b, f in AHEAD_OF_LOOP:
                    fill(-1, 1, f, prepared(b, f), prepares=b)
                for f in range(TURN, LAST):
                    pe.wait_ge(*ring.empty(*prepared(0, f)))
                for n in range(DEEP):
                    scores(0, 0, n)
                pe.wait_ge(*m.ready_made.after(8))
                def attend(i, u, left=2):
                    b = 2 * i + u
                    for n in range(NH):
                        if n + DEEP == NH and left >= 1:
                            for f in range(TURN, V):
                                pe.wait_ge(*ring.empty(*turn(i, u, f)))
                        if n + DEEP < NH or left >= 1:
                            pe.wait_ge(*m.max_ready.after(TPB * (NH * b + n + 1)))
                            scores(*ahead(i, u, n + DEEP))
                        pe.wait_ge(*m.probs_ready.after(TPB * (NH * b + n + 1)))
                        pe.wait_ge(*m.turned_copied.after(NH * b + n - 1))
                        for c in range(3):
                            ins = pe.transpose(t_ps[n % 2][:, c * P:(c + 1) * P], probs[n % (2 * DEEP)][:, c * P:(c + 1) * P], k["ident"])
                        ins.then_inc(m.turned.sem, 1)
                        for f in due[n]:
                            fill(i, u, f, turn(i, u, f), unused=f < (LAST, TURN, 0)[left])
                    for f in range(V, LAST):
                        pe.wait_ge(*ring.empty(*turn(i, u, f)))

                with pe.Fori(0, PAIRS - 1) as i:
                    for u in range(2):
                        attend(i, u)
                attend(PAIRS - 1, 0, left=1)
                attend(PAIRS - 1, 1, left=0)
                for n, f in enumerate(range(LAST, GROUP)):
                    fill(PAIRS, 0, f, (PAIRS, 0, n))
        ring.close(GROUP - LAST)
        for s, n in ((m.loaded, 64), (m.ready_made, 8), (m.step, CHAIN * B), (m.inv_step, 3 * (B + 1)),
                     (m.inv_split, B + 1), (m.unshifted, 1), (m.zeroed, 8), (m.h_moved, B + 1),
                     (m.h_squared, TPB * B), (m.rotated, 4 * TPB * B), (m.squares_ready, TPB * B), (m.powers_ready, TPB * B),
                     (m.normed, TPB * B), (m.scores_ready, NH * B), (m.max_ready, TPB * NH * B),
                     (m.probs_ready, TPB * NH * B), (m.turned, NH * B), (m.turned_copied, NH * B), (m.sums_inverted, B + 1)):
            s.before += n


def gelu_ffn(m, layer):
    nc, d, x, k = m.nc, m.dram, m.x, m.consts
    HID = int(D * 4 * 2 / 3)
    ROWS = [min(P, HID - c * P) for c in range(-(-HID // P))]
    NC = len(ROWS)
    T, BT = B * S, 512
    NB, TB = T // BT, BT // P
    with ExitStack() as ctx:
        sb = lambda name, shape, dt=F32: sbuf(m, ctx, f"{name}_l2f{layer}", shape, dt)
        norm = Norm(m, ctx, NT, f"l2f{layer}", buffers=1)
        w1 = sb("w1", [P, 2 * HID])
        b1 = sb("b1", [P, 2, NC])
        w2 = sb("w2", [P, NC, D])
        b2 = sb("b2", [P, 1])
        yT = [sb(f"yT{u}", [P, BT]) for u in range(2)]
        lg, lb = sb("lg", [P, 1]), sb("lb", [P, 1])
        hb = sb("hb", [P, NT, D])
        hT = sb("hT", [P, T])
        gate = sb("gate", [P, NC, BT])
        prod = sb("prod", [P, NC, T])
        NLOAD = 4 + 3 * NC
        SHIFTS, TURNS = 2, NT // 4
        ring = Ring([psum(m, ctx, f"ring{n}_l2f{layer}", [P, BT]) for n in range(2 * NC)], m.filled, m.drained, NC,
                    lead=SHIFTS + TURNS)
        y_ps = [psum(m, ctx, f"y_ps{u}_l2f{layer}", [P, BT]) for u in range(2)]
        yT_ps = ring.banks[0:2]
        first = lambda f: (0, 0, f - ring.lead)
        assert PAIRS == NB

        with nc.Block() as block:
            @block.sync
            def _(sp):
                loads = [(w1[:], d["L2_ffn_w1"][layer]), (b2[:], d["L2_ffn_b2"][layer].rearrange("(p o) -> p o", o=1)),
                         (lg[:], d["L2_ffn_ln_g"][layer].rearrange("(p o) -> p o", o=1)),
                         (lb[:], d["L2_ffn_ln_b"][layer].rearrange("(p o) -> p o", o=1))]
                for c, r in enumerate(ROWS):
                    loads.append((w2[0:r, c, :], d["L2_ffn_w2"][layer, c * P:c * P + r, :]))
                    for w in range(2):
                        lo = w * HID + c * P
                        loads.append((b1[0:r, w, c:c + 1], d["L2_ffn_b1"][layer, lo:lo + r].rearrange("(p o) -> p o", o=1)))
                assert len(loads) == NLOAD
                for dst, src in loads:
                    sp.dma_start(dst, src).then_inc(m.loaded.sem, 16)
                sp.wait_ge(*m.loaded.after(16 * NLOAD))

            @block.gpsimd
            def _(pool):
                norm.pool(pool, 0)

            @block.vector
            def _(dve):
                shift_tokens(m, None, dve, None, ring, first, hb)
                for w in range(SHIFTS):
                    dve.wait_ge(*ring.empty(*first(w)))
                dve.wait_ge(*m.unshifted.after(1))
                norm.vector(dve, 0, 0, lambda j: hb[:, j, :])
                dve.wait_ge(*m.loaded.after(16 * NLOAD))
                with dve.Fori(0, NB) as i:
                    for c, r in enumerate(ROWS):
                        dve.wait_ge(*ring.empty(i, 0, 2 * c))
                        dve.wait_ge(*ring.full(i, 0, 2 * c + 1))
                        dve.scalar_tensor_tensor(out=prod[0:r, c, bass.ds(i * BT, BT)], in0=ring.bank(0, 2 * c + 1)[0:r, :],
                                                 scalar=b1[0:r, 0, c:c + 1], in1=gate[0:r, c, :], op0=ALU.add, op1=ALU.mult)\
                            .then_inc(ring.drains(0, 2 * c + 1), 1)
                with dve.Fori(0, NB // 2) as i:
                    for u in range(2):
                        n = 2 * i + u
                        dve.wait_ge(*m.turned.after(n + 1))
                        tiles = x[:, bass.ds(TB * n, TB), :]
                        dve.tensor_tensor(tiles, y_ps[u][:].rearrange("p (t d) -> p t d", d=D), tiles, ALU.add)\
                            .then_inc(m.x_updated.sem, 1)
                dve.wait_ge(*m.x_updated.after(NB))

            @block.scalar
            def _(act):
                shift_tokens(m, None, None, act, ring, first, hb)
                act.wait_ge(*m.loaded.after(16 * NLOAD))
                for f in range(TURNS):
                    at = first(SHIFTS + f)
                    act.wait_ge(*ring.full(*at))
                    act.activation(hT[:, f * BT:(f + 1) * BT], ring.bank(*at[1:])[:], ACT.Identity, bias=lb[:, 0:1],
                                   scale=lg[:, 0:1]).then_inc(ring.drains(*at[1:]), 1)
                with act.Fori(0, NB) as i:
                    for c, r in enumerate(ROWS):
                        act.wait_ge(*ring.free(i, 0, 2 * c + 1))
                        act.wait_ge(*ring.full(i, 0, 2 * c))
                        act.activation(gate[0:r, c, :], ring.bank(0, 2 * c)[0:r, :], ACT.Gelu, bias=b1[0:r, 1, c:c + 1])\
                            .then_inc(ring.drains(0, 2 * c), 1)
                with act.Fori(0, NB // 2) as i:
                    for u in range(2):
                        act.wait_ge(*m.pv_done.after(2 * i + u + 1))
                        act.activation(yT[u][:], yT_ps[u][:], ACT.Identity, bias=b2[:, 0:1]).then_inc(m.pv_copied.sem, 1)

            @block.tensor
            def _(pe):
                shift_tokens(m, pe, None, None, ring, first, hb)
                for f in range(TURNS):
                    at = first(SHIFTS + f)
                    pe.wait_ge(*m.normed.after(4 * f + 4))
                    pe.wait_ge(*ring.free(*at))
                    for j in range(4):
                        ins = pe.transpose(ring.bank(*at[1:])[:, j * P:(j + 1) * P], norm.xn[0][:, 4 * f + j, :], k["ident"])
                    ins.then_inc(ring.fills(*at[1:]), 1)
                pe.wait_ge(*m.loaded.after(16 * NLOAD))
                for f in range(TURNS):
                    pe.wait_ge(*ring.empty(*first(SHIFTS + f)))
                with pe.Fori(0, NB) as i:
                    for c, r in enumerate(ROWS):
                        for w, lo in ((0, HID), (1, 0)):
                            pe.wait_ge(*ring.free(i, 0, 2 * c + w))
                            pe.matmul(ring.bank(0, 2 * c + w)[0:r, :], w1[:, lo + c * P:lo + c * P + r], hT[:, bass.ds(i * BT, BT)],
                                      start=True, stop=True).then_inc(ring.fills(0, 2 * c + w), 1)
                for f in range(2 * NC):
                    pe.wait_ge(*ring.empty(NB - 1, 0, f))
                with pe.Fori(0, NB // 2) as i:
                    for u in range(2):
                        for c, r in enumerate(ROWS):
                            ins = pe.matmul(yT_ps[u][:], w2[0:r, c, :], prod[0:r, c, bass.ds((2 * i + u) * BT, BT)], start=(c == 0),
                                            stop=(c == NC - 1))
                        ins.then_inc(m.pv_done.sem, 1)
                    for u in range(2):
                        pe.wait_ge(*m.pv_copied.after(2 * i + u + 1))
                        pe.wait_ge(*m.x_updated.after(2 * i))
                        for t in range(TB):
                            ins = pe.transpose(y_ps[u][:, t * D:(t + 1) * D], yT[u][:, t * P:(t + 1) * P], k["ident"])
                        ins.then_inc(m.turned.sem, 1)
        norm.close(1)
        ring.close()
        for s, n in ((m.loaded, 16 * NLOAD), (m.unshifted, 1), (m.pv_done, NB), (m.pv_copied, NB), (m.turned, NB), (m.x_updated, NB)):
            s.before += n


def l2_local_transformer(m):
    nc, x = m.nc, m.x
    with ExitStack() as ctx:
        norm = Norm(m, ctx, NT, "l2t", buffers=1, dummies=TPB)
        y, m.y_padded = norm.xn[0], norm.padded[0]
        with nc.Block() as block:
            @block.gpsimd
            def _(pool):
                norm.pool(pool, 0)

            @block.vector
            def _(dve):
                norm.vector(dve, 0, 0, lambda j: x[:, j, :])
                dve.memset(m.y_padded[:, 0:TPB, :], 0.0).then_inc(m.zeroed.sem, 1)
                dve.wait_ge(*m.normed.after(NT))
                dve.wait_ge(*m.zeroed.after(1))
        m.zeroed.before += 1
        norm.close(1)
        m.x = y
        for layer in range(2):
            local_attention(m, layer)
            gelu_ffn(m, layer)
        m.x = x
        with nc.Block() as block:
            @block.vector
            def _(dve):
                dve.tensor_tensor(x, x, y, ALU.add).then_inc(m.step.sem, 1)
                dve.wait_ge(*m.step.after(1))
        m.step.before += 1

def l3_quantised_ffn(m):
    nc, d, x, k = m.nc, m.dram, m.x, m.consts
    I = 352
    ROWS = [min(P, I - c * P) for c in range(-(-I // P))]
    NC, LAST = len(ROWS), ROWS[-1]
    QMAX = 127.0
    T = B * S
    BT = 512
    NB, TB = T // BT, BT // P
    with ExitStack() as ctx:
        sb = lambda name, shape, dt=F32: sbuf(m, ctx, f"{name}_l3f", shape, dt)
        norm = Norm(m, ctx, NT, "l3f", buffers=1)
        xn = norm.xn[0]
        w, wd = sb("w", [P, 2, NC, D]), sb("wd", [P, I])
        wq, wdq = sb("wq", [P, 2, NC, D], BF16), sb("wdq", [P, I], BF16)
        wT, wdT = sb("wT", [P, 2, I], BF16), sb("wdT", [P, NC, D], BF16)
        wscale, dscale = sb("wscale", [P, 2, NC]), sb("dscale", [P, 1])
        winv, dinv, inv = sb("winv", [P, 2, NC]), sb("dinv", [P, 1]), sb("inv", [P, 2])
        clips, sig = sb("clips", [P, 2]), sb("sig", [P, 2])
        diag, dB = sb("diag", [P, P]), sb("dB", [P, D])
        top, peak, scale = sb("top", [P, 2]), sb("peak", [1, 2]), sb("scale", [P, 2])
        hscale = sb("hscale", [P, 2, NC])
        xq, xqT = sb("xq", [P, NT, D], BF16), sb("xqT", [P, T], BF16)
        gate = [sb(f"gate{c}", [P, BT]) for c in range(NC)]
        hT, hq = sb("hT", [P, NC, T]), sb("hq", [P, NC, T], BF16)
        part = [sb(f"part{u}", [P, TB, D]) for u in range(2)]
        g_ps = [psum(m, ctx, f"g_ps{c}_l3f", [P, BT]) for c in range(NC)]
        u_ps = [psum(m, ctx, f"u_ps{c}_l3f", [P, BT]) for c in range(NC)]
        y_ps = [psum(m, ctx, f"y_ps{u}_l3f", [P, BT]) for u in range(2)]
        w_bank, wd_bank, d_bank, x_banks, max_banks = g_ps[0], g_ps[1], g_ps[2], u_ps[0:2], (u_ps[2], y_ps[0])

        with nc.Block() as block:
            @block.sync
            def _(sp):
                loads = [(wd[:], d["L3_ffn_w_down"]), (clips[:, 0:1], d["L3_ffn_clip_x"][0, :].partition_broadcast(P)),
                         (clips[:, 1:2], d["L3_ffn_clip_down"][0, :].partition_broadcast(P))]
                for n, name in enumerate(("L3_ffn_w_gate", "L3_ffn_w_up")):
                    for c, r in enumerate(ROWS):
                        loads.append((w[0:r, n, c, :], d[name][c * P:c * P + r, :]))
                assert len(loads) == 3 + 2 * NC
                for dst, src in loads:
                    sp.dma_start(dst, src).then_inc(m.loaded.sem, 16)
                sp.wait_ge(*m.loaded.after(16 * len(loads)))

            @block.gpsimd
            def _(pool):
                norm.pool(pool, 0)

            @block.vector
            def _(dve):
                rows = lambda n, c: w[0:ROWS[c], n, c, :]
                dve.memset(wscale[:], 1.0).then_inc(m.step.sem, 1)
                dve.memset(hT[LAST:P, NC - 1, :], 0.0).then_inc(m.step.sem, 1)
                dve.wait_ge(*m.loaded.after(16 * (3 + 2 * NC)))
                dve.wait_ge(*m.step.after(2))
                dve.tensor_reduce(wscale[:, :, 0:NC - 1], w[:, :, 0:NC - 1, :], AX.X, ALU.max, apply_absolute_value=True)\
                    .then_inc(m.step.sem, 1)
                dve.tensor_reduce(wscale[0:LAST, :, NC - 1], w[0:LAST, :, NC - 1, :], AX.X, ALU.max, apply_absolute_value=True)\
                    .then_inc(m.step.sem, 1)
                dve.tensor_reduce(dscale[:], wd[:], AX.X, ALU.max, apply_absolute_value=True).then_inc(m.step.sem, 1)
                dve.wait_ge(*m.step.after(5))
                dve.tensor_scalar(wscale[:], wscale[:], 1.0 / QMAX, None, ALU.mult).then_inc(m.step.sem, 1)
                dve.tensor_scalar(dscale[:], dscale[:], 1.0 / QMAX, None, ALU.mult).then_inc(m.step.sem, 1)
                dve.wait_ge(*m.step.after(7))
                dve.reciprocal(winv[:], wscale[:]).then_inc(m.step.sem, 1)
                dve.reciprocal(dinv[:], dscale[:]).then_inc(m.step.sem, 1)
                dve.wait_ge(*m.step.after(9))
                for n in range(2):
                    for c, r in enumerate(ROWS):
                        dve.tensor_scalar(rows(n, c), rows(n, c), winv[0:r, n, c:c + 1], MAGIC, ALU.mult, ALU.add)\
                            .then_inc(m.step.sem, 1)
                dve.tensor_scalar(wd[:], wd[:], dinv[:], MAGIC, ALU.mult, ALU.add).then_inc(m.step.sem, 1)
                dve.wait_ge(*m.step.after(10 + 2 * NC))
                for n in range(2):
                    for c, r in enumerate(ROWS):
                        dve.tensor_scalar(wq[0:r, n, c, :], rows(n, c), MAGIC, QMAX, ALU.subtract, ALU.min)\
                            .then_inc(m.ready_made.sem, 1)
                dve.tensor_scalar(wdq[:], wd[:], MAGIC, QMAX, ALU.subtract, ALU.min).then_inc(m.ready_made.sem, 1)
                dve.tensor_scalar(diag[:], k["ident"], dscale[:], None, ALU.mult).then_inc(m.ready_made.sem, 1)

                def find_scale(n, src, waited):
                    dve.tensor_reduce(top[:, n:n + 1], src, AX.X, ALU.max, apply_absolute_value=True).then_inc(m.row_max.sem, 1)
                    dve.wait_ge(*m.max_turned.after(n + 1))
                    dve.tensor_reduce(peak[0:1, n:n + 1], max_banks[n][0:1, 0:P], AX.X, ALU.max).then_inc(m.max_found.sem, 1)
                    dve.wait_ge(*m.max_spread.after(n + 1))
                    dve.wait_ge(*m.act_step.after(1))
                    dve.tensor_scalar(scale[:, n:n + 1], max_banks[n][:, P:P + 1], sig[:, n:n + 1], 1.0 / QMAX, ALU.mult, ALU.mult)\
                        .then_inc(m.step.sem, 1)
                    dve.wait_ge(*m.step.after(waited))
                    dve.reciprocal(inv[:, n:n + 1], scale[:, n:n + 1]).then_inc(m.step.sem, 1)
                    dve.wait_ge(*m.step.after(waited + 1))

                at = 10 + 2 * NC
                norm.vector(dve, 0, 0, lambda j: x[:, j, :])
                dve.wait_ge(*m.normed.after(NT))
                flat = xn[:].rearrange("p t d -> p (t d)")
                find_scale(0, flat, at + 1)
                dve.tensor_scalar(hscale[:], wscale[:], scale[:, 0:1], None, ALU.mult).then_inc(m.scales_ready.sem, 1)
                dve.tensor_scalar(flat, flat, inv[:, 0:1], -QMAX - 1, ALU.mult, ALU.max).then_inc(m.step.sem, 1)
                dve.wait_ge(*m.step.after(at + 3))
                dve.tensor_scalar(flat, flat, QMAX, MAGIC, ALU.min, ALU.add).then_inc(m.step.sem, 1)
                dve.wait_ge(*m.step.after(at + 4))
                dve.tensor_scalar(xq[:].rearrange("p t d -> p (t d)"), flat, MAGIC, None, ALU.subtract).then_inc(m.x_quantised.sem, 1)

                dve.wait_ge(*m.scales_ready.after(1))
                with dve.Fori(0, NB) as n:
                    for c, r in enumerate(ROWS):
                        dve.wait_ge(*m.gate_ready.after(NC * n + c + 1))
                        dve.scalar_tensor_tensor(out=hT[0:r, c, bass.ds(n * BT, BT)], in0=u_ps[c][0:r, :],
                                                 scalar=hscale[0:r, 1, c:c + 1], in1=gate[c][0:r, :], op0=ALU.mult, op1=ALU.mult)\
                            .then_inc(m.hidden_ready.sem, 1)
                dve.wait_ge(*m.hidden_ready.after(NC * NB))
                find_scale(1, hT[:].rearrange("p c t -> p (c t)"), at + 5)
                dve.tensor_scalar(dB[:], d_bank[:, 0:D], scale[:, 1:2], None, ALU.mult).then_inc(m.step.sem, 1)
                with dve.Fori(0, NB) as n:
                    h = hT[:, :, bass.ds(n * BT, BT)]
                    dve.tensor_scalar(h, h, inv[:, 1:2], -QMAX - 1, ALU.mult, ALU.max).then_inc(m.hidden_clipped.sem, 1)
                    dve.wait_ge(*m.hidden_clipped.after(n + 1))
                    dve.tensor_scalar(h, h, QMAX, MAGIC, ALU.min, ALU.add).then_inc(m.hidden_rounded.sem, 1)
                dve.wait_ge(*m.step.after(at + 7))
                with dve.Fori(0, NB // 2) as i:
                    for u in range(2):
                        n = 2 * i + u
                        dve.wait_ge(*m.pv_done.after(n + 1))
                        dve.tensor_tensor(part[u][:], y_ps[u][:].rearrange("p (t d) -> p t d", d=D),
                                          dB[:].unsqueeze(1).to_broadcast([P, TB, D]), ALU.mult).then_inc(m.pv_copied.sem, 1)
                        dve.wait_ge(*m.pv_copied.after(n + 1))
                        tiles = x[:, bass.ds(TB * n, TB), :]
                        dve.tensor_tensor(tiles, tiles, part[u][:], ALU.add).then_inc(m.x_updated.sem, 1)
                dve.wait_ge(*m.x_updated.after(NB))

            @block.scalar
            def _(act):
                act.wait_ge(*m.loaded.after(16 * (3 + 2 * NC)))
                act.activation(sig[:], clips[:], ACT.Sigmoid).then_inc(m.act_step.sem, 1)
                act.wait_ge(*m.turned.after(1))
                act.activation(wT[:].rearrange("p n i -> p (n i)"), w_bank[:, 0:I].bitcast(BF16), ACT.Copy)\
                    .then_inc(m.turned_copied.sem, 1)
                act.wait_ge(*m.turned.after(2))
                low = (NC - 1) * D
                act.activation(wdT[:, 0:NC - 1, :].rearrange("p c d -> p (c d)"), wd_bank[:, 0:low // 2].bitcast(BF16), ACT.Copy)\
                    .then_inc(m.turned_copied.sem, 1)
                act.activation(wdT[0:LAST, NC - 1, :], wd_bank[0:LAST, low // 2:(low + D) // 2].bitcast(BF16), ACT.Copy)\
                    .then_inc(m.turned_copied.sem, 1)
                for n in range(2):
                    act.wait_ge(*m.x_turned.after(n + 1))
                    act.activation(xqT[:, n * T // 2:(n + 1) * T // 2], x_banks[n][:].bitcast(BF16), ACT.Copy)\
                        .then_inc(m.turned_copied.sem, 1)
                act.wait_ge(*m.scales_ready.after(1))
                with act.Fori(0, NB) as n:
                    for c, r in enumerate(ROWS):
                        act.wait_ge(*m.scores_ready.after(NC * n + c + 1))
                        act.activation(gate[c][0:r, :], g_ps[c][0:r, :], ACT.Silu, scale=hscale[0:r, 0, c:c + 1])\
                            .then_inc(m.gate_ready.sem, 1)
                with act.Fori(0, NB) as n:
                    act.wait_ge(*m.hidden_rounded.after(n + 1))
                    act.activation(hq[:, :, bass.ds(n * BT, BT)], hT[:, :, bass.ds(n * BT, BT)], ACT.Copy, bias=-MAGIC)\
                        .then_inc(m.hidden_quantised.sem, 1)

            @block.tensor
            def _(pe):
                pe.wait_ge(*m.ready_made.after(2 * NC))
                bank = w_bank[:, 0:I].bitcast(BF16)
                for n in range(2):
                    for c, r in enumerate(ROWS):
                        ins = pe.transpose(bank[:, n * I + c * P:n * I + c * P + r], wq[0:r, n, c, :], k["ident_bf"][0:r, 0:r])
                ins.then_inc(m.turned.sem, 1)
                pe.wait_ge(*m.ready_made.after(2 * NC + 1))
                bank = wd_bank[:, 0:NC * D // 2].bitcast(BF16)
                for c, r in enumerate(ROWS):
                    ins = pe.transpose(bank[0:r, c * D:(c + 1) * D], wdq[:, c * P:c * P + r], k["ident_bf"])
                ins.then_inc(m.turned.sem, 1)

                def spread_max(n):
                    pe.wait_ge(*m.row_max.after(n + 1))
                    pe.transpose(max_banks[n][0:1, 0:P], top[:, n:n + 1], k["ident"]).then_inc(m.max_turned.sem, 1)
                    pe.wait_ge(*m.max_found.after(n + 1))
                    pe.matmul(max_banks[n][:, P:P + 1], k["ones"][0:1, :], peak[0:1, n:n + 1], start=True, stop=True)\
                        .then_inc(m.max_spread.sem, 1)

                spread_max(0)
                pe.wait_ge(*m.x_quantised.after(1))
                for n in range(2):
                    bank = x_banks[n][:].bitcast(BF16)
                    for j in range(NT // 2):
                        ins = pe.transpose(bank[:, j * P:(j + 1) * P], xq[:, n * NT // 2 + j, :], k["ident_bf"])
                    ins.then_inc(m.x_turned.sem, 1)
                pe.wait_ge(*m.turned_copied.after(5))
                with pe.Fori(0, NB) as n:
                    for c, r in enumerate(ROWS):
                        if c == 0:
                            pe.wait_ge(*m.hidden_ready.after(NC * n))
                        cols = bass.ds(n * BT, BT)
                        pe.matmul(g_ps[c][0:r, :], wT[:, 0, c * P:c * P + r], xqT[:, cols], start=True, stop=True)
                        pe.matmul(u_ps[c][0:r, :], wT[:, 1, c * P:c * P + r], xqT[:, cols], start=True, stop=True)\
                            .then_inc(m.scores_ready.sem, 1)
                pe.wait_ge(*m.hidden_ready.after(NC * NB))
                pe.wait_ge(*m.ready_made.after(2 * NC + 2))
                pe.matmul(d_bank[:, 0:D], k["ones"], diag[:], start=True, stop=True)
                spread_max(1)
                with pe.Fori(0, NB // 2) as i:
                    for u in range(2):
                        n = 2 * i + u
                        pe.wait_ge(*m.hidden_quantised.after(n + 1))
                        pe.wait_ge(*m.pv_copied.after(2 * i))
                        for t in range(TB):
                            for c, r in enumerate(ROWS):
                                ins = pe.matmul(y_ps[u][:, t * D:(t + 1) * D], hq[0:r, c, bass.ds((TB * n + t) * P, P)],
                                                wdT[0:r, c, :], start=(c == 0), stop=(c == NC - 1))
                        ins.then_inc(m.pv_done.sem, 1)
        norm.close(1)
        for s, n in ((m.loaded, 16 * (3 + 2 * NC)), (m.step, 17 + 2 * NC), (m.ready_made, 2 + 2 * NC), (m.act_step, 1), (m.turned, 2),
                     (m.turned_copied, 5), (m.row_max, 2), (m.max_turned, 2), (m.max_found, 2), (m.max_spread, 2), (m.x_quantised, 1),
                     (m.x_turned, 2), (m.scales_ready, 1), (m.scores_ready, NC * NB), (m.gate_ready, NC * NB), (m.hidden_ready, NC * NB),
                     (m.hidden_clipped, NB), (m.hidden_rounded, NB), (m.hidden_quantised, NB), (m.pv_done, NB), (m.pv_copied, NB),
                     (m.x_updated, NB)):
            s.before += n


def store(m, out):
    with m.nc.Block() as block:
        @block.sync
        def _(sp):
            sp.dma_start(out.rearrange("(t p) d -> p t d", p=P), m.x).then_inc(m.loaded.sem, 16)
            sp.wait_ge(*m.loaded.after(16))
    m.loaded.before += 16


PHASES = [l0_cross_attention, convert_constants, l0_block_ffn, l1_cross_attention, l1_bit_ffn, l2_cross_attention,
          l2_local_transformer, l3_cross_attention, l3_quantised_ffn]


def program(nc, dram, out):
    with ExitStack() as ctx:
        m = Machine(nc, ctx, dram)
        load_constants(m, ctx)
        for phase in PHASES:
            phase(m)
        store(m, out)


def shape_constants():
    f = np.float32
    c = {}
    c["ident"] = np.eye(P, dtype=f)
    c["ones"] = np.ones((P, P), f)
    c["shift"] = np.eye(P, k=1, dtype=f)
    last = np.zeros((P, P), f)
    last[P - 1, 0] = 1
    c["last"] = last
    for name, per in (("spread4", 4), ("spread2", 2)):
        groups = HEADS // per
        s = np.zeros((P, groups, P), f)
        for g in range(groups):
            for r in range(P):
                for part in range(3):
                    s[HEADS * part + per * g + r // (P // per), g, r] = 1
        c[name] = s.reshape(P, groups * P)
    c["minus_half"] = np.full((P, 64), -0.5, f)
    half = np.arange(0, 64, 2, dtype=f)
    inv_freq = (f(1.0) / f(10000.0) ** (half / f(64))).astype(f)
    t = np.arange(S, dtype=f)
    freqs = (t[:, None] * inv_freq[None, :]).astype(f)
    freqs = np.concatenate([freqs, freqs], -1)
    base = ((half + f(0.4 * 64)) / f(1.4 * 64)).astype(f)
    power = ((t - S // 2) / f(32)).astype(f)
    scale = (base[None, :] ** power[:, None]).astype(f)
    scale = np.concatenate([scale, scale], -1)
    sign = np.concatenate([-np.ones(32, f), np.ones(32, f)])
    tables = {"rot_qa": 8 * np.cos(freqs) * scale, "rot_qb": 8 * np.sin(freqs) * scale * sign,
              "rot_ka": np.cos(freqs) / scale, "rot_kb": np.sin(freqs) / scale * sign}
    for name, v in tables.items():
        c[name] = v.astype(f).reshape(TPB, P, 64).transpose(1, 0, 2).reshape(P, TPB * 64)
    i = np.arange(P)[:, None]
    band = []
    for q0, k0, n in ((0, 0, P), (P, 0, 2 * P)):
        q, j = q0 + i, k0 + np.arange(n)[None, :]
        band.append(np.where((q < j) | (q > j + 64), -1e30, 0.0))
    c["band"] = np.concatenate(band, 1)
    return np.concatenate([c[n] for n, _ in CONSTS], 1).astype(f)


def lay_out(inputs):
    i = {n: np.asarray(v) for n, v in inputs.items()}
    a = {}
    a["x"] = i["x"].reshape(B * S, D)
    ctx = np.concatenate([i["ctx_1024"], np.zeros((AHEAD, KV, D), np.float32)]).reshape(-1, D)
    a["ctx"] = ctx
    a["ctxT"] = ctx.T
    mask = np.concatenate([i["mask_Bx1xSxS2_ik0"][:, 0], np.zeros((AHEAD, S, KV), np.int32)])
    a["mask"] = mask.reshape(-1, KV)
    a["key_mask"] = i["mask_BxS2_bf1"].view(np.uint8).reshape(1, B * KV)
    a["time_bias"] = np.concatenate([i["fside_BxS2_0"], np.zeros((AHEAD, KV), np.float32)]).reshape(1, -1)
    by_parity = np.arange(D).reshape(HEADS // 2, 2, D // HEADS).transpose(1, 2, 0).reshape(-1)
    for n, v in i.items():
        if n[0] != "L":
            continue
        if n in ("L0_ffn_router_w", "L0_ffn_w1", "L0_ffn_w2", "L1_xattn_Wv", "L1_xattn_Wk", "L1_xattn_Wq", "L1_xattn_Wo",
                 "L1_ffn_w1", "L1_ffn_w2", "L2_xattn_Wout"):
            v = v.T
        elif v.ndim == 1:
            v = v.reshape(1, -1)
        if n in ("L1_xattn_Wq", "L1_xattn_Wk", "L3_xattn_wq", "L3_xattn_wk", "L3_xattn_bq", "L3_xattn_bk"):
            v = v[:, by_parity]
        if n == "L2_xattn_Wkv":
            a["L2_xattn_Wk"], a["L2_xattn_Wv"] = v[:HEADS * 64], v[HEADS * 64:].T
            continue
        if n == "L3_xattn_bv":
            v = v.reshape(4, 4 * D // HEADS).T
        a[n] = v
    a["consts"] = shape_constants()
    return {n: np.ascontiguousarray(v) for n, v in a.items()}


def kernel(**inputs):
    import concourse.bacc as bacc
    from concourse.bass_utils import run_bass_kernel_spmd

    arrays = lay_out(inputs)
    nc = bacc.Bacc("TRN2", target_bir_lowering=False, num_devices=1)
    dram = {n: nc.dram_tensor(f"in_{n}", v.shape, mybir.dt.from_np(v.dtype), kind="ExternalInput").ap()
            for n, v in arrays.items()}
    out = nc.dram_tensor("out_x", (B * S, D), F32, kind="ExternalOutput").ap()
    program(nc, dram, out)
    r = run_bass_kernel_spmd(nc, [{f"in_{n}": v for n, v in arrays.items()}], core_ids=[0])
    return np.asarray(r.results[0]["out_x"]).reshape(B, S, D)
```
